# Optimizing a Trainium2 kernel written in Bass

```python
import numpy as np
import jax
import jax.numpy as jnp

def _softmax(x, axis=-1):
    return jax.nn.softmax(x, axis=axis)

def _gelu(x):
    return jax.nn.gelu(x, approximate=True)

def _silu(x):
    return jax.nn.silu(x)

def _sigmoid(x):
    return jax.nn.sigmoid(x)

def _layernorm(x, axis=-1, eps=1e-05):
    m = jnp.mean(x, axis=axis, keepdims=True)
    v = jnp.var(x, axis=axis, keepdims=True)
    return (x - m) / jnp.sqrt(v + eps)

def _scatter_add(tgt, idx, src, axis=0):
    return tgt.at[idx].add(src)

def _segment_sum(src, seg, n):
    return jax.ops.segment_sum(src, seg, n)
kernel_name = 'mk_recurrent_d4_jaxref_r8_52b260'

def setup_inputs(seed: int=0):
    np.random.seed(seed)
    _w = jnp.asarray

    def _L0_attn_setup():
        import jax, jax.numpy as jnp
        import numpy as np
        B, T, D_IN = (8, 512, 256)
        D_HIDDEN = 256
        D_OUT = 256
        N_BLOCKS = 8
        R_MIN, R_MAX = (0.9, 0.999)
        INIT_IMAG = 0.1

        def _lecun(key, shape, fan_in):
            return (jax.random.normal(key, shape, dtype=jnp.float32) * np.sqrt(1.0 / fan_in)).astype(jnp.float32)

        def _block_diag_linear(x, W, b):
            h, i, j = W.shape
            xb = x.reshape(x.shape[0], x.shape[1], h, i)
            y = jnp.einsum('bthi,hij->bthj', xb, W) + b
            return y.reshape(y.shape[0], y.shape[1], h * j)

        def _linear_scan(a, x):

            def combine(l, r):
                al, bl = l
                ar, br = r
                return (al * ar, ar * bl + br)
            _, h = jax.lax.associative_scan(combine, (a, x), axis=1)
            return h

        def _reference_tuple_inner(x, W_in, b_in, W_gx, b_gx, W_ga, b_ga, a_real, a_imag, W_out, b_out):
            xh = x @ W_in + b_in
            gate_x = jax.nn.sigmoid(_block_diag_linear(xh, W_gx, b_gx))
            gate_a = jax.nn.sigmoid(_block_diag_linear(xh, W_ga, b_ga))
            log_a_re = -8.0 * gate_a * jax.nn.softplus(a_real)
            log_a_im = a_imag * gate_a
            a = jnp.exp(jax.lax.complex(log_a_re, log_a_im))
            a_sq = jnp.exp(jax.lax.complex(2.0 * log_a_re, 2.0 * log_a_im))
            xr, xi = jnp.split(xh, 2, axis=-1)
            xc = jax.lax.complex(xr, xi) * gate_x
            xc = jnp.sqrt(1.0 - a_sq) * xc
            h = _linear_scan(a, xc)
            h_m = jnp.concatenate([h.real, h.imag], axis=-1)
            out = h_m @ W_out + b_out
            h_last = h_m[:, -1]
            return (out, h_last)
        key = jax.random.key(seed)
        ks = jax.random.split(key, 12)
        dh2 = D_HIDDEN // 2
        bin_, bout = (dh2 // N_BLOCKS, None)
        blk_in = D_HIDDEN // N_BLOCKS
        blk_out = dh2 // N_BLOCKS
        u1 = jax.random.uniform(ks[8], (dh2,))
        a_r = 0.5 * jnp.log(u1 * (R_MAX ** 2 - R_MIN ** 2) + R_MIN ** 2 + 1e-08)
        a_real = jnp.log(jnp.exp(-a_r) - 1.0)
        u2 = jax.random.uniform(ks[9], (dh2,))
        a_imag = jnp.pi * INIT_IMAG * u2
        return {'x': jax.random.normal(ks[0], (B, T, D_IN), dtype=jnp.float32), 'W_in': _lecun(ks[1], (D_IN, D_HIDDEN), D_IN), 'b_in': jnp.zeros((D_HIDDEN,), jnp.float32), 'W_gx': _lecun(ks[2], (N_BLOCKS, blk_in, blk_out), blk_in), 'b_gx': _lecun(ks[3], (N_BLOCKS, blk_out), blk_in), 'W_ga': _lecun(ks[4], (N_BLOCKS, blk_in, blk_out), blk_in), 'b_ga': _lecun(ks[5], (N_BLOCKS, blk_out), blk_in), 'a_real': a_real, 'a_imag': a_imag, 'W_out': _lecun(ks[6], (D_HIDDEN, D_OUT), D_HIDDEN), 'b_out': jnp.zeros((D_OUT,), jnp.float32)}
    _L0_attn_in = _L0_attn_setup()

    def _L0_ffn_setup():
        import jax, jax.numpy as jnp
        import numpy as np
        B, S, D, I, E, K = (4, 128, 256, 128, 8, 2)
        key = jax.random.key(seed)
        ks = jax.random.split(key, 7)

        def w(k, shape, fan_in):
            return jax.random.normal(k, shape, dtype=jnp.float32) * fan_in ** (-0.5)
        return {'hidden_states': jax.random.normal(ks[0], (B, S, D), dtype=jnp.float32), 'router_w': w(ks[1], (D, E), D), 'gate_up_w': w(ks[2], (E, D, 2 * I), D), 'down_w': w(ks[3], (E, I, D), I), 'shared_gate_w': w(ks[4], (D, I), D), 'shared_up_w': w(ks[5], (D, I), D), 'shared_down_w': w(ks[6], (I, D), I)}
    _L0_ffn_in = _L0_ffn_setup()

    def _L1_attn_setup():
        import jax, jax.numpy as jnp
        import numpy as np
        B_, L_, D_, E_, N_, R_, K_ = (2, 256, 256, 512, 16, 128, 4)
        key = jax.random.key(seed)
        ks = jax.random.split(key, 12)
        s = lambda k, shape, scale: jax.random.normal(k, shape, dtype=jnp.float32) * scale
        return {'resid': s(ks[0], (B_, L_, D_), 1.0), 'norm_w': jnp.ones((D_,), jnp.float32), 'W_skip': s(ks[1], (E_, D_), D_ ** (-0.5)), 'W_in': s(ks[2], (E_, D_), D_ ** (-0.5)), 'conv_w': s(ks[3], (E_, 1, K_), K_ ** (-0.5)), 'conv_b': s(ks[4], (E_,), 0.02), 'W_d1': s(ks[5], (R_, E_), E_ ** (-0.5)), 'W_d2': s(ks[6], (E_, R_), R_ ** (-0.5)), 'b_d2': s(ks[7], (E_,), 0.02) - 2.0, 'W_Bm': s(ks[8], (N_, E_), E_ ** (-0.5)), 'W_Cm': s(ks[9], (N_, E_), E_ ** (-0.5)), 'A_log': s(ks[10], (E_, N_), 0.5), 'W_D': jnp.ones((E_,), jnp.float32), 'W_out': s(ks[11], (D_, E_), E_ ** (-0.5))}
    _L1_attn_in = _L1_attn_setup()

    def _L1_ffn_setup():
        import jax, jax.numpy as jnp
        import numpy as np
        HID = 256
        INTER = 1024
        NEXP = 8
        TOPK = 2
        EPS = 1e-05

        def _mock_fused_moe(x, selected_experts, routing_weights, expert_weight):
            y = jnp.einsum('bsh,hd->bsd', x, expert_weight)
            scale = routing_weights.sum(axis=-1, keepdims=True)
            return y * scale
        key = jax.random.key(seed)
        ks = jax.random.split(key, 6)
        s = lambda fan_in: 1.0 / np.sqrt(fan_in)
        return {'hidden_states': jax.random.normal(ks[0], (4, 512, HID), dtype=jnp.float32), 'gate_w': jax.random.uniform(ks[1], (HID, NEXP), jnp.float32, -s(HID), s(HID)), 'up_w': jax.random.uniform(ks[2], (HID, INTER), jnp.float32, -s(HID), s(HID)), 'down_w': jax.random.uniform(ks[3], (INTER, HID), jnp.float32, -s(INTER), s(INTER)), 'expert_weight': jax.random.normal(ks[4], (HID, HID), dtype=jnp.float32), 'ln_gamma': jnp.ones((HID,), jnp.float32), 'ln_beta': jnp.zeros((HID,), jnp.float32)}
    _L1_ffn_in = _L1_ffn_setup()

    def _L2_attn_setup():
        import jax, jax.numpy as jnp
        import numpy as np
        B, T, HID, H = (2, 256, 256, 16)
        D = HID // H

        def apply_rope(x):
            b, t, h, d = x.shape
            half = d // 2
            x1, x2 = (x[..., :half], x[..., half:])
            theta = 1.0 / 10000.0 ** (jnp.arange(0, half, 2, dtype=jnp.float32) / half)
            pos = jnp.arange(t, dtype=jnp.float32)
            freq = pos[:, None] * theta[None, :]
            sin = jnp.sin(freq)[None, :, None, :]
            cos = jnp.cos(freq)[None, :, None, :]
            x1e, x1o = (x1[..., ::2], x1[..., 1::2])
            x2e, x2o = (x2[..., ::2], x2[..., 1::2])
            x1r = jnp.concatenate([x1e * cos - x1o * sin, x1e * sin + x1o * cos], axis=-1)
            x2r = jnp.concatenate([x2e * cos - x2o * sin, x2e * sin + x2o * cos], axis=-1)
            return jnp.concatenate([x1r, x2r], axis=-1)
        key = jax.random.key(seed)
        ks = jax.random.split(key, 5)
        s = 0.02
        return {'hidden_states': jax.random.normal(ks[0], (B, T, HID), dtype=jnp.float32), 'Wq': jax.random.normal(ks[1], (HID, HID), dtype=jnp.float32) * s, 'Wk': jax.random.normal(ks[2], (D, HID), dtype=jnp.float32) * s, 'Wv': jax.random.normal(ks[3], (D, HID), dtype=jnp.float32) * s, 'Wo': jax.random.normal(ks[4], (HID, HID), dtype=jnp.float32) * s}
    _L2_attn_in = _L2_attn_setup()

    def _L2_ffn_setup():
        import jax, jax.numpy as jnp
        import numpy as np
        B, S, H = (1, 256, 256)
        E, K, I = (16, 4, 176)
        IS = 352
        CAP = 128
        key = jax.random.key(seed)
        ks = jax.random.split(key, 8)
        sc = 0.02
        return {'hidden_states': jax.random.normal(ks[0], (B, S, H), jnp.float32), 'gate_w': jax.random.normal(ks[1], (E, H), jnp.float32) * sc, 'w_gate': jax.random.normal(ks[2], (E, H, I), jnp.float32) * sc, 'w_up': jax.random.normal(ks[3], (E, H, I), jnp.float32) * sc, 'w_down': jax.random.normal(ks[4], (E, I, H), jnp.float32) * sc, 'sw_gate': jax.random.normal(ks[5], (H, IS), jnp.float32) * sc, 'sw_up': jax.random.normal(ks[6], (H, IS), jnp.float32) * sc, 'sw_down': jax.random.normal(ks[7], (IS, H), jnp.float32) * sc}
    _L2_ffn_in = _L2_ffn_setup()

    def _L3_attn_setup():
        import jax, jax.numpy as jnp
        import numpy as np
        D_MODEL = 256
        N_HEADS = 16
        D_HEAD = 128
        D_LATENT = 64
        key = jax.random.key(seed)
        ks = jax.random.split(key, 5)
        s = lambda fan_in: 1.0 / np.sqrt(fan_in)
        x = jax.random.normal(ks[0], (2, 256, D_MODEL), dtype=jnp.float32)
        W_q = jax.random.uniform(ks[1], (D_MODEL, N_HEADS * D_HEAD), jnp.float32, -s(D_MODEL), s(D_MODEL))
        W_kv_down = jax.random.uniform(ks[2], (D_MODEL, D_LATENT), jnp.float32, -s(D_MODEL), s(D_MODEL))
        W_kv_up = jax.random.uniform(ks[3], (D_LATENT, N_HEADS * D_HEAD), jnp.float32, -s(D_LATENT), s(D_LATENT))
        W_o = jax.random.uniform(ks[4], (N_HEADS * D_HEAD, D_MODEL), jnp.float32, -s(N_HEADS * D_HEAD), s(N_HEADS * D_HEAD))
        return {'x': x, 'W_q': W_q, 'W_kv_down': W_kv_down, 'W_kv_up': W_kv_up, 'W_o': W_o}
    _L3_attn_in = _L3_attn_setup()

    def _L3_ffn_setup():
        import jax, jax.numpy as jnp
        import numpy as np
        BLOCK_SIZE = 32
        HIDDEN_SIZE = 256
        MLP_DIM = 2048
        NVFP4_LUT = jnp.array([0.0, 0.5, 1.0, 1.5, 2.0, 3.0, 4.0, 6.0, 0.0, -0.5, -1.0, -1.5, -2.0, -3.0, -4.0, -6.0], dtype=jnp.float32)

        def dequant_nvfp4(W_packed, scales, block=BLOCK_SIZE):
            N = W_packed.shape[0]
            low = W_packed & 15
            high = W_packed >> 4 & 15
            idx = jnp.stack([low, high], axis=-1).reshape(N, -1)
            vals = NVFP4_LUT[idx]
            K = vals.shape[1]
            vals = vals.reshape(N, K // block, block) * scales[:, :, None]
            return vals.reshape(N, K)
        key = jax.random.key(seed)
        ks = jax.random.split(key, 7)
        x = jax.random.normal(ks[0], (4, 32, HIDDEN_SIZE), dtype=jnp.float32)
        gate_W_packed = jax.random.randint(ks[1], (MLP_DIM, HIDDEN_SIZE // 2), 0, 32, dtype=jnp.int32)
        gate_scales = jax.random.uniform(ks[2], (MLP_DIM, HIDDEN_SIZE // BLOCK_SIZE), dtype=jnp.float32) * 0.1 + 0.001
        up_W_packed = jax.random.randint(ks[3], (MLP_DIM, HIDDEN_SIZE // 2), 0, 32, dtype=jnp.int32)
        up_scales = jax.random.uniform(ks[4], (MLP_DIM, HIDDEN_SIZE // BLOCK_SIZE), dtype=jnp.float32) * 0.1 + 0.001
        down_W_packed = jax.random.randint(ks[5], (HIDDEN_SIZE, MLP_DIM // 2), 0, 32, dtype=jnp.int32)
        down_scales = jax.random.uniform(ks[6], (HIDDEN_SIZE, MLP_DIM // BLOCK_SIZE), dtype=jnp.float32) * 0.1 + 0.001
        return {'x': x, 'gate_W_packed': gate_W_packed, 'gate_scales': gate_scales, 'up_W_packed': up_W_packed, 'up_scales': up_scales, 'down_W_packed': down_W_packed, 'down_scales': down_scales}
    _L3_ffn_in = _L3_ffn_setup()
    _d = {'L0_attn_x': _L0_attn_in['x'], 'L0_attn_W_in': _L0_attn_in['W_in'], 'L0_attn_b_in': _L0_attn_in['b_in'], 'L0_attn_W_gx': _L0_attn_in['W_gx'], 'L0_attn_b_gx': _L0_attn_in['b_gx'], 'L0_attn_W_ga': _L0_attn_in['W_ga'], 'L0_attn_b_ga': _L0_attn_in['b_ga'], 'L0_attn_a_real': _L0_attn_in['a_real'], 'L0_attn_a_imag': _L0_attn_in['a_imag'], 'L0_attn_W_out': _L0_attn_in['W_out'], 'L0_attn_b_out': _L0_attn_in['b_out'], 'L0_ffn_router_w': _L0_ffn_in['router_w'], 'L0_ffn_gate_up_w': _L0_ffn_in['gate_up_w'], 'L0_ffn_down_w': _L0_ffn_in['down_w'], 'L0_ffn_shared_gate_w': _L0_ffn_in['shared_gate_w'], 'L0_ffn_shared_up_w': _L0_ffn_in['shared_up_w'], 'L0_ffn_shared_down_w': _L0_ffn_in['shared_down_w'], 'L1_attn_norm_w': _L1_attn_in['norm_w'], 'L1_attn_W_skip': _L1_attn_in['W_skip'], 'L1_attn_W_in': _L1_attn_in['W_in'], 'L1_attn_conv_w': _L1_attn_in['conv_w'], 'L1_attn_conv_b': _L1_attn_in['conv_b'], 'L1_attn_W_d1': _L1_attn_in['W_d1'], 'L1_attn_W_d2': _L1_attn_in['W_d2'], 'L1_attn_b_d2': _L1_attn_in['b_d2'], 'L1_attn_W_Bm': _L1_attn_in['W_Bm'], 'L1_attn_W_Cm': _L1_attn_in['W_Cm'], 'L1_attn_A_log': _L1_attn_in['A_log'], 'L1_attn_W_D': _L1_attn_in['W_D'], 'L1_attn_W_out': _L1_attn_in['W_out'], 'L1_ffn_gate_w': _L1_ffn_in['gate_w'], 'L1_ffn_up_w': _L1_ffn_in['up_w'], 'L1_ffn_down_w': _L1_ffn_in['down_w'], 'L1_ffn_expert_weight': _L1_ffn_in['expert_weight'], 'L1_ffn_ln_gamma': _L1_ffn_in['ln_gamma'], 'L1_ffn_ln_beta': _L1_ffn_in['ln_beta'], 'L2_attn_Wq': _L2_attn_in['Wq'], 'L2_attn_Wk': _L2_attn_in['Wk'], 'L2_attn_Wv': _L2_attn_in['Wv'], 'L2_attn_Wo': _L2_attn_in['Wo'], 'L2_ffn_gate_w': _L2_ffn_in['gate_w'], 'L2_ffn_w_gate': _L2_ffn_in['w_gate'], 'L2_ffn_w_up': _L2_ffn_in['w_up'], 'L2_ffn_w_down': _L2_ffn_in['w_down'], 'L2_ffn_sw_gate': _L2_ffn_in['sw_gate'], 'L2_ffn_sw_up': _L2_ffn_in['sw_up'], 'L2_ffn_sw_down': _L2_ffn_in['sw_down'], 'L3_attn_W_q': _L3_attn_in['W_q'], 'L3_attn_W_kv_down': _L3_attn_in['W_kv_down'], 'L3_attn_W_kv_up': _L3_attn_in['W_kv_up'], 'L3_attn_W_o': _L3_attn_in['W_o'], 'L3_ffn_gate_W_packed': _L3_ffn_in['gate_W_packed'], 'L3_ffn_gate_scales': _L3_ffn_in['gate_scales'], 'L3_ffn_up_W_packed': _L3_ffn_in['up_W_packed'], 'L3_ffn_up_scales': _L3_ffn_in['up_scales'], 'L3_ffn_down_W_packed': _L3_ffn_in['down_W_packed'], 'L3_ffn_down_scales': _L3_ffn_in['down_scales']}
    _x0 = _d['L0_attn_x']
    _d['L0_attn_x'] = jax.random.normal(jax.random.fold_in(jax.random.key(seed), 1), (4, 256, 256), dtype=_x0.dtype)
    del _x0
    return _d

def reference(L0_attn_x, L0_attn_W_in, L0_attn_b_in, L0_attn_W_gx, L0_attn_b_gx, L0_attn_W_ga, L0_attn_b_ga, L0_attn_a_real, L0_attn_a_imag, L0_attn_W_out, L0_attn_b_out, L0_ffn_router_w, L0_ffn_gate_up_w, L0_ffn_down_w, L0_ffn_shared_gate_w, L0_ffn_shared_up_w, L0_ffn_shared_down_w, L1_attn_norm_w, L1_attn_W_skip, L1_attn_W_in, L1_attn_conv_w, L1_attn_conv_b, L1_attn_W_d1, L1_attn_W_d2, L1_attn_b_d2, L1_attn_W_Bm, L1_attn_W_Cm, L1_attn_A_log, L1_attn_W_D, L1_attn_W_out, L1_ffn_gate_w, L1_ffn_up_w, L1_ffn_down_w, L1_ffn_expert_weight, L1_ffn_ln_gamma, L1_ffn_ln_beta, L2_attn_Wq, L2_attn_Wk, L2_attn_Wv, L2_attn_Wo, L2_ffn_gate_w, L2_ffn_w_gate, L2_ffn_w_up, L2_ffn_w_down, L2_ffn_sw_gate, L2_ffn_sw_up, L2_ffn_sw_down, L3_attn_W_q, L3_attn_W_kv_down, L3_attn_W_kv_up, L3_attn_W_o, L3_ffn_gate_W_packed, L3_ffn_gate_scales, L3_ffn_up_W_packed, L3_ffn_up_scales, L3_ffn_down_W_packed, L3_ffn_down_scales):

    def _L0_attn_ref(x, W_in, b_in, W_gx, b_gx, W_ga, b_ga, a_real, a_imag, W_out, b_out):
        import jax, jax.numpy as jnp
        import numpy as np
        B, T, D_IN = (8, 512, 256)
        D_HIDDEN = 256
        D_OUT = 256
        N_BLOCKS = 8
        R_MIN, R_MAX = (0.9, 0.999)
        INIT_IMAG = 0.1

        def _lecun(key, shape, fan_in):
            return (jax.random.normal(key, shape, dtype=jnp.float32) * np.sqrt(1.0 / fan_in)).astype(jnp.float32)

        def _block_diag_linear(x, W, b):
            h, i, j = W.shape
            xb = x.reshape(x.shape[0], x.shape[1], h, i)
            y = jnp.einsum('bthi,hij->bthj', xb, W) + b
            return y.reshape(y.shape[0], y.shape[1], h * j)

        def _linear_scan(a, x):

            def combine(l, r):
                al, bl = l
                ar, br = r
                return (al * ar, ar * bl + br)
            _, h = jax.lax.associative_scan(combine, (a, x), axis=1)
            return h

        def _reference_tuple_inner(x, W_in, b_in, W_gx, b_gx, W_ga, b_ga, a_real, a_imag, W_out, b_out):
            xh = x @ W_in + b_in
            gate_x = jax.nn.sigmoid(_block_diag_linear(xh, W_gx, b_gx))
            gate_a = jax.nn.sigmoid(_block_diag_linear(xh, W_ga, b_ga))
            log_a_re = -8.0 * gate_a * jax.nn.softplus(a_real)
            log_a_im = a_imag * gate_a
            a = jnp.exp(jax.lax.complex(log_a_re, log_a_im))
            a_sq = jnp.exp(jax.lax.complex(2.0 * log_a_re, 2.0 * log_a_im))
            xr, xi = jnp.split(xh, 2, axis=-1)
            xc = jax.lax.complex(xr, xi) * gate_x
            xc = jnp.sqrt(1.0 - a_sq) * xc
            h = _linear_scan(a, xc)
            h_m = jnp.concatenate([h.real, h.imag], axis=-1)
            out = h_m @ W_out + b_out
            h_last = h_m[:, -1]
            return (out, h_last)
        return _reference_tuple_inner(x, W_in, b_in, W_gx, b_gx, W_ga, b_ga, a_real, a_imag, W_out, b_out)[0]

    def _L0_ffn_ref(hidden_states, router_w, gate_up_w, down_w, shared_gate_w, shared_up_w, shared_down_w):
        import jax, jax.numpy as jnp
        import numpy as np
        B, S, D, I, E, K = (4, 128, 256, 128, 8, 2)
        Bb, Ss, Dd = hidden_states.shape
        x = hidden_states.reshape(-1, Dd)
        T = x.shape[0]
        shared = jax.nn.silu(x @ shared_gate_w) * (x @ shared_up_w) @ shared_down_w
        logits = x @ router_w
        top_val, top_idx = jax.lax.top_k(logits, K)
        probs = jnp.zeros_like(logits).at[jnp.arange(T)[:, None], top_idx].set(jax.nn.sigmoid(top_val))
        xin = probs.T[:, :, None] * x[None]
        gu = jnp.einsum('etd,edf->etf', xin, gate_up_w)
        gate, up = jnp.split(gu, 2, axis=-1)
        h = jax.nn.silu(gate) * up
        expert_out = jnp.einsum('eti,eid->etd', h, down_w)
        combined = shared + expert_out.sum(axis=0)
        return combined.reshape(Bb, Ss, Dd)

    def _L1_attn_ref(resid, norm_w, W_skip, W_in, conv_w, conv_b, W_d1, W_d2, b_d2, W_Bm, W_Cm, A_log, W_D, W_out):
        import jax, jax.numpy as jnp
        import numpy as np
        B_, L_, D_, E_, N_, R_, K_ = (2, 256, 256, 512, 16, 128, 4)
        eps = 1e-05
        E, K = (conv_w.shape[0], conv_w.shape[-1])
        x = resid * jax.lax.rsqrt(jnp.mean(resid * resid, -1, keepdims=True) + eps) * norm_w
        skip = x @ W_skip.T
        x = x @ W_in.T
        xc = jnp.swapaxes(x, 1, 2)
        xc = jax.lax.conv_general_dilated(xc, conv_w, (1,), [(K - 1, 0)], dimension_numbers=('NCH', 'OIH', 'NCH'), feature_group_count=E)
        xc = xc + conv_b[None, :, None]
        x = jax.nn.silu(jnp.swapaxes(xc, 1, 2))
        A = -jnp.exp(A_log)
        delta = jax.nn.softplus(x @ W_d1.T @ W_d2.T + b_d2)
        Bt = x @ W_Bm.T
        Ct = x @ W_Cm.T

        def step(h, inp):
            x_t, d_t, b_t, c_t = inp
            h = jnp.exp(d_t[:, :, None] * A) * h + (d_t * x_t)[:, :, None] * b_t[:, None, :]
            y = jnp.einsum('ben,bn->be', h, c_t)
            return (h, y)
        xs = (jnp.swapaxes(x, 0, 1), jnp.swapaxes(delta, 0, 1), jnp.swapaxes(Bt, 0, 1), jnp.swapaxes(Ct, 0, 1))
        h0 = jnp.zeros((x.shape[0], A.shape[0], A.shape[1]), x.dtype)
        _, ys = jax.lax.scan(step, h0, xs)
        y = jnp.swapaxes(ys, 0, 1)
        y = y + x * W_D
        y = y * jax.nn.silu(skip)
        return resid + y @ W_out.T

    def _L1_ffn_ref(hidden_states, gate_w, up_w, down_w, expert_weight, ln_gamma, ln_beta):
        import jax, jax.numpy as jnp
        import numpy as np
        HID = 256
        INTER = 1024
        NEXP = 8
        TOPK = 2
        EPS = 1e-05

        def _mock_fused_moe(x, selected_experts, routing_weights, expert_weight):
            y = jnp.einsum('bsh,hd->bsd', x, expert_weight)
            scale = routing_weights.sum(axis=-1, keepdims=True)
            return y * scale
        residuals = hidden_states
        logits = jnp.einsum('bsh,he->bse', hidden_states, gate_w)
        routing_weights, selected_experts = jax.lax.top_k(logits, TOPK)
        h = jnp.einsum('bsh,hi->bsi', residuals, up_w)
        h = jnp.square(jax.nn.relu(h))
        shared_out = jnp.einsum('bsi,ih->bsh', h, down_w)
        moe_out = _mock_fused_moe(hidden_states, selected_experts, routing_weights, expert_weight)
        y = shared_out + moe_out
        mu = y.mean(axis=-1, keepdims=True)
        var = jnp.mean(jnp.square(y - mu), axis=-1, keepdims=True)
        return (y - mu) * jax.lax.rsqrt(var + EPS) * ln_gamma + ln_beta

    def _L2_attn_ref(hidden_states, Wq, Wk, Wv, Wo):
        import jax, jax.numpy as jnp
        import numpy as np
        B, T, HID, H = (2, 256, 256, 16)
        D = HID // H

        def apply_rope(x):
            b, t, h, d = x.shape
            half = d // 2
            x1, x2 = (x[..., :half], x[..., half:])
            theta = 1.0 / 10000.0 ** (jnp.arange(0, half, 2, dtype=jnp.float32) / half)
            pos = jnp.arange(t, dtype=jnp.float32)
            freq = pos[:, None] * theta[None, :]
            sin = jnp.sin(freq)[None, :, None, :]
            cos = jnp.cos(freq)[None, :, None, :]
            x1e, x1o = (x1[..., ::2], x1[..., 1::2])
            x2e, x2o = (x2[..., ::2], x2[..., 1::2])
            x1r = jnp.concatenate([x1e * cos - x1o * sin, x1e * sin + x1o * cos], axis=-1)
            x2r = jnp.concatenate([x2e * cos - x2o * sin, x2e * sin + x2o * cos], axis=-1)
            return jnp.concatenate([x1r, x2r], axis=-1)
        b, t, _ = hidden_states.shape
        scaling = D ** (-0.5)
        q = (hidden_states @ Wq.T).reshape(b, t, H, D).transpose(0, 2, 1, 3)
        k = hidden_states @ Wk.T
        v = hidden_states @ Wv.T
        q = apply_rope(q)
        k = apply_rope(k[:, None])
        v = v[:, None]
        scores = jnp.einsum('bhqd,bokd->bhqk', q, k) * scaling
        causal = jnp.tril(jnp.ones((t, t), dtype=bool))
        scores = jnp.where(causal[None, None], scores, -jnp.inf)
        probs = jax.nn.softmax(scores, axis=-1)
        attn = jnp.einsum('bhqk,bokd->bhqd', probs, v)
        attn = attn.transpose(0, 2, 1, 3).reshape(b, t, HID)
        return attn @ Wo.T

    def _L2_ffn_ref(hidden_states, gate_w, w_gate, w_up, w_down, sw_gate, sw_up, sw_down):
        import jax, jax.numpy as jnp
        import numpy as np
        B, S, H = (1, 256, 256)
        E, K, I = (16, 4, 176)
        IS = 352
        CAP = 128
        b, s, h = hidden_states.shape
        x = hidden_states.reshape(-1, h)
        T = x.shape[0]
        scores = jax.nn.softmax(x @ gate_w.T, axis=-1)
        topk_w, topk_i = jax.lax.top_k(scores, K)
        topk_w = topk_w / (topk_w.sum(-1, keepdims=True) + 1e-20)
        flat_i = topk_i.reshape(-1)
        flat_w = topk_w.reshape(-1)
        order = jnp.argsort(flat_i)
        se = flat_i[order]
        counts = jax.ops.segment_sum(jnp.ones_like(flat_i), flat_i, num_segments=E)
        starts = jnp.cumsum(counts) - counts
        rank = jnp.arange(T * K) - starts[se]
        tok = order // K
        slot = jnp.where(rank < CAP, rank, CAP)
        buf = jnp.full((E, CAP + 1), T, dtype=jnp.int32).at[se, slot].set(tok)[:, :CAP]
        wbuf = jnp.zeros((E, CAP + 1), x.dtype).at[se, slot].set(flat_w[order])[:, :CAP]
        xpad = jnp.concatenate([x, jnp.zeros((1, h), x.dtype)], axis=0)
        xg = xpad[buf]
        gact = jax.nn.silu(jnp.einsum('ech,ehi->eci', xg, w_gate))
        mid = gact * jnp.einsum('ech,ehi->eci', xg, w_up)
        eout = jnp.einsum('eci,eih->ech', mid, w_down) * wbuf[..., None]
        y = jnp.zeros((T + 1, h), x.dtype).at[buf.reshape(-1)].add(eout.reshape(-1, h))[:T]
        shared = jax.nn.silu(x @ sw_gate) * (x @ sw_up) @ sw_down
        return (y + shared).reshape(b, s, h)

    def _L3_attn_ref(x, W_q, W_kv_down, W_kv_up, W_o):
        import jax, jax.numpy as jnp
        import numpy as np
        D_MODEL = 256
        N_HEADS = 16
        D_HEAD = 128
        D_LATENT = 64
        B, S, _ = x.shape
        q = (x @ W_q).reshape(B, S, N_HEADS, D_HEAD).transpose(0, 2, 1, 3)
        latent = x @ W_kv_down
        kv = (latent @ W_kv_up).reshape(B, S, N_HEADS, D_HEAD).transpose(0, 2, 1, 3)
        scale = 1.0 / np.sqrt(D_HEAD).astype(np.float32)
        scores = jnp.einsum('bhqd,bhkd->bhqk', q, kv) * scale
        probs = jax.nn.softmax(scores, axis=-1)
        out = jnp.einsum('bhqk,bhkd->bhqd', probs, kv)
        out = out.transpose(0, 2, 1, 3).reshape(B, S, N_HEADS * D_HEAD)
        return out @ W_o

    def _L3_ffn_ref(x, gate_W_packed, gate_scales, up_W_packed, up_scales, down_W_packed, down_scales):
        import jax, jax.numpy as jnp
        import numpy as np
        BLOCK_SIZE = 32
        HIDDEN_SIZE = 256
        MLP_DIM = 2048
        NVFP4_LUT = jnp.array([0.0, 0.5, 1.0, 1.5, 2.0, 3.0, 4.0, 6.0, 0.0, -0.5, -1.0, -1.5, -2.0, -3.0, -4.0, -6.0], dtype=jnp.float32)

        def dequant_nvfp4(W_packed, scales, block=BLOCK_SIZE):
            N = W_packed.shape[0]
            low = W_packed & 15
            high = W_packed >> 4 & 15
            idx = jnp.stack([low, high], axis=-1).reshape(N, -1)
            vals = NVFP4_LUT[idx]
            K = vals.shape[1]
            vals = vals.reshape(N, K // block, block) * scales[:, :, None]
            return vals.reshape(N, K)
        B, S, H = x.shape
        xt = x.reshape(B * S, H)
        Wg = dequant_nvfp4(gate_W_packed, gate_scales)
        Wu = dequant_nvfp4(up_W_packed, up_scales)
        Wd = dequant_nvfp4(down_W_packed, down_scales)
        gate = jnp.einsum('th,nh->tn', xt, Wg)
        up = jnp.einsum('th,nh->tn', xt, Wu)
        gelu = jnp.tanh(0.7978845608028654 * (gate + 0.044715 * gate ** 3)) * gate * 0.5 + gate * 0.5
        inter = gelu * up
        out = jnp.einsum('tn,hn->th', inter, Wd)
        return out.reshape(B, S, H)
    x = L0_attn_x
    xn = _layernorm(x, axis=-1)
    s = _L0_attn_ref(xn, L0_attn_W_in, L0_attn_b_in, L0_attn_W_gx, L0_attn_b_gx, L0_attn_W_ga, L0_attn_b_ga, L0_attn_a_real, L0_attn_a_imag, L0_attn_W_out, L0_attn_b_out)
    g = _silu(_L0_ffn_ref(xn, L0_ffn_router_w, L0_ffn_gate_up_w, L0_ffn_down_w, L0_ffn_shared_gate_w, L0_ffn_shared_up_w, L0_ffn_shared_down_w))
    x = x + s * g
    xn = _layernorm(x, axis=-1)
    s = _L1_attn_ref(xn, L1_attn_norm_w, L1_attn_W_skip, L1_attn_W_in, L1_attn_conv_w, L1_attn_conv_b, L1_attn_W_d1, L1_attn_W_d2, L1_attn_b_d2, L1_attn_W_Bm, L1_attn_W_Cm, L1_attn_A_log, L1_attn_W_D, L1_attn_W_out)
    g = _silu(_L1_ffn_ref(xn, L1_ffn_gate_w, L1_ffn_up_w, L1_ffn_down_w, L1_ffn_expert_weight, L1_ffn_ln_gamma, L1_ffn_ln_beta))
    x = x + s * g
    xn = _layernorm(x, axis=-1)
    s = _L2_attn_ref(xn, L2_attn_Wq, L2_attn_Wk, L2_attn_Wv, L2_attn_Wo)
    g = _silu(_L2_ffn_ref(xn, L2_ffn_gate_w, L2_ffn_w_gate, L2_ffn_w_up, L2_ffn_w_down, L2_ffn_sw_gate, L2_ffn_sw_up, L2_ffn_sw_down))
    x = x + s * g
    xn = _layernorm(x, axis=-1)
    s = _L3_attn_ref(xn, L3_attn_W_q, L3_attn_W_kv_down, L3_attn_W_kv_up, L3_attn_W_o)
    g = _silu(_L3_ffn_ref(xn, L3_ffn_gate_W_packed, L3_ffn_gate_scales, L3_ffn_up_W_packed, L3_ffn_up_scales, L3_ffn_down_W_packed, L3_ffn_down_scales))
    x = x + s * g
    return x

_drawn_inputs = setup_inputs


def setup_inputs(seed=0):
    import zlib

    import numpy as np

    out = dict(_drawn_inputs(seed))
    spreads = {'L0_attn_b_in': (0.0, 0.1),
     'L0_attn_b_out': (0.0, 0.1),
     'L1_attn_norm_w': (1.0, 0.2),
     'L1_attn_W_D': (1.0, 0.2),
     'L1_ffn_ln_gamma': (1.0, 0.2),
     'L1_ffn_ln_beta': (0.0, 0.1)}
    factors = {}
    for name, (base, spread) in spreads.items():
        noise = np.random.default_rng([zlib.crc32(name.encode()), seed]).standard_normal(out[name].shape)
        drawn = base * np.exp(spread * noise) if base else spread * noise
        out[name] = jnp.asarray(drawn.astype(out[name].dtype))
    for name, factor in factors.items():
        out[name] = (out[name] * factor).astype(out[name].dtype)
    return out
```

```python
from contextlib import ExitStack

import numpy as np

import concourse.bass as bass
from concourse import mybir

F32 = mybir.dt.float32
BF16 = mybir.dt.bfloat16
I32 = mybir.dt.int32
U32 = mybir.dt.uint32
ALU = mybir.AluOpType
ACT = mybir.ActivationFunctionType
AX = mybir.AxisListType

P = 128
BATCH, SEQ, D = 4, 256, 256
N = BATCH * SEQ
NT = N // P
KD = D // P
HALF = N // 2
BANK = 512
EPS = 1e-5
DMA = 16


class Steps:

    def __init__(self, eng, sem):
        self.eng, self.sem, self.count = eng, sem, 0

    def add(self, ins):
        ins.then_inc(self.sem, 1)
        self.count += 1

    def join(self):
        self.eng.wait_ge(self.sem, self.count)

    def do(self, ins):
        self.add(ins)
        self.join()


class Core:

    def __init__(self, nc, ctx):
        self.nc, self.ctx = nc, ctx

    def sbuf(self, name, shape, dtype=F32):
        return self.ctx.enter_context(self.nc.sbuf_tensor(name, shape, dtype))

    def sem(self, name):
        return self.ctx.enter_context(self.nc.semaphore(name))

    def scope(self, ctx):
        return Core(self.nc, ctx)


def by_feature(w):
    return w.rearrange("(k p) m -> p k m", p=P)


def norm_stage(nc, layer, x_tok, xn_tok, xnT, ident, banks, loads, parity=False):
    with ExitStack() as ctx:
        m = Core(nc, ctx).scope(ctx)
        stats = m.sbuf(f"stats{layer}", [P, NT, 6])
        mean_var = m.sbuf(f"mean_var{layer}", [P, NT, 2])
        var = m.sbuf(f"var{layer}", [P, NT])
        std = m.sbuf(f"std{layer}", [P, NT])
        rstd = m.sbuf(f"rstd{layer}", [P, NT])
        norm_steps = nc.alloc_semaphore(f"norm_steps{layer}")
        var_ready = nc.alloc_semaphore(f"norm_var_ready{layer}")
        std_ready = nc.alloc_semaphore(f"norm_std_ready{layer}")
        xn_ready = nc.alloc_semaphore(f"xn_ready{layer}")
        turned = nc.alloc_semaphore(f"xn_turned{layer}")
        xnT_ready = nc.alloc_semaphore(f"xnT_ready{layer}")
        loaded = nc.alloc_semaphore(f"weights_loaded{layer}")

        with nc.Block(no_gpsimd_drain=True) as block:

            @block.sync
            def _(sp):
                for dst, src in loads:
                    sp.dma_start(dst, src).then_inc(loaded, DMA)
                sp.wait_ge(loaded, DMA * len(loads))

            @block.vector
            def _(dve):
                steps = Steps(dve, norm_steps)
                for t in range(NT):
                    steps.add(nc.vector.bn_stats(stats[:, t, :], x_tok[:, t, :]))
                steps.join()
                for t in range(NT):
                    steps.add(nc.vector.bn_aggr(mean_var[:, t, :], stats[:, t, :]))
                steps.join()
                nc.vector.tensor_scalar(var[:, :], mean_var[:, :, 1], EPS, None, ALU.add).then_inc(var_ready, 1)
                dve.wait_ge(std_ready, 1)
                steps.do(nc.vector.reciprocal(rstd[:, :], std[:, :]))
                for t in range(NT):
                    nc.vector.tensor_scalar(
                        xn_tok[:, t, :], x_tok[:, t, :], mean_var[:, t, 0:1], rstd[:, t:t + 1],
                        ALU.subtract, ALU.mult).then_inc(xn_ready, 1)

            @block.tensor
            def _(pe):
                for t in range(NT):
                    pe.wait_ge(xn_ready, t + 1)
                    for k in range(KD):
                        part = xn_tok[:, t, k::2] if parity else xn_tok[:, t, k * P:(k + 1) * P]
                        last = nc.tensor.transpose(
                            banks[:, KD * (t // 4) + k, (t % 4) * P:(t % 4 + 1) * P], part, ident[:, :])
                    last.then_inc(turned, 1)

            @block.scalar
            def _(act):
                act.wait_ge(var_ready, 1)
                nc.scalar.activation(std[:, :], var[:, :], ACT.Sqrt).then_inc(std_ready, 1)
                for half in range(2):
                    act.wait_ge(turned, 4 * (half + 1))
                    for k in range(KD):
                        nc.scalar.activation(xnT[:, k, half * HALF:(half + 1) * HALF],
                                             banks[:, KD * half + k, :], ACT.Identity).then_inc(xnT_ready, 1)


def recurrence_stage(nc, w, xnT, s_tok, banks):
    two_pi = 6.283185
    rounder = 1.5 * 2.0 ** 23
    with ExitStack() as ctx:
        m = Core(nc, ctx)
        xh = m.sbuf("xh", [P, 2, N])
        gate_x = m.sbuf("gate_x", [P, N])
        gate_a = m.sbuf("gate_a", [P, N])
        radius = m.sbuf("radius", [P, N])
        radius2 = m.sbuf("radius2", [P, N])
        inside = m.sbuf("inside", [P, N])
        turns = m.sbuf("turns", [P, N])
        phi = m.sbuf("phi", [P, N])
        angle = m.sbuf("angle", [P, 4, N])
        wave = m.sbuf("wave", [P, 4, N])
        zr = m.sbuf("zr", [P, N])
        zi = m.sbuf("zi", [P, N])
        ta = m.sbuf("ta", [P, N])
        tb = m.sbuf("tb", [P, N])
        tc = m.sbuf("tc", [P, N])
        td = m.sbuf("td", [P, N])
        hT = m.sbuf("hT", [P, 2, N])
        coef = m.sbuf("coef", [P, 8])
        xh_done = nc.alloc_semaphore("xh_done")
        xh_ready = nc.alloc_semaphore("xh_ready")
        gates_done = nc.alloc_semaphore("gates_done")
        gate_x_ready = nc.alloc_semaphore("gate_x_ready")
        gate_a_ready = nc.alloc_semaphore("gate_a_ready")
        coef_steps = nc.alloc_semaphore("coef_steps")
        coef_ready = nc.alloc_semaphore("coef_ready")
        radius_ready = nc.alloc_semaphore("radius_ready")
        angles_ready = nc.alloc_semaphore("angles_ready")
        waves_ready = nc.alloc_semaphore("waves_ready")
        square_ready = nc.alloc_semaphore("square_ready")
        modulus_ready = nc.alloc_semaphore("modulus_ready")
        inside_ready = nc.alloc_semaphore("inside_ready")
        rec_steps = nc.alloc_semaphore("rec_steps")
        h_ready = nc.alloc_semaphore("h_ready")
        mixed = nc.alloc_semaphore("mixed0")
        starts = slice(0, N, SEQ)

        with nc.Block(no_gpsimd_drain=True) as block:

            @block.tensor
            def _(pe):
                for part in range(2):
                    for half in range(2):
                        for k in range(KD):
                            last = nc.tensor.matmul(
                                banks[:, 2 * part + half, :], w["W_in"][:, k, part * P:(part + 1) * P],
                                xnT[:, k, half * HALF:(half + 1) * HALF], start=(k == 0), stop=(k == KD - 1))
                        last.then_inc(xh_done, 1)
                pe.wait_ge(xh_ready, 4)
                for gate, name in enumerate(("W_ga", "W_gx")):
                    for half in range(2):
                        for k in range(KD):
                            last = nc.tensor.matmul(
                                banks[:, 4 + 2 * gate + half, :], w[name][:, k, :],
                                xh[:, k, half * HALF:(half + 1) * HALF], start=(k == 0), stop=(k == KD - 1))
                        last.then_inc(gates_done, 1)
                pe.wait_ge(h_ready, 2)
                for t in range(NT):
                    for k in range(KD):
                        last = nc.tensor.matmul(
                            banks[:, t // 2, (t % 2) * D:(t % 2 + 1) * D], hT[:, k, t * P:(t + 1) * P],
                            w["W_out"][:, k, :], start=(k == 0), stop=(k == KD - 1))
                    last.then_inc(mixed, 1)

            @block.scalar
            def _(act):
                steps = Steps(act, coef_steps)
                steps.do(nc.scalar.activation(coef[:, 0:1], w["a_real"][:, :], ACT.Abs))
                steps.do(nc.scalar.activation(coef[:, 1:2], coef[:, 0:1], ACT.Exp, scale=-1.0))
                nc.scalar.activation(coef[:, 2:3], coef[:, 1:2], ACT.Ln, bias=1.0).then_inc(coef_ready, 1)
                for part in range(2):
                    for half in range(2):
                        act.wait_ge(xh_done, 2 * part + half + 1)
                        nc.scalar.activation(
                            xh[:, part, half * HALF:(half + 1) * HALF], banks[:, 2 * part + half, :],
                            ACT.Identity, bias=w["b_in"][:, part:part + 1]).then_inc(xh_ready, 1)
                for gate, (dst, bias, ready) in enumerate(
                        ((gate_a, "b_ga", gate_a_ready), (gate_x, "b_gx", gate_x_ready))):
                    for half in range(2):
                        act.wait_ge(gates_done, 2 * gate + half + 1)
                        nc.scalar.activation(dst[:, half * HALF:(half + 1) * HALF],
                                             banks[:, 4 + 2 * gate + half, :], ACT.Sigmoid,
                                             bias=w[bias][:, 0:1]).then_inc(ready, 1)
                act.wait_ge(coef_ready, 2)
                act.wait_ge(gate_a_ready, 2)
                nc.scalar.activation(radius[:, :], gate_a[:, :], ACT.Exp, scale=coef[:, 4:5]).then_inc(radius_ready, 1)
                nc.scalar.activation(radius2[:, :], gate_a[:, :], ACT.Exp, scale=coef[:, 5:6]).then_inc(radius_ready, 1)
                for q in range(4):
                    act.wait_ge(angles_ready, q + 1)
                    nc.scalar.activation(wave[:, q, :], angle[:, q, :], ACT.Sin, scale=two_pi).then_inc(waves_ready, 1)
                for q in range(2):
                    act.wait_ge(square_ready, q + 1)
                    nc.scalar.activation(tc[:, :], ta[:, :], ACT.Sqrt).then_inc(modulus_ready, 1)

            @block.gpsimd
            def _(pool):
                nc.gpsimd.memset(inside[:, :], 1.0).then_inc(inside_ready, 1)
                pool.wait_ge(inside_ready, 1)
                nc.gpsimd.memset(inside[:, starts], 0.0).then_inc(inside_ready, 1)

            @block.vector
            def _(dve):
                steps = Steps(dve, rec_steps)

                def both(dst, a, op, b):
                    steps.add(nc.vector.tensor_tensor(dst, a, b, op))

                dve.wait_ge(coef_ready, 1)
                steps.do(nc.vector.tensor_scalar(coef[:, 3:4], w["a_real"][:, :], 0.0, None, ALU.max))
                steps.do(nc.vector.tensor_tensor(coef[:, 6:7], coef[:, 2:3], coef[:, 3:4], ALU.add))
                steps.do(nc.vector.tensor_scalar(coef[:, 4:5], coef[:, 6:7], -8.0, None, ALU.mult))
                steps.do(nc.vector.tensor_scalar(coef[:, 5:6], coef[:, 6:7], -16.0, None, ALU.mult))
                nc.vector.tensor_scalar(coef[:, 7:8], w["a_imag"][:, :], 1.0 / (2.0 * np.pi), None,
                                        ALU.mult).then_inc(coef_ready, 1)
                dve.wait_ge(coef_ready, 2)
                dve.wait_ge(gate_a_ready, 2)
                steps.do(nc.vector.tensor_scalar(turns[:, :], gate_a[:, :], coef[:, 7:8], None, ALU.mult))
                dve.wait_ge(inside_ready, 2)
                steps.add(nc.vector.tensor_tensor_scan(phi[:, :], inside[:, :], turns[:, :], 0.0, ALU.mult, ALU.add))
                steps.do(nc.vector.tensor_scalar(ta[:, :], turns[:, :], 2.0, 0.25, ALU.mult, ALU.add))
                for q in range(4):
                    if q == 1:
                        steps.do(nc.vector.tensor_scalar(ta[:, :], turns[:, :], 2.0, None, ALU.mult))
                    if q == 2:
                        steps.do(nc.vector.tensor_scalar(ta[:, :], phi[:, :], 0.25, None, ALU.add))
                    cur = phi if q == 3 else ta
                    steps.do(nc.vector.tensor_scalar(tb[:, :], cur[:, :], rounder, rounder, ALU.add, ALU.subtract))
                    nc.vector.tensor_tensor(angle[:, q, :], cur[:, :], tb[:, :], ALU.subtract).then_inc(angles_ready, 1)
                    dve.wait_ge(angles_ready, q + 1)
                dve.wait_ge(waves_ready, 2)
                dve.wait_ge(radius_ready, 2)
                both(ta[:, :], radius2[:, :], ALU.mult, wave[:, 0, :])
                both(tb[:, :], radius2[:, :], ALU.mult, wave[:, 1, :])
                steps.add(nc.vector.memset(radius[:, starts], 0.0))
                steps.join()
                steps.add(nc.vector.tensor_scalar(zr[:, :], ta[:, :], -1.0, 1.0, ALU.mult, ALU.add))
                steps.add(nc.vector.tensor_scalar(zi[:, :], tb[:, :], -1.0, None, ALU.mult))
                steps.join()
                both(ta[:, :], zr[:, :], ALU.mult, zr[:, :])
                both(tb[:, :], zi[:, :], ALU.mult, zi[:, :])
                steps.join()
                nc.vector.tensor_tensor(ta[:, :], ta[:, :], tb[:, :], ALU.add).then_inc(square_ready, 1)
                dve.wait_ge(modulus_ready, 1)
                steps.do(nc.vector.tensor_tensor(tb[:, :], tc[:, :], zr[:, :], ALU.add))
                nc.vector.tensor_scalar(ta[:, :], tb[:, :], 0.5, 1e-30, ALU.mult, ALU.max).then_inc(square_ready, 1)
                dve.wait_ge(modulus_ready, 2)
                steps.do(nc.vector.reciprocal(tb[:, :], tc[:, :]))
                steps.do(nc.vector.scalar_tensor_tensor(td[:, :], zi[:, :], 0.5, tb[:, :], ALU.mult, ALU.mult))
                dve.wait_ge(gate_x_ready, 2)
                both(tc[:, :], tc[:, :], ALU.mult, gate_x[:, :])
                both(td[:, :], td[:, :], ALU.mult, gate_x[:, :])
                steps.join()
                both(ta[:, :], tc[:, :], ALU.mult, xh[:, 0, :])
                both(tb[:, :], td[:, :], ALU.mult, xh[:, 1, :])
                both(radius2[:, :], tc[:, :], ALU.mult, xh[:, 1, :])
                both(turns[:, :], td[:, :], ALU.mult, xh[:, 0, :])
                steps.join()
                both(zr[:, :], ta[:, :], ALU.subtract, tb[:, :])
                both(zi[:, :], radius2[:, :], ALU.add, turns[:, :])
                steps.join()
                dve.wait_ge(waves_ready, 4)
                cos, sin = wave[:, 2, :], wave[:, 3, :]
                both(ta[:, :], zr[:, :], ALU.mult, cos)
                both(tb[:, :], zi[:, :], ALU.mult, sin)
                both(tc[:, :], zi[:, :], ALU.mult, cos)
                both(td[:, :], zr[:, :], ALU.mult, sin)
                steps.join()
                both(ta[:, :], ta[:, :], ALU.add, tb[:, :])
                both(tc[:, :], tc[:, :], ALU.subtract, td[:, :])
                steps.join()
                steps.add(nc.vector.tensor_tensor_scan(zr[:, :], radius[:, :], ta[:, :], 0.0, ALU.mult, ALU.add))
                steps.add(nc.vector.tensor_tensor_scan(zi[:, :], radius[:, :], tc[:, :], 0.0, ALU.mult, ALU.add))
                steps.join()
                both(ta[:, :], zr[:, :], ALU.mult, cos)
                both(tb[:, :], zi[:, :], ALU.mult, sin)
                both(tc[:, :], zr[:, :], ALU.mult, sin)
                both(td[:, :], zi[:, :], ALU.mult, cos)
                steps.join()
                nc.vector.tensor_tensor(hT[:, 0, :], ta[:, :], tb[:, :], ALU.subtract).then_inc(h_ready, 1)
                nc.vector.tensor_tensor(hT[:, 1, :], tc[:, :], td[:, :], ALU.add).then_inc(h_ready, 1)
                for b in range(NT // 2):
                    dve.wait_ge(mixed, 2 * b + 2)
                    nc.vector.tensor_tensor(
                        s_tok[:, 2 * b:2 * b + 2, :], banks[:, b, :].rearrange("p (t d) -> p t d", t=2),
                        w["b_out"][:, :].unsqueeze(1).broadcast_to([P, 2, D]), ALU.add)


def rank_mask(nc, steps, mask, values, scratch, earlier, experts, top):
    shape = [P, NT, experts, experts]
    others = values.unsqueeze(2).broadcast_to(shape)
    own = values.unsqueeze(3).broadcast_to(shape)
    above, equal, count = scratch
    steps.add(nc.vector.tensor_tensor(above, others, own, ALU.is_gt))
    steps.do(nc.vector.tensor_tensor(equal, others, own, ALU.is_equal))
    steps.do(nc.vector.tensor_tensor(
        equal, equal, earlier[:, 0:experts, 0:experts].unsqueeze(1).broadcast_to(shape), ALU.mult))
    steps.do(nc.vector.tensor_tensor(above, above, equal, ALU.add))
    steps.do(nc.vector.tensor_reduce(count, above, AX.X, ALU.add))
    steps.do(nc.vector.tensor_scalar(mask, count, float(top), None, ALU.is_lt))


def silu_sum(nc, act, gated, banks, ready, count, gate_ready):
    act.wait_ge(ready, count)
    for b in range(NT // 2):
        nc.scalar.activation(gated[:, 2 * b:2 * b + 2, :].rearrange("p t d -> p (t d)"), banks[:, b, :],
                             ACT.Silu).then_inc(gate_ready, 1)


def add_gated(nc, dve, x_tok, s_tok, gated, gate_ready, x_ready):
    for b in range(NT // 2):
        pair = slice(2 * b, 2 * b + 2)
        dve.wait_ge(gate_ready, b + 1)
        nc.vector.tensor_tensor(gated[:, pair, :], gated[:, pair, :], s_tok[:, pair, :], ALU.mult
                                ).then_inc(x_ready, 1)
        dve.wait_ge(x_ready, 2 * b + 1)
        nc.vector.tensor_tensor(x_tok[:, pair, :], x_tok[:, pair, :], gated[:, pair, :], ALU.add
                                ).then_inc(x_ready, 1)


def top2_expert_stage(nc, w, weights, scratch, x_tok, xnT, s_tok, ident, earlier, banks):
    experts, top, width = 8, 2, 128
    gate_up, down = weights
    with ExitStack() as ctx:
        m = Core(nc, ctx)
        logits = m.sbuf("logits0", [P, NT, experts])
        chance = m.sbuf("chance0", [P, NT, experts])
        above = m.sbuf("above0", [P, NT, experts, experts])
        equal = m.sbuf("equal0", [P, NT, experts, experts])
        count = m.sbuf("count0", [P, NT, experts])
        mask = m.sbuf("mask0", [P, NT, experts])
        probs = m.sbuf("probs0", [P, NT, experts])
        probsT = m.sbuf("probsT0", [experts, N])
        gate_up_w = m.sbuf("gate_up_w", [P, 2, KD, 2 * width])
        down_w = m.sbuf("down_w", [P, 2, D])
        prob = m.sbuf("prob_row", [P, 2, N])
        scaled = m.sbuf("scaled_gate", [P, N])
        up = m.sbuf("scaled_up", [P, N])
        act_out = m.sbuf("silu_gate", [P, N])
        hT = m.sbuf("expert_hT", [P, N])
        gated = m.sbuf("gated0", [P, NT, D])
        logits_done = nc.alloc_semaphore("logits_done0")
        logits_ready = nc.alloc_semaphore("logits_ready0")
        router_steps = nc.alloc_semaphore("router_steps0")
        chance_ready = nc.alloc_semaphore("chance_ready0")
        probs_ready = nc.alloc_semaphore("probs_ready0")
        probs_turned = nc.alloc_semaphore("probs_turned0")
        probsT_ready = nc.alloc_semaphore("probsT_ready0")
        probs_stored = nc.alloc_semaphore("probs_stored0")
        loaded = [nc.alloc_semaphore(f"expert_loaded0_{s}") for s in range(2)]
        products_done = nc.alloc_semaphore("products_done0")
        gate_scaled = nc.alloc_semaphore("gate_scaled0")
        up_scaled = nc.alloc_semaphore("up_scaled0")
        silu_ready = nc.alloc_semaphore("silu_ready0")
        h_ready = nc.alloc_semaphore("expert_h_ready0")
        down_done = nc.alloc_semaphore("down_done0")
        gate_ready = nc.alloc_semaphore("gate_ready0")
        x_ready = nc.alloc_semaphore("x_ready0")
        cols = [slice(h * HALF, (h + 1) * HALF) for h in range(2)]

        with nc.Block(no_gpsimd_drain=True) as block:

            @block.sync
            def _(sp):
                def load(e, s):
                    sp.dma_start(gate_up_w[:, s, :, :],
                                 gate_up[bass.ds(e, 1), :, :].rearrange("e (k p) n -> p (e k) n", p=P)
                                 ).then_inc(loaded[s], DMA)
                    sp.dma_start(down_w[:, s, :], down[bass.ds(e, 1), :, :].rearrange("e p n -> p (e n)")
                                 ).then_inc(loaded[s], DMA)
                    sp.dma_start(prob[:, s, :], scratch[bass.ds(e, 1), :].rearrange("e n -> (e n)")
                                 .partition_broadcast(P)).then_inc(loaded[s], DMA)

                sp.wait_ge(probsT_ready, 2)
                sp.dma_start(scratch[:, :], probsT[:, :]).then_inc(probs_stored, DMA)
                sp.wait_ge(probs_stored, DMA)
                for s in range(2):
                    load(s, s)
                with sp.Fori(1, experts // 2) as i:
                    for s in range(2):
                        sp.wait_ge(down_done, 2 * i + s)
                        load(2 * i + s, s)

            @block.tensor
            def _(pe):
                def products(half, gate_w, up_w):
                    for j, wt in enumerate((gate_w, up_w)):
                        for k in range(KD):
                            last = nc.tensor.matmul(banks[:, 4 + 2 * half + j, :], wt(k), xnT[:, k, cols[half]],
                                                    start=(k == 0), stop=(k == KD - 1))
                    last.then_inc(products_done, 1)

                def project(half, wt, first):
                    for t in range(4 * half, 4 * half + 4):
                        last = nc.tensor.matmul(
                            banks[:, t // 2, (t % 2) * D:(t % 2 + 1) * D], hT[:, t * P:(t + 1) * P], wt,
                            start=first and t % 2 == 0, stop=False, skip_group_check=True)
                    return last

                for t in range(NT):
                    for k in range(KD):
                        last = nc.tensor.matmul(banks[:, 0, t * experts:(t + 1) * experts],
                                                xnT[:, k, t * P:(t + 1) * P], w["router_w"][:, k, :],
                                                start=(k == 0), stop=(k == KD - 1))
                last.then_inc(logits_done, 1)
                for half in range(2):
                    products(half, lambda k: w["shared_gate_w"][:, k, :], lambda k: w["shared_up_w"][:, k, :])
                pe.wait_ge(probs_ready, 1)
                for t in range(NT):
                    last = nc.tensor.transpose(banks[0:experts, 1 + t // 4, (t % 4) * P:(t % 4 + 1) * P],
                                               probs[:, t, :], ident[:, :])
                last.then_inc(probs_turned, 1)
                pe.wait_ge(probsT_ready, 2)
                for half in range(2):
                    pe.wait_ge(h_ready, half + 1)
                    last = project(half, w["shared_down_w"][:, 0, :], True)
                last.then_inc(down_done, 1)
                with pe.Fori(0, experts // 2) as i:
                    for s in range(2):
                        pe.wait_ge(loaded[s], 3 * DMA * i + 3 * DMA)
                        for half in range(2):
                            products(half, lambda k: gate_up_w[:, s, k, 0:width],
                                     lambda k: gate_up_w[:, s, k, width:2 * width])
                        for half in range(2):
                            pe.wait_ge(h_ready, 4 * i + 2 * s + half + 3)
                            last = project(half, down_w[:, s, :], False)
                        last.then_inc(down_done, 1)

            @block.scalar
            def _(act):
                act.wait_ge(logits_ready, 1)
                nc.scalar.activation(chance[:, :, :], logits[:, :, :], ACT.Sigmoid).then_inc(chance_ready, 1)
                for half in range(2):
                    act.wait_ge(products_done, half + 1)
                    nc.scalar.activation(act_out[:, cols[half]], banks[:, 4 + 2 * half, :], ACT.Silu
                                         ).then_inc(silu_ready, 1)
                act.wait_ge(probs_turned, 1)
                for half in range(2):
                    nc.scalar.activation(probsT[:, cols[half]], banks[0:experts, 1 + half, :], ACT.Identity
                                         ).then_inc(probsT_ready, 1)
                with act.Fori(0, experts) as e:
                    for half in range(2):
                        act.wait_ge(gate_scaled, 2 * e + half + 1)
                        nc.scalar.activation(act_out[:, cols[half]], scaled[:, cols[half]], ACT.Silu
                                             ).then_inc(silu_ready, 1)
                silu_sum(nc, act, gated, banks, down_done, experts + 1, gate_ready)

            @block.vector
            def _(dve):
                steps = Steps(dve, router_steps)
                dve.wait_ge(logits_done, 1)
                nc.vector.tensor_copy(logits[:, :, :].rearrange("p t e -> p (t e)"), banks[:, 0, 0:NT * experts]
                                      ).then_inc(logits_ready, 1)
                dve.wait_ge(logits_ready, 1)
                rank_mask(nc, steps, mask[:, :, :], logits[:, :, :],
                          (above[:, :, :, :], equal[:, :, :, :], count[:, :, :]), earlier, experts, top)
                dve.wait_ge(chance_ready, 1)
                nc.vector.tensor_tensor(probs[:, :, :], mask[:, :, :], chance[:, :, :], ALU.mult
                                        ).then_inc(probs_ready, 1)
                for half in range(2):
                    dve.wait_ge(silu_ready, half + 1)
                    nc.vector.tensor_tensor(hT[:, cols[half]], act_out[:, cols[half]],
                                            banks[:, 5 + 2 * half, :], ALU.mult).then_inc(h_ready, 1)
                with dve.Fori(0, experts // 2) as i:
                    for s in range(2):
                        dve.wait_ge(loaded[s], 3 * DMA * i + 3 * DMA)
                        for half in range(2):
                            dve.wait_ge(products_done, 4 * i + 2 * s + half + 3)
                            nc.vector.tensor_tensor(scaled[:, cols[half]], banks[:, 4 + 2 * half, :],
                                                    prob[:, s, cols[half]], ALU.mult).then_inc(gate_scaled, 1)
                            nc.vector.tensor_tensor(up[:, cols[half]], banks[:, 5 + 2 * half, :],
                                                    prob[:, s, cols[half]], ALU.mult).then_inc(up_scaled, 1)
                            dve.wait_ge(up_scaled, 4 * i + 2 * s + half + 1)
                            dve.wait_ge(silu_ready, 4 * i + 2 * s + half + 3)
                            nc.vector.tensor_tensor(hT[:, cols[half]], act_out[:, cols[half]], up[:, cols[half]],
                                                    ALU.mult).then_inc(h_ready, 1)
                add_gated(nc, dve, x_tok, s_tok, gated, gate_ready, x_ready)


STATES = 16
INNER = 512
MI = INNER // P


def scan_prepare_stage(nc, w, xn_tok, ident, banks, keep, rows):
    taps = 4
    skip, xs, delta, dx, A, diag = keep
    with ExitStack() as ctx:
        m = Core(nc, ctx)
        junk = m.sbuf("rms_junk", [P, D])
        mean_sq = m.sbuf("mean_sq", [P, NT])
        rms = m.sbuf("rms", [P, NT])
        rrms = m.sbuf("rrms", [P, NT])
        x1_tok = m.sbuf("x1_tok", [P, NT, D])
        x1T = m.sbuf("x1T", [P, KD, N])
        padded = m.sbuf("conv_in", [P, MI, BATCH, SEQ + taps - 1])
        low = m.sbuf("delta_low", [P, N])
        soft = m.sbuf("softplus_tail", [P, MI, N])
        bc = m.sbuf("bc_rows", [2 * STATES, N])
        sq_ready = nc.alloc_semaphore("sq_ready1")
        rms_in = nc.alloc_semaphore("rms_in1")
        rms_ready = nc.alloc_semaphore("rms_ready1")
        rms_steps = nc.alloc_semaphore("rms_steps1")
        x1_ready = nc.alloc_semaphore("x1_ready1")
        products = nc.alloc_semaphore("products1")
        emptied = nc.alloc_semaphore("emptied1")
        pad_ready = nc.alloc_semaphore("pad_ready1")
        conv_steps = nc.alloc_semaphore("conv_steps1")
        conv_ready = nc.alloc_semaphore("conv_ready1")
        xs_ready = nc.alloc_semaphore("xs_ready1")
        soft_steps = nc.alloc_semaphore("soft_steps1")
        soft_ready = nc.alloc_semaphore("soft_ready1")
        a_ready = nc.alloc_semaphore("a_ready1")
        delta_ready = nc.alloc_semaphore("delta_ready1")
        rows_stored = nc.alloc_semaphore("rows_stored1")
        cols = [slice(h * HALF, (h + 1) * HALF) for h in range(2)]
        turn0, skip0, in0 = 0, 4, 12
        low0, bc0, up0 = 20, 22, 24

        with nc.Block(no_gpsimd_drain=True) as block:

            @block.sync
            def _(sp):
                sp.wait_ge(emptied, bc0 + 2)
                sp.dma_start(rows, bc[:, :]).then_inc(rows_stored, DMA)
                sp.wait_ge(rows_stored, DMA)

            @block.gpsimd
            def _(pool):
                nc.gpsimd.memset(padded[:, :, :, 0:taps - 1], 0.0).then_inc(pad_ready, 1)

            @block.tensor
            def _(pe):
                def group(g, rows_, pairs):
                    if g >= 8:
                        pe.wait_ge(emptied, g - 7)
                    for k, (wt, act_in) in enumerate(pairs):
                        last = nc.tensor.matmul(banks[0:rows_, g % 8, :], wt, act_in, start=(k == 0),
                                                stop=(k == len(pairs) - 1))
                    last.then_inc(products, 1)

                for half in range(2):
                    pe.wait_ge(x1_ready, 4 * half + 4)
                    for k in range(KD):
                        for t in range(4):
                            last = nc.tensor.transpose(banks[:, turn0 + 2 * half + k, t * P:(t + 1) * P],
                                                       x1_tok[:, 4 * half + t, k * P:(k + 1) * P], ident[:, :])
                        last.then_inc(products, 1)
                pe.wait_ge(emptied, in0 - 8)
                for base, name in ((skip0, "W_skip"), (in0, "W_in")):
                    for mi in range(MI):
                        for half in range(2):
                            group(base + 2 * mi + half, P,
                                  [(w[name][:, k, mi * P:(mi + 1) * P], x1T[:, k, cols[half]]) for k in range(KD)])
                pe.wait_ge(xs_ready, MI)
                for half in range(2):
                    group(low0 + half, P, [(w["W_d1"][:, k, :], xs[:, k, cols[half]]) for k in range(MI)])
                for half in range(2):
                    group(bc0 + half, 2 * STATES, [(w["W_BC"][:, k, :], xs[:, k, cols[half]]) for k in range(MI)])
                for mi in range(MI):
                    for half in range(2):
                        pe.wait_ge(emptied, low0 + half + 1)
                        group(up0 + 2 * mi + half, P, [(w["W_d2"][:, 0, mi * P:(mi + 1) * P], low[:, cols[half]])])

            @block.scalar
            def _(act):
                def empty(g, dst, rows_=P, func=ACT.Identity, **kw):
                    act.wait_ge(products, g + 1)
                    nc.scalar.activation(dst, banks[0:rows_, g % 8, :], func, **kw).then_inc(emptied, 1)

                nc.scalar.activation(A[:, :, :], w["A_log"][:, :, :], ACT.Exp).then_inc(a_ready, 1)
                for t in range(NT):
                    nc.scalar.activation(junk[:, :], xn_tok[:, t, :], ACT.Square,
                                         accum_out=mean_sq[:, t:t + 1]).then_inc(sq_ready, 1)
                    act.wait_ge(sq_ready, t + 1)
                act.wait_ge(rms_in, 1)
                nc.scalar.activation(rms[:, :], mean_sq[:, :], ACT.Sqrt).then_inc(rms_ready, 1)
                for half in range(2):
                    for k in range(KD):
                        empty(turn0 + 2 * half + k, x1T[:, k, cols[half]], scale=w["norm_w"][:, k:k + 1])
                for mi in range(MI):
                    for half in range(2):
                        empty(skip0 + 2 * mi + half, skip[:, mi, cols[half]], func=ACT.Silu)
                act.wait_ge(pad_ready, 1)
                for mi in range(MI):
                    for half in range(2):
                        act.wait_ge(products, in0 + 2 * mi + half + 1)
                        nc.scalar.activation(
                            padded[:, mi, 2 * half:2 * half + 2, taps - 1:],
                            banks[:, (in0 + 2 * mi + half) % 8, :].rearrange("p (b t) -> p b t", b=2),
                            ACT.Identity).then_inc(emptied, 1)
                for mi in range(MI):
                    act.wait_ge(conv_ready, mi + 1)
                    nc.scalar.activation(xs[:, mi, :], xs[:, mi, :], ACT.Silu).then_inc(xs_ready, 1)
                for half in range(2):
                    empty(low0 + half, low[:, cols[half]])
                for half in range(2):
                    empty(bc0 + half, bc[:, cols[half]], rows_=2 * STATES)
                for mi in range(MI):
                    for half in range(2):
                        empty(up0 + 2 * mi + half, delta[:, mi, cols[half]], bias=w["b_d2"][:, mi:mi + 1])
                steps = Steps(act, soft_steps)
                act.wait_ge(emptied, up0 + 2 * MI)
                for mi in range(MI):
                    steps.add(nc.scalar.activation(soft[:, mi, :], delta[:, mi, :], ACT.Abs))
                steps.join()
                for mi in range(MI):
                    steps.add(nc.scalar.activation(soft[:, mi, :], soft[:, mi, :], ACT.Exp, scale=-1.0))
                steps.join()
                for mi in range(MI):
                    nc.scalar.activation(soft[:, mi, :], soft[:, mi, :], ACT.Ln, bias=1.0).then_inc(soft_ready, 1)

            @block.vector
            def _(dve):
                steps = Steps(dve, rms_steps)
                dve.wait_ge(a_ready, 1)
                steps.add(nc.vector.tensor_scalar(A[:, :, :], A[:, :, :], -1.0, None, ALU.mult))
                for mi in range(MI):
                    steps.add(nc.vector.tensor_scalar(diag[:, mi, :], ident[:, :], w["W_D"][:, mi:mi + 1], None, ALU.mult))
                dve.wait_ge(sq_ready, NT)
                nc.vector.tensor_scalar(mean_sq[:, :], mean_sq[:, :], 1.0 / D, EPS, ALU.mult, ALU.add
                                        ).then_inc(rms_in, 1)
                dve.wait_ge(rms_ready, 1)
                steps.do(nc.vector.reciprocal(rrms[:, :], rms[:, :]))
                for t in range(NT):
                    nc.vector.tensor_scalar(x1_tok[:, t, :], xn_tok[:, t, :], rrms[:, t:t + 1], None, ALU.mult
                                            ).then_inc(x1_ready, 1)
                conv = Steps(dve, conv_steps)
                for mi in range(MI):
                    dve.wait_ge(emptied, in0 + 2 * mi + 2)
                    out = xs[:, mi, :].rearrange("p (b t) -> p b t", b=BATCH)
                    conv.do(nc.vector.tensor_scalar(
                        out, padded[:, mi, :, taps - 1:], w["conv_w"][:, mi, taps - 1:taps], w["conv_b"][:, mi:mi + 1],
                        ALU.mult, ALU.add))
                    for j in range(taps - 2, -1, -1):
                        ins = nc.vector.scalar_tensor_tensor(
                            out, padded[:, mi, :, j:j + SEQ], w["conv_w"][:, mi, j:j + 1], out, ALU.mult, ALU.add)
                        if j:
                            conv.do(ins)
                        else:
                            ins.then_inc(conv_ready, 1)
                for mi in range(MI):
                    dve.wait_ge(soft_ready, mi + 1)
                    nc.vector.scalar_tensor_tensor(delta[:, mi, :], delta[:, mi, :], 0.0, soft[:, mi, :],
                                                   ALU.max, ALU.add).then_inc(delta_ready, 1)
                    dve.wait_ge(delta_ready, mi + 1)
                    nc.vector.tensor_tensor(dx[:, mi, :], delta[:, mi, :], xs[:, mi, :], ALU.mult)


def scan_stage(nc, w, xn_tok, s_tok, ident, banks, keep, rows):
    skip, xs, delta, dx, A, diag = keep
    steps_all = STATES * MI
    with ExitStack() as ctx:
        m = Core(nc, ctx)
        b_row = m.sbuf("b_row", [P, 2, N])
        c_row = m.sbuf("c_row", [P, 2, N])
        decay = m.sbuf("decay", [P, 2, BATCH, SEQ])
        drive = m.sbuf("drive", [P, 2, N])
        state = m.sbuf("state", [P, 2, N])
        seen = m.sbuf("seen", [P, 2, N])
        loaded = [nc.alloc_semaphore(f"bc_loaded{s}") for s in range(2)]
        decay_ready = nc.alloc_semaphore("decay_ready")
        drive_ready = nc.alloc_semaphore("drive_ready")
        scanned = nc.alloc_semaphore("scanned")
        seen_ready = nc.alloc_semaphore("seen_ready")
        summed = nc.alloc_semaphore("summed")
        y_ready = nc.alloc_semaphore("y_ready1")
        mixed = nc.alloc_semaphore("mixed1")
        cols = [slice(h * HALF, (h + 1) * HALF) for h in range(2)]

        with nc.Block(no_gpsimd_drain=True) as block:

            @block.sync
            def _(sp):
                def load(n, s):
                    for dst, first in ((b_row, 0), (c_row, STATES)):
                        sp.dma_start(dst[:, s, :], rows[bass.ds(n + first, 1), :].rearrange("n t -> (n t)")
                                     .partition_broadcast(P)).then_inc(loaded[s], DMA)

                for s in range(2):
                    load(s, s)
                with sp.Fori(1, STATES // 2) as i:
                    for s in range(2):
                        sp.wait_ge(drive_ready, MI * (2 * i + s - 1))
                        sp.wait_ge(seen_ready, MI * (2 * i + s - 1))
                        load(2 * i + s, s)

            @block.scalar
            def _(act):
                with act.Fori(0, STATES // 2) as i:
                    for s in range(2):
                        for mi in range(MI):
                            j = MI * s + mi
                            act.wait_ge(scanned, 2 * MI * i + j + 1)
                            nc.scalar.activation(
                                decay[:, j % 2, :, 1:],
                                delta[:, mi, :].rearrange("p (b t) -> p b t", b=BATCH)[:, :, 1:], ACT.Exp,
                                scale=A[:, mi, bass.ds(2 * i + s, 1)]).then_inc(decay_ready, 1)

            @block.gpsimd
            def _(pool):
                with pool.Fori(0, STATES // 2) as i:
                    for s in range(2):
                        pool.wait_ge(loaded[s], 2 * DMA * i + 2 * DMA)
                        for mi in range(MI):
                            j = MI * s + mi
                            pool.wait_ge(scanned, 2 * MI * i + j + 1)
                            nc.gpsimd.tensor_tensor(drive[:, j % 2, :], dx[:, mi, :], b_row[:, s, :], ALU.mult
                                                    ).then_inc(drive_ready, 1)

            @block.vector
            def _(dve):
                for s in range(2):
                    nc.vector.memset(decay[:, s, :, 0:1], 0.0).then_inc(scanned, 1)
                with dve.Fori(0, STATES // 2) as i:
                    for s in range(2):
                        for mi in range(MI):
                            j = MI * s + mi
                            dve.wait_ge(decay_ready, 2 * MI * i + j + 1)
                            dve.wait_ge(drive_ready, 2 * MI * i + j + 1)
                            nc.vector.tensor_tensor_scan(
                                state[:, j % 2, :], decay[:, j % 2, :, :].rearrange("p b t -> p (b t)"),
                                drive[:, j % 2, :], 0.0, ALU.mult, ALU.add).then_inc(scanned, 1)
                            if mi == 0:
                                dve.wait_ge(loaded[s], 2 * DMA * i + 2 * DMA)
                            dve.wait_ge(scanned, 2 * MI * i + j + 3)
                            dve.wait_ge(summed, 2 * MI * i + j + 1)
                            nc.vector.tensor_tensor(seen[:, j % 2, :], state[:, j % 2, :], c_row[:, s, :], ALU.mult
                                                    ).then_inc(seen_ready, 1)
                dve.wait_ge(summed, steps_all + 2)
                for mi in range(MI):
                    for half in range(2):
                        nc.vector.tensor_tensor(dx[:, mi, cols[half]], banks[:, 2 * mi + half, :],
                                                skip[:, mi, cols[half]], ALU.mult).then_inc(y_ready, 1)
                for b in range(NT // 2):
                    dve.wait_ge(mixed, b + 1)
                    nc.vector.tensor_tensor(s_tok[:, 2 * b:2 * b + 2, :],
                                            banks[:, b, :].rearrange("p (t d) -> p t d", t=2),
                                            xn_tok[:, 2 * b:2 * b + 2, :], ALU.add)

            @block.tensor
            def _(pe):
                for mi in range(MI):
                    for half in range(2):
                        last = nc.tensor.matmul(banks[:, 2 * mi + half, :], diag[:, mi, :], xs[:, mi, cols[half]],
                                                start=True, stop=False, skip_group_check=True)
                    if mi % 2:
                        last.then_inc(summed, 1)
                with pe.Fori(0, STATES // 2) as i:
                    for s in range(2):
                        for mi in range(MI):
                            j = MI * s + mi
                            pe.wait_ge(seen_ready, 2 * MI * i + j + 1)
                            for half in range(2):
                                last = nc.tensor.matmul(banks[:, 2 * mi + half, :], ident[:, :],
                                                        seen[:, j % 2, cols[half]], start=False, stop=False,
                                                        skip_group_check=True)
                            last.then_inc(summed, 1)
                pe.wait_ge(y_ready, 2 * MI)
                for t in range(NT):
                    for k in range(MI):
                        last = nc.tensor.matmul(banks[:, t // 2, (t % 2) * D:(t % 2 + 1) * D],
                                                dx[:, k, t * P:(t + 1) * P], w["W_out"][:, k, :],
                                                start=(k == 0), stop=(k == MI - 1))
                    if t % 2:
                        last.then_inc(mixed, 1)


def squared_relu_stage(nc, w, up_w, down_w, x_tok, xnT, s_tok, banks):
    experts, hidden = 8, 1024
    tiles = hidden // P
    with ExitStack() as ctx:
        m = Core(nc, ctx)
        up = m.sbuf("up_w1", [P, 2, KD, P])
        down = m.sbuf("down_w1", [P, 2, D])
        logits = m.sbuf("logits1", [P, NT, experts])
        best = m.sbuf("best1", [P, NT, 8])
        factor = m.sbuf("factor1", [P, NT])
        relu = m.sbuf("relu1", [P, 2, N])
        hT = m.sbuf("hidden_T1", [P, 2, N])
        y = m.sbuf("y1", [P, NT, D])
        stats = m.sbuf("y_stats", [P, NT, 6])
        mean_var = m.sbuf("y_mean_var", [P, NT, 2])
        var = m.sbuf("y_var", [P, NT])
        std = m.sbuf("y_std", [P, NT])
        rstd = m.sbuf("y_rstd", [P, NT])
        logits_done = nc.alloc_semaphore("logits_done1")
        steps_done = nc.alloc_semaphore("ffn_steps1")
        loaded = [nc.alloc_semaphore(f"ffn_loaded1_{s}") for s in range(2)]
        up_done = nc.alloc_semaphore("up_done1")
        relu_ready = nc.alloc_semaphore("relu_ready1")
        h_ready = nc.alloc_semaphore("h_ready1")
        down_done = nc.alloc_semaphore("down_done1")
        expert_done = nc.alloc_semaphore("expert_done1")
        factor_ready = nc.alloc_semaphore("factor_ready1")
        scaled_ready = nc.alloc_semaphore("scaled_ready1")
        var_ready = nc.alloc_semaphore("y_var_ready1")
        std_ready = nc.alloc_semaphore("y_std_ready1")
        norm_ready = nc.alloc_semaphore("y_norm_ready1")
        gate_ready = nc.alloc_semaphore("gate_ready1")
        x_ready = nc.alloc_semaphore("x_ready1")
        cols = [slice(h * HALF, (h + 1) * HALF) for h in range(2)]

        with nc.Block(no_gpsimd_drain=True) as block:

            @block.sync
            def _(sp):
                def load(n, s):
                    sp.dma_start(up[:, s, :, :], up_w.rearrange("(k p) (n c) -> p n k c", p=P, c=P)
                                 [:, bass.ds(n, 1), :, :].rearrange("p n k c -> p (n k) c")).then_inc(loaded[s], DMA)
                    sp.dma_start(down[:, s, :], down_w.rearrange("(n p) d -> n p d", p=P)[bass.ds(n, 1), :, :]
                                 .rearrange("n p d -> p (n d)")).then_inc(loaded[s], DMA)

                for s in range(2):
                    load(s, s)
                with sp.Fori(1, tiles // 2) as i:
                    for s in range(2):
                        sp.wait_ge(down_done, 2 * i + s - 1)
                        load(2 * i + s, s)

            @block.tensor
            def _(pe):
                def raise_(i, s):
                    pe.wait_ge(loaded[s], 2 * DMA * i + 2 * DMA)
                    for half in range(2):
                        for k in range(KD):
                            last = nc.tensor.matmul(banks[:, 4 + 2 * s + half, :], up[:, s, k, :], xnT[:, k, cols[half]],
                                                    start=(k == 0), stop=(k == KD - 1))
                        last.then_inc(up_done, 1)

                def lower(i, s, first=False):
                    for t in range(NT):
                        if t % 4 == 0:
                            pe.wait_ge(h_ready, 4 * i + 2 * s + t // 4 + 1)
                        last = nc.tensor.matmul(
                            banks[:, t // 2, (t % 2) * D:(t % 2 + 1) * D], hT[:, s, t * P:(t + 1) * P], down[:, s, :],
                            start=first and t % 2 == 0, stop=False, skip_group_check=True)
                    last.then_inc(down_done, 1)

                for t in range(NT):
                    for k in range(KD):
                        last = nc.tensor.matmul(banks[:, 0, t * experts:(t + 1) * experts],
                                                xnT[:, k, t * P:(t + 1) * P], w["gate_w"][:, k, :],
                                                start=(k == 0), stop=(k == KD - 1))
                last.then_inc(logits_done, 1)
                raise_(0, 0)
                raise_(0, 1)
                pe.wait_ge(factor_ready, 1)
                lower(0, 0, True)
                with pe.Fori(1, tiles // 2) as i:
                    raise_(i, 0)
                    lower(i - 1, 1)
                    raise_(i, 1)
                    lower(i, 0)
                pe.wait_ge(h_ready, 2 * tiles)
                for t in range(NT):
                    for k in range(KD):
                        last = nc.tensor.matmul(banks[:, 4 + t // 2, (t % 2) * D:(t % 2 + 1) * D],
                                                xnT[:, k, t * P:(t + 1) * P], w["expert_weight"][:, k, :],
                                                start=(k == 0), stop=(k == KD - 1))
                    if t % 2:
                        last.then_inc(expert_done, 1)
                lower(tiles // 2 - 1, 1)

            @block.scalar
            def _(act):
                with act.Fori(0, tiles // 2) as i:
                    for s in range(2):
                        for half in range(2):
                            act.wait_ge(up_done, 4 * i + 2 * s + half + 1)
                            nc.scalar.activation(relu[:, s, cols[half]], banks[:, 4 + 2 * s + half, :], ACT.Relu
                                                 ).then_inc(relu_ready, 1)
                act.wait_ge(factor_ready, 1)
                for t in range(NT):
                    if t % 2 == 0:
                        act.wait_ge(expert_done, t // 2 + 1)
                    nc.scalar.activation(y[:, t, :], banks[:, 4 + t // 2, (t % 2) * D:(t % 2 + 1) * D], ACT.Identity,
                                         scale=factor[:, t:t + 1]).then_inc(scaled_ready, 1)
                act.wait_ge(var_ready, 1)
                nc.scalar.activation(std[:, :], var[:, :], ACT.Sqrt).then_inc(std_ready, 1)
                for b in range(NT // 2):
                    act.wait_ge(norm_ready, 6 * b + 6)
                    nc.scalar.activation(y[:, 2 * b:2 * b + 2, :], y[:, 2 * b:2 * b + 2, :], ACT.Silu
                                         ).then_inc(gate_ready, 1)

            @block.vector
            def _(dve):
                steps = Steps(dve, steps_done)
                dve.wait_ge(logits_done, 1)
                steps.do(nc.vector.tensor_copy(logits[:, :, :].rearrange("p t e -> p (t e)"),
                                               banks[:, 0, 0:NT * experts]))
                for t in range(NT):
                    steps.add(nc.vector.max(best[:, t, :], logits[:, t, :]))
                steps.join()
                nc.vector.tensor_tensor(factor[:, :], best[:, :, 0], best[:, :, 1], ALU.add).then_inc(factor_ready, 1)
                with dve.Fori(0, tiles // 2) as i:
                    for s in range(2):
                        for half in range(2):
                            dve.wait_ge(relu_ready, 4 * i + 2 * s + half + 1)
                            nc.vector.tensor_tensor(hT[:, s, cols[half]], relu[:, s, cols[half]],
                                                    relu[:, s, cols[half]], ALU.mult).then_inc(h_ready, 1)
                dve.wait_ge(down_done, tiles)
                for b in range(NT // 2):
                    pair = slice(2 * b, 2 * b + 2)
                    dve.wait_ge(scaled_ready, 2 * b + 2)
                    steps.add(nc.vector.tensor_tensor(y[:, pair, :], y[:, pair, :],
                                                      banks[:, b, :].rearrange("p (t d) -> p t d", t=2), ALU.add))
                steps.join()
                for t in range(NT):
                    steps.add(nc.vector.bn_stats(stats[:, t, :], y[:, t, :]))
                steps.join()
                for t in range(NT):
                    steps.add(nc.vector.bn_aggr(mean_var[:, t, :], stats[:, t, :]))
                steps.join()
                nc.vector.tensor_scalar(var[:, :], mean_var[:, :, 1], EPS, None, ALU.add).then_inc(var_ready, 1)
                dve.wait_ge(std_ready, 1)
                steps.do(nc.vector.reciprocal(rstd[:, :], std[:, :]))
                for t in range(NT):
                    for ins in range(3):
                        if ins == 0:
                            last = nc.vector.tensor_scalar(y[:, t, :], y[:, t, :], mean_var[:, t, 0:1], rstd[:, t:t + 1],
                                                           ALU.subtract, ALU.mult)
                        else:
                            dve.wait_ge(norm_ready, 3 * t + ins)
                            last = nc.vector.tensor_tensor(y[:, t, :], y[:, t, :],
                                                           w["ln_gamma" if ins == 1 else "ln_beta"][:, :],
                                                           ALU.mult if ins == 1 else ALU.add)
                        last.then_inc(norm_ready, 1)
                add_gated(nc, dve, x_tok, s_tok, y, gate_ready, x_ready)


HEADS2, HEAD2 = 16, 16


def rotary_stage(nc, w, xnT, keep, banks):
    q, keys, v = keep
    with ExitStack() as ctx:
        m = Core(nc, ctx)
        krep = m.sbuf("krep", [P, N])
        straight_done = nc.alloc_semaphore("straight_done2")
        swapped_done = nc.alloc_semaphore("swapped_done2")
        straight_ready = nc.alloc_semaphore("straight_ready2")
        k_done = nc.alloc_semaphore("k_done2")
        k_ready = nc.alloc_semaphore("k_ready2")
        v_done = nc.alloc_semaphore("v_done2")
        cols = [slice(h * HALF, (h + 1) * HALF) for h in range(2)]

        with nc.Block(no_gpsimd_drain=True) as block:

            @block.tensor
            def _(pe):
                def product(bank, wt, half):
                    for k in range(KD):
                        last = nc.tensor.matmul(banks[:, bank, :], wt[:, k, :], xnT[:, k, cols[half]],
                                                start=(k == 0), stop=(k == KD - 1))
                    return last

                for half in range(2):
                    product(6 + half, w["Wk"], half).then_inc(k_done, 1)
                for g in range(2):
                    for half in range(2):
                        bank = 4 * g + 2 * half
                        if bank == 6:
                            pe.wait_ge(k_ready, 2)
                        part = slice(g * P, (g + 1) * P)
                        product(bank, w["Wq"][:, :, part], half).then_inc(straight_done, 1)
                        product(bank + 1, w["Wq_swap"][:, :, part], half).then_inc(swapped_done, 1)
                pe.wait_ge(straight_ready, 1)
                for t in range(NT):
                    for k in range(KD):
                        last = nc.tensor.matmul(banks[:, 0, t * HEAD2:(t + 1) * HEAD2], xnT[:, k, t * P:(t + 1) * P],
                                                w["Wv"][:, k, :], start=(k == 0), stop=(k == KD - 1))
                last.then_inc(v_done, 1)

            @block.scalar
            def _(act):
                for half in range(2):
                    act.wait_ge(k_done, half + 1)
                    nc.scalar.activation(krep[:, cols[half]], banks[:, 6 + half, :], ACT.Identity).then_inc(k_ready, 1)
                for g in range(2):
                    for half in range(2):
                        act.wait_ge(straight_done, 2 * g + half + 1)
                        nc.scalar.activation(q[:, g, cols[half]], banks[:, 4 * g + 2 * half, :], ACT.Identity,
                                             scale=w["cos"][:, g:g + 1]).then_inc(straight_ready, 1)
                act.wait_ge(v_done, 1)
                nc.scalar.activation(v[:, :, :].rearrange("p t d -> p (t d)"), banks[:, 0, 0:NT * HEAD2], ACT.Identity)

            @block.vector
            def _(dve):
                dve.wait_ge(k_ready, 2)
                for h in range(8):
                    nc.vector.tensor_scalar(keys[:, h, :], krep[:, :], w["head_rows"][:, h:h + 1], None, ALU.mult)
                for g in range(2):
                    for half in range(2):
                        dve.wait_ge(swapped_done, 2 * g + half + 1)
                        dve.wait_ge(straight_ready, 2 * g + half + 1)
                        nc.vector.scalar_tensor_tensor(
                            q[:, g, cols[half]], banks[:, 4 * g + 2 * half + 1, :], w["sin"][:, g:g + 1],
                            q[:, g, cols[half]], ALU.mult, ALU.add)


def causal_attention_stage(nc, w, keep, s_tok, ident, banks):
    q, keys, v = keep
    group, units = 4, 8
    round_ = 2 * units
    rounds = BATCH // 2
    scale = HEAD2 ** -0.5
    with ExitStack() as ctx:
        m = Core(nc, ctx)
        q_now = m.sbuf("q_now", [P, 2, 2, SEQ])
        masked = m.sbuf("masked", [P, 3, group, SEQ])
        top = m.sbuf("score_top", [P, 4, group])
        shift = m.sbuf("score_shift", [P, 4, group])
        total = m.sbuf("prob_total", [P, 4, group])
        inverse = m.sbuf("prob_inverse", [P, 4, group])
        prob = m.sbuf("prob", [P, 3, group, SEQ])
        probT = m.sbuf("probT", [P, 2, 2 * group, P])
        o_tok = m.sbuf("o_tok", [P, NT, D])
        oT = m.sbuf("oT2", [P, KD, N])
        q_ready = nc.alloc_semaphore("q_ready2")
        scored = nc.alloc_semaphore("scored2")
        masked_ready = nc.alloc_semaphore("masked_ready2")
        top_ready = nc.alloc_semaphore("top_ready2")
        shift_ready = nc.alloc_semaphore("shift_ready2")
        prob_ready = nc.alloc_semaphore("prob_ready2")
        prob_turned = nc.alloc_semaphore("prob_turned2")
        probT_low = nc.alloc_semaphore("probT_low2")
        probT_high = nc.alloc_semaphore("probT_high2")
        summed = nc.alloc_semaphore("pv_summed2")
        inverse_ready = nc.alloc_semaphore("inverse_ready2")
        o_ready = nc.alloc_semaphore("o_ready2")
        o_turned = nc.alloc_semaphore("o_turned2")
        oT_ready = nc.alloc_semaphore("oT_ready2")
        mixed = nc.alloc_semaphore("mixed2")

        def unit(j):
            s, u = j // units, j % units
            return s, u % 2, group * (u // 2), (u % 2 + 1) * P

        with nc.Block(no_gpsimd_drain=True) as block:

            @block.gpsimd
            def _(pool):
                def copy(b, s):
                    nc.gpsimd.tensor_copy(q_now[:, s, :, :], q[:, :, bass.ds(b * SEQ, SEQ)]).then_inc(q_ready, 1)

                copy(0, 0)
                copy(1, 1)
                with pool.Fori(1, rounds) as i:
                    for s in range(2):
                        pool.wait_ge(scored, round_ * i - units + units * s)
                        copy(2 * i + s, s)

            @block.tensor
            def _(pe):
                def score(i, j):
                    s, qt, head, n_keys = unit(j)
                    if j % units == 0:
                        pe.wait_ge(q_ready, 2 * i + s + 1)
                    if j >= 2:
                        pe.wait_ge(masked_ready, 2 * round_ * i + 2 * (j - 1))
                    for pair in range(2):
                        last = nc.tensor.matmul(
                            banks[:, 2 * (j % 2) + pair, 0:2 * n_keys],
                            q_now[:, s, head // 8, qt * P:(qt + 1) * P],
                            keys[:, head % 8 + 2 * pair:head % 8 + 2 * pair + 2, bass.ds((2 * i + s) * SEQ, n_keys)],
                            start=True, stop=True)
                    last.then_inc(scored, 1)

                def turn(i, j):
                    s, qt, head, n_keys = unit(j)
                    pe.wait_ge(prob_ready, round_ * i + j + 1)
                    if j:
                        pe.wait_ge(probT_low, round_ * i + j)
                    if j >= 2 and qt:
                        pe.wait_ge(probT_high, round_ // 2 * i + j // 2)
                    for h in range(group):
                        for kt in range(qt + 1):
                            c = h * (qt + 1) + kt
                            last = nc.tensor.transpose(banks[:, 4 + c // 4, (c % 4) * P:(c % 4 + 1) * P],
                                                       prob[:, j % 3, h, kt * P:(kt + 1) * P], ident[:, :])
                    last.then_inc(prob_turned, 1)

                def weigh(i, j):
                    s, qt, head, n_keys = unit(j)
                    pe.wait_ge(probT_low, round_ * i + j + 1)
                    if qt:
                        pe.wait_ge(probT_high, round_ // 2 * i + j // 2 + 1)
                    if j >= 2:
                        pe.wait_ge(o_ready, round_ * i + j - 1)
                    for h in range(group):
                        for kt in range(qt + 1):
                            last = nc.tensor.matmul(banks[:, 6 + j % 2, h * HEAD2:(h + 1) * HEAD2],
                                                    probT[:, j % 2, h * (qt + 1) + kt, :],
                                                    v[:, bass.ds(4 * i + 2 * s + kt, 1), :].rearrange("p a d -> p (a d)"),
                                                    start=(kt == 0), stop=(kt == qt))
                    last.then_inc(summed, 1)

                with pe.Fori(0, rounds) as i:
                    score(i, 0)
                    score(i, 1)
                    for j in range(round_):
                        if j + 2 < round_:
                            score(i, j + 2)
                        turn(i, j)
                        if j:
                            weigh(i, j - 1)
                    weigh(i, round_ - 1)
                    pe.wait_ge(o_ready, round_ * i + round_)
                for half in range(2):
                    for k in range(KD):
                        for t in range(4):
                            last = nc.tensor.transpose(banks[:, 2 * half + k, t * P:(t + 1) * P],
                                                       o_tok[:, 4 * half + t, k * P:(k + 1) * P], ident[:, :])
                        last.then_inc(o_turned, 1)
                for t in range(NT):
                    pe.wait_ge(oT_ready, 2 * (t // 4) + 2)
                    for k in range(KD):
                        last = nc.tensor.matmul(banks[:, 4 + t // 2, (t % 2) * D:(t % 2 + 1) * D],
                                                oT[:, k, t * P:(t + 1) * P], w["Wo"][:, k, :],
                                                start=(k == 0), stop=(k == KD - 1))
                    if t % 2:
                        last.then_inc(mixed, 1)

            @block.vector
            def _(dve):
                def tops(i, j):
                    s, qt, head, n_keys = unit(j)
                    dve.wait_ge(scored, round_ * i + j + 1)
                    if j >= 3:
                        dve.wait_ge(prob_ready, round_ * i + j - 2)
                    for pair in range(2):
                        nc.vector.tensor_tensor(
                            masked[:, j % 3, 2 * pair:2 * pair + 2, 0:n_keys],
                            banks[:, 2 * (j % 2) + pair, 0:2 * n_keys].rearrange("p (h k) -> p h k", h=2),
                            w["causal"][:, SEQ - n_keys:SEQ].unsqueeze(1).broadcast_to([P, 2, n_keys]),
                            ALU.add).then_inc(masked_ready, 1)
                    dve.wait_ge(masked_ready, 2 * round_ * i + 2 * j + 2)
                    nc.vector.tensor_reduce(top[:, j % 4, :], masked[:, j % 3, :, 0:n_keys], AX.X, ALU.max
                                            ).then_inc(top_ready, 1)
                    dve.wait_ge(top_ready, round_ * i + j + 1)
                    nc.vector.tensor_scalar(shift[:, j % 4, :], top[:, j % 4, :], -scale, None, ALU.mult
                                            ).then_inc(shift_ready, 1)

                def evacuate(i, j):
                    dve.wait_ge(prob_turned, round_ * i + j + 1)
                    nc.vector.tensor_copy(probT[:, j % 2, 0:4, :], banks[:, 4, :].rearrange("p (c k) -> p c k", c=4)
                                          ).then_inc(probT_low, 1)
                    nc.vector.reciprocal(inverse[:, j % 4, :], total[:, j % 4, :]).then_inc(inverse_ready, 1)

                def normalize(i, j):
                    s, qt, head, n_keys = unit(j)
                    dve.wait_ge(inverse_ready, round_ * i + j + 1)
                    dve.wait_ge(summed, round_ * i + j + 1)
                    nc.vector.tensor_tensor(
                        o_tok[:, bass.ds(4 * i + 2 * s + qt, 1), head * HEAD2:(head + group) * HEAD2]
                        .rearrange("p a (h d) -> p (a h) d", h=group),
                        banks[:, 6 + j % 2, 0:group * HEAD2].rearrange("p (h d) -> p h d", h=group),
                        inverse[:, j % 4, :].unsqueeze(2).broadcast_to([P, group, HEAD2]), ALU.mult
                        ).then_inc(o_ready, 1)

                with dve.Fori(0, rounds) as i:
                    tops(i, 0)
                    tops(i, 1)
                    for j in range(round_):
                        if j + 2 < round_:
                            tops(i, j + 2)
                        evacuate(i, j)
                        if j:
                            normalize(i, j - 1)
                    normalize(i, round_ - 1)
                for b in range(NT // 2):
                    dve.wait_ge(mixed, b + 1)
                    nc.vector.tensor_copy(s_tok[:, 2 * b:2 * b + 2, :],
                                          banks[:, 4 + b, :].rearrange("p (t d) -> p t d", t=2))

            @block.scalar
            def _(act):
                def exps(i, j):
                    s, qt, head, n_keys = unit(j)
                    act.wait_ge(shift_ready, round_ * i + j + 1)
                    if j >= 3:
                        act.wait_ge(prob_turned, round_ * i + j - 2)
                    for h in range(group):
                        last = nc.scalar.activation(prob[:, j % 3, h, 0:n_keys], masked[:, j % 3, h, 0:n_keys], ACT.Exp,
                                                    bias=shift[:, j % 4, h:h + 1], scale=scale,
                                                    accum_out=total[:, j % 4, h:h + 1])
                    last.then_inc(prob_ready, 1)

                with act.Fori(0, rounds) as i:
                    exps(i, 0)
                    for j in range(round_):
                        if j + 1 < round_:
                            exps(i, j + 1)
                        if unit(j)[1]:
                            act.wait_ge(prob_turned, round_ * i + j + 1)
                            nc.scalar.activation(probT[:, j % 2, 4:8, :].rearrange("p c k -> p (c k)"), banks[:, 5, :],
                                                 ACT.Identity).then_inc(probT_high, 1)
                for half in range(2):
                    for k in range(KD):
                        act.wait_ge(o_turned, 2 * half + k + 1)
                        nc.scalar.activation(oT[:, k, half * HALF:(half + 1) * HALF], banks[:, 2 * half + k, :],
                                             ACT.Identity).then_inc(oT_ready, 1)


EXPERTS2, TOP2, CAPACITY = 16, 4, 128
WIDE2, SHARED2 = 176, 352
ROWS2 = WIDE2 // 2
INFO = 6


def route_stage(nc, w, xn_tok, xnT, ident, earlier, banks, tables, xn_dram, y_dram):
    slot_token, slot_target, slot_weight = tables
    tiles = SHARED2 // ROWS2
    jobs = [(i, half) for i in range(tiles) for half in range(2)]
    before = 3
    with ExitStack() as ctx:
        m = Core(nc, ctx)
        shape = [P, NT, EXPERTS2]
        logits = m.sbuf("logits2", shape)
        best = m.sbuf("best2", [P, NT])
        powers = m.sbuf("powers2", shape)
        total = m.sbuf("total2", [P, NT])
        score = m.sbuf("score2", shape)
        above = m.sbuf("above2", [P, NT, EXPERTS2, EXPERTS2])
        equal = m.sbuf("equal2", [P, NT, EXPERTS2, EXPERTS2])
        count = m.sbuf("count2", shape)
        chosen = m.sbuf("chosen2", shape)
        chosen_bf = m.sbuf("chosen_bf2", shape, BF16)
        weight = m.sbuf("weight2", shape)
        place = m.sbuf("place2", shape)
        kept = m.sbuf("kept2", shape)
        before_bf = m.sbuf("before_bf2", [P, P], BF16)
        ones_bf = m.sbuf("ones_bf2", [P, P], BF16)
        one_hot = m.sbuf("one_hot2", [P, NT, EXPERTS2, CAPACITY], BF16)
        info = m.sbuf("info2", [P, NT, EXPERTS2, INFO], BF16)
        rest = m.sbuf("rest2", shape)
        table = m.sbuf("table2", [P, EXPERTS2, INFO])
        empty = m.sbuf("empty2", [P, EXPERTS2])
        token = m.sbuf("token2", [P, EXPERTS2])
        silu = m.sbuf("shared_silu2", [ROWS2, 2, HALF])
        mid = m.sbuf("shared_mid2", [ROWS2, tiles, N])
        y_shared = m.sbuf("shared_y2", [P, NT, D])
        zeros = m.sbuf("zeros2", [P, D])
        consts_ready = nc.alloc_semaphore("route_consts2")
        logits_done = nc.alloc_semaphore("logits_done2")
        route_steps = nc.alloc_semaphore("route_steps2")
        shifted = nc.alloc_semaphore("shifted2")
        powers_ready = nc.alloc_semaphore("powers_ready2")
        chosen_ready = nc.alloc_semaphore("chosen_ready2")
        places_done = nc.alloc_semaphore("places_done2")
        slots_ready = nc.alloc_semaphore("slots_ready2")
        table_done = nc.alloc_semaphore("table_done2")
        shared_done = nc.alloc_semaphore("shared_done2")
        silu_ready = nc.alloc_semaphore("shared_silu_ready2")
        mid_ready = nc.alloc_semaphore("shared_mid_ready2")
        y_done = nc.alloc_semaphore("shared_y_done2")
        y_ready = nc.alloc_semaphore("shared_y_ready2")
        stored = nc.alloc_semaphore("route_stored2")
        cols = [slice(h * HALF, (h + 1) * HALF) for h in range(2)]

        with nc.Block(no_gpsimd_drain=True) as block:

            @block.sync
            def _(sp):
                def by_token(dram):
                    return dram.rearrange("(n p) d -> p n d", p=P)

                sp.dma_start(by_token(xn_dram), xn_tok[:, :, :]).then_inc(stored, DMA)
                sp.wait_ge(consts_ready, 2)
                sp.dma_start(y_dram[N:N + P, :], zeros[:, :]).then_inc(stored, DMA)
                sp.wait_ge(y_ready, NT // 2)
                sp.dma_start(by_token(y_dram[0:N, :]), y_shared[:, :, :]).then_inc(stored, DMA)
                sp.wait_ge(stored, 3 * DMA)

            @block.gpsimd
            def _(pool):
                nc.gpsimd.memset(ones_bf[:, :], 1.0).then_inc(consts_ready, 1)
                nc.gpsimd.memset(zeros[:, :], 0.0).then_inc(consts_ready, 1)
                nc.gpsimd.memset(info[:, :, :, INFO - 1:INFO], 1.0).then_inc(consts_ready, 1)

            @block.tensor
            def _(pe):
                def shared(n):
                    i, half = jobs[n]
                    if n >= 3:
                        pe.wait_ge(mid_ready, n - 2)
                    for j, name in enumerate(("sw_gate", "sw_up")):
                        for k in range(KD):
                            last = nc.tensor.matmul(banks[0:ROWS2, 2 + 2 * (n % 3) + j, :],
                                                    w[name][:, k, i * ROWS2:(i + 1) * ROWS2], xnT[:, k, cols[half]],
                                                    start=(k == 0), stop=(k == KD - 1))
                    last.then_inc(shared_done, 1)

                for t in range(NT):
                    for k in range(KD):
                        last = nc.tensor.matmul(banks[:, 0, t * EXPERTS2:(t + 1) * EXPERTS2],
                                                xnT[:, k, t * P:(t + 1) * P], w["gate_w"][:, k, :],
                                                start=(k == 0), stop=(k == KD - 1))
                last.then_inc(logits_done, 1)
                for n in range(before):
                    shared(n)
                pe.wait_ge(consts_ready, 1)
                pe.wait_ge(chosen_ready, 1)
                for t in range(NT):
                    for other in range(t + 1):
                        last = nc.tensor.matmul(banks[:, 1, t * EXPERTS2:(t + 1) * EXPERTS2],
                                                (before_bf if other == t else ones_bf)[:, :], chosen_bf[:, other, :],
                                                start=(other == 0), stop=(other == t))
                last.then_inc(places_done, 1)
                for n in range(before, len(jobs)):
                    shared(n)
                pe.wait_ge(mid_ready, len(jobs))
                for t in range(NT):
                    for i in range(tiles):
                        last = nc.tensor.matmul(banks[:, 4 + t // 2, (t % 2) * D:(t % 2 + 1) * D],
                                                mid[:, i, t * P:(t + 1) * P], w["sw_down"][:, i, :],
                                                start=(i == 0), stop=(i == tiles - 1))
                    if t % 2:
                        last.then_inc(y_done, 1)
                pe.wait_ge(consts_ready, 3)
                pe.wait_ge(slots_ready, 1)
                for e in range(EXPERTS2):
                    for t in range(NT):
                        last = nc.tensor.matmul(banks[:, 0, e * INFO:(e + 1) * INFO], one_hot[:, t, e, :],
                                                info[:, t, e, :], start=(t == 0), stop=(t == NT - 1))
                last.then_inc(table_done, 1)

            @block.scalar
            def _(act):
                def shared(n):
                    act.wait_ge(shared_done, n + 1)
                    if n >= 2:
                        act.wait_ge(mid_ready, n - 1)
                    nc.scalar.activation(silu[:, n % 2, :], banks[0:ROWS2, 2 + 2 * (n % 3), :], ACT.Silu
                                         ).then_inc(silu_ready, 1)

                act.wait_ge(shifted, 1)
                nc.scalar.activation(powers[:, :, :], powers[:, :, :], ACT.Exp).then_inc(powers_ready, 1)
                for n in range(len(jobs)):
                    shared(n)
                for b in range(NT // 2):
                    act.wait_ge(y_done, b + 1)
                    nc.scalar.activation(y_shared[:, 2 * b:2 * b + 2, :].rearrange("p t d -> p (t d)"), banks[:, 4 + b, :],
                                         ACT.Identity).then_inc(y_ready, 1)

            @block.vector
            def _(dve):
                steps = Steps(dve, route_steps)

                def shared(n):
                    i, half = jobs[n]
                    dve.wait_ge(silu_ready, n + 1)
                    nc.vector.tensor_tensor(mid[:, i, cols[half]], silu[:, n % 2, :],
                                            banks[0:ROWS2, 3 + 2 * (n % 3), :], ALU.mult).then_inc(mid_ready, 1)

                def per_token(v):
                    return v.unsqueeze(2).broadcast_to(shape)

                steps.add(nc.vector.tensor_copy(before_bf[:, :], w["before"][:, :]))
                dve.wait_ge(logits_done, 1)
                steps.do(nc.vector.tensor_copy(logits[:, :, :].rearrange("p t e -> p (t e)"),
                                               banks[:, 0, 0:NT * EXPERTS2]))
                steps.do(nc.vector.tensor_reduce(best[:, :], logits[:, :, :], AX.X, ALU.max))
                nc.vector.tensor_tensor(powers[:, :, :], logits[:, :, :], per_token(best[:, :]), ALU.subtract
                                        ).then_inc(shifted, 1)
                dve.wait_ge(powers_ready, 1)
                steps.do(nc.vector.tensor_reduce(total[:, :], powers[:, :, :], AX.X, ALU.add))
                steps.do(nc.vector.reciprocal(best[:, :], total[:, :]))
                steps.do(nc.vector.tensor_tensor(score[:, :, :], powers[:, :, :], per_token(best[:, :]), ALU.mult))
                rank_mask(nc, steps, chosen[:, :, :], score[:, :, :],
                          (above[:, :, :, :], equal[:, :, :, :], count[:, :, :]), earlier, EXPERTS2, TOP2)
                nc.vector.tensor_copy(chosen_bf[:, :, :], chosen[:, :, :]).then_inc(chosen_ready, 1)
                for n in range(before):
                    shared(n)
                steps.do(nc.vector.tensor_tensor(weight[:, :, :], chosen[:, :, :], score[:, :, :], ALU.mult))
                steps.do(nc.vector.tensor_reduce(total[:, :], weight[:, :, :], AX.X, ALU.add))
                steps.do(nc.vector.tensor_scalar(total[:, :], total[:, :], 1e-20, None, ALU.add))
                steps.do(nc.vector.reciprocal(best[:, :], total[:, :]))
                steps.do(nc.vector.tensor_tensor(weight[:, :, :], weight[:, :, :], per_token(best[:, :]), ALU.mult))
                steps.add(nc.vector.tensor_copy(
                    info[:, :, :, 0:2], w["token_place"][:, :, :].unsqueeze(2).broadcast_to([P, NT, EXPERTS2, 2])))
                rest_of = weight
                for part in range(3):
                    steps.do(nc.vector.tensor_copy(info[:, :, :, 2 + part], rest_of[:, :, :]))
                    if part < 2:
                        steps.do(nc.vector.tensor_tensor(rest[:, :, :], rest_of[:, :, :], info[:, :, :, 2 + part],
                                                         ALU.subtract))
                        rest_of = rest
                dve.wait_ge(places_done, 1)
                steps.do(nc.vector.tensor_copy(place[:, :, :].rearrange("p t e -> p (t e)"),
                                               banks[:, 1, 0:NT * EXPERTS2]))
                steps.do(nc.vector.scalar_tensor_tensor(kept[:, :, :], place[:, :, :], float(CAPACITY), chosen[:, :, :],
                                                        ALU.is_lt, ALU.mult))
                steps.do(nc.vector.scalar_tensor_tensor(place[:, :, :], place[:, :, :], 1.0, kept[:, :, :],
                                                        ALU.add, ALU.mult))
                steps.do(nc.vector.tensor_scalar(place[:, :, :], place[:, :, :], -1.0, None, ALU.add))
                for t in range(NT):
                    ins = nc.vector.tensor_tensor(
                        one_hot[:, t, :, :], w["slots"][:, :].unsqueeze(1).broadcast_to([P, EXPERTS2, CAPACITY]),
                        place[:, t, :].unsqueeze(2).broadcast_to([P, EXPERTS2, CAPACITY]), ALU.is_equal)
                    if t == NT - 1:
                        ins.then_inc(slots_ready, 1)
                    else:
                        steps.add(ins)
                    if before + t < len(jobs):
                        shared(before + t)
                dve.wait_ge(table_done, 1)
                steps.do(nc.vector.tensor_copy(table[:, :, :].rearrange("p e i -> p (e i)"),
                                               banks[:, 0, 0:EXPERTS2 * INFO]))
                steps.do(nc.vector.tensor_tensor(token[:, :], table[:, :, 0], table[:, :, 1], ALU.add))
                steps.add(nc.vector.tensor_copy(slot_token[:, :], token[:, :]))
                steps.do(nc.vector.tensor_scalar(empty[:, :], table[:, :, INFO - 1], -1.0, 1.0, ALU.mult, ALU.add))
                steps.do(nc.vector.scalar_tensor_tensor(token[:, :], empty[:, :], w["spare_row"][:, 0:1], token[:, :],
                                                        ALU.mult, ALU.add))
                steps.add(nc.vector.tensor_copy(slot_target[:, :], token[:, :]))
                steps.do(nc.vector.tensor_tensor(slot_weight[:, :], table[:, :, 3], table[:, :, 4], ALU.add))
                steps.do(nc.vector.tensor_tensor(slot_weight[:, :], slot_weight[:, :], table[:, :, 2], ALU.add))


def slot_expert_stage(nc, expert_w, x_tok, s_tok, ident, banks, tables, xn_dram, y_dram):
    slot_token, slot_target, slot_weight = tables
    w_gate, w_up, w_down = expert_w
    pairs = EXPERTS2 // 2
    with ExitStack() as ctx:
        m = Core(nc, ctx)
        gate_w = m.sbuf("slot_gate_w", [P, 2, KD, WIDE2])
        up_w = m.sbuf("slot_up_w", [P, 2, KD, WIDE2])
        down_w = m.sbuf("slot_down_w", [ROWS2, 2, 2, D])
        xg = m.sbuf("slot_x", [P, 2, D])
        xgT = m.sbuf("slot_xT", [P, 2, D])
        silu = m.sbuf("slot_silu", [ROWS2, 2, 2 * P])
        mid = m.sbuf("slot_mid", [ROWS2, 2, 2 * P])
        result = m.sbuf("slot_result", [P, 2, D])
        gated = m.sbuf("gated2", [P, NT, D])
        loaded = [nc.alloc_semaphore(f"slot_loaded{s}") for s in range(2)]
        gathered = [nc.alloc_semaphore(f"slot_gathered{s}") for s in range(2)]
        turned = nc.alloc_semaphore("slot_turned")
        xgT_ready = nc.alloc_semaphore("slot_xT_ready")
        widened = nc.alloc_semaphore("slot_widened")
        silu_ready = nc.alloc_semaphore("slot_silu_ready")
        mid_ready = nc.alloc_semaphore("slot_mid_ready")
        lowered = nc.alloc_semaphore("slot_lowered")
        result_ready = nc.alloc_semaphore("slot_result_ready")
        scattered = nc.alloc_semaphore("slot_scattered")
        y_loaded = nc.alloc_semaphore("y_loaded2")
        gate_ready = nc.alloc_semaphore("gate_ready2")
        x_ready = nc.alloc_semaphore("x_ready2")

        with nc.Block(no_gpsimd_drain=True) as block:

            @block.sync
            def _(sp):
                def load(e, s):
                    for dst, src in ((gate_w, w_gate), (up_w, w_up)):
                        sp.dma_start(dst[:, s, :, :], src[bass.ds(e, 1), :, :].rearrange("e (k p) n -> p (e k) n", p=P)
                                     ).then_inc(loaded[s], DMA)
                    sp.dma_start(down_w[:, s, :, :], w_down[bass.ds(e, 1), :, :]
                                 .rearrange("e (i p) d -> p (e i) d", p=ROWS2)).then_inc(loaded[s], DMA)

                for s in range(2):
                    load(s, s)
                with sp.Fori(1, pairs) as i:
                    for s in range(2):
                        sp.wait_ge(lowered, 2 * i + s - 1)
                        load(2 * i + s, s)
                sp.wait_ge(scattered, DMA * EXPERTS2)
                sp.dma_start(gated[:, :, :], y_dram[0:N, :].rearrange("(n p) d -> p n d", p=P)).then_inc(y_loaded, DMA)
                sp.wait_ge(y_loaded, DMA)

            @block.gpsimd
            def _(pool):
                def gather(e):
                    pool.indirect_dma_start(out=xg[:, e % 2, :], out_offset=None, in_=xn_dram[:, :],
                                            in_offset=bass.IndirectOffsetOnAxis(ap=slot_token[:, e:e + 1], axis=0)
                                            ).then_inc(gathered[e % 2], DMA)

                gather(0)
                gather(1)
                for e in range(EXPERTS2):
                    pool.wait_ge(result_ready, e + 1)
                    if e:
                        pool.wait_ge(scattered, DMA * e)
                    pool.indirect_dma_start(out=y_dram[:, :],
                                            out_offset=bass.IndirectOffsetOnAxis(ap=slot_target[:, e:e + 1], axis=0),
                                            in_=result[:, e % 2, :], in_offset=None, compute_op=ALU.add
                                            ).then_inc(scattered, DMA)
                    if e + 2 < EXPERTS2:
                        gather(e + 2)
                pool.wait_ge(scattered, DMA * EXPERTS2)

            @block.tensor
            def _(pe):
                def turn(i, s):
                    pe.wait_ge(gathered[s], DMA * i + DMA)
                    for k in range(KD):
                        last = nc.tensor.transpose(banks[:, 4 + s, k * P:(k + 1) * P], xg[:, s, k * P:(k + 1) * P],
                                                   ident[:, :])
                    last.then_inc(turned, 1)

                def widen(i, s):
                    pe.wait_ge(loaded[s], 3 * DMA * i + 3 * DMA)
                    pe.wait_ge(xgT_ready, 2 * i + s + 1)
                    for j, wt in enumerate((gate_w, up_w)):
                        for part in range(2):
                            for k in range(KD):
                                last = nc.tensor.matmul(
                                    banks[0:ROWS2, 6 + s, (2 * j + part) * P:(2 * j + part + 1) * P],
                                    wt[:, s, k, part * ROWS2:(part + 1) * ROWS2], xgT[:, s, k * P:(k + 1) * P],
                                    start=(k == 0), stop=(k == KD - 1))
                    last.then_inc(widened, 1)

                def lower(i, s, first):
                    pe.wait_ge(mid_ready, 2 * i + s + 1)
                    if not first:
                        pe.wait_ge(result_ready, 2 * i + s - 1)
                    for part in range(2):
                        last = nc.tensor.matmul(banks[:, s, 0:D], mid[:, s, part * P:(part + 1) * P],
                                                down_w[:, s, part, :], start=(part == 0), stop=(part == 1))
                    last.then_inc(lowered, 1)

                turn(0, 0)
                widen(0, 0)
                turn(0, 1)
                lower(0, 0, True)
                widen(0, 1)
                turn(1, 0)
                lower(0, 1, True)
                with pe.Fori(1, pairs - 1) as i:
                    widen(i, 0)
                    turn(i, 1)
                    lower(i, 0, False)
                    widen(i, 1)
                    turn(i + 1, 0)
                    lower(i, 1, False)
                last_pair = pairs - 1
                widen(last_pair, 0)
                turn(last_pair, 1)
                lower(last_pair, 0, False)
                widen(last_pair, 1)
                lower(last_pair, 1, False)

            @block.scalar
            def _(act):
                def expert(i, s, last=False):
                    act.wait_ge(widened, 2 * i + s + 1)
                    nc.scalar.activation(silu[:, s, :], banks[0:ROWS2, 6 + s, 0:2 * P], ACT.Silu).then_inc(silu_ready, 1)
                    if not last:
                        turn(i + (s == 1), 1 - s)

                def turn(i, s):
                    act.wait_ge(turned, 2 * i + s + 1)
                    nc.scalar.activation(xgT[:, s, :], banks[:, 4 + s, 0:D], ACT.Identity).then_inc(xgT_ready, 1)

                turn(0, 0)
                with act.Fori(0, pairs - 1) as i:
                    for s in range(2):
                        expert(i, s)
                expert(pairs - 1, 0)
                expert(pairs - 1, 1, last=True)
                act.wait_ge(y_loaded, DMA)
                for b in range(NT // 2):
                    pair = slice(2 * b, 2 * b + 2)
                    nc.scalar.activation(gated[:, pair, :], gated[:, pair, :], ACT.Silu).then_inc(gate_ready, 1)

            @block.vector
            def _(dve):
                def expert(i, s, first=False):
                    dve.wait_ge(silu_ready, 2 * i + s + 1)
                    nc.vector.tensor_tensor(mid[:, s, :], silu[:, s, :], banks[0:ROWS2, 6 + s, 2 * P:4 * P], ALU.mult
                                            ).then_inc(mid_ready, 1)
                    dve.wait_ge(lowered, 2 * i + s + 1)
                    if not first:
                        dve.wait_ge(scattered, DMA * (2 * i + s - 1))
                    nc.vector.tensor_scalar(result[:, s, :], banks[:, s, 0:D], slot_weight[:, bass.ds(2 * i + s, 1)],
                                            None, ALU.mult).then_inc(result_ready, 1)

                for s in range(2):
                    expert(0, s, True)
                with dve.Fori(1, pairs) as i:
                    for s in range(2):
                        expert(i, s)
                add_gated(nc, dve, x_tok, s_tok, gated, gate_ready, x_ready)


HEADS3, LATENT, HEAD3 = 16, 64, 128
UNITS3 = HEADS3 // 2


def latent_prepare_stage(nc, w, xnT, banks, keep):
    q_weight, o_weight, latT, lat_tok = keep
    with ExitStack() as ctx:
        m = Core(nc, ctx)
        done = nc.alloc_semaphore("latent_done3")
        ready = nc.alloc_semaphore("latent_ready3")
        cols = [slice(h * HALF, (h + 1) * HALF) for h in range(2)]

        with nc.Block(no_gpsimd_drain=True) as block:

            @block.tensor
            def _(pe):
                for k in range(KD):
                    for h in range(HEADS3):
                        last = nc.tensor.matmul(banks[:, 2 * k + h // 8, (h % 8) * LATENT:(h % 8 + 1) * LATENT],
                                                w["WqT"][:, h, k * P:(k + 1) * P], w["WupT"][:, h, :],
                                                start=True, stop=True)
                        if h % 8 == 7:
                            last.then_inc(done, 1)
                for half in range(2):
                    for k in range(KD):
                        last = nc.tensor.matmul(banks[:, 4 + half, :], w["Wdown2"][:, k, :], xnT[:, k, cols[half]],
                                                start=(k == 0), stop=(k == KD - 1))
                    last.then_inc(done, 1)
                for t in range(NT):
                    for k in range(KD):
                        last = nc.tensor.matmul(banks[:, 6, t * LATENT:(t + 1) * LATENT], xnT[:, k, t * P:(t + 1) * P],
                                                w["Wdown2"][:, k, 0:LATENT], start=(k == 0), stop=(k == KD - 1))
                last.then_inc(done, 1)
                for u in range(UNITS3):
                    if u % 2 == 0:
                        pe.wait_ge(ready, u // 2 + 1)
                    for part in range(2):
                        last = nc.tensor.matmul(
                            banks[part * LATENT:(part + 1) * LATENT, u // 2, (u % 2) * D:(u % 2 + 1) * D],
                            w["WupT"][:, 2 * u + part, :], w["Wo"][:, 2 * u + part, :], start=True, stop=True)
                    if u % 2:
                        last.then_inc(done, 1)

            @block.scalar
            def _(act):
                targets = [q_weight[:, k, 8 * P // 2 * j:8 * P // 2 * (j + 1)] for k in range(KD) for j in range(2)]
                targets += [latT[:, cols[0]], latT[:, cols[1]], lat_tok[:, :, :].rearrange("p t c -> p (t c)")]
                targets += [o_weight[:, 2 * b:2 * b + 2, :].rearrange("p u d -> p (u d)") for b in range(UNITS3 // 2)]
                for n, dst in enumerate(targets):
                    bank = n if n < 7 else n - 7
                    act.wait_ge(done, n + 1)
                    nc.scalar.activation(dst, banks[:, bank, :], ACT.Identity).then_inc(ready, 1)


def latent_attention_stage(nc, xnT, s_tok, ident, banks, keep):
    q_weight, o_weight, latT, lat_tok = keep
    scale = 1.0 / np.sqrt(HEAD3)
    round_ = 2 * HEADS3
    with ExitStack() as ctx:
        m = Core(nc, ctx)
        latT_now = m.sbuf("latT_now", [P, 2, SEQ])
        lat_now = m.sbuf("lat_now", [P, 2, 2, LATENT])
        q_now = m.sbuf("q_now3", [P, 2, SEQ])
        top = m.sbuf("top3", [P, 4, 2])
        shift = m.sbuf("shift3", [P, 4, 2])
        total = m.sbuf("total3", [P, 4, 2])
        inverse = m.sbuf("inverse3", [P, 4, 2])
        prob = m.sbuf("prob3", [P, 3, 2, SEQ])
        probT = m.sbuf("probT3", [P, 2, 2, SEQ])
        o_tok = m.sbuf("o_tok3", [P, NT, HEADS3 * LATENT])
        oT = m.sbuf("oT3", [P, UNITS3, N])
        lat_ready = nc.alloc_semaphore("lat_now_ready3")
        q_done = nc.alloc_semaphore("q_done3")
        q_ready = nc.alloc_semaphore("q_ready3")
        scored = nc.alloc_semaphore("scored3")
        top_ready = nc.alloc_semaphore("top_ready3")
        shift_ready = nc.alloc_semaphore("shift_ready3")
        prob_ready = nc.alloc_semaphore("prob_ready3")
        prob_turned = nc.alloc_semaphore("prob_turned3")
        probT_ready = nc.alloc_semaphore("probT_ready3")
        summed = nc.alloc_semaphore("pv_summed3")
        inverse_ready = nc.alloc_semaphore("inverse_ready3")
        o_ready = nc.alloc_semaphore("o_ready3")
        o_turned = nc.alloc_semaphore("o_turned3")
        oT_ready = nc.alloc_semaphore("oT_ready3")
        mixed = nc.alloc_semaphore("mixed3")
        rounds = BATCH // 2

        with nc.Block(no_gpsimd_drain=True) as block:

            @block.gpsimd
            def _(pool):
                def copy(b, s):
                    nc.gpsimd.tensor_copy(latT_now[:, s, :], latT[:, bass.ds(b * SEQ, SEQ)]).then_inc(lat_ready, 1)
                    nc.gpsimd.tensor_copy(lat_now[:, s, :, :], lat_tok[:, bass.ds(2 * b, 2), :]).then_inc(lat_ready, 1)

                copy(0, 0)
                copy(1, 1)
                with pool.Fori(1, rounds) as i:
                    for s in range(2):
                        pool.wait_ge(summed, round_ * i - HEADS3 + HEADS3 * s)
                        copy(2 * i + s, s)

            @block.tensor
            def _(pe):
                def query(i, u):
                    s, pair = u // UNITS3, u % UNITS3
                    if u >= 1:
                        pe.wait_ge(q_ready, 2 * UNITS3 * i + u)
                    for k in range(KD):
                        last = nc.tensor.matmul(banks[:, 7, 0:SEQ], q_weight[:, k, pair * P:(pair + 1) * P],
                                                xnT[:, k, bass.ds((2 * i + s) * SEQ, SEQ)],
                                                start=(k == 0), stop=(k == KD - 1))
                    last.then_inc(q_done, 1)

                def score(i, j):
                    rows = slice((j % 2) * LATENT, (j % 2 + 1) * LATENT)
                    if j % HEADS3 == 0:
                        pe.wait_ge(lat_ready, 4 * i + 2 * (j // HEADS3) + 2)
                    if j % 2 == 0:
                        pe.wait_ge(q_ready, 2 * UNITS3 * i + j // 2 + 1)
                    for qt in range(2):
                        last = nc.tensor.matmul(banks[:, j % 3, qt * SEQ:(qt + 1) * SEQ],
                                                q_now[rows, (j // 2) % 2, qt * P:(qt + 1) * P],
                                                latT_now[rows, j // HEADS3, :], start=True, stop=True)
                    last.then_inc(scored, 1)

                def turn(i, j):
                    pe.wait_ge(prob_ready, round_ * i + j + 1)
                    for kt in range(2):
                        for qt in range(2):
                            last = nc.tensor.transpose(banks[:, 3 + j % 2, kt * SEQ + qt * P:kt * SEQ + (qt + 1) * P],
                                                       prob[:, j % 3, qt, kt * P:(kt + 1) * P], ident[:, :])
                    last.then_inc(prob_turned, 1)

                def weigh(i, j):
                    pe.wait_ge(probT_ready, round_ * i + j + 1)
                    if j >= 2:
                        pe.wait_ge(o_ready, round_ * i + j - 1)
                    for qt in range(2):
                        for kt in range(2):
                            last = nc.tensor.matmul(banks[:, 5 + j % 2, qt * LATENT:(qt + 1) * LATENT],
                                                    probT[:, j % 2, kt, qt * P:(qt + 1) * P],
                                                    lat_now[:, j // HEADS3, kt, :], start=(kt == 0), stop=(kt == 1))
                    last.then_inc(summed, 1)

                def mix(t):
                    pe.wait_ge(oT_ready, 2 * t + 2)
                    for u in range(UNITS3):
                        last = nc.tensor.matmul(banks[:, 4 + t // 2, (t % 2) * D:(t % 2 + 1) * D], oT[:, u, t * P:(t + 1) * P],
                                                o_weight[:, u, :], start=(u == 0), stop=(u == UNITS3 - 1))
                    if t % 2:
                        last.then_inc(mixed, 1)

                with pe.Fori(0, rounds) as i:
                    query(i, 0)
                    query(i, 1)
                    score(i, 0)
                    score(i, 1)
                    for j in range(round_):
                        if j % 2 == 0 and j // 2 + 2 < 2 * UNITS3:
                            query(i, j // 2 + 2)
                        if j + 2 < round_:
                            score(i, j + 2)
                        turn(i, j)
                        if j:
                            weigh(i, j - 1)
                    weigh(i, round_ - 1)
                    pe.wait_ge(o_ready, round_ * i + round_)
                for t in range(NT):
                    for u in range(UNITS3):
                        if t >= 2 and u % 4 == 0:
                            pe.wait_ge(oT_ready, 2 * (t - 2) + u // 4 + 1)
                        last = nc.tensor.transpose(banks[:, 2 * (t % 2) + u // 4, (u % 4) * P:(u % 4 + 1) * P],
                                                   o_tok[:, t, u * P:(u + 1) * P], ident[:, :])
                        if u % 4 == 3:
                            last.then_inc(o_turned, 1)
                    if t:
                        mix(t - 1)
                mix(NT - 1)

            @block.vector
            def _(dve):
                def tops(i, j):
                    dve.wait_ge(scored, round_ * i + j + 1)
                    nc.vector.tensor_reduce(top[:, j % 4, :], banks[:, j % 3, :].rearrange("p (q k) -> p q k", q=2),
                                            AX.X, ALU.max).then_inc(top_ready, 1)
                    dve.wait_ge(top_ready, round_ * i + j + 1)
                    nc.vector.tensor_scalar(shift[:, j % 4, :], top[:, j % 4, :], -scale, None, ALU.mult
                                            ).then_inc(shift_ready, 1)

                def evacuate(i, j):
                    dve.wait_ge(prob_turned, round_ * i + j + 1)
                    nc.vector.tensor_copy(probT[:, j % 2, :, :].rearrange("p a q -> p (a q)"), banks[:, 3 + j % 2, :]
                                          ).then_inc(probT_ready, 1)
                    nc.vector.reciprocal(inverse[:, j % 4, :], total[:, j % 4, :]).then_inc(inverse_ready, 1)

                def normalize(i, j):
                    s, h = j // HEADS3, j % HEADS3
                    dve.wait_ge(inverse_ready, round_ * i + j + 1)
                    dve.wait_ge(summed, round_ * i + j + 1)
                    nc.vector.tensor_tensor(
                        o_tok[:, bass.ds(4 * i + 2 * s, 2), h * LATENT:(h + 1) * LATENT],
                        banks[:, 5 + j % 2, 0:2 * LATENT].rearrange("p (q c) -> p q c", q=2),
                        inverse[:, j % 4, :].unsqueeze(2).broadcast_to([P, 2, LATENT]), ALU.mult).then_inc(o_ready, 1)

                with dve.Fori(0, rounds) as i:
                    tops(i, 0)
                    tops(i, 1)
                    for j in range(round_):
                        if j + 2 < round_:
                            tops(i, j + 2)
                        evacuate(i, j)
                        if j:
                            normalize(i, j - 1)
                    normalize(i, round_ - 1)
                for t in range(NT):
                    dve.wait_ge(o_turned, 2 * t + 1)
                    nc.vector.tensor_copy(oT[:, 0:4, t * P:(t + 1) * P],
                                          banks[:, 2 * (t % 2), :].rearrange("p (u c) -> p u c", u=4)).then_inc(oT_ready, 1)
                    dve.wait_ge(o_turned, 2 * t + 2)
                    nc.vector.tensor_copy(oT[:, 4:8, t * P:(t + 1) * P],
                                          banks[:, 2 * (t % 2) + 1, :].rearrange("p (u c) -> p u c", u=4)
                                          ).then_inc(oT_ready, 1)

            @block.scalar
            def _(act):
                def query(i, u):
                    act.wait_ge(q_done, 2 * UNITS3 * i + u + 1)
                    nc.scalar.activation(q_now[:, u % 2, :], banks[:, 7, 0:SEQ], ACT.Identity).then_inc(q_ready, 1)

                with act.Fori(0, rounds) as i:
                    query(i, 0)
                    query(i, 1)
                    for j in range(round_):
                        if j % 2 == 0 and j // 2 + 2 < 2 * UNITS3:
                            query(i, j // 2 + 2)
                        act.wait_ge(shift_ready, round_ * i + j + 1)
                        for qt in range(2):
                            last = nc.scalar.activation(prob[:, j % 3, qt, :], banks[:, j % 3, qt * SEQ:(qt + 1) * SEQ],
                                                        ACT.Exp, bias=shift[:, j % 4, qt:qt + 1], scale=float(scale),
                                                        accum_out=total[:, j % 4, qt:qt + 1])
                        last.then_inc(prob_ready, 1)
                for b in range(NT // 2):
                    act.wait_ge(mixed, b + 1)
                    nc.scalar.activation(s_tok[:, 2 * b:2 * b + 2, :].rearrange("p t d -> p (t d)"), banks[:, 4 + b, :],
                                         ACT.Identity)


MLP3 = 2048
PACKS3 = MLP3 // (2 * P)


def four_bit_stage(nc, packed, scales, x_tok, xnT, s_tok, banks):
    with ExitStack() as ctx:
        m = Core(nc, ctx)
        shape = [P, 3, 2, D]
        pack = m.sbuf("pack3", [P, 2, 3, D], I32)
        scale = m.sbuf("scale3", [P, 2, 3, D])
        code = m.sbuf("code3", shape, I32)
        eight = m.sbuf("eight3", shape, BF16)
        size = m.sbuf("size3", shape, BF16)
        twice = m.sbuf("twice3", shape, BF16)
        fourfold = m.sbuf("fourfold3", shape, BF16)
        sign = m.sbuf("sign3", shape, BF16)
        weight = m.sbuf("weight3", [P, 2, 3, 2, D])
        gelu = m.sbuf("gelu3", [P, 2, HALF])
        inter = m.sbuf("inter3", [P, 2, N])
        gated = m.sbuf("gated3", [P, NT, D])
        loaded = [nc.alloc_semaphore(f"pack_loaded{s}") for s in range(2)]
        unpack_steps = nc.alloc_semaphore("unpack_steps3")
        weight_ready = nc.alloc_semaphore("weight_ready3")
        widened = nc.alloc_semaphore("widened3")
        gelu_ready = nc.alloc_semaphore("gelu_ready3")
        inter_ready = nc.alloc_semaphore("inter_ready3")
        lowered = nc.alloc_semaphore("lowered3")
        gate_ready = nc.alloc_semaphore("gate_ready3")
        x_ready = nc.alloc_semaphore("x_ready3")
        cols = [slice(h * HALF, (h + 1) * HALF) for h in range(2)]
        rounds = PACKS3 // 2
        unpack_waits = 10

        with nc.Block(no_gpsimd_drain=True) as block:

            @block.sync
            def _(sp):
                def load(n, s):
                    for j in range(3):
                        for dst, src in ((pack, packed[j]), (scale, scales[j])):
                            sp.dma_start(dst[:, s, j, :], src[bass.ds(n, 1), :, :].rearrange("n p c -> p (n c)")
                                         ).then_inc(loaded[s], DMA)

                load(0, 0)
                load(1, 1)
                with sp.Fori(1, rounds) as i:
                    for s in range(2):
                        sp.wait_ge(weight_ready, 2 * i + s - 1)
                        load(2 * i + s, s)

            @block.tensor
            def _(pe):
                def widen(i, job):
                    s, tile, half = job // 4, job // 2 % 2, job % 2
                    if job % 4 == 0:
                        pe.wait_ge(weight_ready, 2 * i + s + 1)
                    for j in range(2):
                        for k in range(KD):
                            last = nc.tensor.matmul(banks[:, 4 + 2 * half + j, :], weight[:, s, j, k, tile * P:(tile + 1) * P],
                                                    xnT[:, k, cols[half]], start=(k == 0), stop=(k == KD - 1))
                    last.then_inc(widened, 1)

                def lower(i, job, first=False):
                    s, tile, half = job // 4, job // 2 % 2, job % 2
                    pe.wait_ge(inter_ready, 8 * i + job + 1)
                    for t in range(4 * half, 4 * half + 4):
                        last = nc.tensor.matmul(banks[:, t // 2, (t % 2) * D:(t % 2 + 1) * D],
                                                inter[:, tile, t * P:(t + 1) * P], weight[:, s, 2, tile, :],
                                                start=first and t % 2 == 0, stop=False, skip_group_check=True)
                    last.then_inc(lowered, 1)

                def round_(i, first=False, final=False):
                    for job in range(8):
                        if job < 7:
                            widen(i, job + 1)
                        elif not final:
                            widen(i + 1, 0)
                        lower(i, job, first and job < 2)

                widen(0, 0)
                round_(0, first=True)
                with pe.Fori(1, rounds - 1) as i:
                    round_(i)
                round_(rounds - 1, final=True)

            @block.scalar
            def _(act):
                with act.Fori(0, rounds) as i:
                    for job in range(8):
                        act.wait_ge(widened, 8 * i + job + 1)
                        nc.scalar.activation(gelu[:, job % 2, :], banks[:, 4 + 2 * (job % 2), :], ACT.Gelu_apprx_tanh
                                             ).then_inc(gelu_ready, 1)
                silu_sum(nc, act, gated, banks, lowered, 8 * rounds, gate_ready)

            @block.vector
            def _(dve):
                def multiply(i, job):
                    tile, half = job // 2 % 2, job % 2
                    dve.wait_ge(gelu_ready, 8 * i + job + 1)
                    nc.vector.tensor_tensor(inter[:, tile, cols[half]], gelu[:, half, :], banks[:, 5 + 2 * half, :],
                                            ALU.mult).then_inc(inter_ready, 1)

                def unpack(i, s, part, first=False):
                    done = unpack_waits * (2 * i + s)

                    def steps(at, *made):
                        for ins in made:
                            ins.then_inc(unpack_steps, 1)
                        dve.wait_ge(unpack_steps, done + at)

                    if part == 0:
                        dve.wait_ge(loaded[s], 6 * DMA * i + 6 * DMA)
                        steps(2, nc.vector.tensor_scalar(code[:, :, 0, :], pack[:, s, :, :], 15, None, ALU.bitwise_and),
                              nc.vector.tensor_scalar(code[:, :, 1, :], pack[:, s, :, :], 4, 15, ALU.logical_shift_right,
                                                      ALU.bitwise_and))
                        steps(3, nc.vector.tensor_scalar(eight[:], code[:], 8.0, 8.0, ALU.is_ge, ALU.mult))
                    if part == 1:
                        steps(4, nc.vector.tensor_tensor(size[:], code[:], eight[:], ALU.subtract))
                        steps(6, nc.vector.tensor_scalar(twice[:], size[:], 2.0, -4.0, ALU.mult, ALU.add),
                              nc.vector.tensor_scalar(fourfold[:], size[:], 4.0, -16.0, ALU.mult, ALU.add))
                    if part == 2:
                        steps(7, nc.vector.tensor_tensor(twice[:], twice[:], fourfold[:], ALU.max))
                        steps(9, nc.vector.tensor_tensor(size[:], size[:], twice[:], ALU.max),
                              nc.vector.tensor_scalar(sign[:], eight[:], -0.125, 0.5, ALU.mult, ALU.add))
                    if part == 3:
                        steps(10, nc.vector.tensor_tensor(size[:], size[:], sign[:], ALU.mult))
                        if not first:
                            dve.wait_ge(lowered, 4 * (2 * i + s) - 4)
                        for j in range(3):
                            ins = nc.vector.tensor_tensor(
                                weight[:, s, j, :, :], size[:, j, :, :],
                                scale[:, s, j, :].unsqueeze(1).broadcast_to([P, 2, D]), ALU.mult)
                        ins.then_inc(weight_ready, 1)

                def round_(i, first=False, final=False):
                    for job in range(8):
                        s = job // 4
                        multiply(i, job)
                        if s == 0:
                            unpack(i, 1, job % 4, first)
                        elif not final:
                            unpack(i + 1, 0, job % 4)

                for part in range(4):
                    unpack(0, 0, part, True)
                round_(0, first=True)
                with dve.Fori(1, rounds - 1) as i:
                    round_(i)
                round_(rounds - 1, final=True)
                add_gated(nc, dve, x_tok, s_tok, gated, gate_ready, x_ready)


def build(nc, A, out):
    with ExitStack() as ctx:
        m = Core(nc, ctx)
        banks = ctx.enter_context(nc.psum_tensor("banks", [P, 8, BANK], F32))
        x_tok = m.sbuf("x_tok", [P, NT, D])
        xn_tok = m.sbuf("xn_tok", [P, NT, D])
        s_tok = m.sbuf("s_tok", [P, NT, D])
        xnT = m.sbuf("xnT", [P, KD, N])
        ident = m.sbuf("ident", [P, P])
        earlier = m.sbuf("earlier", [P, 16, 16])

        first_loads = nc.alloc_semaphore("first_loads")
        with nc.Block(no_gpsimd_drain=True) as block:
            @block.sync
            def _(sp):
                sp.dma_start(x_tok[:, :, :], A["L0_attn_x"].rearrange("b t d -> (b t) d")
                             .rearrange("(n p) d -> p n d", p=P)).then_inc(first_loads, DMA)
                sp.dma_start(ident[:, :], A["ident"]).then_inc(first_loads, DMA)
                sp.dma_start(earlier[:, :, :].rearrange("p a b -> p (a b)"), A["earlier"].partition_broadcast(P)
                             ).then_inc(first_loads, DMA)
                sp.wait_ge(first_loads, 3 * DMA)

        def new_layer():
            nc.clear_and_free_semaphores(nc.allocated_since(outer))
            nc.all_engine_barrier()

        outer = nc.snapshot_sems()
        with ExitStack() as layer:
            w, loads = load_layer0(Core(nc, layer), A)
            norm_stage(nc, 0, x_tok, xn_tok, xnT, ident, banks, loads)
            recurrence_stage(nc, w, xnT, s_tok, banks)
            scratch = nc.dram_tensor("probs_dram0", [8, N], F32).ap()
            top2_expert_stage(nc, w, (A["L0_ffn_gate_up_w"], A["L0_ffn_down_w"]), scratch, x_tok, xnT, s_tok,
                              ident, earlier, banks)
        new_layer()
        with ExitStack() as layer:
            inner = Core(nc, layer)
            w, loads = load_layer1(inner, A)
            norm_stage(nc, 1, x_tok, xn_tok, xnT, ident, banks, loads)
            rows = nc.dram_tensor("bc_dram", [2 * STATES, N], F32).ap()
            with ExitStack() as mixer:
                inner = Core(nc, mixer)
                keep = (inner.sbuf("skip", [P, MI, N]), inner.sbuf("xs", [P, MI, N]), inner.sbuf("delta", [P, MI, N]),
                        inner.sbuf("delta_x", [P, MI, N]), inner.sbuf("A", [P, MI, STATES]),
                        inner.sbuf("diag_D", [P, MI, P]))
                scan_prepare_stage(nc, w, xn_tok, ident, banks, keep, rows)
                scan_stage(nc, w, xn_tok, s_tok, ident, banks, keep, rows)
            squared_relu_stage(nc, w, A["L1_ffn_up_w"], A["L1_ffn_down_w"], x_tok, xnT, s_tok, banks)
        new_layer()
        with ExitStack() as layer:
            w, loads = load_layer2(Core(nc, layer), A)
            norm_stage(nc, 2, x_tok, xn_tok, xnT, ident, banks, loads)
            with ExitStack() as mixer:
                inner = Core(nc, mixer)
                keep = (inner.sbuf("q2", [P, 2, N]), inner.sbuf("keys2", [P, 8, N]), inner.sbuf("v2", [P, NT, HEAD2]))
                rotary_stage(nc, w, xnT, keep, banks)
                causal_attention_stage(nc, w, keep, s_tok, ident, banks)
            xn_dram = nc.dram_tensor("xn_dram2", [N, D], F32).ap()
            y_dram = nc.dram_tensor("y_dram2", [N + P, D], F32).ap()
            inner = Core(nc, layer)
            tables = (inner.sbuf("slot_token", [P, EXPERTS2], U32), inner.sbuf("slot_target", [P, EXPERTS2], U32),
                      inner.sbuf("slot_weight", [P, EXPERTS2]))
            route_stage(nc, w, xn_tok, xnT, ident, earlier, banks, tables, xn_dram, y_dram)
            slot_expert_stage(nc, (A["L2_ffn_w_gate"], A["L2_ffn_w_up"], A["L2_ffn_w_down"]), x_tok, s_tok, ident,
                              banks, tables, xn_dram, y_dram)
        new_layer()
        with ExitStack() as layer:
            w, loads = load_layer3(Core(nc, layer), A)
            norm_stage(nc, 3, x_tok, xn_tok, xnT, ident, banks, loads, parity=True)
            inner = Core(nc, layer)
            keep = (inner.sbuf("q_weight3", [P, KD, HEADS3 * LATENT]), inner.sbuf("o_weight3", [P, UNITS3, D]),
                    inner.sbuf("latT3", [P, N]), inner.sbuf("lat_tok3", [P, NT, LATENT]))
            latent_prepare_stage(nc, w, xnT, banks, keep)
            latent_attention_stage(nc, xnT, s_tok, ident, banks, keep)
        four_bit_stage(nc, [A[f"L3_ffn_{name}_W_packed"] for name in ("gate", "up", "down")],
                       [A[f"L3_ffn_{name}_scales"] for name in ("gate", "up", "down")], x_tok, xnT, s_tok, banks)

        stored = nc.alloc_semaphore("out_stored")
        with nc.Block(no_gpsimd_drain=True) as block:
            @block.sync
            def _(sp):
                sp.dma_start(out.rearrange("b t d -> (b t) d").rearrange("(n p) d -> p n d", p=P),
                             x_tok[:, :, :]).then_inc(stored, DMA)
                sp.wait_ge(stored, DMA)


def load_layer0(m, A):
    w, loads = {}, []

    def add(name, shape, src):
        w[name] = m.sbuf("w0_" + name, shape)
        loads.append((w[name][:], src))

    add("W_in", [P, KD, D], by_feature(A["L0_attn_W_in"]))
    add("W_ga", [P, KD, P], by_feature(A["L0_gates_a"]))
    add("W_gx", [P, KD, P], by_feature(A["L0_gates_x"]))
    add("W_out", [P, KD, D], by_feature(A["L0_attn_W_out"]))
    add("b_in", [P, KD], A["L0_attn_b_in"])
    add("b_ga", [P, 1], A["L0_attn_b_ga"])
    add("b_gx", [P, 1], A["L0_attn_b_gx"])
    add("a_real", [P, 1], A["L0_attn_a_real"])
    add("a_imag", [P, 1], A["L0_attn_a_imag"])
    add("b_out", [P, D], A["L0_attn_b_out"].partition_broadcast(P))
    add("router_w", [P, KD, 8], by_feature(A["L0_ffn_router_w"]))
    add("shared_gate_w", [P, KD, P], by_feature(A["L0_ffn_shared_gate_w"]))
    add("shared_up_w", [P, KD, P], by_feature(A["L0_ffn_shared_up_w"]))
    add("shared_down_w", [P, 1, D], by_feature(A["L0_ffn_shared_down_w"]))
    return w, loads


def load_layer1(m, A):
    w, loads = {}, []

    def add(name, shape, src):
        w[name] = m.sbuf("w1_" + name, shape)
        loads.append((w[name][:], src))

    add("A_log", [P, MI, STATES], by_feature(A["L1_attn_A_log"]))
    add("W_D", [P, MI], A["L1_attn_W_D"])
    add("norm_w", [P, KD], A["L1_attn_norm_w"])
    add("W_skip", [P, KD, INNER], by_feature(A["L1_attn_W_skip"]))
    add("W_in", [P, KD, INNER], by_feature(A["L1_attn_W_in"]))
    add("conv_w", [P, MI, 4], A["L1_attn_conv_w"].rearrange("(k p) a j -> p k (a j)", p=P))
    add("conv_b", [P, MI], A["L1_attn_conv_b"])
    add("W_d1", [P, MI, P], by_feature(A["L1_attn_W_d1"]))
    add("W_BC", [P, MI, 2 * STATES], by_feature(A["L1_attn_W_BC"]))
    add("W_d2", [P, 1, INNER], by_feature(A["L1_attn_W_d2"]))
    add("b_d2", [P, MI], A["L1_attn_b_d2"])
    add("W_out", [P, MI, D], by_feature(A["L1_attn_W_out"]))
    add("gate_w", [P, KD, 8], by_feature(A["L1_ffn_gate_w"]))
    add("expert_weight", [P, KD, D], by_feature(A["L1_ffn_expert_weight"]))
    add("ln_gamma", [P, D], A["L1_ffn_ln_gamma"].partition_broadcast(P))
    add("ln_beta", [P, D], A["L1_ffn_ln_beta"].partition_broadcast(P))
    return w, loads


def load_layer2(m, A):
    w, loads = {}, []

    def add(name, shape, src, dtype=F32):
        w[name] = m.sbuf("w2_" + name, shape, dtype)
        loads.append((w[name][:], src))

    for name in ("Wq", "Wq_swap", "Wo"):
        add(name, [P, KD, D], by_feature(A["L2_attn_" + name]))
    add("Wk", [P, KD, P], by_feature(A["L2_attn_Wk"]))
    add("Wv", [P, KD, HEAD2], by_feature(A["L2_attn_Wv"]))
    add("gate_w", [P, KD, EXPERTS2], by_feature(A["L2_ffn_gate_w"]))
    add("sw_gate", [P, KD, SHARED2], by_feature(A["L2_ffn_sw_gate"]))
    add("sw_up", [P, KD, SHARED2], by_feature(A["L2_ffn_sw_up"]))
    add("sw_down", [ROWS2, SHARED2 // ROWS2, D], A["L2_ffn_sw_down"].rearrange("(i p) d -> p i d", p=ROWS2))
    for name in ("cos", "sin", "head_rows", "causal", "before", "slots", "token_place", "spare_row"):
        add(name, list(A[name].shape), A[name])
    return w, loads


def load_layer3(m, A):
    w, loads = {}, []

    def add(name, shape, src):
        w[name] = m.sbuf("w3_" + name, shape)
        loads.append((w[name][:], src))

    add("WqT", [P, HEADS3, D], by_feature(A["L3_attn_W_q"]))
    add("WupT", [P, HEADS3, LATENT], by_feature(A["L3_attn_W_kv_up"]))
    add("Wdown2", [P, KD, 2 * LATENT], by_feature(A["L3_attn_W_kv_down"]))
    add("Wo", [P, HEADS3, D], by_feature(A["L3_attn_W_o"]))
    return w, loads


COLUMNS = ("L0_attn_b_in", "L0_attn_b_ga", "L0_attn_b_gx", "L0_attn_a_real", "L0_attn_a_imag",
           "L1_attn_W_D", "L1_attn_norm_w", "L1_attn_conv_b", "L1_attn_b_d2")
TRANSPOSED = ("L1_attn_W_skip", "L1_attn_W_in", "L1_attn_W_d1", "L1_attn_W_d2", "L1_attn_W_out")


def block_diagonal(blocks):
    h, i, j = blocks.shape
    full = np.zeros((h, i, h, j), blocks.dtype)
    for n in range(h):
        full[n, :, n, :] = blocks[n]
    return full.reshape(h * i, h * j)


def laid_out(inputs):
    A = {name: np.ascontiguousarray(value) for name, value in inputs.items()}
    A["L0_gates_a"] = block_diagonal(A.pop("L0_attn_W_ga"))
    A["L0_gates_x"] = block_diagonal(A.pop("L0_attn_W_gx"))
    A["ident"] = np.eye(P, dtype=np.float32)
    A["earlier"] = np.tril(np.ones((16, 16), np.float32), -1).reshape(-1)
    for name in COLUMNS:
        A[name] = A[name].reshape(-1, P).T
    A["L1_attn_W_BC"] = np.concatenate([A.pop("L1_attn_W_Bm"), A.pop("L1_attn_W_Cm")]).T
    for name in TRANSPOSED:
        A[name] = A[name].T
    A["L2_attn_Wq_swap"] = A["L2_attn_Wq"][np.arange(D) ^ 1].T
    A["L2_attn_Wk"] = np.tile(A["L2_attn_Wk"], (8, 1)).T
    A["L2_attn_Wq"] = A["L2_attn_Wq"].T
    A["L2_attn_Wv"], A["L2_attn_Wo"] = A["L2_attn_Wv"].T, A["L2_attn_Wo"].T
    half = HEAD2 // 2
    theta = 1.0 / np.float32(10000.0) ** (np.arange(0, half, 2, dtype=np.float32) / np.float32(half))
    freq = np.arange(HEADS2, dtype=np.float32)[:, None] * theta.astype(np.float32)[None, :]
    head, place = np.arange(D) // HEAD2, np.arange(D) % half
    A["cos"] = np.cos(freq)[head, place // 2].reshape(KD, P).T
    A["sin"] = (np.sin(freq)[head, place // 2] * np.where(place % 2, 1, -1).astype(np.float32)).reshape(KD, P).T
    A["head_rows"] = np.repeat(np.eye(8, dtype=np.float32), HEAD2, axis=0)
    later = np.triu(np.full((P, P), -1e30, np.float32), 1)
    A["causal"] = np.concatenate([np.zeros((P, P), np.float32), later], axis=1)
    A["L2_ffn_gate_w"] = A["L2_ffn_gate_w"].T
    A["before"] = np.triu(np.ones((P, P), np.float32), 1)
    A["slots"] = np.tile(np.arange(CAPACITY, dtype=np.float32), (P, 1))
    token = np.arange(N).reshape(NT, P).T
    A["token_place"] = np.stack([token % P, token - token % P], axis=-1).astype(np.float32)
    A["spare_row"] = np.arange(N, N + P, dtype=np.float32)[:, None]
    parity = np.concatenate([np.arange(0, D, 2), np.arange(1, D, 2)])
    A["L3_attn_W_q"] = A["L3_attn_W_q"][parity].T
    A["L3_attn_W_kv_up"] = A["L3_attn_W_kv_up"].T
    A["L3_attn_W_kv_down"] = np.tile(A["L3_attn_W_kv_down"][parity], (1, 2))
    hidden = np.arange(MLP3).reshape(PACKS3, P, 2).transpose(0, 2, 1).reshape(PACKS3, 2 * P)
    for name in ("gate", "up"):
        A[f"L3_ffn_{name}_W_packed"] = A[f"L3_ffn_{name}_W_packed"][hidden].transpose(0, 2, 1)
        A[f"L3_ffn_{name}_scales"] = np.repeat(A[f"L3_ffn_{name}_scales"][hidden].transpose(0, 2, 1), 16, axis=1)
    A["L3_ffn_down_W_packed"] = A["L3_ffn_down_W_packed"].T.reshape(PACKS3, P, D)
    A["L3_ffn_down_scales"] = np.repeat(A["L3_ffn_down_scales"].T, 16, axis=0).reshape(PACKS3, P, D)
    return {name: np.ascontiguousarray(value) for name, value in A.items()}


def kernel(**inputs):
    import concourse.bacc as bacc
    from concourse.bass_utils import run_bass_kernel_spmd

    nc = bacc.Bacc("TRN2", target_bir_lowering=False, num_devices=1)
    arrays = laid_out(inputs)
    aps = {name: nc.dram_tensor("in_" + name, a.shape, mybir.dt.from_np(a.dtype), kind="ExternalInput").ap()
           for name, a in arrays.items()}
    out = nc.dram_tensor("out_dram", (BATCH, SEQ, D), F32, kind="ExternalOutput").ap()
    build(nc, aps, out)
    result = run_bass_kernel_spmd(nc, [{"in_" + name: a for name, a in arrays.items()}], core_ids=[0])
    return result.results[0]["out_dram"]
```

```python
from contextlib import ExitStack

import numpy as np

import concourse.bass as bass
from concourse import mybir

F32 = mybir.dt.float32
BF16 = mybir.dt.bfloat16
I32 = mybir.dt.int32
U32 = mybir.dt.uint32
ALU = mybir.AluOpType
ACT = mybir.ActivationFunctionType
AX = mybir.AxisListType

P = 128
BATCH, SEQ, D = 4, 256, 256
N = BATCH * SEQ
NT = N // P
KD = D // P
HALF = N // 2
BANK = 512
EPS = 1e-5
DMA = 16


class Steps:

    def __init__(self, eng, sem):
        self.eng, self.sem, self.count = eng, sem, 0

    def add(self, ins):
        ins.then_inc(self.sem, 1)
        self.count += 1

    def join(self):
        self.eng.wait_ge(self.sem, self.count)

    def do(self, ins):
        self.add(ins)
        self.join()


class Core:

    def __init__(self, nc, ctx):
        self.nc, self.ctx = nc, ctx

    def sbuf(self, name, shape, dtype=F32):
        return self.ctx.enter_context(self.nc.sbuf_tensor(name, shape, dtype))

    def sem(self, name):
        return self.ctx.enter_context(self.nc.semaphore(name))

    def scope(self, ctx):
        return Core(self.nc, ctx)


def by_feature(w):
    return w.rearrange("(k p) m -> p k m", p=P)


def norm_stage(nc, layer, x_tok, xn_tok, xnT, ident, banks, loads, parity=False):
    with ExitStack() as ctx:
        m = Core(nc, ctx).scope(ctx)
        stats = m.sbuf(f"stats{layer}", [P, NT, 6])
        mean_var = m.sbuf(f"mean_var{layer}", [P, NT, 2])
        var = m.sbuf(f"var{layer}", [P, NT])
        std = m.sbuf(f"std{layer}", [P, NT])
        rstd = m.sbuf(f"rstd{layer}", [P, NT])
        norm_steps = nc.alloc_semaphore(f"norm_steps{layer}")
        var_ready = nc.alloc_semaphore(f"norm_var_ready{layer}")
        std_ready = nc.alloc_semaphore(f"norm_std_ready{layer}")
        xn_ready = nc.alloc_semaphore(f"xn_ready{layer}")
        turned = nc.alloc_semaphore(f"xn_turned{layer}")
        xnT_ready = nc.alloc_semaphore(f"xnT_ready{layer}")
        loaded = nc.alloc_semaphore(f"weights_loaded{layer}")

        with nc.Block(no_gpsimd_drain=True) as block:

            @block.sync
            def _(sp):
                for dst, src in loads:
                    sp.dma_start(dst, src).then_inc(loaded, DMA)
                sp.wait_ge(loaded, DMA * len(loads))

            @block.vector
            def _(dve):
                steps = Steps(dve, norm_steps)
                for t in range(NT):
                    steps.add(nc.vector.bn_stats(stats[:, t, :], x_tok[:, t, :]))
                steps.join()
                for t in range(NT):
                    steps.add(nc.vector.bn_aggr(mean_var[:, t, :], stats[:, t, :]))
                steps.join()
                nc.vector.tensor_scalar(var[:, :], mean_var[:, :, 1], EPS, None, ALU.add).then_inc(var_ready, 1)
                dve.wait_ge(std_ready, 1)
                steps.do(nc.vector.reciprocal(rstd[:, :], std[:, :]))
                for t in range(NT):
                    nc.vector.tensor_scalar(
                        xn_tok[:, t, :], x_tok[:, t, :], mean_var[:, t, 0:1], rstd[:, t:t + 1],
                        ALU.subtract, ALU.mult).then_inc(xn_ready, 1)

            @block.tensor
            def _(pe):
                for t in range(NT):
                    pe.wait_ge(xn_ready, t + 1)
                    for k in range(KD):
                        part = xn_tok[:, t, k::2] if parity else xn_tok[:, t, k * P:(k + 1) * P]
                        last = nc.tensor.transpose(
                            banks[:, KD * (t // 4) + k, (t % 4) * P:(t % 4 + 1) * P], part, ident[:, :])
                    last.then_inc(turned, 1)

            @block.scalar
            def _(act):
                act.wait_ge(var_ready, 1)
                nc.scalar.activation(std[:, :], var[:, :], ACT.Sqrt).then_inc(std_ready, 1)
                for half in range(2):
                    act.wait_ge(turned, 4 * (half + 1))
                    for k in range(KD):
                        nc.scalar.activation(xnT[:, k, half * HALF:(half + 1) * HALF],
                                             banks[:, KD * half + k, :], ACT.Identity).then_inc(xnT_ready, 1)


def rank_mask(nc, steps, mask, values, scratch, earlier, experts, top):
    shape = [P, NT, experts, experts]
    others = values.unsqueeze(2).broadcast_to(shape)
    own = values.unsqueeze(3).broadcast_to(shape)
    above, equal, count = scratch
    steps.add(nc.vector.tensor_tensor(above, others, own, ALU.is_gt))
    steps.do(nc.vector.tensor_tensor(equal, others, own, ALU.is_equal))
    steps.do(nc.vector.tensor_tensor(
        equal, equal, earlier[:, 0:experts, 0:experts].unsqueeze(1).broadcast_to(shape), ALU.mult))
    steps.do(nc.vector.tensor_tensor(above, above, equal, ALU.add))
    steps.do(nc.vector.tensor_reduce(count, above, AX.X, ALU.add))
    steps.do(nc.vector.tensor_scalar(mask, count, float(top), None, ALU.is_lt))


def silu_sum(nc, act, gated, banks, ready, count, gate_ready):
    act.wait_ge(ready, count)
    for b in range(NT // 2):
        nc.scalar.activation(gated[:, 2 * b:2 * b + 2, :].rearrange("p t d -> p (t d)"), banks[:, b, :],
                             ACT.Silu).then_inc(gate_ready, 1)


def add_gated(nc, dve, x_tok, s_tok, gated, gate_ready, x_ready):
    for b in range(NT // 2):
        pair = slice(2 * b, 2 * b + 2)
        dve.wait_ge(gate_ready, b + 1)
        nc.vector.tensor_tensor(gated[:, pair, :], gated[:, pair, :], s_tok[:, pair, :], ALU.mult
                                ).then_inc(x_ready, 1)
        dve.wait_ge(x_ready, 2 * b + 1)
        nc.vector.tensor_tensor(x_tok[:, pair, :], x_tok[:, pair, :], gated[:, pair, :], ALU.add
                                ).then_inc(x_ready, 1)


def recurrent_layer_stage(nc, w, weights, scratch, x_tok, xnT, s_tok, ident, earlier, banks):
    experts, top, width = 8, 2, 128
    jobs = 2 * (experts + 1)
    gate_up, down = weights
    two_pi = 6.283185
    rounder = 1.5 * 2.0 ** 23
    with ExitStack() as ctx:
        m = Core(nc, ctx)
        xh = m.sbuf("xh", [P, 2, N])
        gate_x = m.sbuf("gate_x", [P, N])
        gate_a = m.sbuf("gate_a", [P, N])
        radius = m.sbuf("radius", [P, N])
        radius2 = m.sbuf("radius2", [P, N])
        inside = m.sbuf("inside", [P, N])
        turns = m.sbuf("turns", [P, N])
        phi = m.sbuf("phi", [P, N])
        angle = m.sbuf("angle", [P, 4, N])
        wave = m.sbuf("wave", [P, 4, N])
        zr = m.sbuf("zr", [P, N])
        zi = m.sbuf("zi", [P, N])
        ta = m.sbuf("ta", [P, N])
        tb = m.sbuf("tb", [P, N])
        tc = m.sbuf("tc", [P, N])
        td = m.sbuf("td", [P, N])
        hT = m.sbuf("hT", [P, 2, N])
        coef = m.sbuf("coef", [P, 8])
        logits = m.sbuf("logits0", [P, NT, experts])
        chance = m.sbuf("chance0", [P, NT, experts])
        above = m.sbuf("above0", [P, NT, experts, experts])
        equal = m.sbuf("equal0", [P, NT, experts, experts])
        count = m.sbuf("count0", [P, NT, experts])
        mask = m.sbuf("mask0", [P, NT, experts])
        probs = m.sbuf("probs0", [P, NT, experts])
        probsT = m.sbuf("probsT0", [experts, N])
        gate_up_w = m.sbuf("gate_up_w", [P, 2, KD, 2 * width])
        down_w = m.sbuf("down_w", [P, 2, D])
        prob = m.sbuf("prob_row", [P, 2, N])
        x_in = m.sbuf("expert_x", [P, 2, KD, N])
        silu = m.sbuf("expert_silu", [P, 2, HALF])
        up = m.sbuf("expert_up", [P, 2, HALF])
        ffn_hT = m.sbuf("expert_hT", [P, 2, HALF])
        gated = m.sbuf("gated0", [P, NT, D])
        logits_done = nc.alloc_semaphore("logits_done0")
        logits_ready = nc.alloc_semaphore("logits_ready0")
        router_steps = nc.alloc_semaphore("router_steps0")
        chance_ready = nc.alloc_semaphore("chance_ready0")
        probs_ready = nc.alloc_semaphore("probs_ready0")
        probs_turned = nc.alloc_semaphore("probs_turned0")
        probsT_ready = nc.alloc_semaphore("probsT_ready0")
        probs_stored = nc.alloc_semaphore("probs_stored0")
        gate_up_loaded = [nc.alloc_semaphore(f"gate_up_loaded0_{s}") for s in range(2)]
        down_loaded = [nc.alloc_semaphore(f"down_loaded0_{s}") for s in range(2)]
        prob_loaded = [nc.alloc_semaphore(f"prob_loaded0_{s}") for s in range(2)]
        x_in_ready = nc.alloc_semaphore("expert_x_ready0")
        raised = nc.alloc_semaphore("raised0")
        evacuated = nc.alloc_semaphore("evacuated0")
        ffn_h_ready = nc.alloc_semaphore("expert_h_ready0")
        lowered = nc.alloc_semaphore("lowered0")
        gate_ready = nc.alloc_semaphore("gate_ready0")
        x_ready = nc.alloc_semaphore("x_ready0")
        cols = [slice(h * HALF, (h + 1) * HALF) for h in range(2)]
        xh_done = nc.alloc_semaphore("xh_done")
        xh_ready = nc.alloc_semaphore("xh_ready")
        gates_done = nc.alloc_semaphore("gates_done")
        gate_x_ready = nc.alloc_semaphore("gate_x_ready")
        gate_a_ready = nc.alloc_semaphore("gate_a_ready")
        coef_steps = nc.alloc_semaphore("coef_steps")
        coef_ready = nc.alloc_semaphore("coef_ready")
        radius_ready = nc.alloc_semaphore("radius_ready")
        angles_ready = nc.alloc_semaphore("angles_ready")
        waves_ready = nc.alloc_semaphore("waves_ready")
        square_ready = nc.alloc_semaphore("square_ready")
        modulus_ready = nc.alloc_semaphore("modulus_ready")
        inside_ready = nc.alloc_semaphore("inside_ready")
        rec_steps = nc.alloc_semaphore("rec_steps")
        h_ready = nc.alloc_semaphore("h_ready")
        mixed = nc.alloc_semaphore("mixed0")
        s_ready = nc.alloc_semaphore("s_ready0")
        starts = slice(0, N, SEQ)

        with nc.Block(no_gpsimd_drain=True) as block:

            @block.sync
            def _(sp):
                def load_gate_up(e, s):
                    sp.dma_start(gate_up_w[:, s, :, :],
                                 gate_up[bass.ds(e, 1), :, :].rearrange("e (k p) n -> p (e k) n", p=P)
                                 ).then_inc(gate_up_loaded[s], DMA)

                def load_down(e, s):
                    sp.dma_start(down_w[:, s, :], down[bass.ds(e, 1), :, :].rearrange("e p n -> p (e n)")
                                 ).then_inc(down_loaded[s], DMA)

                def load_prob(e, s):
                    sp.dma_start(prob[:, s, :], scratch[bass.ds(e, 1), :].rearrange("e n -> (e n)")
                                 .partition_broadcast(P)).then_inc(prob_loaded[s], DMA)

                for s in range(2):
                    load_gate_up(s, s)
                    load_down(s, s)
                sp.wait_ge(probsT_ready, 2)
                sp.dma_start(scratch[:, :], probsT[:, :]).then_inc(probs_stored, DMA)
                sp.wait_ge(probs_stored, DMA)
                for s in range(2):
                    load_prob(s, s)
                with sp.Fori(1, experts // 2) as i:
                    for s in range(2):
                        sp.wait_ge(x_in_ready, 4 * i + 2 * s - 2)
                        load_prob(2 * i + s, s)
                        sp.wait_ge(raised, 4 * i + 2 * s)
                        load_gate_up(2 * i + s, s)
                        sp.wait_ge(lowered, 4 * i + 2 * s)
                        load_down(2 * i + s, s)

            @block.tensor
            def _(pe):
                def raise_(half, wide, x, count=None):
                    if count is not None:
                        pe.wait_ge(evacuated, count)
                    for j in range(2):
                        for k in range(KD):
                            last = nc.tensor.matmul(banks[:, 4 + 2 * half + j, :], wide(j, k), x(k)[:, cols[half]],
                                                    start=(k == 0), stop=(k == KD - 1))
                    last.then_inc(raised, 1)

                def lower(half, wt, count, first=False):
                    pe.wait_ge(ffn_h_ready, count)
                    for t in range(4):
                        last = nc.tensor.matmul(
                            banks[:, 2 * half + t // 2, (t % 2) * D:(t % 2 + 1) * D], ffn_hT[:, half, t * P:(t + 1) * P], wt,
                            start=first and t % 2 == 0, stop=False, skip_group_check=True)
                    last.then_inc(lowered, 1)

                def expert(i, s, first=False):
                    pe.wait_ge(gate_up_loaded[s], DMA * (i + 1))
                    for half in range(2):
                        job = 4 * i + 2 * s + half
                        pe.wait_ge(x_in_ready, job + 1)
                        raise_(half, lambda j, k: gate_up_w[:, s, k, j * width:(j + 1) * width],
                               lambda k: x_in[:, s, k, :], 2 * job + 2)
                        if first and s == 0:
                            lower(half, w["shared_down_w"][:, 0, :], job + 1, True)
                        else:
                            if half == 0:
                                pe.wait_ge(down_loaded[1 - s], DMA * (i + s))
                            lower(half, down_w[:, 1 - s, :], job + 1)

                for t in range(NT):
                    for k in range(KD):
                        last = nc.tensor.matmul(banks[:, 4, t * experts:(t + 1) * experts],
                                                xnT[:, k, t * P:(t + 1) * P], w["router_w"][:, k, :],
                                                start=(k == 0), stop=(k == KD - 1))
                last.then_inc(logits_done, 1)
                for part in range(2):
                    for half in range(2):
                        for k in range(KD):
                            last = nc.tensor.matmul(
                                banks[:, 2 * part + half, :], w["W_in"][:, k, part * P:(part + 1) * P],
                                xnT[:, k, half * HALF:(half + 1) * HALF], start=(k == 0), stop=(k == KD - 1))
                        last.then_inc(xh_done, 1)
                pe.wait_ge(xh_ready, 4)
                pe.wait_ge(logits_ready, 1)
                for gate, name in enumerate(("W_ga", "W_gx")):
                    for half in range(2):
                        for k in range(KD):
                            last = nc.tensor.matmul(
                                banks[:, 4 + 2 * gate + half, :], w[name][:, k, :],
                                xh[:, k, half * HALF:(half + 1) * HALF], start=(k == 0), stop=(k == KD - 1))
                        last.then_inc(gates_done, 1)
                pe.wait_ge(probs_ready, 1)
                for t in range(NT):
                    last = nc.tensor.transpose(banks[0:experts, t // 4, (t % 4) * P:(t % 4 + 1) * P],
                                               probs[:, t, :], ident[:, :])
                last.then_inc(probs_turned, 1)
                for half, ready in enumerate((gate_a_ready, gate_x_ready)):
                    pe.wait_ge(ready, 2)
                    raise_(half, lambda j, k: w[("shared_gate_w", "shared_up_w")[j]][:, k, :], lambda k: xnT[:, k, :])
                pe.wait_ge(probsT_ready, 2)
                expert(0, 0, first=True)
                expert(0, 1, first=True)
                with pe.Fori(1, experts // 2) as i:
                    expert(i, 0)
                    expert(i, 1)
                pe.wait_ge(down_loaded[1], DMA * (experts // 2))
                for half in range(2):
                    lower(half, down_w[:, 1, :], jobs - 1 + half)
                pe.wait_ge(evacuated, 2 * jobs)
                pe.wait_ge(h_ready, 2)
                for t in range(NT):
                    for k in range(KD):
                        last = nc.tensor.matmul(
                            banks[:, 4 + t // 2, (t % 2) * D:(t % 2 + 1) * D], hT[:, k, t * P:(t + 1) * P],
                            w["W_out"][:, k, :], start=(k == 0), stop=(k == KD - 1))
                    last.then_inc(mixed, 1)

            @block.scalar
            def _(act):
                def evacuate(job, half, count=None):
                    act.wait_ge(raised, job + 1)
                    if count is not None:
                        act.wait_ge(ffn_h_ready, count)
                    nc.scalar.activation(silu[:, half, :], banks[:, 4 + 2 * half, :], ACT.Silu).then_inc(evacuated, 1)
                    nc.scalar.activation(up[:, half, :], banks[:, 5 + 2 * half, :], ACT.Identity).then_inc(evacuated, 1)

                def expert(e):
                    for half in range(2):
                        evacuate(2 * e + 2 + half, half, 2 * e + 1 + half)

                def root(q):
                    act.wait_ge(square_ready, q + 1)
                    nc.scalar.activation(tc[:, :], ta[:, :], ACT.Sqrt).then_inc(modulus_ready, 1)

                steps = Steps(act, coef_steps)
                steps.do(nc.scalar.activation(coef[:, 0:1], w["a_real"][:, :], ACT.Abs))
                steps.do(nc.scalar.activation(coef[:, 1:2], coef[:, 0:1], ACT.Exp, scale=-1.0))
                nc.scalar.activation(coef[:, 2:3], coef[:, 1:2], ACT.Ln, bias=1.0).then_inc(coef_ready, 1)
                act.wait_ge(logits_ready, 1)
                nc.scalar.activation(chance[:, :, :], logits[:, :, :], ACT.Sigmoid).then_inc(chance_ready, 1)
                for part in range(2):
                    for half in range(2):
                        act.wait_ge(xh_done, 2 * part + half + 1)
                        nc.scalar.activation(
                            xh[:, part, half * HALF:(half + 1) * HALF], banks[:, 2 * part + half, :],
                            ACT.Identity, bias=w["b_in"][:, part:part + 1]).then_inc(xh_ready, 1)
                for gate, (dst, bias, ready) in enumerate(
                        ((gate_a, "b_ga", gate_a_ready), (gate_x, "b_gx", gate_x_ready))):
                    for half in range(2):
                        act.wait_ge(gates_done, 2 * gate + half + 1)
                        nc.scalar.activation(dst[:, half * HALF:(half + 1) * HALF],
                                             banks[:, 4 + 2 * gate + half, :], ACT.Sigmoid,
                                             bias=w[bias][:, 0:1]).then_inc(ready, 1)
                act.wait_ge(probs_turned, 1)
                for half in range(2):
                    nc.scalar.activation(probsT[:, cols[half]], banks[0:experts, half, :], ACT.Identity
                                         ).then_inc(probsT_ready, 1)
                act.wait_ge(coef_ready, 2)
                act.wait_ge(gate_a_ready, 2)
                nc.scalar.activation(radius[:, :], gate_a[:, :], ACT.Exp, scale=coef[:, 4:5]).then_inc(radius_ready, 1)
                nc.scalar.activation(radius2[:, :], gate_a[:, :], ACT.Exp, scale=coef[:, 5:6]).then_inc(radius_ready, 1)
                for half in range(2):
                    evacuate(half, half)
                for q in range(4):
                    act.wait_ge(angles_ready, q + 1)
                    nc.scalar.activation(wave[:, q, :], angle[:, q, :], ACT.Sin, scale=two_pi).then_inc(waves_ready, 1)
                for e in range(2):
                    expert(e)
                    root(e)
                with act.Fori(2, experts) as e:
                    expert(e)
                silu_sum(nc, act, gated, banks, lowered, jobs, gate_ready)

            @block.gpsimd
            def _(pool):
                nc.gpsimd.memset(inside[:, :], 1.0).then_inc(inside_ready, 1)
                pool.wait_ge(inside_ready, 1)
                nc.gpsimd.memset(inside[:, starts], 0.0).then_inc(inside_ready, 1)

                def weigh(i, s, first=False):
                    pool.wait_ge(prob_loaded[s], DMA * (i + 1))
                    for half in range(2):
                        if not first:
                            pool.wait_ge(raised, 4 * i + 2 * s + half - 1)
                        nc.gpsimd.tensor_tensor(
                            x_in[:, s, :, cols[half]], xnT[:, :, cols[half]],
                            prob[:, s, cols[half]].unsqueeze(1).broadcast_to([P, KD, HALF]), ALU.mult
                            ).then_inc(x_in_ready, 1)

                def hidden(job, half, count=None):
                    pool.wait_ge(evacuated, 2 * job + 2)
                    if count is not None:
                        pool.wait_ge(lowered, count)
                    nc.gpsimd.tensor_tensor(ffn_hT[:, half, :], silu[:, half, :], up[:, half, :], ALU.mult
                                            ).then_inc(ffn_h_ready, 1)

                def expert(i, s):
                    for half in range(2):
                        job = 4 * i + 2 * s + 2 + half
                        hidden(job, half, job - 1)

                for half in range(2):
                    hidden(half, half)
                for s in range(2):
                    weigh(0, s, True)
                with pool.Fori(0, experts // 2 - 1) as i:
                    for s in range(2):
                        expert(i, s)
                        weigh(i + 1, s)
                for s in range(2):
                    expert(experts // 2 - 1, s)

            @block.vector
            def _(dve):
                steps = Steps(dve, rec_steps)

                def both(dst, a, op, b):
                    steps.add(nc.vector.tensor_tensor(dst, a, b, op))

                router = Steps(dve, router_steps)
                dve.wait_ge(logits_done, 1)
                nc.vector.tensor_copy(logits[:, :, :].rearrange("p t e -> p (t e)"), banks[:, 4, 0:NT * experts]
                                      ).then_inc(logits_ready, 1)
                dve.wait_ge(logits_ready, 1)
                rank_mask(nc, router, mask[:, :, :], logits[:, :, :],
                          (above[:, :, :, :], equal[:, :, :, :], count[:, :, :]), earlier, experts, top)
                dve.wait_ge(chance_ready, 1)
                nc.vector.tensor_tensor(probs[:, :, :], mask[:, :, :], chance[:, :, :], ALU.mult
                                        ).then_inc(probs_ready, 1)
                dve.wait_ge(coef_ready, 1)
                steps.do(nc.vector.tensor_scalar(coef[:, 3:4], w["a_real"][:, :], 0.0, None, ALU.max))
                steps.do(nc.vector.tensor_tensor(coef[:, 6:7], coef[:, 2:3], coef[:, 3:4], ALU.add))
                steps.do(nc.vector.tensor_scalar(coef[:, 4:5], coef[:, 6:7], -8.0, None, ALU.mult))
                steps.do(nc.vector.tensor_scalar(coef[:, 5:6], coef[:, 6:7], -16.0, None, ALU.mult))
                nc.vector.tensor_scalar(coef[:, 7:8], w["a_imag"][:, :], 1.0 / (2.0 * np.pi), None,
                                        ALU.mult).then_inc(coef_ready, 1)
                dve.wait_ge(coef_ready, 2)
                dve.wait_ge(gate_a_ready, 2)
                steps.do(nc.vector.tensor_scalar(turns[:, :], gate_a[:, :], coef[:, 7:8], None, ALU.mult))
                dve.wait_ge(inside_ready, 2)
                steps.add(nc.vector.tensor_tensor_scan(phi[:, :], inside[:, :], turns[:, :], 0.0, ALU.mult, ALU.add))
                steps.do(nc.vector.tensor_scalar(ta[:, :], turns[:, :], 2.0, 0.25, ALU.mult, ALU.add))
                for q in range(4):
                    if q == 1:
                        steps.do(nc.vector.tensor_scalar(ta[:, :], turns[:, :], 2.0, None, ALU.mult))
                    if q == 2:
                        steps.do(nc.vector.tensor_scalar(ta[:, :], phi[:, :], 0.25, None, ALU.add))
                    cur = phi if q == 3 else ta
                    steps.do(nc.vector.tensor_scalar(tb[:, :], cur[:, :], rounder, rounder, ALU.add, ALU.subtract))
                    nc.vector.tensor_tensor(angle[:, q, :], cur[:, :], tb[:, :], ALU.subtract).then_inc(angles_ready, 1)
                    dve.wait_ge(angles_ready, q + 1)
                dve.wait_ge(waves_ready, 2)
                dve.wait_ge(radius_ready, 2)
                both(ta[:, :], radius2[:, :], ALU.mult, wave[:, 0, :])
                both(tb[:, :], radius2[:, :], ALU.mult, wave[:, 1, :])
                steps.add(nc.vector.memset(radius[:, starts], 0.0))
                steps.join()
                steps.add(nc.vector.tensor_scalar(zr[:, :], ta[:, :], -1.0, 1.0, ALU.mult, ALU.add))
                steps.add(nc.vector.tensor_scalar(zi[:, :], tb[:, :], -1.0, None, ALU.mult))
                steps.join()
                both(ta[:, :], zr[:, :], ALU.mult, zr[:, :])
                both(tb[:, :], zi[:, :], ALU.mult, zi[:, :])
                steps.join()
                nc.vector.tensor_tensor(ta[:, :], ta[:, :], tb[:, :], ALU.add).then_inc(square_ready, 1)
                dve.wait_ge(modulus_ready, 1)
                steps.do(nc.vector.tensor_tensor(tb[:, :], tc[:, :], zr[:, :], ALU.add))
                nc.vector.tensor_scalar(ta[:, :], tb[:, :], 0.5, 1e-30, ALU.mult, ALU.max).then_inc(square_ready, 1)
                dve.wait_ge(modulus_ready, 2)
                steps.do(nc.vector.reciprocal(tb[:, :], tc[:, :]))
                steps.do(nc.vector.scalar_tensor_tensor(td[:, :], zi[:, :], 0.5, tb[:, :], ALU.mult, ALU.mult))
                dve.wait_ge(gate_x_ready, 2)
                both(tc[:, :], tc[:, :], ALU.mult, gate_x[:, :])
                both(td[:, :], td[:, :], ALU.mult, gate_x[:, :])
                steps.join()
                both(ta[:, :], tc[:, :], ALU.mult, xh[:, 0, :])
                both(tb[:, :], td[:, :], ALU.mult, xh[:, 1, :])
                both(radius2[:, :], tc[:, :], ALU.mult, xh[:, 1, :])
                both(turns[:, :], td[:, :], ALU.mult, xh[:, 0, :])
                steps.join()
                both(zr[:, :], ta[:, :], ALU.subtract, tb[:, :])
                both(zi[:, :], radius2[:, :], ALU.add, turns[:, :])
                steps.join()
                dve.wait_ge(waves_ready, 4)
                cos, sin = wave[:, 2, :], wave[:, 3, :]
                both(ta[:, :], zr[:, :], ALU.mult, cos)
                both(tb[:, :], zi[:, :], ALU.mult, sin)
                both(tc[:, :], zi[:, :], ALU.mult, cos)
                both(td[:, :], zr[:, :], ALU.mult, sin)
                steps.join()
                both(ta[:, :], ta[:, :], ALU.add, tb[:, :])
                both(tc[:, :], tc[:, :], ALU.subtract, td[:, :])
                steps.join()
                steps.add(nc.vector.tensor_tensor_scan(zr[:, :], radius[:, :], ta[:, :], 0.0, ALU.mult, ALU.add))
                steps.add(nc.vector.tensor_tensor_scan(zi[:, :], radius[:, :], tc[:, :], 0.0, ALU.mult, ALU.add))
                steps.join()
                both(ta[:, :], zr[:, :], ALU.mult, cos)
                both(tb[:, :], zi[:, :], ALU.mult, sin)
                both(tc[:, :], zr[:, :], ALU.mult, sin)
                both(td[:, :], zi[:, :], ALU.mult, cos)
                steps.join()
                nc.vector.tensor_tensor(hT[:, 0, :], ta[:, :], tb[:, :], ALU.subtract).then_inc(h_ready, 1)
                nc.vector.tensor_tensor(hT[:, 1, :], tc[:, :], td[:, :], ALU.add).then_inc(h_ready, 1)
                for b in range(NT // 2):
                    dve.wait_ge(mixed, 2 * b + 2)
                    nc.vector.tensor_tensor(
                        s_tok[:, 2 * b:2 * b + 2, :], banks[:, 4 + b, :].rearrange("p (t d) -> p t d", t=2),
                        w["b_out"][:, :].unsqueeze(1).broadcast_to([P, 2, D]), ALU.add).then_inc(s_ready, 1)
                dve.wait_ge(s_ready, NT // 2)
                add_gated(nc, dve, x_tok, s_tok, gated, gate_ready, x_ready)




STATES = 16
INNER = 512
MI = INNER // P


def scan_prepare_stage(nc, w, xn_tok, xnT, ident, banks, keep, rows, y):
    taps, experts = 4, 8
    skip, xs, delta, dx, A, diag = keep
    with ExitStack() as ctx:
        m = Core(nc, ctx)
        junk = m.sbuf("rms_junk", [P, D])
        mean_sq = m.sbuf("mean_sq", [P, NT])
        rms = m.sbuf("rms", [P, NT])
        rrms = m.sbuf("rrms", [P, NT])
        x1_tok = m.sbuf("x1_tok", [P, NT, D])
        x1T = m.sbuf("x1T", [P, KD, N])
        padded = m.sbuf("conv_in", [P, MI, BATCH, SEQ + taps - 1])
        low = m.sbuf("delta_low", [P, N])
        soft = m.sbuf("softplus_tail", [P, MI, N])
        bc = m.sbuf("bc_rows", [2 * STATES, N])
        logits = m.sbuf("logits1", [P, NT, experts])
        best = m.sbuf("best1", [P, NT, 8])
        factor = m.sbuf("factor1", [P, NT])
        logits_done = nc.alloc_semaphore("logits_done1")
        expert_steps = nc.alloc_semaphore("expert_steps1")
        expert_done = nc.alloc_semaphore("expert_done1")
        sq_ready = nc.alloc_semaphore("sq_ready1")
        rms_in = nc.alloc_semaphore("rms_in1")
        rms_ready = nc.alloc_semaphore("rms_ready1")
        rms_steps = nc.alloc_semaphore("rms_steps1")
        x1_ready = nc.alloc_semaphore("x1_ready1")
        products = nc.alloc_semaphore("products1")
        emptied = nc.alloc_semaphore("emptied1")
        pad_ready = nc.alloc_semaphore("pad_ready1")
        conv_steps = nc.alloc_semaphore("conv_steps1")
        conv_ready = nc.alloc_semaphore("conv_ready1")
        xs_ready = nc.alloc_semaphore("xs_ready1")
        soft_steps = nc.alloc_semaphore("soft_steps1")
        soft_ready = nc.alloc_semaphore("soft_ready1")
        a_ready = nc.alloc_semaphore("a_ready1")
        delta_ready = nc.alloc_semaphore("delta_ready1")
        rows_stored = nc.alloc_semaphore("rows_stored1")
        cols = [slice(h * HALF, (h + 1) * HALF) for h in range(2)]
        turn0, skip0, in0 = 0, 4, 12
        low0, bc0, up0 = 20, 22, 24

        with nc.Block(no_gpsimd_drain=True) as block:

            @block.sync
            def _(sp):
                sp.wait_ge(emptied, bc0 + 2)
                sp.dma_start(rows, bc[:, :]).then_inc(rows_stored, DMA)
                sp.wait_ge(rows_stored, DMA)

            @block.gpsimd
            def _(pool):
                nc.gpsimd.memset(padded[:, :, :, 0:taps - 1], 0.0).then_inc(pad_ready, 1)

            @block.tensor
            def _(pe):
                def group(g, rows_, pairs):
                    if g >= 8:
                        pe.wait_ge(emptied, g - 7)
                    for k, (wt, act_in) in enumerate(pairs):
                        last = nc.tensor.matmul(banks[0:rows_, g % 8, :], wt, act_in, start=(k == 0),
                                                stop=(k == len(pairs) - 1))
                    last.then_inc(products, 1)

                for half in range(2):
                    pe.wait_ge(x1_ready, 4 * half + 4)
                    for k in range(KD):
                        for t in range(4):
                            last = nc.tensor.transpose(banks[:, turn0 + 2 * half + k, t * P:(t + 1) * P],
                                                       x1_tok[:, 4 * half + t, k * P:(k + 1) * P], ident[:, :])
                        last.then_inc(products, 1)
                pe.wait_ge(emptied, in0 - 8)
                for base, name in ((skip0, "W_skip"), (in0, "W_in")):
                    for mi in range(MI):
                        for half in range(2):
                            group(base + 2 * mi + half, P,
                                  [(w[name][:, k, mi * P:(mi + 1) * P], x1T[:, k, cols[half]]) for k in range(KD)])
                pe.wait_ge(xs_ready, MI)
                for half in range(2):
                    group(low0 + half, P, [(w["W_d1"][:, k, :], xs[:, k, cols[half]]) for k in range(MI)])
                for half in range(2):
                    group(bc0 + half, 2 * STATES, [(w["W_BC"][:, k, :], xs[:, k, cols[half]]) for k in range(MI)])
                for mi in range(MI):
                    for half in range(2):
                        pe.wait_ge(emptied, low0 + half + 1)
                        group(up0 + 2 * mi + half, P, [(w["W_d2"][:, 0, mi * P:(mi + 1) * P], low[:, cols[half]])])
                pe.wait_ge(emptied, up0 + 2 * MI)
                for t in range(NT):
                    for k in range(KD):
                        last = nc.tensor.matmul(banks[:, 0, t * experts:(t + 1) * experts],
                                                xnT[:, k, t * P:(t + 1) * P], w["gate_w"][:, k, :],
                                                start=(k == 0), stop=(k == KD - 1))
                last.then_inc(logits_done, 1)
                for t in range(NT):
                    for k in range(KD):
                        last = nc.tensor.matmul(banks[:, 4 + t // 2, (t % 2) * D:(t % 2 + 1) * D],
                                                xnT[:, k, t * P:(t + 1) * P], w["expert_weight"][:, k, :],
                                                start=(k == 0), stop=(k == KD - 1))
                    if t % 2:
                        last.then_inc(expert_done, 1)

            @block.scalar
            def _(act):
                def empty(g, dst, rows_=P, func=ACT.Identity, **kw):
                    act.wait_ge(products, g + 1)
                    nc.scalar.activation(dst, banks[0:rows_, g % 8, :], func, **kw).then_inc(emptied, 1)

                nc.scalar.activation(A[:, :, :], w["A_log"][:, :, :], ACT.Exp).then_inc(a_ready, 1)
                for t in range(NT):
                    nc.scalar.activation(junk[:, :], xn_tok[:, t, :], ACT.Square,
                                         accum_out=mean_sq[:, t:t + 1]).then_inc(sq_ready, 1)
                    act.wait_ge(sq_ready, t + 1)
                act.wait_ge(rms_in, 1)
                nc.scalar.activation(rms[:, :], mean_sq[:, :], ACT.Sqrt).then_inc(rms_ready, 1)
                for half in range(2):
                    for k in range(KD):
                        empty(turn0 + 2 * half + k, x1T[:, k, cols[half]], scale=w["norm_w"][:, k:k + 1])
                for mi in range(MI):
                    for half in range(2):
                        empty(skip0 + 2 * mi + half, skip[:, mi, cols[half]], func=ACT.Silu)
                act.wait_ge(pad_ready, 1)
                for mi in range(MI):
                    for half in range(2):
                        act.wait_ge(products, in0 + 2 * mi + half + 1)
                        nc.scalar.activation(
                            padded[:, mi, 2 * half:2 * half + 2, taps - 1:],
                            banks[:, (in0 + 2 * mi + half) % 8, :].rearrange("p (b t) -> p b t", b=2),
                            ACT.Identity).then_inc(emptied, 1)
                for mi in range(MI):
                    act.wait_ge(conv_ready, mi + 1)
                    nc.scalar.activation(xs[:, mi, :], xs[:, mi, :], ACT.Silu).then_inc(xs_ready, 1)
                for half in range(2):
                    empty(low0 + half, low[:, cols[half]])
                for half in range(2):
                    empty(bc0 + half, bc[:, cols[half]], rows_=2 * STATES)
                for mi in range(MI):
                    for half in range(2):
                        empty(up0 + 2 * mi + half, delta[:, mi, cols[half]], bias=w["b_d2"][:, mi:mi + 1])
                steps = Steps(act, soft_steps)
                act.wait_ge(emptied, up0 + 2 * MI)
                for mi in range(MI):
                    steps.add(nc.scalar.activation(soft[:, mi, :], delta[:, mi, :], ACT.Abs))
                steps.join()
                for mi in range(MI):
                    steps.add(nc.scalar.activation(soft[:, mi, :], soft[:, mi, :], ACT.Exp, scale=-1.0))
                steps.join()
                for mi in range(MI):
                    nc.scalar.activation(soft[:, mi, :], soft[:, mi, :], ACT.Ln, bias=1.0).then_inc(soft_ready, 1)

            @block.vector
            def _(dve):
                steps = Steps(dve, rms_steps)
                dve.wait_ge(a_ready, 1)
                steps.add(nc.vector.tensor_scalar(A[:, :, :], A[:, :, :], -1.0, None, ALU.mult))
                for mi in range(MI):
                    steps.add(nc.vector.tensor_scalar(diag[:, mi, :], ident[:, :], w["W_D"][:, mi:mi + 1], None, ALU.mult))
                dve.wait_ge(sq_ready, NT)
                nc.vector.tensor_scalar(mean_sq[:, :], mean_sq[:, :], 1.0 / D, EPS, ALU.mult, ALU.add
                                        ).then_inc(rms_in, 1)
                dve.wait_ge(rms_ready, 1)
                steps.do(nc.vector.reciprocal(rrms[:, :], rms[:, :]))
                for t in range(NT):
                    nc.vector.tensor_scalar(x1_tok[:, t, :], xn_tok[:, t, :], rrms[:, t:t + 1], None, ALU.mult
                                            ).then_inc(x1_ready, 1)
                conv = Steps(dve, conv_steps)
                for mi in range(MI):
                    dve.wait_ge(emptied, in0 + 2 * mi + 2)
                    out = xs[:, mi, :].rearrange("p (b t) -> p b t", b=BATCH)
                    conv.do(nc.vector.tensor_scalar(
                        out, padded[:, mi, :, taps - 1:], w["conv_w"][:, mi, taps - 1:taps], w["conv_b"][:, mi:mi + 1],
                        ALU.mult, ALU.add))
                    for j in range(taps - 2, -1, -1):
                        ins = nc.vector.scalar_tensor_tensor(
                            out, padded[:, mi, :, j:j + SEQ], w["conv_w"][:, mi, j:j + 1], out, ALU.mult, ALU.add)
                        if j:
                            conv.do(ins)
                        else:
                            ins.then_inc(conv_ready, 1)
                best_steps = Steps(dve, expert_steps)
                dve.wait_ge(logits_done, 1)
                best_steps.do(nc.vector.tensor_copy(logits[:, :, :].rearrange("p t e -> p (t e)"),
                                                    banks[:, 0, 0:NT * experts]))
                for t in range(NT):
                    best_steps.add(nc.vector.max(best[:, t, :], logits[:, t, :]))
                best_steps.join()
                best_steps.do(nc.vector.tensor_tensor(factor[:, :], best[:, :, 0], best[:, :, 1], ALU.add))
                for t in range(NT):
                    dve.wait_ge(expert_done, t // 2 + 1)
                    nc.vector.tensor_scalar(y[:, t, :], banks[:, 4 + t // 2, (t % 2) * D:(t % 2 + 1) * D],
                                            factor[:, t:t + 1], None, ALU.mult)
                for mi in range(MI):
                    dve.wait_ge(soft_ready, mi + 1)
                    nc.vector.scalar_tensor_tensor(delta[:, mi, :], delta[:, mi, :], 0.0, soft[:, mi, :],
                                                   ALU.max, ALU.add).then_inc(delta_ready, 1)
                    dve.wait_ge(delta_ready, mi + 1)
                    nc.vector.tensor_tensor(dx[:, mi, :], delta[:, mi, :], xs[:, mi, :], ALU.mult)


def scan_stage(nc, w, up_w, down_w, x_tok, xn_tok, xnT, s_tok, ident, banks, keep, rows, y):
    hidden = up_w.shape[1]
    skip, xs, delta, dx, A, diag = keep
    passes = 2
    turn, tiles = 4, 2
    rounds = STATES // turn
    pass_steps = STATES * MI
    round_steps = turn * MI
    tile_steps = round_steps // tiles
    pass_tiles = hidden // P
    assert pass_tiles == rounds * tiles
    with ExitStack() as ctx:
        m = Core(nc, ctx)
        b_row = m.sbuf("b_row", [P, turn, HALF])
        c_row = m.sbuf("c_row", [P, turn, HALF])
        decay = m.sbuf("decay", [P, MI, BATCH // 2, SEQ])
        drive = m.sbuf("drive", [P, MI, HALF])
        state = m.sbuf("state", [P, MI, HALF])
        seen = m.sbuf("seen", [P, MI, HALF])
        up = m.sbuf("up_w1", [P, 2, KD, P])
        down = m.sbuf("down_w1", [P, 2, D])
        hT = m.sbuf("hidden_T1", [P, 2, HALF])
        zeros = m.sbuf("zeros1", [P, BANK])
        stats = m.sbuf("y_stats", [P, NT, 6])
        mean_var = m.sbuf("y_mean_var", [P, NT, 2])
        var = m.sbuf("y_var", [P, NT])
        std = m.sbuf("y_std", [P, NT])
        rstd = m.sbuf("y_rstd", [P, NT])
        offset = m.sbuf("y_offset", [P, NT])
        loaded = [nc.alloc_semaphore(f"bc_loaded{q}") for q in range(turn)]
        decay_ready = nc.alloc_semaphore("decay_ready")
        drive_ready = nc.alloc_semaphore("drive_ready")
        scanned = nc.alloc_semaphore("scanned")
        seen_ready = nc.alloc_semaphore("seen_ready")
        summed = nc.alloc_semaphore("summed")
        gated_ready = nc.alloc_semaphore("gated_ready1")
        mixed = nc.alloc_semaphore("mixed1")
        s_ready = nc.alloc_semaphore("s_ready1")
        ffn_loaded = [nc.alloc_semaphore(f"ffn_loaded1_{s}") for s in range(2)]
        zeros_ready = nc.alloc_semaphore("zeros_ready1")
        up_done = nc.alloc_semaphore("up_done1")
        relu_ready = nc.alloc_semaphore("relu_ready1")
        h_ready = nc.alloc_semaphore("h_ready1")
        down_done = nc.alloc_semaphore("down_done1")
        y_ready = nc.alloc_semaphore("y_ready1")
        y_steps = nc.alloc_semaphore("y_steps1")
        var_ready = nc.alloc_semaphore("y_var_ready1")
        std_ready = nc.alloc_semaphore("y_std_ready1")
        offset_ready = nc.alloc_semaphore("y_offset_ready1")
        norm_ready = nc.alloc_semaphore("y_norm_ready1")
        gamma_ready = nc.alloc_semaphore("y_gamma_ready1")
        beta_ready = nc.alloc_semaphore("y_beta_ready1")
        gate_ready = nc.alloc_semaphore("gate_ready1")
        x_ready = nc.alloc_semaphore("x_ready1")
        cols = [slice(h * HALF, (h + 1) * HALF) for h in range(2)]

        with nc.Block(no_gpsimd_drain=True) as block:

            @block.sync
            def _(sp):
                def load_rows(p, n, q):
                    for dst, first in ((b_row, 0), (c_row, STATES)):
                        sp.dma_start(dst[:, q, :], rows[bass.ds(n + first, 1), cols[p]].rearrange("n t -> (n t)")
                                     .partition_broadcast(P)).then_inc(loaded[q], DMA)

                def load_weights(n, s):
                    sp.dma_start(up[:, s, :, :], up_w.rearrange("(k p) (n c) -> p n k c", p=P, c=P)
                                 [:, bass.ds(n, 1), :, :].rearrange("p n k c -> p (n k) c")).then_inc(ffn_loaded[s], DMA)
                    sp.dma_start(down[:, s, :], down_w.rearrange("(n p) d -> n p d", p=P)[bass.ds(n, 1), :, :]
                                 .rearrange("n p d -> p (n d)")).then_inc(ffn_loaded[s], DMA)

                def refill(p, i, wrap=False):
                    for q in range(turn):
                        done = pass_steps * p + round_steps * i + MI * (q + 1)
                        sp.wait_ge(drive_ready, done)
                        sp.wait_ge(seen_ready, done)
                        load_rows(p + 1 if wrap else p, q if wrap else turn * (i + 1) + q, q)
                        if q % 2:
                            s = q // 2
                            sp.wait_ge(down_done, pass_tiles * p + tiles * i + s + 1)
                            load_weights(s if wrap else tiles * (i + 1) + s, s)

                for q in range(turn):
                    load_rows(0, q, q)
                    if q % 2:
                        load_weights(q // 2, q // 2)
                for p in range(passes):
                    with sp.Fori(0, rounds - 1) as i:
                        refill(p, i)
                    if p + 1 < passes:
                        refill(p, rounds - 1, wrap=True)

            @block.scalar
            def _(act):
                for p in range(passes):
                    with act.Fori(0, rounds) as i:
                        for e in range(round_steps):
                            mi = e % MI
                            act.wait_ge(scanned, pass_steps * p + round_steps * i + e + 1)
                            nc.scalar.activation(
                                decay[:, mi, :, 1:],
                                delta[:, mi, cols[p]].rearrange("p (b t) -> p b t", b=BATCH // 2)[:, :, 1:], ACT.Exp,
                                scale=A[:, mi, bass.ds(turn * i + e // MI, 1)]).then_inc(decay_ready, 1)
                            if e % tile_steps == tile_steps - 1:
                                s = e // tile_steps
                                act.wait_ge(up_done, pass_tiles * p + tiles * i + s + 1)
                                nc.scalar.activation(hT[:, s, :], banks[:, 6 + s, :], ACT.Relu).then_inc(relu_ready, 1)
                act.wait_ge(var_ready, 1)
                nc.scalar.activation(std[:, :], var[:, :], ACT.Sqrt).then_inc(std_ready, 1)
                act.wait_ge(offset_ready, 1)
                for t in range(NT):
                    nc.scalar.activation(y[:, t, :], y[:, t, :], ACT.Identity, bias=offset[:, t:t + 1],
                                         scale=rstd[:, t:t + 1]).then_inc(norm_ready, 1)
                for b in range(NT // 2):
                    act.wait_ge(beta_ready, b + 1)
                    nc.scalar.activation(y[:, 2 * b:2 * b + 2, :], y[:, 2 * b:2 * b + 2, :], ACT.Silu
                                         ).then_inc(gate_ready, 1)

            @block.gpsimd
            def _(pool):
                nc.gpsimd.memset(zeros[:, :], 0.0).then_inc(zeros_ready, 1)
                for p in range(passes):
                    with pool.Fori(0, rounds) as i:
                        for e in range(round_steps):
                            q, mi = e // MI, e % MI
                            if mi == 0:
                                pool.wait_ge(loaded[q], 2 * DMA * (rounds * p + i + 1))
                            pool.wait_ge(scanned, pass_steps * p + round_steps * i + e + 1)
                            nc.gpsimd.tensor_tensor(drive[:, mi, :], dx[:, mi, cols[p]], b_row[:, q, :], ALU.mult
                                                    ).then_inc(drive_ready, 1)
                for b in range(NT // 2):
                    two = slice(2 * b, 2 * b + 2)
                    pool.wait_ge(gamma_ready, b + 1)
                    nc.gpsimd.tensor_tensor(y[:, two, :], y[:, two, :],
                                            w["ln_beta"][:, :].unsqueeze(1).broadcast_to([P, 2, D]), ALU.add
                                            ).then_inc(beta_ready, 1)

            @block.vector
            def _(dve):
                def scan(p, i, e):
                    count = pass_steps * p + round_steps * i + e + 1
                    dve.wait_ge(decay_ready, count)
                    dve.wait_ge(drive_ready, count)
                    if e >= MI:
                        dve.wait_ge(seen_ready, count - MI)
                    nc.vector.tensor_tensor_scan(
                        state[:, e % MI, :], decay[:, e % MI, :, :].rearrange("p b t -> p (b t)"),
                        drive[:, e % MI, :], 0.0, ALU.mult, ALU.add).then_inc(scanned, 1)

                def see(p, i, e):
                    q = e // MI
                    count = pass_steps * p + round_steps * i + e + 1
                    if e % MI == 0:
                        dve.wait_ge(loaded[q], 2 * DMA * (rounds * p + i + 1))
                    dve.wait_ge(scanned, count + MI)
                    dve.wait_ge(summed, count)
                    nc.vector.tensor_tensor(seen[:, e % MI, :], state[:, e % MI, :], c_row[:, q, :], ALU.mult
                                            ).then_inc(seen_ready, 1)

                def square(p, i, s):
                    dve.wait_ge(relu_ready, pass_tiles * p + tiles * i + s + 1)
                    nc.vector.tensor_tensor(hT[:, s, :], hT[:, s, :], hT[:, s, :], ALU.mult).then_inc(h_ready, 1)

                for mi in range(MI):
                    nc.vector.memset(decay[:, mi, :, 0:1], 0.0).then_inc(scanned, 1)
                for p in range(passes):
                    with dve.Fori(0, rounds) as i:
                        scan(p, i, 0)
                        for e in range(round_steps):
                            if e + 1 < round_steps:
                                scan(p, i, e + 1)
                            see(p, i, e)
                            if e % tile_steps == tile_steps - 2:
                                square(p, i, e // tile_steps)
                        dve.wait_ge(seen_ready, pass_steps * p + round_steps * (i + 1))
                    dve.wait_ge(summed, pass_steps * (p + 1) + MI)
                    for mi in range(MI):
                        nc.vector.tensor_tensor(dx[:, mi, cols[p]], banks[:, mi, :], skip[:, mi, cols[p]], ALU.mult
                                                ).then_inc(gated_ready, 1)
                    dve.wait_ge(down_done, pass_tiles * (p + 1))
                    for b in range(2):
                        two = slice(4 * p + 2 * b, 4 * p + 2 * b + 2)
                        nc.vector.tensor_tensor(y[:, two, :], y[:, two, :],
                                                banks[:, 4 + b, :].rearrange("p (t d) -> p t d", t=2), ALU.add
                                                ).then_inc(y_ready, 1)
                steps = Steps(dve, y_steps)
                dve.wait_ge(y_ready, 2 * passes)
                for t in range(NT):
                    steps.add(nc.vector.bn_stats(stats[:, t, :], y[:, t, :]))
                steps.join()
                for t in range(NT):
                    steps.add(nc.vector.bn_aggr(mean_var[:, t, :], stats[:, t, :]))
                steps.join()
                nc.vector.tensor_scalar(var[:, :], mean_var[:, :, 1], EPS, None, ALU.add).then_inc(var_ready, 1)
                dve.wait_ge(std_ready, 1)
                steps.do(nc.vector.reciprocal(rstd[:, :], std[:, :]))
                nc.vector.scalar_tensor_tensor(offset[:, :], mean_var[:, :, 0], -1.0, rstd[:, :], ALU.mult, ALU.mult
                                               ).then_inc(offset_ready, 1)
                for b in range(NT // 2):
                    two = slice(2 * b, 2 * b + 2)
                    dve.wait_ge(mixed, b + 1)
                    nc.vector.tensor_tensor(s_tok[:, two, :], banks[:, b, :].rearrange("p (t d) -> p t d", t=2),
                                            xn_tok[:, two, :], ALU.add).then_inc(s_ready, 1)
                    dve.wait_ge(norm_ready, 2 * b + 2)
                    nc.vector.tensor_tensor(y[:, two, :], y[:, two, :],
                                            w["ln_gamma"][:, :].unsqueeze(1).broadcast_to([P, 2, D]), ALU.mult
                                            ).then_inc(gamma_ready, 1)
                dve.wait_ge(s_ready, NT // 2)
                add_gated(nc, dve, x_tok, s_tok, y, gate_ready, x_ready)

            @block.tensor
            def _(pe):
                def total(p, i, e):
                    pe.wait_ge(seen_ready, pass_steps * p + round_steps * i + e + 1)
                    nc.tensor.matmul(banks[:, e % MI, :], ident[:, :], seen[:, e % MI, :],
                                     start=False, stop=False, skip_group_check=True).then_inc(summed, 1)

                def raise_(p, i, s):
                    pe.wait_ge(ffn_loaded[s], 2 * DMA * (rounds * p + i + 1))
                    for k in range(KD):
                        last = nc.tensor.matmul(banks[:, 6 + s, :], up[:, s, k, :], xnT[:, k, cols[p]],
                                                start=(k == 0), stop=(k == KD - 1))
                    last.then_inc(up_done, 1)

                def lower(p, i, s):
                    pe.wait_ge(h_ready, pass_tiles * p + tiles * i + s + 1)
                    for t in range(4):
                        last = nc.tensor.matmul(banks[:, 4 + t // 2, (t % 2) * D:(t % 2 + 1) * D],
                                                hT[:, s, t * P:(t + 1) * P], down[:, s, :],
                                                start=False, stop=False, skip_group_check=True)
                    last.then_inc(down_done, 1)

                pe.wait_ge(zeros_ready, 1)
                for p in range(passes):
                    if p:
                        pe.wait_ge(gated_ready, MI * p)
                    for mi in range(MI):
                        last = nc.tensor.matmul(banks[:, mi, :], diag[:, mi, :], xs[:, mi, cols[p]],
                                                start=True, stop=False, skip_group_check=True)
                        if p == 0:
                            last.then_inc(summed, 1)
                    if p:
                        pe.wait_ge(y_ready, 2 * p)
                    for b in range(2):
                        nc.tensor.matmul(banks[:, 4 + b, :], zeros[0:1, 0:P], zeros[0:1, :],
                                         start=True, stop=False, skip_group_check=True)
                    with pe.Fori(0, rounds) as i:
                        for s in range(tiles):
                            for e in range(tile_steps * s, tile_steps * (s + 1)):
                                total(p, i, e)
                                if e % tile_steps == 1:
                                    raise_(p, i, s)
                            lower(p, i, s)
                pe.wait_ge(gated_ready, passes * MI)
                for t in range(NT):
                    for k in range(MI):
                        last = nc.tensor.matmul(banks[:, t // 2, (t % 2) * D:(t % 2 + 1) * D],
                                                dx[:, k, t * P:(t + 1) * P], w["W_out"][:, k, :],
                                                start=(k == 0), stop=(k == MI - 1))
                    if t % 2:
                        last.then_inc(mixed, 1)




HEADS2, HEAD2 = 16, 16


def rotary_stage(nc, w, xnT, keep, banks):
    q, keys, v = keep
    with ExitStack() as ctx:
        m = Core(nc, ctx)
        krep = m.sbuf("krep", [P, N])
        straight_done = nc.alloc_semaphore("straight_done2")
        swapped_done = nc.alloc_semaphore("swapped_done2")
        straight_ready = nc.alloc_semaphore("straight_ready2")
        k_done = nc.alloc_semaphore("k_done2")
        k_ready = nc.alloc_semaphore("k_ready2")
        v_done = nc.alloc_semaphore("v_done2")
        cols = [slice(h * HALF, (h + 1) * HALF) for h in range(2)]

        with nc.Block(no_gpsimd_drain=True) as block:

            @block.tensor
            def _(pe):
                def product(bank, wt, half):
                    for k in range(KD):
                        last = nc.tensor.matmul(banks[:, bank, :], wt[:, k, :], xnT[:, k, cols[half]],
                                                start=(k == 0), stop=(k == KD - 1))
                    return last

                for half in range(2):
                    product(6 + half, w["Wk"], half).then_inc(k_done, 1)
                for g in range(2):
                    for half in range(2):
                        bank = 4 * g + 2 * half
                        if bank == 6:
                            pe.wait_ge(k_ready, 2)
                        part = slice(g * P, (g + 1) * P)
                        product(bank, w["Wq"][:, :, part], half).then_inc(straight_done, 1)
                        product(bank + 1, w["Wq_swap"][:, :, part], half).then_inc(swapped_done, 1)
                pe.wait_ge(straight_ready, 1)
                for t in range(NT):
                    for k in range(KD):
                        last = nc.tensor.matmul(banks[:, 0, t * HEAD2:(t + 1) * HEAD2], xnT[:, k, t * P:(t + 1) * P],
                                                w["Wv"][:, k, :], start=(k == 0), stop=(k == KD - 1))
                last.then_inc(v_done, 1)

            @block.scalar
            def _(act):
                for half in range(2):
                    act.wait_ge(k_done, half + 1)
                    nc.scalar.activation(krep[:, cols[half]], banks[:, 6 + half, :], ACT.Identity).then_inc(k_ready, 1)
                for g in range(2):
                    for half in range(2):
                        act.wait_ge(straight_done, 2 * g + half + 1)
                        nc.scalar.activation(q[:, g, cols[half]], banks[:, 4 * g + 2 * half, :], ACT.Identity,
                                             scale=w["cos"][:, g:g + 1]).then_inc(straight_ready, 1)
                act.wait_ge(v_done, 1)
                nc.scalar.activation(v[:, :, :].rearrange("p t d -> p (t d)"), banks[:, 0, 0:NT * HEAD2], ACT.Identity)

            @block.vector
            def _(dve):
                dve.wait_ge(k_ready, 2)
                for h in range(8):
                    nc.vector.tensor_scalar(keys[:, h, :], krep[:, :], w["head_rows"][:, h:h + 1], None, ALU.mult)
                for g in range(2):
                    for half in range(2):
                        dve.wait_ge(swapped_done, 2 * g + half + 1)
                        dve.wait_ge(straight_ready, 2 * g + half + 1)
                        nc.vector.scalar_tensor_tensor(
                            q[:, g, cols[half]], banks[:, 4 * g + 2 * half + 1, :], w["sin"][:, g:g + 1],
                            q[:, g, cols[half]], ALU.mult, ALU.add)


EXPERTS2, TOP2, CAPACITY = 16, 4, 128
WIDE2, SHARED2 = 176, 352
ROWS2 = WIDE2 // 2
INFO = 6


def route_stage(nc, w, xn_tok, xnT, ident, earlier, banks, tables, xn_dram, y_dram):
    slot_token, slot_target, slot_weight = tables
    tiles = SHARED2 // ROWS2
    jobs = [(i, half) for i in range(tiles) for half in range(2)]
    before = 3
    with ExitStack() as ctx:
        m = Core(nc, ctx)
        shape = [P, NT, EXPERTS2]
        logits = m.sbuf("logits2", shape)
        best = m.sbuf("best2", [P, NT])
        powers = m.sbuf("powers2", shape)
        total = m.sbuf("total2", [P, NT])
        score = m.sbuf("score2", shape)
        above = m.sbuf("above2", [P, NT, EXPERTS2, EXPERTS2])
        equal = m.sbuf("equal2", [P, NT, EXPERTS2, EXPERTS2])
        count = m.sbuf("count2", shape)
        chosen = m.sbuf("chosen2", shape)
        chosen_bf = m.sbuf("chosen_bf2", shape, BF16)
        weight = m.sbuf("weight2", shape)
        place = m.sbuf("place2", shape)
        kept = m.sbuf("kept2", shape)
        before_bf = m.sbuf("before_bf2", [P, P], BF16)
        ones_bf = m.sbuf("ones_bf2", [P, P], BF16)
        one_hot = m.sbuf("one_hot2", [P, NT, EXPERTS2, CAPACITY], BF16)
        info = m.sbuf("info2", [P, NT, EXPERTS2, INFO], BF16)
        rest = m.sbuf("rest2", shape)
        table = m.sbuf("table2", [P, EXPERTS2, INFO])
        empty = m.sbuf("empty2", [P, EXPERTS2])
        token = m.sbuf("token2", [P, EXPERTS2])
        silu = m.sbuf("shared_silu2", [ROWS2, 2, HALF])
        mid = m.sbuf("shared_mid2", [ROWS2, tiles, N])
        y_shared = m.sbuf("shared_y2", [P, NT, D])
        zeros = m.sbuf("zeros2", [P, D])
        consts_ready = nc.alloc_semaphore("route_consts2")
        logits_done = nc.alloc_semaphore("logits_done2")
        route_steps = nc.alloc_semaphore("route_steps2")
        shifted = nc.alloc_semaphore("shifted2")
        powers_ready = nc.alloc_semaphore("powers_ready2")
        chosen_ready = nc.alloc_semaphore("chosen_ready2")
        places_done = nc.alloc_semaphore("places_done2")
        slots_ready = nc.alloc_semaphore("slots_ready2")
        table_done = nc.alloc_semaphore("table_done2")
        shared_done = nc.alloc_semaphore("shared_done2")
        silu_ready = nc.alloc_semaphore("shared_silu_ready2")
        mid_ready = nc.alloc_semaphore("shared_mid_ready2")
        y_done = nc.alloc_semaphore("shared_y_done2")
        y_ready = nc.alloc_semaphore("shared_y_ready2")
        stored = nc.alloc_semaphore("route_stored2")
        cols = [slice(h * HALF, (h + 1) * HALF) for h in range(2)]

        with nc.Block(no_gpsimd_drain=True) as block:

            @block.sync
            def _(sp):
                def by_token(dram):
                    return dram.rearrange("(n p) d -> p n d", p=P)

                sp.dma_start(by_token(xn_dram), xn_tok[:, :, :]).then_inc(stored, DMA)
                sp.wait_ge(consts_ready, 2)
                sp.dma_start(y_dram[N:N + P, :], zeros[:, :]).then_inc(stored, DMA)
                sp.wait_ge(y_ready, NT // 2)
                sp.dma_start(by_token(y_dram[0:N, :]), y_shared[:, :, :]).then_inc(stored, DMA)
                sp.wait_ge(stored, 3 * DMA)

            @block.gpsimd
            def _(pool):
                nc.gpsimd.memset(ones_bf[:, :], 1.0).then_inc(consts_ready, 1)
                nc.gpsimd.memset(zeros[:, :], 0.0).then_inc(consts_ready, 1)
                nc.gpsimd.memset(info[:, :, :, INFO - 1:INFO], 1.0).then_inc(consts_ready, 1)

            @block.tensor
            def _(pe):
                def shared(n):
                    i, half = jobs[n]
                    if n >= 3:
                        pe.wait_ge(mid_ready, n - 2)
                    for j, name in enumerate(("sw_gate", "sw_up")):
                        for k in range(KD):
                            last = nc.tensor.matmul(banks[0:ROWS2, 2 + 2 * (n % 3) + j, :],
                                                    w[name][:, k, i * ROWS2:(i + 1) * ROWS2], xnT[:, k, cols[half]],
                                                    start=(k == 0), stop=(k == KD - 1))
                    last.then_inc(shared_done, 1)

                for t in range(NT):
                    for k in range(KD):
                        last = nc.tensor.matmul(banks[:, 0, t * EXPERTS2:(t + 1) * EXPERTS2],
                                                xnT[:, k, t * P:(t + 1) * P], w["gate_w"][:, k, :],
                                                start=(k == 0), stop=(k == KD - 1))
                last.then_inc(logits_done, 1)
                for n in range(before):
                    shared(n)
                pe.wait_ge(consts_ready, 1)
                pe.wait_ge(chosen_ready, 1)
                for t in range(NT):
                    for other in range(t + 1):
                        last = nc.tensor.matmul(banks[:, 1, t * EXPERTS2:(t + 1) * EXPERTS2],
                                                (before_bf if other == t else ones_bf)[:, :], chosen_bf[:, other, :],
                                                start=(other == 0), stop=(other == t))
                last.then_inc(places_done, 1)
                for n in range(before, len(jobs)):
                    shared(n)
                pe.wait_ge(mid_ready, len(jobs))
                for t in range(NT):
                    for i in range(tiles):
                        last = nc.tensor.matmul(banks[:, 4 + t // 2, (t % 2) * D:(t % 2 + 1) * D],
                                                mid[:, i, t * P:(t + 1) * P], w["sw_down"][:, i, :],
                                                start=(i == 0), stop=(i == tiles - 1))
                    if t % 2:
                        last.then_inc(y_done, 1)
                pe.wait_ge(consts_ready, 3)
                pe.wait_ge(slots_ready, 1)
                for e in range(EXPERTS2):
                    for t in range(NT):
                        last = nc.tensor.matmul(banks[:, 0, e * INFO:(e + 1) * INFO], one_hot[:, t, e, :],
                                                info[:, t, e, :], start=(t == 0), stop=(t == NT - 1))
                last.then_inc(table_done, 1)

            @block.scalar
            def _(act):
                def shared(n):
                    act.wait_ge(shared_done, n + 1)
                    if n >= 2:
                        act.wait_ge(mid_ready, n - 1)
                    nc.scalar.activation(silu[:, n % 2, :], banks[0:ROWS2, 2 + 2 * (n % 3), :], ACT.Silu
                                         ).then_inc(silu_ready, 1)

                act.wait_ge(shifted, 1)
                nc.scalar.activation(powers[:, :, :], powers[:, :, :], ACT.Exp).then_inc(powers_ready, 1)
                for n in range(len(jobs)):
                    shared(n)
                for b in range(NT // 2):
                    act.wait_ge(y_done, b + 1)
                    nc.scalar.activation(y_shared[:, 2 * b:2 * b + 2, :].rearrange("p t d -> p (t d)"), banks[:, 4 + b, :],
                                         ACT.Identity).then_inc(y_ready, 1)

            @block.vector
            def _(dve):
                steps = Steps(dve, route_steps)

                def shared(n):
                    i, half = jobs[n]
                    dve.wait_ge(silu_ready, n + 1)
                    nc.vector.tensor_tensor(mid[:, i, cols[half]], silu[:, n % 2, :],
                                            banks[0:ROWS2, 3 + 2 * (n % 3), :], ALU.mult).then_inc(mid_ready, 1)

                def per_token(v):
                    return v.unsqueeze(2).broadcast_to(shape)

                steps.add(nc.vector.tensor_copy(before_bf[:, :], w["before"][:, :]))
                dve.wait_ge(logits_done, 1)
                steps.do(nc.vector.tensor_copy(logits[:, :, :].rearrange("p t e -> p (t e)"),
                                               banks[:, 0, 0:NT * EXPERTS2]))
                steps.do(nc.vector.tensor_reduce(best[:, :], logits[:, :, :], AX.X, ALU.max))
                nc.vector.tensor_tensor(powers[:, :, :], logits[:, :, :], per_token(best[:, :]), ALU.subtract
                                        ).then_inc(shifted, 1)
                dve.wait_ge(powers_ready, 1)
                steps.do(nc.vector.tensor_reduce(total[:, :], powers[:, :, :], AX.X, ALU.add))
                steps.do(nc.vector.reciprocal(best[:, :], total[:, :]))
                steps.do(nc.vector.tensor_tensor(score[:, :, :], powers[:, :, :], per_token(best[:, :]), ALU.mult))
                rank_mask(nc, steps, chosen[:, :, :], score[:, :, :],
                          (above[:, :, :, :], equal[:, :, :, :], count[:, :, :]), earlier, EXPERTS2, TOP2)
                nc.vector.tensor_copy(chosen_bf[:, :, :], chosen[:, :, :]).then_inc(chosen_ready, 1)
                for n in range(before):
                    shared(n)
                steps.do(nc.vector.tensor_tensor(weight[:, :, :], chosen[:, :, :], score[:, :, :], ALU.mult))
                steps.do(nc.vector.tensor_reduce(total[:, :], weight[:, :, :], AX.X, ALU.add))
                steps.do(nc.vector.tensor_scalar(total[:, :], total[:, :], 1e-20, None, ALU.add))
                steps.do(nc.vector.reciprocal(best[:, :], total[:, :]))
                steps.do(nc.vector.tensor_tensor(weight[:, :, :], weight[:, :, :], per_token(best[:, :]), ALU.mult))
                steps.add(nc.vector.tensor_copy(
                    info[:, :, :, 0:2], w["token_place"][:, :, :].unsqueeze(2).broadcast_to([P, NT, EXPERTS2, 2])))
                rest_of = weight
                for part in range(3):
                    steps.do(nc.vector.tensor_copy(info[:, :, :, 2 + part], rest_of[:, :, :]))
                    if part < 2:
                        steps.do(nc.vector.tensor_tensor(rest[:, :, :], rest_of[:, :, :], info[:, :, :, 2 + part],
                                                         ALU.subtract))
                        rest_of = rest
                dve.wait_ge(places_done, 1)
                steps.do(nc.vector.tensor_copy(place[:, :, :].rearrange("p t e -> p (t e)"),
                                               banks[:, 1, 0:NT * EXPERTS2]))
                steps.do(nc.vector.scalar_tensor_tensor(kept[:, :, :], place[:, :, :], float(CAPACITY), chosen[:, :, :],
                                                        ALU.is_lt, ALU.mult))
                steps.do(nc.vector.scalar_tensor_tensor(place[:, :, :], place[:, :, :], 1.0, kept[:, :, :],
                                                        ALU.add, ALU.mult))
                steps.do(nc.vector.tensor_scalar(place[:, :, :], place[:, :, :], -1.0, None, ALU.add))
                for t in range(NT):
                    ins = nc.vector.tensor_tensor(
                        one_hot[:, t, :, :], w["slots"][:, :].unsqueeze(1).broadcast_to([P, EXPERTS2, CAPACITY]),
                        place[:, t, :].unsqueeze(2).broadcast_to([P, EXPERTS2, CAPACITY]), ALU.is_equal)
                    if t == NT - 1:
                        ins.then_inc(slots_ready, 1)
                    else:
                        steps.add(ins)
                    if before + t < len(jobs):
                        shared(before + t)
                dve.wait_ge(table_done, 1)
                steps.do(nc.vector.tensor_copy(table[:, :, :].rearrange("p e i -> p (e i)"),
                                               banks[:, 0, 0:EXPERTS2 * INFO]))
                steps.do(nc.vector.tensor_tensor(token[:, :], table[:, :, 0], table[:, :, 1], ALU.add))
                steps.add(nc.vector.tensor_copy(slot_token[:, :], token[:, :]))
                steps.do(nc.vector.tensor_scalar(empty[:, :], table[:, :, INFO - 1], -1.0, 1.0, ALU.mult, ALU.add))
                steps.do(nc.vector.scalar_tensor_tensor(token[:, :], empty[:, :], w["spare_row"][:, 0:1], token[:, :],
                                                        ALU.mult, ALU.add))
                steps.add(nc.vector.tensor_copy(slot_target[:, :], token[:, :]))
                steps.do(nc.vector.tensor_tensor(slot_weight[:, :], table[:, :, 3], table[:, :, 4], ALU.add))
                steps.do(nc.vector.tensor_tensor(slot_weight[:, :], slot_weight[:, :], table[:, :, 2], ALU.add))


def attention_and_expert_stage(nc, w, keep, expert_w, tables, xn_dram, y_dram, x_tok, s_tok, ident, banks):
    q, keys, v = keep
    slot_token, slot_target, slot_weight = tables
    w_gate, w_up, w_down = expert_w
    pairs = EXPERTS2 // 2
    group = 4
    seq_units = 3 * HEADS2 // group
    round_ = 2 * seq_units
    rounds = BATCH // 2
    turns = round_ // 3
    assert turns * rounds == EXPERTS2
    scale = HEAD2 ** -0.5
    with ExitStack() as ctx:
        m = Core(nc, ctx)
        q_now = m.sbuf("q_now", [P, 2, 2, SEQ])
        top = m.sbuf("score_top", [P, 4, group])
        shift = m.sbuf("score_shift", [P, 4, group])
        total = m.sbuf("prob_total", [P, 4, group])
        inverse = m.sbuf("prob_inverse", [P, 4, group])
        prob = m.sbuf("prob", [P, 4, BANK])
        probT = m.sbuf("probT", [P, 2, BANK // P, P])
        o_tok = m.sbuf("o_tok", [P, NT, D])
        oT = m.sbuf("oT2", [P, KD, N])
        gate_w = m.sbuf("slot_gate_w", [P, 2, KD, WIDE2])
        up_w = m.sbuf("slot_up_w", [P, 2, KD, WIDE2])
        down_w = m.sbuf("slot_down_w", [ROWS2, 2, 2, D])
        xg = m.sbuf("slot_x", [P, 2, D])
        xgT = m.sbuf("slot_xT", [P, 2, D])
        silu = m.sbuf("slot_silu", [ROWS2, 2, 2 * P])
        mid = m.sbuf("slot_mid", [ROWS2, 2, 2 * P])
        result = m.sbuf("slot_result", [P, 2, D])
        gated = m.sbuf("gated2", [P, NT, D])
        loaded = [nc.alloc_semaphore(f"slot_loaded{s}") for s in range(2)]
        gathered = [nc.alloc_semaphore(f"slot_gathered{s}") for s in range(2)]
        turned = nc.alloc_semaphore("slot_turned")
        xgT_ready = nc.alloc_semaphore("slot_xT_ready")
        widened = nc.alloc_semaphore("slot_widened")
        silu_ready = nc.alloc_semaphore("slot_silu_ready")
        mid_ready = nc.alloc_semaphore("slot_mid_ready")
        lowered = nc.alloc_semaphore("slot_lowered")
        result_ready = nc.alloc_semaphore("slot_result_ready")
        scattered = nc.alloc_semaphore("slot_scattered")
        y_loaded = nc.alloc_semaphore("y_loaded2")
        gate_ready = nc.alloc_semaphore("gate_ready2")
        x_ready = nc.alloc_semaphore("x_ready2")
        s_ready = nc.alloc_semaphore("s_ready2")
        q_ready = nc.alloc_semaphore("q_ready2")
        scored = nc.alloc_semaphore("scored2")
        masked_ready = nc.alloc_semaphore("masked_ready2")
        top_ready = nc.alloc_semaphore("top_ready2")
        shift_ready = nc.alloc_semaphore("shift_ready2")
        prob_ready = nc.alloc_semaphore("prob_ready2")
        prob_turned = nc.alloc_semaphore("prob_turned2")
        probT_ready = nc.alloc_semaphore("probT_ready2")
        summed = nc.alloc_semaphore("pv_summed2")
        inverse_ready = nc.alloc_semaphore("inverse_ready2")
        o_ready = nc.alloc_semaphore("o_ready2")
        o_turned = nc.alloc_semaphore("o_turned2")
        oT_ready = nc.alloc_semaphore("oT_ready2")
        mixed = nc.alloc_semaphore("mixed2")

        def unit(j):
            s, k, part = j // seq_units, j % seq_units // 3, j % 3
            if part == 0:
                return s, 0, group * k, group, P
            return s, 1, group * k + group // 2 * (part - 1), group // 2, SEQ

        def by_head(flat, j):
            return flat.rearrange("p (h k) -> p h k", h=unit(j)[3])


        with nc.Block(no_gpsimd_drain=True) as block:

            @block.sync
            def _(sp):
                def load(e, s):
                    for dst, src in ((gate_w, w_gate), (up_w, w_up)):
                        sp.dma_start(dst[:, s, :, :], src[bass.ds(e, 1), :, :].rearrange("e (k p) n -> p (e k) n", p=P)
                                     ).then_inc(loaded[s], DMA)
                    sp.dma_start(down_w[:, s, :, :], w_down[bass.ds(e, 1), :, :]
                                 .rearrange("e (i p) d -> p (e i) d", p=ROWS2)).then_inc(loaded[s], DMA)

                for s in range(2):
                    load(s, s)
                with sp.Fori(1, pairs) as i:
                    for s in range(2):
                        sp.wait_ge(lowered, 2 * i + s - 1)
                        load(2 * i + s, s)
                sp.wait_ge(scattered, DMA * EXPERTS2)
                sp.dma_start(gated[:, :, :], y_dram[0:N, :].rearrange("(n p) d -> p n d", p=P)).then_inc(y_loaded, DMA)
                sp.wait_ge(y_loaded, DMA)

            @block.gpsimd
            def _(pool):
                def copy(b):
                    nc.gpsimd.tensor_copy(q_now[:, b % 2, :, :], q[:, :, b * SEQ:(b + 1) * SEQ]).then_inc(q_ready, 1)

                def gather(e):
                    pool.indirect_dma_start(out=xg[:, e % 2, :], out_offset=None, in_=xn_dram[:, :],
                                            in_offset=bass.IndirectOffsetOnAxis(ap=slot_token[:, e:e + 1], axis=0)
                                            ).then_inc(gathered[e % 2], DMA)

                copy(0)
                copy(1)
                gather(0)
                gather(1)
                for e in range(EXPERTS2):
                    if e + 2 < EXPERTS2:
                        pool.wait_ge(turned, e + 1)
                        gather(e + 2)
                    pool.wait_ge(result_ready, e + 1)
                    if e:
                        pool.wait_ge(scattered, DMA * e)
                    pool.indirect_dma_start(out=y_dram[:, :],
                                            out_offset=bass.IndirectOffsetOnAxis(ap=slot_target[:, e:e + 1], axis=0),
                                            in_=result[:, e % 2, :], in_offset=None, compute_op=ALU.add
                                            ).then_inc(scattered, DMA)
                    if e in (turns // 2, turns - 1):
                        b = 2 if e < turns - 1 else 3
                        pool.wait_ge(scored, seq_units * (b - 1))
                        copy(b)
                pool.wait_ge(scattered, DMA * EXPERTS2)

            @block.tensor
            def _(pe):
                def score(i, j):
                    s, qt, head, heads, n_keys = unit(j)
                    if j % seq_units == 0:
                        pe.wait_ge(q_ready, 2 * i + s + 1)
                    if j >= 3:
                        pe.wait_ge(prob_ready, round_ * i + j - 2)
                    nc.tensor.matmul(
                        banks[:, j % 3, :], q_now[:, s, head // 8, qt * P:(qt + 1) * P],
                        keys[:, head % 8:head % 8 + heads, bass.ds((2 * i + s) * SEQ, n_keys)],
                        start=True, stop=True).then_inc(scored, 1)

                def turn(i, j):
                    s, qt, head, heads, n_keys = unit(j)
                    pe.wait_ge(prob_ready, round_ * i + j + 1)
                    if j >= 2:
                        pe.wait_ge(probT_ready, round_ * i + j - 1)
                    for c in range(BANK // P):
                        last = nc.tensor.transpose(banks[:, 3 + j % 2, c * P:(c + 1) * P],
                                                   prob[:, j % 4, c * P:(c + 1) * P], ident[:, :])
                    last.then_inc(prob_turned, 1)

                def weigh(i, j):
                    s, qt, head, heads, n_keys = unit(j)
                    pe.wait_ge(probT_ready, round_ * i + j + 1)
                    if j:
                        pe.wait_ge(o_ready, round_ * i + j)
                    for h in range(heads):
                        for kt in range(qt + 1):
                            last = nc.tensor.matmul(banks[:, 5, h * HEAD2:(h + 1) * HEAD2],
                                                    probT[:, j % 2, h * (qt + 1) + kt, :],
                                                    v[:, bass.ds(4 * i + 2 * s + kt, 1), :].rearrange("p a d -> p (a d)"),
                                                    start=(kt == 0), stop=(kt == qt))
                    last.then_inc(summed, 1)

                def turn_tokens(i, n):
                    e, s = turns * i + n, n % 2
                    pe.wait_ge(gathered[s], DMA * (turns // 2 * i + n // 2 + 1))
                    if n >= 2:
                        pe.wait_ge(result_ready, e - 1)
                    for k in range(KD):
                        last = nc.tensor.transpose(banks[:, 6, k * P:(k + 1) * P], xg[:, s, k * P:(k + 1) * P], ident[:, :])
                    last.then_inc(turned, 1)

                def widen(i, n):
                    e, s = turns * i + n, n % 2
                    pe.wait_ge(loaded[s], 3 * DMA * (turns // 2 * i + n // 2 + 1))
                    pe.wait_ge(xgT_ready, e + 1)
                    if n:
                        pe.wait_ge(mid_ready, e)
                    for j, wt in enumerate((gate_w, up_w)):
                        for part in range(2):
                            for k in range(KD):
                                last = nc.tensor.matmul(
                                    banks[0:ROWS2, 7, (2 * j + part) * P:(2 * j + part + 1) * P],
                                    wt[:, s, k, part * ROWS2:(part + 1) * ROWS2], xgT[:, s, k * P:(k + 1) * P],
                                    start=(k == 0), stop=(k == KD - 1))
                    last.then_inc(widened, 1)

                def lower(i, n):
                    e, s = turns * i + n, n % 2
                    pe.wait_ge(mid_ready, e + 1)
                    if n + 1 < turns:
                        pe.wait_ge(xgT_ready, e + 2)
                    for part in range(2):
                        last = nc.tensor.matmul(banks[:, 6, D:2 * D], mid[:, s, part * P:(part + 1) * P],
                                                down_w[:, s, part, :], start=(part == 0), stop=(part == 1))
                    last.then_inc(lowered, 1)

                with pe.Fori(0, rounds) as i:
                    for j in range(3):
                        score(i, j)
                    for j in range(round_):
                        turn(i, j)
                        if j % 3 == 0:
                            turn_tokens(i, j // 3)
                        if j + 3 < round_:
                            score(i, j + 3)
                        if j:
                            weigh(i, j - 1)
                        if j % 3 == 1:
                            if j > 1:
                                lower(i, j // 3 - 1)
                            widen(i, j // 3)
                    weigh(i, round_ - 1)
                    lower(i, turns - 1)
                    pe.wait_ge(o_ready, round_ * i + round_)
                    pe.wait_ge(result_ready, turns * (i + 1))
                for half in range(2):
                    for k in range(KD):
                        for t in range(4):
                            last = nc.tensor.transpose(banks[:, 2 * half + k, t * P:(t + 1) * P],
                                                       o_tok[:, 4 * half + t, k * P:(k + 1) * P], ident[:, :])
                        last.then_inc(o_turned, 1)
                for t in range(NT):
                    pe.wait_ge(oT_ready, 2 * (t // 4) + 2)
                    for k in range(KD):
                        last = nc.tensor.matmul(banks[:, 4 + t // 2, (t % 2) * D:(t % 2 + 1) * D],
                                                oT[:, k, t * P:(t + 1) * P], w["Wo"][:, k, :],
                                                start=(k == 0), stop=(k == KD - 1))
                    if t % 2:
                        last.then_inc(mixed, 1)

            @block.vector
            def _(dve):
                def tops(i, j):
                    s, qt, head, heads, n_keys = unit(j)
                    bank = by_head(banks[:, j % 3, :], j)
                    dve.wait_ge(scored, round_ * i + j + 1)
                    last_keys = bank[:, :, n_keys - P:n_keys]
                    nc.vector.tensor_tensor(last_keys, last_keys,
                                            w["causal"][:, SEQ - P:SEQ].unsqueeze(1).broadcast_to([P, heads, P]),
                                            ALU.add).then_inc(masked_ready, 1)
                    dve.wait_ge(masked_ready, round_ * i + j + 1)
                    nc.vector.tensor_reduce(top[:, j % 4, 0:heads], bank, AX.X, ALU.max).then_inc(top_ready, 1)
                    dve.wait_ge(top_ready, round_ * i + j + 1)
                    nc.vector.tensor_scalar(shift[:, j % 4, 0:heads], top[:, j % 4, 0:heads], -scale, None, ALU.mult
                                            ).then_inc(shift_ready, 1)

                def evacuate(i, j):
                    heads = unit(j)[3]
                    dve.wait_ge(prob_turned, round_ * i + j + 1)
                    nc.vector.tensor_copy(probT[:, j % 2, :, :].rearrange("p c k -> p (c k)"), banks[:, 3 + j % 2, :]
                                          ).then_inc(probT_ready, 1)
                    nc.vector.reciprocal(inverse[:, j % 4, 0:heads], total[:, j % 4, 0:heads]).then_inc(inverse_ready, 1)

                def normalize(i, j):
                    s, qt, head, heads, n_keys = unit(j)
                    dve.wait_ge(inverse_ready, round_ * i + j + 1)
                    dve.wait_ge(summed, round_ * i + j + 1)
                    nc.vector.tensor_tensor(
                        o_tok[:, bass.ds(4 * i + 2 * s + qt, 1), head * HEAD2:(head + heads) * HEAD2]
                        .rearrange("p a (h d) -> p (a h) d", h=heads),
                        banks[:, 5, 0:heads * HEAD2].rearrange("p (h d) -> p h d", h=heads),
                        inverse[:, j % 4, 0:heads].unsqueeze(2).broadcast_to([P, heads, HEAD2]), ALU.mult
                        ).then_inc(o_ready, 1)

                def middle(i, n):
                    e, s = turns * i + n, n % 2
                    dve.wait_ge(silu_ready, e + 1)
                    nc.vector.tensor_tensor(mid[:, s, :], silu[:, s, :], banks[0:ROWS2, 7, 2 * P:4 * P], ALU.mult
                                            ).then_inc(mid_ready, 1)

                def weigh_result(i, n):
                    e, s = turns * i + n, n % 2
                    dve.wait_ge(lowered, e + 1)
                    if n >= 2:
                        dve.wait_ge(scattered, DMA * (e - 1))
                    nc.vector.tensor_scalar(result[:, s, :], banks[:, 6, D:2 * D], slot_weight[:, bass.ds(e, 1)],
                                            None, ALU.mult).then_inc(result_ready, 1)

                with dve.Fori(0, rounds) as i:
                    for j in range(3):
                        tops(i, j)
                    for j in range(round_):
                        evacuate(i, j)
                        if j % 3 == 2 and j > 2:
                            weigh_result(i, j // 3 - 1)
                        if j + 3 < round_:
                            tops(i, j + 3)
                        if j:
                            normalize(i, j - 1)
                        if j % 3 == 2:
                            middle(i, j // 3)
                    normalize(i, round_ - 1)
                    weigh_result(i, turns - 1)
                    dve.wait_ge(scattered, DMA * (turns * (i + 1) - 1))
                for b in range(NT // 2):
                    dve.wait_ge(mixed, b + 1)
                    nc.vector.tensor_copy(s_tok[:, 2 * b:2 * b + 2, :],
                                          banks[:, 4 + b, :].rearrange("p (t d) -> p t d", t=2)).then_inc(s_ready, 1)
                dve.wait_ge(s_ready, NT // 2)
                add_gated(nc, dve, x_tok, s_tok, gated, gate_ready, x_ready)

            @block.scalar
            def _(act):
                def exps(i, j):
                    heads = unit(j)[3]
                    act.wait_ge(shift_ready, round_ * i + j + 1)
                    if j >= 4:
                        act.wait_ge(prob_turned, round_ * i + j - 3)
                    for h in range(heads):
                        last = nc.scalar.activation(by_head(prob[:, j % 4, :], j)[:, h, :],
                                                    by_head(banks[:, j % 3, :], j)[:, h, :], ACT.Exp,
                                                    bias=shift[:, j % 4, h:h + 1], scale=scale,
                                                    accum_out=total[:, j % 4, h:h + 1])
                    last.then_inc(prob_ready, 1)

                def copy_tokens(i, n):
                    e, s = turns * i + n, n % 2
                    act.wait_ge(turned, e + 1)
                    nc.scalar.activation(xgT[:, s, :], banks[:, 6, 0:D], ACT.Identity).then_inc(xgT_ready, 1)

                def gate(i, n):
                    e, s = turns * i + n, n % 2
                    act.wait_ge(widened, e + 1)
                    nc.scalar.activation(silu[:, s, :], banks[0:ROWS2, 7, 0:2 * P], ACT.Silu
                                         ).then_inc(silu_ready, 1)

                with act.Fori(0, rounds) as i:
                    exps(i, 0)
                    exps(i, 1)
                    for j in range(round_):
                        if j % 3 == 0:
                            copy_tokens(i, j // 3)
                        if j + 2 < round_:
                            exps(i, j + 2)
                        if j % 3 == 1:
                            gate(i, j // 3)
                for half in range(2):
                    for k in range(KD):
                        act.wait_ge(o_turned, 2 * half + k + 1)
                        nc.scalar.activation(oT[:, k, half * HALF:(half + 1) * HALF], banks[:, 2 * half + k, :],
                                             ACT.Identity).then_inc(oT_ready, 1)
                act.wait_ge(y_loaded, DMA)
                for b in range(NT // 2):
                    pair = slice(2 * b, 2 * b + 2)
                    nc.scalar.activation(gated[:, pair, :], gated[:, pair, :], ACT.Silu).then_inc(gate_ready, 1)




HEADS3, LATENT, HEAD3 = 16, 64, 128
UNITS3 = HEADS3 // 2


def latent_prepare_stage(nc, w, xnT, banks, keep):
    q_weight, o_weight, latT, lat_tok = keep
    with ExitStack() as ctx:
        m = Core(nc, ctx)
        done = nc.alloc_semaphore("latent_done3")
        ready = nc.alloc_semaphore("latent_ready3")
        cols = [slice(h * HALF, (h + 1) * HALF) for h in range(2)]

        with nc.Block(no_gpsimd_drain=True) as block:

            @block.tensor
            def _(pe):
                for k in range(KD):
                    for h in range(HEADS3):
                        last = nc.tensor.matmul(banks[:, 2 * k + h // 8, (h % 8) * LATENT:(h % 8 + 1) * LATENT],
                                                w["WqT"][:, h, k * P:(k + 1) * P], w["WupT"][:, h, :],
                                                start=True, stop=True)
                        if h % 8 == 7:
                            last.then_inc(done, 1)
                for half in range(2):
                    for k in range(KD):
                        last = nc.tensor.matmul(banks[:, 4 + half, :], w["Wdown2"][:, k, :], xnT[:, k, cols[half]],
                                                start=(k == 0), stop=(k == KD - 1))
                    last.then_inc(done, 1)
                for t in range(NT):
                    for k in range(KD):
                        last = nc.tensor.matmul(banks[:, 6, t * LATENT:(t + 1) * LATENT], xnT[:, k, t * P:(t + 1) * P],
                                                w["Wdown2"][:, k, 0:LATENT], start=(k == 0), stop=(k == KD - 1))
                last.then_inc(done, 1)
                for u in range(UNITS3):
                    if u % 2 == 0:
                        pe.wait_ge(ready, u // 2 + 1)
                    for part in range(2):
                        last = nc.tensor.matmul(
                            banks[part * LATENT:(part + 1) * LATENT, u // 2, (u % 2) * D:(u % 2 + 1) * D],
                            w["WupT"][:, 2 * u + part, :], w["Wo"][:, 2 * u + part, :], start=True, stop=True)
                    if u % 2:
                        last.then_inc(done, 1)

            @block.scalar
            def _(act):
                targets = [q_weight[:, k, 8 * P // 2 * j:8 * P // 2 * (j + 1)] for k in range(KD) for j in range(2)]
                targets += [latT[:, cols[0]], latT[:, cols[1]], lat_tok[:, :, :].rearrange("p t c -> p (t c)")]
                targets += [o_weight[:, 2 * b:2 * b + 2, :].rearrange("p u d -> p (u d)") for b in range(UNITS3 // 2)]
                for n, dst in enumerate(targets):
                    bank = n if n < 7 else n - 7
                    act.wait_ge(done, n + 1)
                    nc.scalar.activation(dst, banks[:, bank, :], ACT.Identity).then_inc(ready, 1)


def latent_attention_stage(nc, xnT, s_tok, ident, banks, keep):
    q_weight, o_weight, latT, lat_tok = keep
    scale = 1.0 / np.sqrt(HEAD3)
    round_ = 2 * HEADS3
    with ExitStack() as ctx:
        m = Core(nc, ctx)
        latT_now = m.sbuf("latT_now", [P, 2, 2, SEQ])
        lat_now = m.sbuf("lat_now", [P, 2, 2, LATENT])
        q_now = m.sbuf("q_now3", [P, 2, SEQ])
        top = m.sbuf("top3", [P, 4, 2])
        shift = m.sbuf("shift3", [P, 4, 2])
        total = m.sbuf("total3", [P, 4, 2])
        inverse = m.sbuf("inverse3", [P, 4, 2])
        prob = m.sbuf("prob3", [P, 3, 2, SEQ])
        probT = m.sbuf("probT3", [P, 2, 2, SEQ])
        o_tok = m.sbuf("o_tok3", [P, NT, HEADS3 * LATENT])
        oT = m.sbuf("oT3", [P, UNITS3, N])
        cleared = nc.alloc_semaphore("lat_now_cleared3")
        lat_ready = nc.alloc_semaphore("lat_now_ready3")
        q_done = nc.alloc_semaphore("q_done3")
        q_ready = nc.alloc_semaphore("q_ready3")
        scored = nc.alloc_semaphore("scored3")
        top_ready = nc.alloc_semaphore("top_ready3")
        shift_ready = nc.alloc_semaphore("shift_ready3")
        prob_ready = nc.alloc_semaphore("prob_ready3")
        prob_turned = nc.alloc_semaphore("prob_turned3")
        probT_ready = nc.alloc_semaphore("probT_ready3")
        summed = nc.alloc_semaphore("pv_summed3")
        inverse_ready = nc.alloc_semaphore("inverse_ready3")
        o_ready = nc.alloc_semaphore("o_ready3")
        o_turned = nc.alloc_semaphore("o_turned3")
        oT_ready = nc.alloc_semaphore("oT_ready3")
        mixed = nc.alloc_semaphore("mixed3")
        rounds = BATCH // 2

        with nc.Block(no_gpsimd_drain=True) as block:

            @block.gpsimd
            def _(pool):
                def copy(i, s):
                    b = 2 * i + s
                    for part in range(2):
                        rows = slice(part * LATENT, (part + 1) * LATENT)
                        nc.gpsimd.tensor_copy(latT_now[rows, s, part, :], latT[rows, bass.ds(b * SEQ, SEQ)]
                                              ).then_inc(lat_ready, 1)
                        pool.wait_ge(lat_ready, 6 * i + 3 * s + part + 1)
                    nc.gpsimd.tensor_copy(lat_now[:, s, :, :], lat_tok[:, bass.ds(2 * b, 2), :]).then_inc(lat_ready, 1)
                    pool.wait_ge(lat_ready, 6 * i + 3 * s + 3)

                nc.gpsimd.memset(latT_now[:, :, :, :], 0.0).then_inc(cleared, 1)
                pool.wait_ge(cleared, 1)
                copy(0, 0)
                copy(0, 1)
                with pool.Fori(1, rounds) as i:
                    for s in range(2):
                        pool.wait_ge(summed, round_ * i - HEADS3 + HEADS3 * s)
                        copy(i, s)

            @block.tensor
            def _(pe):
                def query(i, u):
                    s, pair = u // UNITS3, u % UNITS3
                    if u >= 1:
                        pe.wait_ge(q_ready, 2 * UNITS3 * i + u)
                    for k in range(KD):
                        last = nc.tensor.matmul(banks[:, 7, 0:SEQ], q_weight[:, k, pair * P:(pair + 1) * P],
                                                xnT[:, k, bass.ds((2 * i + s) * SEQ, SEQ)],
                                                start=(k == 0), stop=(k == KD - 1))
                    last.then_inc(q_done, 1)

                def score(i, j):
                    if j % HEADS3 == 0:
                        pe.wait_ge(lat_ready, 6 * i + 3 * (j // HEADS3) + 3)
                    if j % 2 == 0:
                        pe.wait_ge(q_ready, 2 * UNITS3 * i + j // 2 + 1)
                    for qt in range(2):
                        last = nc.tensor.matmul(banks[:, j % 3, qt * SEQ:(qt + 1) * SEQ],
                                                q_now[:, (j // 2) % 2, qt * P:(qt + 1) * P],
                                                latT_now[:, j // HEADS3, j % 2, :], start=True, stop=True)
                    last.then_inc(scored, 1)

                def turn(i, j):
                    pe.wait_ge(prob_ready, round_ * i + j + 1)
                    for kt in range(2):
                        for qt in range(2):
                            last = nc.tensor.transpose(banks[:, 3 + j % 2, kt * SEQ + qt * P:kt * SEQ + (qt + 1) * P],
                                                       prob[:, j % 3, qt, kt * P:(kt + 1) * P], ident[:, :])
                    last.then_inc(prob_turned, 1)

                def weigh(i, j):
                    pe.wait_ge(probT_ready, round_ * i + j + 1)
                    if j >= 2:
                        pe.wait_ge(o_ready, round_ * i + j - 1)
                    for qt in range(2):
                        for kt in range(2):
                            last = nc.tensor.matmul(banks[:, 5 + j % 2, qt * LATENT:(qt + 1) * LATENT],
                                                    probT[:, j % 2, kt, qt * P:(qt + 1) * P],
                                                    lat_now[:, j // HEADS3, kt, :], start=(kt == 0), stop=(kt == 1))
                    last.then_inc(summed, 1)

                def mix(t):
                    pe.wait_ge(oT_ready, 2 * t + 2)
                    for u in range(UNITS3):
                        last = nc.tensor.matmul(banks[:, 4 + t // 2, (t % 2) * D:(t % 2 + 1) * D], oT[:, u, t * P:(t + 1) * P],
                                                o_weight[:, u, :], start=(u == 0), stop=(u == UNITS3 - 1))
                    if t % 2:
                        last.then_inc(mixed, 1)

                with pe.Fori(0, rounds) as i:
                    query(i, 0)
                    query(i, 1)
                    score(i, 0)
                    score(i, 1)
                    for j in range(round_):
                        if j % 2 == 0 and j // 2 + 2 < 2 * UNITS3:
                            query(i, j // 2 + 2)
                        if j + 2 < round_:
                            score(i, j + 2)
                        turn(i, j)
                        if j:
                            weigh(i, j - 1)
                    weigh(i, round_ - 1)
                    pe.wait_ge(o_ready, round_ * i + round_)
                for t in range(NT):
                    for u in range(UNITS3):
                        if t >= 2 and u % 4 == 0:
                            pe.wait_ge(oT_ready, 2 * (t - 2) + u // 4 + 1)
                        last = nc.tensor.transpose(banks[:, 2 * (t % 2) + u // 4, (u % 4) * P:(u % 4 + 1) * P],
                                                   o_tok[:, t, u * P:(u + 1) * P], ident[:, :])
                        if u % 4 == 3:
                            last.then_inc(o_turned, 1)
                    if t:
                        mix(t - 1)
                mix(NT - 1)

            @block.vector
            def _(dve):
                def tops(i, j):
                    dve.wait_ge(scored, round_ * i + j + 1)
                    nc.vector.tensor_reduce(top[:, j % 4, :], banks[:, j % 3, :].rearrange("p (q k) -> p q k", q=2),
                                            AX.X, ALU.max).then_inc(top_ready, 1)
                    dve.wait_ge(top_ready, round_ * i + j + 1)
                    nc.vector.tensor_scalar(shift[:, j % 4, :], top[:, j % 4, :], -scale, None, ALU.mult
                                            ).then_inc(shift_ready, 1)

                def evacuate(i, j):
                    dve.wait_ge(prob_turned, round_ * i + j + 1)
                    nc.vector.tensor_copy(probT[:, j % 2, :, :].rearrange("p a q -> p (a q)"), banks[:, 3 + j % 2, :]
                                          ).then_inc(probT_ready, 1)
                    nc.vector.reciprocal(inverse[:, j % 4, :], total[:, j % 4, :]).then_inc(inverse_ready, 1)

                def normalize(i, j):
                    s, h = j // HEADS3, j % HEADS3
                    dve.wait_ge(inverse_ready, round_ * i + j + 1)
                    dve.wait_ge(summed, round_ * i + j + 1)
                    nc.vector.tensor_tensor(
                        o_tok[:, bass.ds(4 * i + 2 * s, 2), h * LATENT:(h + 1) * LATENT],
                        banks[:, 5 + j % 2, 0:2 * LATENT].rearrange("p (q c) -> p q c", q=2),
                        inverse[:, j % 4, :].unsqueeze(2).broadcast_to([P, 2, LATENT]), ALU.mult).then_inc(o_ready, 1)

                with dve.Fori(0, rounds) as i:
                    tops(i, 0)
                    tops(i, 1)
                    for j in range(round_):
                        if j + 2 < round_:
                            tops(i, j + 2)
                        evacuate(i, j)
                        if j:
                            normalize(i, j - 1)
                    normalize(i, round_ - 1)
                for t in range(NT):
                    dve.wait_ge(o_turned, 2 * t + 1)
                    nc.vector.tensor_copy(oT[:, 0:4, t * P:(t + 1) * P],
                                          banks[:, 2 * (t % 2), :].rearrange("p (u c) -> p u c", u=4)).then_inc(oT_ready, 1)
                    dve.wait_ge(o_turned, 2 * t + 2)
                    nc.vector.tensor_copy(oT[:, 4:8, t * P:(t + 1) * P],
                                          banks[:, 2 * (t % 2) + 1, :].rearrange("p (u c) -> p u c", u=4)
                                          ).then_inc(oT_ready, 1)

            @block.scalar
            def _(act):
                def query(i, u):
                    act.wait_ge(q_done, 2 * UNITS3 * i + u + 1)
                    nc.scalar.activation(q_now[:, u % 2, :], banks[:, 7, 0:SEQ], ACT.Identity).then_inc(q_ready, 1)

                with act.Fori(0, rounds) as i:
                    query(i, 0)
                    query(i, 1)
                    for j in range(round_):
                        if j % 2 == 0 and j // 2 + 2 < 2 * UNITS3:
                            query(i, j // 2 + 2)
                        act.wait_ge(shift_ready, round_ * i + j + 1)
                        for qt in range(2):
                            last = nc.scalar.activation(prob[:, j % 3, qt, :], banks[:, j % 3, qt * SEQ:(qt + 1) * SEQ],
                                                        ACT.Exp, bias=shift[:, j % 4, qt:qt + 1], scale=float(scale),
                                                        accum_out=total[:, j % 4, qt:qt + 1])
                        last.then_inc(prob_ready, 1)
                for b in range(NT // 2):
                    act.wait_ge(mixed, b + 1)
                    nc.scalar.activation(s_tok[:, 2 * b:2 * b + 2, :].rearrange("p t d -> p (t d)"), banks[:, 4 + b, :],
                                         ACT.Identity)


MLP3 = 2048
PACKS3 = MLP3 // (2 * P)


def four_bit_stage(nc, packed, scales, x_tok, xnT, s_tok, banks):
    with ExitStack() as ctx:
        m = Core(nc, ctx)
        shape = [P, 3, 2, D]
        pack = m.sbuf("pack3", [P, 2, 3, D], I32)
        scale = m.sbuf("scale3", [P, 2, 3, D])
        code = m.sbuf("code3", shape, I32)
        eight = m.sbuf("eight3", shape, BF16)
        size = m.sbuf("size3", shape, BF16)
        twice = m.sbuf("twice3", shape, BF16)
        fourfold = m.sbuf("fourfold3", shape, BF16)
        sign = m.sbuf("sign3", shape, BF16)
        weight = m.sbuf("weight3", [P, 2, 3, 2, D])
        gelu = m.sbuf("gelu3", [P, 2, HALF])
        inter = m.sbuf("inter3", [P, 2, N])
        gated = m.sbuf("gated3", [P, NT, D])
        loaded = [nc.alloc_semaphore(f"pack_loaded{s}") for s in range(2)]
        unpack_steps = nc.alloc_semaphore("unpack_steps3")
        weight_ready = nc.alloc_semaphore("weight_ready3")
        widened = nc.alloc_semaphore("widened3")
        gelu_ready = nc.alloc_semaphore("gelu_ready3")
        inter_ready = nc.alloc_semaphore("inter_ready3")
        lowered = nc.alloc_semaphore("lowered3")
        gate_ready = nc.alloc_semaphore("gate_ready3")
        x_ready = nc.alloc_semaphore("x_ready3")
        cols = [slice(h * HALF, (h + 1) * HALF) for h in range(2)]
        rounds = PACKS3 // 2
        unpack_waits = 10

        with nc.Block(no_gpsimd_drain=True) as block:

            @block.sync
            def _(sp):
                def load(n, s):
                    for j in range(3):
                        for dst, src in ((pack, packed[j]), (scale, scales[j])):
                            sp.dma_start(dst[:, s, j, :], src[bass.ds(n, 1), :, :].rearrange("n p c -> p (n c)")
                                         ).then_inc(loaded[s], DMA)

                load(0, 0)
                load(1, 1)
                with sp.Fori(1, rounds) as i:
                    for s in range(2):
                        sp.wait_ge(weight_ready, 2 * i + s - 1)
                        load(2 * i + s, s)

            @block.tensor
            def _(pe):
                def widen(i, job):
                    s, tile, half = job // 4, job // 2 % 2, job % 2
                    if job % 4 == 0:
                        pe.wait_ge(weight_ready, 2 * i + s + 1)
                    for j in range(2):
                        for k in range(KD):
                            last = nc.tensor.matmul(banks[:, 4 + 2 * half + j, :], weight[:, s, j, k, tile * P:(tile + 1) * P],
                                                    xnT[:, k, cols[half]], start=(k == 0), stop=(k == KD - 1))
                    last.then_inc(widened, 1)

                def lower(i, job, first=False):
                    s, tile, half = job // 4, job // 2 % 2, job % 2
                    pe.wait_ge(inter_ready, 8 * i + job + 1)
                    for t in range(4 * half, 4 * half + 4):
                        last = nc.tensor.matmul(banks[:, t // 2, (t % 2) * D:(t % 2 + 1) * D],
                                                inter[:, tile, t * P:(t + 1) * P], weight[:, s, 2, tile, :],
                                                start=first and t % 2 == 0, stop=False, skip_group_check=True)
                    last.then_inc(lowered, 1)

                def round_(i, first=False, final=False):
                    for job in range(8):
                        if job < 7:
                            widen(i, job + 1)
                        elif not final:
                            widen(i + 1, 0)
                        lower(i, job, first and job < 2)

                widen(0, 0)
                round_(0, first=True)
                with pe.Fori(1, rounds - 1) as i:
                    round_(i)
                round_(rounds - 1, final=True)

            @block.scalar
            def _(act):
                with act.Fori(0, rounds) as i:
                    for job in range(8):
                        act.wait_ge(widened, 8 * i + job + 1)
                        nc.scalar.activation(gelu[:, job % 2, :], banks[:, 4 + 2 * (job % 2), :], ACT.Gelu_apprx_tanh
                                             ).then_inc(gelu_ready, 1)
                silu_sum(nc, act, gated, banks, lowered, 8 * rounds, gate_ready)

            @block.vector
            def _(dve):
                def multiply(i, job):
                    tile, half = job // 2 % 2, job % 2
                    dve.wait_ge(gelu_ready, 8 * i + job + 1)
                    nc.vector.tensor_tensor(inter[:, tile, cols[half]], gelu[:, half, :], banks[:, 5 + 2 * half, :],
                                            ALU.mult).then_inc(inter_ready, 1)

                def unpack(i, s, part, first=False):
                    done = unpack_waits * (2 * i + s)

                    def steps(at, *made):
                        for ins in made:
                            ins.then_inc(unpack_steps, 1)
                        dve.wait_ge(unpack_steps, done + at)

                    if part == 0:
                        dve.wait_ge(loaded[s], 6 * DMA * i + 6 * DMA)
                        steps(2, nc.vector.tensor_scalar(code[:, :, 0, :], pack[:, s, :, :], 15, None, ALU.bitwise_and),
                              nc.vector.tensor_scalar(code[:, :, 1, :], pack[:, s, :, :], 4, 15, ALU.logical_shift_right,
                                                      ALU.bitwise_and))
                        steps(3, nc.vector.tensor_scalar(eight[:], code[:], 8.0, 8.0, ALU.is_ge, ALU.mult))
                    if part == 1:
                        steps(4, nc.vector.tensor_tensor(size[:], code[:], eight[:], ALU.subtract))
                        steps(6, nc.vector.tensor_scalar(twice[:], size[:], 2.0, -4.0, ALU.mult, ALU.add),
                              nc.vector.tensor_scalar(fourfold[:], size[:], 4.0, -16.0, ALU.mult, ALU.add))
                    if part == 2:
                        steps(7, nc.vector.tensor_tensor(twice[:], twice[:], fourfold[:], ALU.max))
                        steps(9, nc.vector.tensor_tensor(size[:], size[:], twice[:], ALU.max),
                              nc.vector.tensor_scalar(sign[:], eight[:], -0.125, 0.5, ALU.mult, ALU.add))
                    if part == 3:
                        steps(10, nc.vector.tensor_tensor(size[:], size[:], sign[:], ALU.mult))
                        if not first:
                            dve.wait_ge(lowered, 4 * (2 * i + s) - 4)
                        for j in range(3):
                            ins = nc.vector.tensor_tensor(
                                weight[:, s, j, :, :], size[:, j, :, :],
                                scale[:, s, j, :].unsqueeze(1).broadcast_to([P, 2, D]), ALU.mult)
                        ins.then_inc(weight_ready, 1)

                def round_(i, first=False, final=False):
                    for job in range(8):
                        s = job // 4
                        multiply(i, job)
                        if s == 0:
                            unpack(i, 1, job % 4, first)
                        elif not final:
                            unpack(i + 1, 0, job % 4)

                for part in range(4):
                    unpack(0, 0, part, True)
                round_(0, first=True)
                with dve.Fori(1, rounds - 1) as i:
                    round_(i)
                round_(rounds - 1, final=True)
                add_gated(nc, dve, x_tok, s_tok, gated, gate_ready, x_ready)


def build(nc, A, out):
    with ExitStack() as ctx:
        m = Core(nc, ctx)
        banks = ctx.enter_context(nc.psum_tensor("banks", [P, 8, BANK], F32))
        x_tok = m.sbuf("x_tok", [P, NT, D])
        xn_tok = m.sbuf("xn_tok", [P, NT, D])
        s_tok = m.sbuf("s_tok", [P, NT, D])
        xnT = m.sbuf("xnT", [P, KD, N])
        ident = m.sbuf("ident", [P, P])
        earlier = m.sbuf("earlier", [P, 16, 16])

        first_loads = nc.alloc_semaphore("first_loads")
        with nc.Block(no_gpsimd_drain=True) as block:
            @block.sync
            def _(sp):
                sp.dma_start(x_tok[:, :, :], A["L0_attn_x"].rearrange("b t d -> (b t) d")
                             .rearrange("(n p) d -> p n d", p=P)).then_inc(first_loads, DMA)
                sp.dma_start(ident[:, :], A["ident"]).then_inc(first_loads, DMA)
                sp.dma_start(earlier[:, :, :].rearrange("p a b -> p (a b)"), A["earlier"].partition_broadcast(P)
                             ).then_inc(first_loads, DMA)
                sp.wait_ge(first_loads, 3 * DMA)

        def new_layer():
            nc.clear_and_free_semaphores(nc.allocated_since(outer))
            nc.all_engine_barrier()

        outer = nc.snapshot_sems()
        with ExitStack() as layer:
            w, loads = load_layer0(Core(nc, layer), A)
            norm_stage(nc, 0, x_tok, xn_tok, xnT, ident, banks, loads)
            scratch = nc.dram_tensor("probs_dram0", [8, N], F32).ap()
            recurrent_layer_stage(nc, w, (A["L0_ffn_gate_up_w"], A["L0_ffn_down_w"]), scratch, x_tok, xnT, s_tok,
                                  ident, earlier, banks)
        new_layer()
        with ExitStack() as layer:
            inner = Core(nc, layer)
            w, loads = load_layer1(inner, A)
            norm_stage(nc, 1, x_tok, xn_tok, xnT, ident, banks, loads)
            rows = nc.dram_tensor("bc_dram", [2 * STATES, N], F32).ap()
            with ExitStack() as mixer:
                inner = Core(nc, mixer)
                keep = (inner.sbuf("skip", [P, MI, N]), inner.sbuf("xs", [P, MI, N]), inner.sbuf("delta", [P, MI, N]),
                        inner.sbuf("delta_x", [P, MI, N]), inner.sbuf("A", [P, MI, STATES]),
                        inner.sbuf("diag_D", [P, MI, P]))
                y = inner.sbuf("y1", [P, NT, D])
                scan_prepare_stage(nc, w, xn_tok, xnT, ident, banks, keep, rows, y)
                scan_stage(nc, w, A["L1_ffn_up_w"], A["L1_ffn_down_w"], x_tok, xn_tok, xnT, s_tok, ident, banks,
                           keep, rows, y)
        new_layer()
        with ExitStack() as layer:
            w, loads = load_layer2(Core(nc, layer), A)
            norm_stage(nc, 2, x_tok, xn_tok, xnT, ident, banks, loads)
            xn_dram = nc.dram_tensor("xn_dram2", [N, D], F32).ap()
            y_dram = nc.dram_tensor("y_dram2", [N + P, D], F32).ap()
            inner = Core(nc, layer)
            tables = (inner.sbuf("slot_token", [P, EXPERTS2], U32), inner.sbuf("slot_target", [P, EXPERTS2], U32),
                      inner.sbuf("slot_weight", [P, EXPERTS2]))
            route_stage(nc, w, xn_tok, xnT, ident, earlier, banks, tables, xn_dram, y_dram)
            keep = (inner.sbuf("q2", [P, 2, N]), inner.sbuf("keys2", [P, 8, N]), inner.sbuf("v2", [P, NT, HEAD2]))
            rotary_stage(nc, w, xnT, keep, banks)
            attention_and_expert_stage(nc, w, keep, (A["L2_ffn_w_gate"], A["L2_ffn_w_up"], A["L2_ffn_w_down"]), tables,
                                       xn_dram, y_dram, x_tok, s_tok, ident, banks)
        new_layer()
        with ExitStack() as layer:
            w, loads = load_layer3(Core(nc, layer), A)
            norm_stage(nc, 3, x_tok, xn_tok, xnT, ident, banks, loads, parity=True)
            inner = Core(nc, layer)
            keep = (inner.sbuf("q_weight3", [P, KD, HEADS3 * LATENT]), inner.sbuf("o_weight3", [P, UNITS3, D]),
                    inner.sbuf("latT3", [P, N]), inner.sbuf("lat_tok3", [P, NT, LATENT]))
            latent_prepare_stage(nc, w, xnT, banks, keep)
            latent_attention_stage(nc, xnT, s_tok, ident, banks, keep)
        four_bit_stage(nc, [A[f"L3_ffn_{name}_W_packed"] for name in ("gate", "up", "down")],
                       [A[f"L3_ffn_{name}_scales"] for name in ("gate", "up", "down")], x_tok, xnT, s_tok, banks)

        stored = nc.alloc_semaphore("out_stored")
        with nc.Block(no_gpsimd_drain=True) as block:
            @block.sync
            def _(sp):
                sp.dma_start(out.rearrange("b t d -> (b t) d").rearrange("(n p) d -> p n d", p=P),
                             x_tok[:, :, :]).then_inc(stored, DMA)
                sp.wait_ge(stored, DMA)


def load_layer0(m, A):
    w, loads = {}, []

    def add(name, shape, src):
        w[name] = m.sbuf("w0_" + name, shape)
        loads.append((w[name][:], src))

    add("W_in", [P, KD, D], by_feature(A["L0_attn_W_in"]))
    add("W_ga", [P, KD, P], by_feature(A["L0_gates_a"]))
    add("W_gx", [P, KD, P], by_feature(A["L0_gates_x"]))
    add("W_out", [P, KD, D], by_feature(A["L0_attn_W_out"]))
    add("b_in", [P, KD], A["L0_attn_b_in"])
    add("b_ga", [P, 1], A["L0_attn_b_ga"])
    add("b_gx", [P, 1], A["L0_attn_b_gx"])
    add("a_real", [P, 1], A["L0_attn_a_real"])
    add("a_imag", [P, 1], A["L0_attn_a_imag"])
    add("b_out", [P, D], A["L0_attn_b_out"].partition_broadcast(P))
    add("router_w", [P, KD, 8], by_feature(A["L0_ffn_router_w"]))
    add("shared_gate_w", [P, KD, P], by_feature(A["L0_ffn_shared_gate_w"]))
    add("shared_up_w", [P, KD, P], by_feature(A["L0_ffn_shared_up_w"]))
    add("shared_down_w", [P, 1, D], by_feature(A["L0_ffn_shared_down_w"]))
    return w, loads


def load_layer1(m, A):
    w, loads = {}, []

    def add(name, shape, src):
        w[name] = m.sbuf("w1_" + name, shape)
        loads.append((w[name][:], src))

    add("A_log", [P, MI, STATES], by_feature(A["L1_attn_A_log"]))
    add("W_D", [P, MI], A["L1_attn_W_D"])
    add("norm_w", [P, KD], A["L1_attn_norm_w"])
    add("W_skip", [P, KD, INNER], by_feature(A["L1_attn_W_skip"]))
    add("W_in", [P, KD, INNER], by_feature(A["L1_attn_W_in"]))
    add("conv_w", [P, MI, 4], A["L1_attn_conv_w"].rearrange("(k p) a j -> p k (a j)", p=P))
    add("conv_b", [P, MI], A["L1_attn_conv_b"])
    add("W_d1", [P, MI, P], by_feature(A["L1_attn_W_d1"]))
    add("W_BC", [P, MI, 2 * STATES], by_feature(A["L1_attn_W_BC"]))
    add("W_d2", [P, 1, INNER], by_feature(A["L1_attn_W_d2"]))
    add("b_d2", [P, MI], A["L1_attn_b_d2"])
    add("W_out", [P, MI, D], by_feature(A["L1_attn_W_out"]))
    add("gate_w", [P, KD, 8], by_feature(A["L1_ffn_gate_w"]))
    add("expert_weight", [P, KD, D], by_feature(A["L1_ffn_expert_weight"]))
    add("ln_gamma", [P, D], A["L1_ffn_ln_gamma"].partition_broadcast(P))
    add("ln_beta", [P, D], A["L1_ffn_ln_beta"].partition_broadcast(P))
    return w, loads


def load_layer2(m, A):
    w, loads = {}, []

    def add(name, shape, src, dtype=F32):
        w[name] = m.sbuf("w2_" + name, shape, dtype)
        loads.append((w[name][:], src))

    for name in ("Wq", "Wq_swap", "Wo"):
        add(name, [P, KD, D], by_feature(A["L2_attn_" + name]))
    add("Wk", [P, KD, P], by_feature(A["L2_attn_Wk"]))
    add("Wv", [P, KD, HEAD2], by_feature(A["L2_attn_Wv"]))
    add("gate_w", [P, KD, EXPERTS2], by_feature(A["L2_ffn_gate_w"]))
    add("sw_gate", [P, KD, SHARED2], by_feature(A["L2_ffn_sw_gate"]))
    add("sw_up", [P, KD, SHARED2], by_feature(A["L2_ffn_sw_up"]))
    add("sw_down", [ROWS2, SHARED2 // ROWS2, D], A["L2_ffn_sw_down"].rearrange("(i p) d -> p i d", p=ROWS2))
    for name in ("cos", "sin", "head_rows", "causal", "before", "slots", "token_place", "spare_row"):
        add(name, list(A[name].shape), A[name])
    return w, loads


def load_layer3(m, A):
    w, loads = {}, []

    def add(name, shape, src):
        w[name] = m.sbuf("w3_" + name, shape)
        loads.append((w[name][:], src))

    add("WqT", [P, HEADS3, D], by_feature(A["L3_attn_W_q"]))
    add("WupT", [P, HEADS3, LATENT], by_feature(A["L3_attn_W_kv_up"]))
    add("Wdown2", [P, KD, 2 * LATENT], by_feature(A["L3_attn_W_kv_down"]))
    add("Wo", [P, HEADS3, D], by_feature(A["L3_attn_W_o"]))
    return w, loads


COLUMNS = ("L0_attn_b_in", "L0_attn_b_ga", "L0_attn_b_gx", "L0_attn_a_real", "L0_attn_a_imag",
           "L1_attn_W_D", "L1_attn_norm_w", "L1_attn_conv_b", "L1_attn_b_d2")
TRANSPOSED = ("L1_attn_W_skip", "L1_attn_W_in", "L1_attn_W_d1", "L1_attn_W_d2", "L1_attn_W_out")


def block_diagonal(blocks):
    h, i, j = blocks.shape
    full = np.zeros((h, i, h, j), blocks.dtype)
    for n in range(h):
        full[n, :, n, :] = blocks[n]
    return full.reshape(h * i, h * j)


def laid_out(inputs):
    A = {name: np.ascontiguousarray(value) for name, value in inputs.items()}
    A["L0_gates_a"] = block_diagonal(A.pop("L0_attn_W_ga"))
    A["L0_gates_x"] = block_diagonal(A.pop("L0_attn_W_gx"))
    A["ident"] = np.eye(P, dtype=np.float32)
    A["earlier"] = np.tril(np.ones((16, 16), np.float32), -1).reshape(-1)
    for name in COLUMNS:
        A[name] = A[name].reshape(-1, P).T
    A["L1_attn_W_BC"] = np.concatenate([A.pop("L1_attn_W_Bm"), A.pop("L1_attn_W_Cm")]).T
    for name in TRANSPOSED:
        A[name] = A[name].T
    A["L2_attn_Wq_swap"] = A["L2_attn_Wq"][np.arange(D) ^ 1].T
    A["L2_attn_Wk"] = np.tile(A["L2_attn_Wk"], (8, 1)).T
    A["L2_attn_Wq"] = A["L2_attn_Wq"].T
    A["L2_attn_Wv"], A["L2_attn_Wo"] = A["L2_attn_Wv"].T, A["L2_attn_Wo"].T
    half = HEAD2 // 2
    theta = 1.0 / np.float32(10000.0) ** (np.arange(0, half, 2, dtype=np.float32) / np.float32(half))
    freq = np.arange(HEADS2, dtype=np.float32)[:, None] * theta.astype(np.float32)[None, :]
    head, place = np.arange(D) // HEAD2, np.arange(D) % half
    A["cos"] = np.cos(freq)[head, place // 2].reshape(KD, P).T
    A["sin"] = (np.sin(freq)[head, place // 2] * np.where(place % 2, 1, -1).astype(np.float32)).reshape(KD, P).T
    A["head_rows"] = np.repeat(np.eye(8, dtype=np.float32), HEAD2, axis=0)
    later = np.triu(np.full((P, P), -1e30, np.float32), 1)
    A["causal"] = np.concatenate([np.zeros((P, P), np.float32), later], axis=1)
    A["L2_ffn_gate_w"] = A["L2_ffn_gate_w"].T
    A["before"] = np.triu(np.ones((P, P), np.float32), 1)
    A["slots"] = np.tile(np.arange(CAPACITY, dtype=np.float32), (P, 1))
    token = np.arange(N).reshape(NT, P).T
    A["token_place"] = np.stack([token % P, token - token % P], axis=-1).astype(np.float32)
    A["spare_row"] = np.arange(N, N + P, dtype=np.float32)[:, None]
    parity = np.concatenate([np.arange(0, D, 2), np.arange(1, D, 2)])
    A["L3_attn_W_q"] = A["L3_attn_W_q"][parity].T
    A["L3_attn_W_kv_up"] = A["L3_attn_W_kv_up"].T
    A["L3_attn_W_kv_down"] = np.tile(A["L3_attn_W_kv_down"][parity], (1, 2))
    hidden = np.arange(MLP3).reshape(PACKS3, P, 2).transpose(0, 2, 1).reshape(PACKS3, 2 * P)
    for name in ("gate", "up"):
        A[f"L3_ffn_{name}_W_packed"] = A[f"L3_ffn_{name}_W_packed"][hidden].transpose(0, 2, 1)
        A[f"L3_ffn_{name}_scales"] = np.repeat(A[f"L3_ffn_{name}_scales"][hidden].transpose(0, 2, 1), 16, axis=1)
    A["L3_ffn_down_W_packed"] = A["L3_ffn_down_W_packed"].T.reshape(PACKS3, P, D)
    A["L3_ffn_down_scales"] = np.repeat(A["L3_ffn_down_scales"].T, 16, axis=0).reshape(PACKS3, P, D)
    return {name: np.ascontiguousarray(value) for name, value in A.items()}


def kernel(**inputs):
    import concourse.bacc as bacc
    from concourse.bass_utils import run_bass_kernel_spmd

    nc = bacc.Bacc("TRN2", target_bir_lowering=False, num_devices=1)
    arrays = laid_out(inputs)
    aps = {name: nc.dram_tensor("in_" + name, a.shape, mybir.dt.from_np(a.dtype), kind="ExternalInput").ap()
           for name, a in arrays.items()}
    out = nc.dram_tensor("out_dram", (BATCH, SEQ, D), F32, kind="ExternalOutput").ap()
    build(nc, aps, out)
    result = run_bass_kernel_spmd(nc, [{"in_" + name: a for name, a in arrays.items()}], core_ids=[0])
    return result.results[0]["out_dram"]
```

```python
from contextlib import ExitStack

import numpy as np

import concourse.bass as bass
from concourse import mybir

F32 = mybir.dt.float32
BF16 = mybir.dt.bfloat16
I32 = mybir.dt.int32
U32 = mybir.dt.uint32
ALU = mybir.AluOpType
ACT = mybir.ActivationFunctionType
AX = mybir.AxisListType

P = 128
BATCH, SEQ, D = 4, 256, 256
N = BATCH * SEQ
NT = N // P
KD = D // P
HALF = N // 2
BANK = 512
EPS = 1e-5
DMA = 16


class Steps:

    def __init__(self, eng, sem):
        self.eng, self.sem, self.count = eng, sem, 0

    def add(self, ins):
        ins.then_inc(self.sem, 1)
        self.count += 1

    def join(self):
        self.eng.wait_ge(self.sem, self.count)

    def do(self, ins):
        self.add(ins)
        self.join()


class Core:

    def __init__(self, nc, ctx):
        self.nc, self.ctx = nc, ctx

    def sbuf(self, name, shape, dtype=F32):
        return self.ctx.enter_context(self.nc.sbuf_tensor(name, shape, dtype))

    def sem(self, name):
        return self.ctx.enter_context(self.nc.semaphore(name))

    def scope(self, ctx):
        return Core(self.nc, ctx)


def by_feature(w):
    return w.rearrange("(k p) m -> p k m", p=P)


def norm_stage(nc, layer, x_tok, stats, xn_tok, xnT, ident, banks, loads, late=None, parity=False, rms_tok=None, beside=None):
    with ExitStack() as ctx:
        m = Core(nc, ctx).scope(ctx)
        mean_var = m.sbuf(f"mean_var{layer}", [P, NT, 2])
        var = m.sbuf(f"var{layer}", [P, NT])
        std = m.sbuf(f"std{layer}", [P, NT])
        rstd = m.sbuf(f"rstd{layer}", [P, NT])
        square = m.sbuf(f"mean_square{layer}", [P, NT])
        rms = m.sbuf(f"rms{layer}", [P, NT])
        norm_steps = nc.alloc_semaphore(f"norm_steps{layer}")
        var_ready = nc.alloc_semaphore(f"norm_var_ready{layer}")
        std_ready = nc.alloc_semaphore(f"norm_std_ready{layer}")
        square_ready = nc.alloc_semaphore(f"mean_square_ready{layer}")
        rms_ready = nc.alloc_semaphore(f"rms_ready{layer}")
        xn_ready = nc.alloc_semaphore(f"xn_ready{layer}")
        turned = nc.alloc_semaphore(f"xn_turned{layer}")
        xnT_ready = nc.alloc_semaphore(f"xnT_ready{layer}")
        loaded = nc.alloc_semaphore(f"weights_loaded{layer}")

        with nc.Block(no_gpsimd_drain=True) as block:

            @block.sync
            def _(sp):
                for dst, src in loads:
                    sp.dma_start(dst, src).then_inc(loaded, DMA)
                if late is not None:
                    for dst, src in late[0]:
                        sp.dma_start(dst, src).then_inc(late[1], DMA)
                if loads:
                    sp.wait_ge(loaded, DMA * len(loads))
                if beside is not None:
                    beside["sync"](sp)

            @block.vector
            def _(dve):
                steps = Steps(dve, norm_steps)
                for t in range(NT):
                    steps.add(nc.vector.bn_aggr(mean_var[:, t, :], stats[:, t, :]))
                steps.join()
                nc.vector.tensor_scalar(var[:, :], mean_var[:, :, 1], EPS, None, ALU.add).then_inc(var_ready, 1)
                dve.wait_ge(std_ready, 1)
                steps.do(nc.vector.reciprocal(rstd[:, :], std[:, :]))
                if rms_tok is not None:
                    steps.do(nc.vector.tensor_tensor(square[:, :], mean_var[:, :, 1], rstd[:, :], ALU.mult))
                    steps.do(nc.vector.tensor_tensor(square[:, :], square[:, :], rstd[:, :], ALU.mult))
                    nc.vector.tensor_scalar(square[:, :], square[:, :], EPS, None, ALU.add).then_inc(square_ready, 1)
                for t in range(NT):
                    nc.vector.tensor_scalar(
                        xn_tok[:, t, :], x_tok[:, t, :], mean_var[:, t, 0:1], rstd[:, t:t + 1],
                        ALU.subtract, ALU.mult).then_inc(xn_ready, 1)
                if rms_tok is not None:
                    dve.wait_ge(rms_ready, 1)
                    steps.do(nc.vector.reciprocal(square[:, :], rms[:, :]))
                    dve.wait_ge(xn_ready, NT)
                    for t in range(NT):
                        nc.vector.tensor_scalar(rms_tok[:, t, :], xn_tok[:, t, :], square[:, t:t + 1], None, ALU.mult)
                if beside is not None:
                    beside["vector"](dve)

            @block.tensor
            def _(pe):
                if beside is not None:
                    beside["tensor"](pe)
                for t in range(NT):
                    pe.wait_ge(xn_ready, t + 1)
                    for k in range(KD):
                        part = xn_tok[:, t, k::2] if parity else xn_tok[:, t, k * P:(k + 1) * P]
                        last = nc.tensor.transpose(
                            banks[:, KD * (t // 4) + k, (t % 4) * P:(t % 4 + 1) * P], part, ident[:, :])
                    last.then_inc(turned, 1)

            @block.scalar
            def _(act):
                act.wait_ge(var_ready, 1)
                nc.scalar.activation(std[:, :], var[:, :], ACT.Sqrt).then_inc(std_ready, 1)
                if rms_tok is not None:
                    act.wait_ge(square_ready, 1)
                    nc.scalar.activation(rms[:, :], square[:, :], ACT.Sqrt).then_inc(rms_ready, 1)
                if beside is not None:
                    beside["scalar"](act)
                for half in range(2):
                    act.wait_ge(turned, 4 * (half + 1))
                    for k in range(KD):
                        nc.scalar.activation(xnT[:, k, half * HALF:(half + 1) * HALF],
                                             banks[:, KD * half + k, :], ACT.Identity).then_inc(xnT_ready, 1)


def rank_mask(nc, steps, mask, values, scratch, earlier, experts, top):
    shape = [P, NT, experts, experts]
    others = values.unsqueeze(2).broadcast_to(shape)
    own = values.unsqueeze(3).broadcast_to(shape)
    above, equal, count = scratch
    steps.add(nc.vector.tensor_tensor(above, others, own, ALU.is_gt))
    steps.do(nc.vector.tensor_tensor(equal, others, own, ALU.is_equal))
    steps.do(nc.vector.tensor_tensor(
        equal, equal, earlier[:, 0:experts, 0:experts].unsqueeze(1).broadcast_to(shape), ALU.mult))
    steps.do(nc.vector.tensor_tensor(above, above, equal, ALU.add))
    steps.do(nc.vector.tensor_reduce(count, above, AX.X, ALU.add))
    steps.do(nc.vector.tensor_scalar(mask, count, float(top), None, ALU.is_lt))


def silu_sum(nc, act, gated, banks, ready, count, gate_ready):
    for b in range(NT // 2):
        act.wait_ge(ready, count - 1 if b < 2 else count)
        nc.scalar.activation(gated[:, 2 * b:2 * b + 2, :].rearrange("p t d -> p (t d)"), banks[:, b, :],
                             ACT.Silu).then_inc(gate_ready, 1)


def add_gated(nc, dve, b, x_tok, s, gated, gate_ready, x_ready, stats=None):
    pair = slice(2 * b, 2 * b + 2)
    dve.wait_ge(gate_ready, b + 1)
    nc.vector.tensor_tensor(gated[:, pair, :], gated[:, pair, :], s, ALU.mult).then_inc(x_ready, 1)
    dve.wait_ge(x_ready, 2 * b + 1)
    nc.vector.tensor_tensor(x_tok[:, pair, :], x_tok[:, pair, :], gated[:, pair, :], ALU.add).then_inc(x_ready, 1)
    if stats is not None:
        dve.wait_ge(x_ready, 2 * b + 2)
        for t in range(2 * b, 2 * b + 2):
            nc.vector.bn_stats(stats[:, t, :], x_tok[:, t, :])


def recurrent_layer_stage(nc, w, late_weights, weights, scratch, x_tok, stats, xnT, s_tok, ident, earlier, banks):
    experts, top, width = 8, 2, 128
    jobs = 2 * (experts + 1)
    gate_up, down = weights
    two_pi = 6.283185
    rounder = 1.5 * 2.0 ** 23
    with ExitStack() as ctx:
        m = Core(nc, ctx)
        xh = m.sbuf("xh", [P, 2, N])
        gate_x = m.sbuf("gate_x", [P, N])
        gate_a = m.sbuf("gate_a", [P, N])
        radius = m.sbuf("radius", [P, N])
        radius2 = m.sbuf("radius2", [P, N])
        inside = m.sbuf("inside", [P, N])
        turns = m.sbuf("turns", [P, N])
        phi = m.sbuf("phi", [P, N])
        angle = m.sbuf("angle", [P, 4, N])
        wave = m.sbuf("wave", [P, 4, N])
        zr = m.sbuf("zr", [P, N])
        zi = m.sbuf("zi", [P, N])
        ta = m.sbuf("ta", [P, N])
        tb = m.sbuf("tb", [P, N])
        tc = m.sbuf("tc", [P, N])
        td = m.sbuf("td", [P, N])
        hT = m.sbuf("hT", [P, 2, N])
        coef = m.sbuf("coef", [P, 8])
        logits = m.sbuf("logits0", [P, NT, experts])
        chance = m.sbuf("chance0", [P, NT, experts])
        above = m.sbuf("above0", [P, NT, experts, experts])
        equal = m.sbuf("equal0", [P, NT, experts, experts])
        count = m.sbuf("count0", [P, NT, experts])
        mask = m.sbuf("mask0", [P, NT, experts])
        probs = m.sbuf("probs0", [P, NT, experts])
        probsT = m.sbuf("probsT0", [experts, N])
        gate_up_w = m.sbuf("gate_up_w", [P, 2, KD, 2 * width])
        down_w = m.sbuf("down_w", [P, 2, D])
        prob = m.sbuf("prob_row", [P, 2, N])
        x_in = m.sbuf("expert_x", [P, 2, KD, N])
        silu = m.sbuf("expert_silu", [P, 2, HALF])
        up = m.sbuf("expert_up", [P, 2, HALF])
        ffn_hT = m.sbuf("expert_hT", [P, 2, HALF])
        gated = m.sbuf("gated0", [P, NT, D])
        logits_done = nc.alloc_semaphore("logits_done0")
        logits_ready = nc.alloc_semaphore("logits_ready0")
        router_steps = nc.alloc_semaphore("router_steps0")
        chance_ready = nc.alloc_semaphore("chance_ready0")
        probs_ready = nc.alloc_semaphore("probs_ready0")
        probs_turned = nc.alloc_semaphore("probs_turned0")
        probsT_ready = nc.alloc_semaphore("probsT_ready0")
        probs_stored = nc.alloc_semaphore("probs_stored0")
        gate_up_loaded = [nc.alloc_semaphore(f"gate_up_loaded0_{s}") for s in range(2)]
        down_loaded = [nc.alloc_semaphore(f"down_loaded0_{s}") for s in range(2)]
        prob_loaded = [nc.alloc_semaphore(f"prob_loaded0_{s}") for s in range(2)]
        x_in_ready = nc.alloc_semaphore("expert_x_ready0")
        raised = nc.alloc_semaphore("raised0")
        evacuated = nc.alloc_semaphore("evacuated0")
        ffn_h_ready = nc.alloc_semaphore("expert_h_ready0")
        lowered = nc.alloc_semaphore("lowered0")
        gate_ready = nc.alloc_semaphore("gate_ready0")
        x_ready = nc.alloc_semaphore("x_ready0")
        cols = [slice(h * HALF, (h + 1) * HALF) for h in range(2)]
        xh_done = nc.alloc_semaphore("xh_done")
        xh_ready = nc.alloc_semaphore("xh_ready")
        gates_done = nc.alloc_semaphore("gates_done")
        gate_x_ready = nc.alloc_semaphore("gate_x_ready")
        gate_a_ready = nc.alloc_semaphore("gate_a_ready")
        coef_steps = nc.alloc_semaphore("coef_steps")
        coef_ready = nc.alloc_semaphore("coef_ready")
        radius_ready = nc.alloc_semaphore("radius_ready")
        angles_ready = nc.alloc_semaphore("angles_ready")
        waves_ready = nc.alloc_semaphore("waves_ready")
        square_ready = nc.alloc_semaphore("square_ready")
        modulus_ready = nc.alloc_semaphore("modulus_ready")
        inside_ready = nc.alloc_semaphore("inside_ready")
        rec_steps = nc.alloc_semaphore("rec_steps")
        h_ready = nc.alloc_semaphore("h_ready")
        mixed = nc.alloc_semaphore("mixed0")
        s_ready = nc.alloc_semaphore("s_ready0")
        starts = slice(0, N, SEQ)

        with nc.Block(no_gpsimd_drain=True) as block:

            @block.sync
            def _(sp):
                def load_gate_up(e, s):
                    sp.dma_start(gate_up_w[:, s, :, :],
                                 gate_up[bass.ds(e, 1), :, :].rearrange("e (k p) n -> p (e k) n", p=P)
                                 ).then_inc(gate_up_loaded[s], DMA)

                def load_down(e, s):
                    sp.dma_start(down_w[:, s, :], down[bass.ds(e, 1), :, :].rearrange("e p n -> p (e n)")
                                 ).then_inc(down_loaded[s], DMA)

                def load_prob(e, s):
                    sp.dma_start(prob[:, s, :], scratch[bass.ds(e, 1), :].rearrange("e n -> (e n)")
                                 .partition_broadcast(P)).then_inc(prob_loaded[s], DMA)

                for s in range(2):
                    load_gate_up(s, s)
                    load_down(s, s)
                sp.wait_ge(probsT_ready, 2)
                sp.dma_start(scratch[:, :], probsT[:, :]).then_inc(probs_stored, DMA)
                sp.wait_ge(probs_stored, DMA)
                for s in range(2):
                    load_prob(s, s)
                with sp.Fori(1, experts // 2) as i:
                    for s in range(2):
                        sp.wait_ge(x_in_ready, 4 * i + 2 * s - 2)
                        load_prob(2 * i + s, s)
                        sp.wait_ge(raised, 4 * i + 2 * s)
                        load_gate_up(2 * i + s, s)
                        sp.wait_ge(lowered, 4 * i + 2 * s)
                        load_down(2 * i + s, s)

            @block.tensor
            def _(pe):
                def raise_(half, wide, x, count=None):
                    if count is not None:
                        pe.wait_ge(evacuated, count)
                    for j in range(2):
                        for k in range(KD):
                            last = nc.tensor.matmul(banks[:, 4 + 2 * half + j, :], wide(j, k), x(k)[:, cols[half]],
                                                    start=(k == 0), stop=(k == KD - 1))
                    last.then_inc(raised, 1)

                def lower(half, wt, count, first=False):
                    pe.wait_ge(ffn_h_ready, count)
                    for t in range(4):
                        last = nc.tensor.matmul(
                            banks[:, 2 * half + t // 2, (t % 2) * D:(t % 2 + 1) * D], ffn_hT[:, half, t * P:(t + 1) * P], wt,
                            start=first and t % 2 == 0, stop=False, skip_group_check=True)
                    last.then_inc(lowered, 1)

                def expert(i, s, first=False):
                    pe.wait_ge(gate_up_loaded[s], DMA * (i + 1))
                    for half in range(2):
                        job = 4 * i + 2 * s + half
                        pe.wait_ge(x_in_ready, job + 1)
                        raise_(half, lambda j, k: gate_up_w[:, s, k, j * width:(j + 1) * width],
                               lambda k: x_in[:, s, k, :], 2 * job + 2)
                        if first and s == 0:
                            lower(half, w["shared_down_w"][:, 0, :], job + 1, True)
                        else:
                            if half == 0:
                                pe.wait_ge(down_loaded[1 - s], DMA * (i + s))
                            lower(half, down_w[:, 1 - s, :], job + 1)

                for t in range(NT):
                    for k in range(KD):
                        last = nc.tensor.matmul(banks[:, 4, t * experts:(t + 1) * experts],
                                                xnT[:, k, t * P:(t + 1) * P], w["router_w"][:, k, :],
                                                start=(k == 0), stop=(k == KD - 1))
                last.then_inc(logits_done, 1)
                pe.wait_ge(*late_weights)
                for part in range(2):
                    for half in range(2):
                        for k in range(KD):
                            last = nc.tensor.matmul(
                                banks[:, 2 * part + half, :], w["W_in"][:, k, part * P:(part + 1) * P],
                                xnT[:, k, half * HALF:(half + 1) * HALF], start=(k == 0), stop=(k == KD - 1))
                        last.then_inc(xh_done, 1)
                pe.wait_ge(xh_ready, 4)
                pe.wait_ge(logits_ready, 1)
                for gate, name in enumerate(("W_ga", "W_gx")):
                    for half in range(2):
                        for k in range(KD):
                            last = nc.tensor.matmul(
                                banks[:, 4 + 2 * gate + half, :], w[name][:, k, :],
                                xh[:, k, half * HALF:(half + 1) * HALF], start=(k == 0), stop=(k == KD - 1))
                        last.then_inc(gates_done, 1)
                pe.wait_ge(probs_ready, 1)
                for t in range(NT):
                    last = nc.tensor.transpose(banks[0:experts, t // 4, (t % 4) * P:(t % 4 + 1) * P],
                                               probs[:, t, :], ident[:, :])
                last.then_inc(probs_turned, 1)
                for half, ready in enumerate((gate_a_ready, gate_x_ready)):
                    pe.wait_ge(ready, 2)
                    raise_(half, lambda j, k: w[("shared_gate_w", "shared_up_w")[j]][:, k, :], lambda k: xnT[:, k, :])
                pe.wait_ge(probsT_ready, 2)
                expert(0, 0, first=True)
                expert(0, 1, first=True)
                with pe.Fori(1, experts // 2) as i:
                    expert(i, 0)
                    expert(i, 1)
                pe.wait_ge(down_loaded[1], DMA * (experts // 2))
                for half in range(2):
                    lower(half, down_w[:, 1, :], jobs - 1 + half)
                pe.wait_ge(evacuated, 2 * jobs)
                pe.wait_ge(h_ready, 2)
                for t in range(NT):
                    for k in range(KD):
                        last = nc.tensor.matmul(
                            banks[:, 4 + t // 2, (t % 2) * D:(t % 2 + 1) * D], hT[:, k, t * P:(t + 1) * P],
                            w["W_out"][:, k, :], start=(k == 0), stop=(k == KD - 1))
                    last.then_inc(mixed, 1)

            @block.scalar
            def _(act):
                def evacuate(job, half, count=None):
                    act.wait_ge(raised, job + 1)
                    if count is not None:
                        act.wait_ge(ffn_h_ready, count)
                    nc.scalar.activation(silu[:, half, :], banks[:, 4 + 2 * half, :], ACT.Silu).then_inc(evacuated, 1)
                    nc.scalar.activation(up[:, half, :], banks[:, 5 + 2 * half, :], ACT.Identity).then_inc(evacuated, 1)

                def expert(e):
                    for half in range(2):
                        evacuate(2 * e + 2 + half, half, 2 * e + 1 + half)

                def root(q):
                    act.wait_ge(square_ready, q + 1)
                    nc.scalar.activation(tc[:, :], ta[:, :], ACT.Sqrt).then_inc(modulus_ready, 1)

                steps = Steps(act, coef_steps)
                steps.do(nc.scalar.activation(coef[:, 0:1], w["a_real"][:, :], ACT.Abs))
                steps.do(nc.scalar.activation(coef[:, 1:2], coef[:, 0:1], ACT.Exp, scale=-1.0))
                nc.scalar.activation(coef[:, 2:3], coef[:, 1:2], ACT.Ln, bias=1.0).then_inc(coef_ready, 1)
                act.wait_ge(logits_ready, 1)
                nc.scalar.activation(chance[:, :, :], logits[:, :, :], ACT.Sigmoid).then_inc(chance_ready, 1)
                for part in range(2):
                    for half in range(2):
                        act.wait_ge(xh_done, 2 * part + half + 1)
                        nc.scalar.activation(
                            xh[:, part, half * HALF:(half + 1) * HALF], banks[:, 2 * part + half, :],
                            ACT.Identity, bias=w["b_in"][:, part:part + 1]).then_inc(xh_ready, 1)
                for gate, (dst, bias, ready) in enumerate(
                        ((gate_a, "b_ga", gate_a_ready), (gate_x, "b_gx", gate_x_ready))):
                    for half in range(2):
                        act.wait_ge(gates_done, 2 * gate + half + 1)
                        nc.scalar.activation(dst[:, half * HALF:(half + 1) * HALF],
                                             banks[:, 4 + 2 * gate + half, :], ACT.Sigmoid,
                                             bias=w[bias][:, 0:1]).then_inc(ready, 1)
                act.wait_ge(probs_turned, 1)
                for half in range(2):
                    nc.scalar.activation(probsT[:, cols[half]], banks[0:experts, half, :], ACT.Identity
                                         ).then_inc(probsT_ready, 1)
                act.wait_ge(coef_ready, 2)
                act.wait_ge(gate_a_ready, 2)
                nc.scalar.activation(radius[:, :], gate_a[:, :], ACT.Exp, scale=coef[:, 4:5]).then_inc(radius_ready, 1)
                nc.scalar.activation(radius2[:, :], gate_a[:, :], ACT.Exp, scale=coef[:, 5:6]).then_inc(radius_ready, 1)
                for half in range(2):
                    evacuate(half, half)
                for q in range(4):
                    act.wait_ge(angles_ready, q + 1)
                    nc.scalar.activation(wave[:, q, :], angle[:, q, :], ACT.Sin, scale=two_pi).then_inc(waves_ready, 1)
                for e in range(2):
                    expert(e)
                    root(e)
                with act.Fori(2, experts) as e:
                    expert(e)
                silu_sum(nc, act, gated, banks, lowered, jobs, gate_ready)

            @block.gpsimd
            def _(pool):
                nc.gpsimd.memset(inside[:, :], 1.0).then_inc(inside_ready, 1)
                pool.wait_ge(inside_ready, 1)
                nc.gpsimd.memset(inside[:, starts], 0.0).then_inc(inside_ready, 1)

                def weigh(i, s, first=False):
                    pool.wait_ge(prob_loaded[s], DMA * (i + 1))
                    for half in range(2):
                        if not first:
                            pool.wait_ge(raised, 4 * i + 2 * s + half - 1)
                        nc.gpsimd.tensor_tensor(
                            x_in[:, s, :, cols[half]], xnT[:, :, cols[half]],
                            prob[:, s, cols[half]].unsqueeze(1).broadcast_to([P, KD, HALF]), ALU.mult
                            ).then_inc(x_in_ready, 1)

                def hidden(job, half, count=None):
                    pool.wait_ge(evacuated, 2 * job + 2)
                    if count is not None:
                        pool.wait_ge(lowered, count)
                    nc.gpsimd.tensor_tensor(ffn_hT[:, half, :], silu[:, half, :], up[:, half, :], ALU.mult
                                            ).then_inc(ffn_h_ready, 1)

                def expert(i, s):
                    for half in range(2):
                        job = 4 * i + 2 * s + 2 + half
                        hidden(job, half, job - 1)

                for half in range(2):
                    hidden(half, half)
                for s in range(2):
                    weigh(0, s, True)
                with pool.Fori(0, experts // 2 - 1) as i:
                    for s in range(2):
                        expert(i, s)
                        weigh(i + 1, s)
                for s in range(2):
                    expert(experts // 2 - 1, s)

            @block.vector
            def _(dve):
                steps = Steps(dve, rec_steps)

                def both(dst, a, op, b):
                    steps.add(nc.vector.tensor_tensor(dst, a, b, op))

                router = Steps(dve, router_steps)
                dve.wait_ge(logits_done, 1)
                nc.vector.tensor_copy(logits[:, :, :].rearrange("p t e -> p (t e)"), banks[:, 4, 0:NT * experts]
                                      ).then_inc(logits_ready, 1)
                dve.wait_ge(logits_ready, 1)
                rank_mask(nc, router, mask[:, :, :], logits[:, :, :],
                          (above[:, :, :, :], equal[:, :, :, :], count[:, :, :]), earlier, experts, top)
                dve.wait_ge(chance_ready, 1)
                nc.vector.tensor_tensor(probs[:, :, :], mask[:, :, :], chance[:, :, :], ALU.mult
                                        ).then_inc(probs_ready, 1)
                dve.wait_ge(coef_ready, 1)
                steps.do(nc.vector.tensor_scalar(coef[:, 3:4], w["a_real"][:, :], 0.0, None, ALU.max))
                steps.do(nc.vector.tensor_tensor(coef[:, 6:7], coef[:, 2:3], coef[:, 3:4], ALU.add))
                steps.do(nc.vector.tensor_scalar(coef[:, 4:5], coef[:, 6:7], -8.0, None, ALU.mult))
                steps.do(nc.vector.tensor_scalar(coef[:, 5:6], coef[:, 6:7], -16.0, None, ALU.mult))
                nc.vector.tensor_scalar(coef[:, 7:8], w["a_imag"][:, :], 1.0 / (2.0 * np.pi), None,
                                        ALU.mult).then_inc(coef_ready, 1)
                dve.wait_ge(coef_ready, 2)
                dve.wait_ge(gate_a_ready, 2)
                steps.do(nc.vector.tensor_scalar(turns[:, :], gate_a[:, :], coef[:, 7:8], None, ALU.mult))
                dve.wait_ge(inside_ready, 2)
                steps.add(nc.vector.tensor_tensor_scan(phi[:, :], inside[:, :], turns[:, :], 0.0, ALU.mult, ALU.add))
                steps.do(nc.vector.tensor_scalar(ta[:, :], turns[:, :], 2.0, 0.25, ALU.mult, ALU.add))
                for q in range(4):
                    if q == 1:
                        steps.do(nc.vector.tensor_scalar(ta[:, :], turns[:, :], 2.0, None, ALU.mult))
                    if q == 2:
                        steps.do(nc.vector.tensor_scalar(ta[:, :], phi[:, :], 0.25, None, ALU.add))
                    cur = phi if q == 3 else ta
                    steps.do(nc.vector.tensor_scalar(tb[:, :], cur[:, :], rounder, rounder, ALU.add, ALU.subtract))
                    nc.vector.tensor_tensor(angle[:, q, :], cur[:, :], tb[:, :], ALU.subtract).then_inc(angles_ready, 1)
                    dve.wait_ge(angles_ready, q + 1)
                dve.wait_ge(waves_ready, 2)
                dve.wait_ge(radius_ready, 2)
                both(ta[:, :], radius2[:, :], ALU.mult, wave[:, 0, :])
                both(tb[:, :], radius2[:, :], ALU.mult, wave[:, 1, :])
                steps.add(nc.vector.memset(radius[:, starts], 0.0))
                steps.join()
                steps.add(nc.vector.tensor_scalar(zr[:, :], ta[:, :], -1.0, 1.0, ALU.mult, ALU.add))
                steps.add(nc.vector.tensor_scalar(zi[:, :], tb[:, :], -1.0, None, ALU.mult))
                steps.join()
                both(ta[:, :], zr[:, :], ALU.mult, zr[:, :])
                both(tb[:, :], zi[:, :], ALU.mult, zi[:, :])
                steps.join()
                nc.vector.tensor_tensor(ta[:, :], ta[:, :], tb[:, :], ALU.add).then_inc(square_ready, 1)
                dve.wait_ge(modulus_ready, 1)
                steps.do(nc.vector.tensor_tensor(tb[:, :], tc[:, :], zr[:, :], ALU.add))
                nc.vector.tensor_scalar(ta[:, :], tb[:, :], 0.5, 1e-30, ALU.mult, ALU.max).then_inc(square_ready, 1)
                dve.wait_ge(modulus_ready, 2)
                steps.do(nc.vector.reciprocal(tb[:, :], tc[:, :]))
                steps.do(nc.vector.scalar_tensor_tensor(td[:, :], zi[:, :], 0.5, tb[:, :], ALU.mult, ALU.mult))
                dve.wait_ge(gate_x_ready, 2)
                both(tc[:, :], tc[:, :], ALU.mult, gate_x[:, :])
                both(td[:, :], td[:, :], ALU.mult, gate_x[:, :])
                steps.join()
                both(ta[:, :], tc[:, :], ALU.mult, xh[:, 0, :])
                both(tb[:, :], td[:, :], ALU.mult, xh[:, 1, :])
                both(radius2[:, :], tc[:, :], ALU.mult, xh[:, 1, :])
                both(turns[:, :], td[:, :], ALU.mult, xh[:, 0, :])
                steps.join()
                both(zr[:, :], ta[:, :], ALU.subtract, tb[:, :])
                both(zi[:, :], radius2[:, :], ALU.add, turns[:, :])
                steps.join()
                dve.wait_ge(waves_ready, 4)
                cos, sin = wave[:, 2, :], wave[:, 3, :]
                both(ta[:, :], zr[:, :], ALU.mult, cos)
                both(tb[:, :], zi[:, :], ALU.mult, sin)
                both(tc[:, :], zi[:, :], ALU.mult, cos)
                both(td[:, :], zr[:, :], ALU.mult, sin)
                steps.join()
                both(ta[:, :], ta[:, :], ALU.add, tb[:, :])
                both(tc[:, :], tc[:, :], ALU.subtract, td[:, :])
                steps.join()
                steps.add(nc.vector.tensor_tensor_scan(zr[:, :], radius[:, :], ta[:, :], 0.0, ALU.mult, ALU.add))
                steps.add(nc.vector.tensor_tensor_scan(zi[:, :], radius[:, :], tc[:, :], 0.0, ALU.mult, ALU.add))
                steps.join()
                both(ta[:, :], zr[:, :], ALU.mult, cos)
                both(tb[:, :], zi[:, :], ALU.mult, sin)
                both(tc[:, :], zr[:, :], ALU.mult, sin)
                both(td[:, :], zi[:, :], ALU.mult, cos)
                steps.join()
                nc.vector.tensor_tensor(hT[:, 0, :], ta[:, :], tb[:, :], ALU.subtract).then_inc(h_ready, 1)
                nc.vector.tensor_tensor(hT[:, 1, :], tc[:, :], td[:, :], ALU.add).then_inc(h_ready, 1)
                for b in range(NT // 2):
                    dve.wait_ge(mixed, 2 * b + 2)
                    nc.vector.tensor_tensor(
                        s_tok[:, 2 * b:2 * b + 2, :], banks[:, 4 + b, :].rearrange("p (t d) -> p t d", t=2),
                        w["b_out"][:, :].unsqueeze(1).broadcast_to([P, 2, D]), ALU.add).then_inc(s_ready, 1)
                    dve.wait_ge(s_ready, b + 1)
                    add_gated(nc, dve, b, x_tok, s_tok[:, 2 * b:2 * b + 2, :], gated, gate_ready, x_ready, stats)




STATES = 16
INNER = 512
MI = INNER // P


def scan_prepare_stage(nc, w, late_weights, xnT, ident, banks, keep, rows, y):
    taps, experts = 4, 8
    skip, xs, delta, dx, A, diag = keep
    with ExitStack() as ctx:
        m = Core(nc, ctx)
        x1T = m.sbuf("x1T", [P, KD, N])
        padded = m.sbuf("conv_in", [P, MI, BATCH, SEQ + taps - 1])
        low = m.sbuf("delta_low", [P, N])
        soft = m.sbuf("softplus_tail", [P, MI, N])
        bc = m.sbuf("bc_rows", [2 * STATES, N])
        logits = m.sbuf("logits1", [P, NT, experts])
        best = m.sbuf("best1", [P, NT, 8])
        factor = m.sbuf("factor1", [P, NT])
        logits_done = nc.alloc_semaphore("logits_done1")
        expert_steps = nc.alloc_semaphore("expert_steps1")
        expert_done = nc.alloc_semaphore("expert_done1")
        first_steps = nc.alloc_semaphore("first_steps1")
        products = nc.alloc_semaphore("products1")
        emptied = nc.alloc_semaphore("emptied1")
        pad_ready = nc.alloc_semaphore("pad_ready1")
        conv_steps = nc.alloc_semaphore("conv_steps1")
        conv_ready = nc.alloc_semaphore("conv_ready1")
        xs_ready = nc.alloc_semaphore("xs_ready1")
        soft_steps = nc.alloc_semaphore("soft_steps1")
        magnitude_ready = nc.alloc_semaphore("magnitude_ready1")
        soft_ready = nc.alloc_semaphore("soft_ready1")
        a_ready = nc.alloc_semaphore("a_ready1")
        delta_ready = nc.alloc_semaphore("delta_ready1")
        rows_stored = nc.alloc_semaphore("rows_stored1")
        cols = [slice(h * HALF, (h + 1) * HALF) for h in range(2)]
        turn0, in0, skip0 = 0, 4, 12
        low0, bc0, up0 = 20, 22, 24

        with nc.Block(no_gpsimd_drain=True) as block:

            @block.sync
            def _(sp):
                sp.wait_ge(emptied, bc0 + 2)
                sp.dma_start(rows, bc[:, :]).then_inc(rows_stored, DMA)
                sp.wait_ge(rows_stored, DMA)

            @block.gpsimd
            def _(pool):
                nc.gpsimd.memset(padded[:, :, :, 0:taps - 1], 0.0).then_inc(pad_ready, 1)

            @block.tensor
            def _(pe):
                def group(g, rows_, pairs):
                    if g >= 8:
                        pe.wait_ge(emptied, g - 7)
                    for k, (wt, act_in) in enumerate(pairs):
                        last = nc.tensor.matmul(banks[0:rows_, g % 8, :], wt, act_in, start=(k == 0),
                                                stop=(k == len(pairs) - 1))
                    last.then_inc(products, 1)

                for half in range(2):
                    for k in range(KD):
                        for t in range(4):
                            last = nc.tensor.transpose(banks[:, turn0 + 2 * half + k, t * P:(t + 1) * P],
                                                       y[:, 4 * half + t, k * P:(k + 1) * P], ident[:, :])
                        last.then_inc(products, 1)
                pe.wait_ge(emptied, turn0 + 2 * KD)
                pe.wait_ge(*late_weights)
                for base, name in ((in0, "W_in"), (skip0, "W_skip")):
                    for mi in range(MI):
                        for half in range(2):
                            group(base + 2 * mi + half, P,
                                  [(w[name][:, k, mi * P:(mi + 1) * P], x1T[:, k, cols[half]]) for k in range(KD)])
                pe.wait_ge(xs_ready, MI)
                for half in range(2):
                    group(low0 + half, P, [(w["W_d1"][:, k, :], xs[:, k, cols[half]]) for k in range(MI)])
                for half in range(2):
                    group(bc0 + half, 2 * STATES, [(w["W_BC"][:, k, :], xs[:, k, cols[half]]) for k in range(MI)])
                for mi in range(MI):
                    for half in range(2):
                        pe.wait_ge(emptied, low0 + half + 1)
                        group(up0 + 2 * mi + half, P, [(w["W_d2"][:, 0, mi * P:(mi + 1) * P], low[:, cols[half]])])
                pe.wait_ge(emptied, up0 + 2 * MI)
                for t in range(NT):
                    for k in range(KD):
                        last = nc.tensor.matmul(banks[:, 0, t * experts:(t + 1) * experts],
                                                xnT[:, k, t * P:(t + 1) * P], w["gate_w"][:, k, :],
                                                start=(k == 0), stop=(k == KD - 1))
                last.then_inc(logits_done, 1)
                for t in range(NT):
                    for k in range(KD):
                        last = nc.tensor.matmul(banks[:, 4 + t // 2, (t % 2) * D:(t % 2 + 1) * D],
                                                xnT[:, k, t * P:(t + 1) * P], w["expert_weight"][:, k, :],
                                                start=(k == 0), stop=(k == KD - 1))
                    if t % 2:
                        last.then_inc(expert_done, 1)

            @block.scalar
            def _(act):
                def empty(g, dst, rows_=P, func=ACT.Identity, **kw):
                    act.wait_ge(products, g + 1)
                    nc.scalar.activation(dst, banks[0:rows_, g % 8, :], func, **kw).then_inc(emptied, 1)

                nc.scalar.activation(A[:, :, :], w["A_log"][:, :, :], ACT.Exp).then_inc(a_ready, 1)
                for half in range(2):
                    for k in range(KD):
                        empty(turn0 + 2 * half + k, x1T[:, k, cols[half]], scale=w["norm_w"][:, k:k + 1])
                act.wait_ge(pad_ready, 1)
                for mi in range(MI):
                    for half in range(2):
                        act.wait_ge(products, in0 + 2 * mi + half + 1)
                        nc.scalar.activation(
                            padded[:, mi, 2 * half:2 * half + 2, taps - 1:],
                            banks[:, (in0 + 2 * mi + half) % 8, :].rearrange("p (b t) -> p b t", b=2),
                            ACT.Identity).then_inc(emptied, 1)
                for mi in range(MI):
                    for half in range(2):
                        empty(skip0 + 2 * mi + half, skip[:, mi, cols[half]], func=ACT.Silu)
                for mi in range(MI):
                    act.wait_ge(conv_ready, mi + 1)
                    nc.scalar.activation(xs[:, mi, :], xs[:, mi, :], ACT.Silu).then_inc(xs_ready, 1)
                for half in range(2):
                    empty(low0 + half, low[:, cols[half]])
                for half in range(2):
                    empty(bc0 + half, bc[:, cols[half]], rows_=2 * STATES)
                for mi in range(MI):
                    for half in range(2):
                        empty(up0 + 2 * mi + half, delta[:, mi, cols[half]], bias=w["b_d2"][:, mi:mi + 1])
                steps = Steps(act, soft_steps)
                for mi in range(MI):
                    act.wait_ge(magnitude_ready, mi + 1)
                    steps.add(nc.scalar.activation(soft[:, mi, :], soft[:, mi, :], ACT.Exp, scale=-1.0))
                steps.join()
                for mi in range(MI):
                    nc.scalar.activation(soft[:, mi, :], soft[:, mi, :], ACT.Ln, bias=1.0).then_inc(soft_ready, 1)

            @block.vector
            def _(dve):
                steps = Steps(dve, first_steps)
                dve.wait_ge(a_ready, 1)
                steps.add(nc.vector.tensor_scalar(A[:, :, :], A[:, :, :], -1.0, None, ALU.mult))
                for mi in range(MI):
                    steps.add(nc.vector.tensor_scalar(diag[:, mi, :], ident[:, :], w["W_D"][:, mi:mi + 1], None, ALU.mult))
                conv = Steps(dve, conv_steps)
                for mi in range(MI):
                    dve.wait_ge(emptied, in0 + 2 * mi + 2)
                    out = xs[:, mi, :].rearrange("p (b t) -> p b t", b=BATCH)
                    conv.do(nc.vector.tensor_scalar(
                        out, padded[:, mi, :, taps - 1:], w["conv_w"][:, mi, taps - 1:taps], w["conv_b"][:, mi:mi + 1],
                        ALU.mult, ALU.add))
                    for j in range(taps - 2, -1, -1):
                        ins = nc.vector.scalar_tensor_tensor(
                            out, padded[:, mi, :, j:j + SEQ], w["conv_w"][:, mi, j:j + 1], out, ALU.mult, ALU.add)
                        if j:
                            conv.do(ins)
                        else:
                            ins.then_inc(conv_ready, 1)
                for mi in range(MI):
                    dve.wait_ge(emptied, up0 + 2 * mi + 2)
                    nc.vector.scalar_tensor_tensor(soft[:, mi, :], delta[:, mi, :], -1.0, delta[:, mi, :],
                                                   ALU.mult, ALU.max).then_inc(magnitude_ready, 1)
                best_steps = Steps(dve, expert_steps)
                dve.wait_ge(logits_done, 1)
                best_steps.do(nc.vector.tensor_copy(logits[:, :, :].rearrange("p t e -> p (t e)"),
                                                    banks[:, 0, 0:NT * experts]))
                for t in range(NT):
                    best_steps.add(nc.vector.max(best[:, t, :], logits[:, t, :]))
                best_steps.join()
                best_steps.do(nc.vector.tensor_tensor(factor[:, :], best[:, :, 0], best[:, :, 1], ALU.add))
                for t in range(NT):
                    dve.wait_ge(expert_done, t // 2 + 1)
                    nc.vector.tensor_scalar(y[:, t, :], banks[:, 4 + t // 2, (t % 2) * D:(t % 2 + 1) * D],
                                            factor[:, t:t + 1], None, ALU.mult)
                for mi in range(MI):
                    dve.wait_ge(soft_ready, mi + 1)
                    nc.vector.scalar_tensor_tensor(delta[:, mi, :], delta[:, mi, :], 0.0, soft[:, mi, :],
                                                   ALU.max, ALU.add).then_inc(delta_ready, 1)
                    dve.wait_ge(delta_ready, mi + 1)
                    nc.vector.tensor_tensor(dx[:, mi, :], delta[:, mi, :], xs[:, mi, :], ALU.mult)


def scan_stage(nc, w, up_w, down_w, x_tok, x_stats, xn_tok, xnT, s_tok, ident, banks, keep, rows, y):
    hidden = up_w.shape[1]
    skip, xs, delta, dx, A, diag = keep
    passes = 2
    turn, tiles = 4, 2
    rounds = STATES // turn
    pass_steps = STATES * MI
    round_steps = turn * MI
    tile_steps = round_steps // tiles
    pass_tiles = hidden // P
    assert pass_tiles == rounds * tiles
    with ExitStack() as ctx:
        m = Core(nc, ctx)
        b_row = m.sbuf("b_row", [P, turn, HALF])
        c_row = m.sbuf("c_row", [P, turn, HALF])
        decay = m.sbuf("decay", [P, MI, BATCH // 2, SEQ])
        drive = m.sbuf("drive", [P, MI, HALF])
        state = m.sbuf("state", [P, MI, HALF])
        seen = m.sbuf("seen", [P, MI, HALF])
        up = m.sbuf("up_w1", [P, 2, KD, P])
        down = m.sbuf("down_w1", [P, 2, D])
        hT = m.sbuf("hidden_T1", [P, 2, HALF])
        zeros = m.sbuf("zeros1", [P, BANK])
        stats = m.sbuf("y_stats", [P, NT, 6])
        mean_var = m.sbuf("y_mean_var", [P, NT, 2])
        var = m.sbuf("y_var", [P, NT])
        std = m.sbuf("y_std", [P, NT])
        rstd = m.sbuf("y_rstd", [P, NT])
        offset = m.sbuf("y_offset", [P, NT])
        loaded = [nc.alloc_semaphore(f"bc_loaded{q}") for q in range(turn)]
        decay_ready = nc.alloc_semaphore("decay_ready")
        drive_ready = nc.alloc_semaphore("drive_ready")
        scanned = nc.alloc_semaphore("scanned")
        seen_ready = nc.alloc_semaphore("seen_ready")
        summed = nc.alloc_semaphore("summed")
        gated_ready = nc.alloc_semaphore("gated_ready1")
        mixed = nc.alloc_semaphore("mixed1")
        s_ready = nc.alloc_semaphore("s_ready1")
        ffn_loaded = [nc.alloc_semaphore(f"ffn_loaded1_{s}") for s in range(2)]
        zeros_ready = nc.alloc_semaphore("zeros_ready1")
        up_done = nc.alloc_semaphore("up_done1")
        relu_ready = nc.alloc_semaphore("relu_ready1")
        h_ready = nc.alloc_semaphore("h_ready1")
        down_done = nc.alloc_semaphore("down_done1")
        y_ready = nc.alloc_semaphore("y_ready1")
        y_steps = nc.alloc_semaphore("y_steps1")
        var_ready = nc.alloc_semaphore("y_var_ready1")
        std_ready = nc.alloc_semaphore("y_std_ready1")
        offset_ready = nc.alloc_semaphore("y_offset_ready1")
        norm_ready = nc.alloc_semaphore("y_norm_ready1")
        gamma_ready = nc.alloc_semaphore("y_gamma_ready1")
        beta_ready = nc.alloc_semaphore("y_beta_ready1")
        gate_ready = nc.alloc_semaphore("gate_ready1")
        x_ready = nc.alloc_semaphore("x_ready1")
        cols = [slice(h * HALF, (h + 1) * HALF) for h in range(2)]

        with nc.Block(no_gpsimd_drain=True) as block:

            @block.sync
            def _(sp):
                def load_rows(p, n, q):
                    for dst, first in ((b_row, 0), (c_row, STATES)):
                        sp.dma_start(dst[:, q, :], rows[bass.ds(n + first, 1), cols[p]].rearrange("n t -> (n t)")
                                     .partition_broadcast(P)).then_inc(loaded[q], DMA)

                def load_weights(n, s):
                    sp.dma_start(up[:, s, :, :], up_w.rearrange("(k p) (n c) -> p n k c", p=P, c=P)
                                 [:, bass.ds(n, 1), :, :].rearrange("p n k c -> p (n k) c")).then_inc(ffn_loaded[s], DMA)
                    sp.dma_start(down[:, s, :], down_w.rearrange("(n p) d -> n p d", p=P)[bass.ds(n, 1), :, :]
                                 .rearrange("n p d -> p (n d)")).then_inc(ffn_loaded[s], DMA)

                def refill(p, i, wrap=False):
                    for q in range(turn):
                        done = pass_steps * p + round_steps * i + MI * (q + 1)
                        sp.wait_ge(drive_ready, done)
                        sp.wait_ge(seen_ready, done)
                        load_rows(p + 1 if wrap else p, q if wrap else turn * (i + 1) + q, q)
                        if q % 2:
                            s = q // 2
                            sp.wait_ge(down_done, pass_tiles * p + tiles * i + s + 1)
                            load_weights(s if wrap else tiles * (i + 1) + s, s)

                for q in range(turn):
                    load_rows(0, q, q)
                    if q % 2:
                        load_weights(q // 2, q // 2)
                for p in range(passes):
                    with sp.Fori(0, rounds - 1) as i:
                        refill(p, i)
                    if p + 1 < passes:
                        refill(p, rounds - 1, wrap=True)

            @block.scalar
            def _(act):
                for p in range(passes):
                    with act.Fori(0, rounds) as i:
                        for e in range(round_steps):
                            mi = e % MI
                            act.wait_ge(scanned, pass_steps * p + round_steps * i + e + 1)
                            nc.scalar.activation(
                                decay[:, mi, :, 1:],
                                delta[:, mi, cols[p]].rearrange("p (b t) -> p b t", b=BATCH // 2)[:, :, 1:], ACT.Exp,
                                scale=A[:, mi, bass.ds(turn * i + e // MI, 1)]).then_inc(decay_ready, 1)
                            if e % tile_steps == tile_steps - 1:
                                s = e // tile_steps
                                act.wait_ge(up_done, pass_tiles * p + tiles * i + s + 1)
                                nc.scalar.activation(hT[:, s, :], banks[:, 6 + s, :], ACT.Relu).then_inc(relu_ready, 1)
                act.wait_ge(var_ready, 1)
                nc.scalar.activation(std[:, :], var[:, :], ACT.Sqrt).then_inc(std_ready, 1)
                act.wait_ge(offset_ready, 1)
                for t in range(NT):
                    nc.scalar.activation(y[:, t, :], y[:, t, :], ACT.Identity, bias=offset[:, t:t + 1],
                                         scale=rstd[:, t:t + 1]).then_inc(norm_ready, 1)
                for b in range(NT // 2):
                    act.wait_ge(beta_ready, b + 1)
                    nc.scalar.activation(y[:, 2 * b:2 * b + 2, :], y[:, 2 * b:2 * b + 2, :], ACT.Silu
                                         ).then_inc(gate_ready, 1)

            @block.gpsimd
            def _(pool):
                nc.gpsimd.memset(zeros[:, :], 0.0).then_inc(zeros_ready, 1)
                for p in range(passes):
                    with pool.Fori(0, rounds) as i:
                        for e in range(round_steps):
                            q, mi = e // MI, e % MI
                            if mi == 0:
                                pool.wait_ge(loaded[q], 2 * DMA * (rounds * p + i + 1))
                            pool.wait_ge(scanned, pass_steps * p + round_steps * i + e + 1)
                            nc.gpsimd.tensor_tensor(drive[:, mi, :], dx[:, mi, cols[p]], b_row[:, q, :], ALU.mult
                                                    ).then_inc(drive_ready, 1)
                for b in range(NT // 2):
                    two = slice(2 * b, 2 * b + 2)
                    pool.wait_ge(gamma_ready, b + 1)
                    nc.gpsimd.tensor_tensor(y[:, two, :], y[:, two, :],
                                            w["ln_beta"][:, :].unsqueeze(1).broadcast_to([P, 2, D]), ALU.add
                                            ).then_inc(beta_ready, 1)

            @block.vector
            def _(dve):
                def scan(p, i, e):
                    count = pass_steps * p + round_steps * i + e + 1
                    dve.wait_ge(decay_ready, count)
                    dve.wait_ge(drive_ready, count)
                    if e >= MI:
                        dve.wait_ge(seen_ready, count - MI)
                    nc.vector.tensor_tensor_scan(
                        state[:, e % MI, :], decay[:, e % MI, :, :].rearrange("p b t -> p (b t)"),
                        drive[:, e % MI, :], 0.0, ALU.mult, ALU.add).then_inc(scanned, 1)

                def see(p, i, e):
                    q = e // MI
                    count = pass_steps * p + round_steps * i + e + 1
                    if e % MI == 0:
                        dve.wait_ge(loaded[q], 2 * DMA * (rounds * p + i + 1))
                    dve.wait_ge(scanned, count + MI)
                    dve.wait_ge(summed, count)
                    nc.vector.tensor_tensor(seen[:, e % MI, :], state[:, e % MI, :], c_row[:, q, :], ALU.mult
                                            ).then_inc(seen_ready, 1)

                def square(p, i, s):
                    dve.wait_ge(relu_ready, pass_tiles * p + tiles * i + s + 1)
                    nc.vector.tensor_tensor(hT[:, s, :], hT[:, s, :], hT[:, s, :], ALU.mult).then_inc(h_ready, 1)

                for mi in range(MI):
                    nc.vector.memset(decay[:, mi, :, 0:1], 0.0).then_inc(scanned, 1)
                for p in range(passes):
                    with dve.Fori(0, rounds) as i:
                        scan(p, i, 0)
                        for e in range(round_steps):
                            if e + 1 < round_steps:
                                scan(p, i, e + 1)
                            see(p, i, e)
                            if e % tile_steps == tile_steps - 2:
                                square(p, i, e // tile_steps)
                        dve.wait_ge(seen_ready, pass_steps * p + round_steps * (i + 1))
                    dve.wait_ge(summed, pass_steps * (p + 1) + MI)
                    for mi in range(MI):
                        nc.vector.tensor_tensor(dx[:, mi, cols[p]], banks[:, mi, :], skip[:, mi, cols[p]], ALU.mult
                                                ).then_inc(gated_ready, 1)
                    dve.wait_ge(down_done, pass_tiles * (p + 1))
                    for b in range(2):
                        two = slice(4 * p + 2 * b, 4 * p + 2 * b + 2)
                        nc.vector.tensor_tensor(y[:, two, :], y[:, two, :],
                                                banks[:, 4 + b, :].rearrange("p (t d) -> p t d", t=2), ALU.add
                                                ).then_inc(y_ready, 1)
                steps = Steps(dve, y_steps)
                dve.wait_ge(y_ready, 2 * passes)
                for t in range(NT):
                    steps.add(nc.vector.bn_stats(stats[:, t, :], y[:, t, :]))
                steps.join()
                for t in range(NT):
                    steps.add(nc.vector.bn_aggr(mean_var[:, t, :], stats[:, t, :]))
                steps.join()
                nc.vector.tensor_scalar(var[:, :], mean_var[:, :, 1], EPS, None, ALU.add).then_inc(var_ready, 1)
                dve.wait_ge(std_ready, 1)
                steps.do(nc.vector.reciprocal(rstd[:, :], std[:, :]))
                nc.vector.scalar_tensor_tensor(offset[:, :], mean_var[:, :, 0], -1.0, rstd[:, :], ALU.mult, ALU.mult
                                               ).then_inc(offset_ready, 1)

                def gamma(b):
                    two = slice(2 * b, 2 * b + 2)
                    dve.wait_ge(norm_ready, 2 * b + 2)
                    nc.vector.tensor_tensor(y[:, two, :], y[:, two, :],
                                            w["ln_gamma"][:, :].unsqueeze(1).broadcast_to([P, 2, D]), ALU.mult
                                            ).then_inc(gamma_ready, 1)

                def mix(b):
                    two = slice(2 * b, 2 * b + 2)
                    dve.wait_ge(mixed, b + 1)
                    nc.vector.tensor_tensor(s_tok[:, two, :], banks[:, b, :].rearrange("p (t d) -> p t d", t=2),
                                            xn_tok[:, two, :], ALU.add).then_inc(s_ready, 1)

                def finish(b):
                    dve.wait_ge(s_ready, b + 1)
                    add_gated(nc, dve, b, x_tok, s_tok[:, 2 * b:2 * b + 2, :], y, gate_ready, x_ready, x_stats)

                gamma(0)
                mix(0)
                gamma(1)
                mix(1)
                gamma(2)
                gamma(3)
                mix(2)
                finish(0)
                finish(1)
                mix(3)
                finish(2)
                finish(3)

            @block.tensor
            def _(pe):
                def total(p, i, e):
                    pe.wait_ge(seen_ready, pass_steps * p + round_steps * i + e + 1)
                    nc.tensor.matmul(banks[:, e % MI, :], ident[:, :], seen[:, e % MI, :],
                                     start=False, stop=False, skip_group_check=True).then_inc(summed, 1)

                def raise_(p, i, s):
                    pe.wait_ge(ffn_loaded[s], 2 * DMA * (rounds * p + i + 1))
                    for k in range(KD):
                        last = nc.tensor.matmul(banks[:, 6 + s, :], up[:, s, k, :], xnT[:, k, cols[p]],
                                                start=(k == 0), stop=(k == KD - 1))
                    last.then_inc(up_done, 1)

                def lower(p, i, s):
                    pe.wait_ge(h_ready, pass_tiles * p + tiles * i + s + 1)
                    for t in range(4):
                        last = nc.tensor.matmul(banks[:, 4 + t // 2, (t % 2) * D:(t % 2 + 1) * D],
                                                hT[:, s, t * P:(t + 1) * P], down[:, s, :],
                                                start=False, stop=False, skip_group_check=True)
                    last.then_inc(down_done, 1)

                pe.wait_ge(zeros_ready, 1)
                for p in range(passes):
                    if p:
                        pe.wait_ge(gated_ready, MI * p)
                    for mi in range(MI):
                        last = nc.tensor.matmul(banks[:, mi, :], diag[:, mi, :], xs[:, mi, cols[p]],
                                                start=True, stop=False, skip_group_check=True)
                        if p == 0:
                            last.then_inc(summed, 1)
                    if p:
                        pe.wait_ge(y_ready, 2 * p)
                    for b in range(2):
                        nc.tensor.matmul(banks[:, 4 + b, :], zeros[0:1, 0:P], zeros[0:1, :],
                                         start=True, stop=False, skip_group_check=True)
                    with pe.Fori(0, rounds) as i:
                        for s in range(tiles):
                            for e in range(tile_steps * s, tile_steps * (s + 1)):
                                total(p, i, e)
                                if e % tile_steps == 1:
                                    raise_(p, i, s)
                            lower(p, i, s)
                pe.wait_ge(gated_ready, passes * MI)
                for t in range(NT):
                    for k in range(MI):
                        last = nc.tensor.matmul(banks[:, t // 2, (t % 2) * D:(t % 2 + 1) * D],
                                                dx[:, k, t * P:(t + 1) * P], w["W_out"][:, k, :],
                                                start=(k == 0), stop=(k == MI - 1))
                    if t % 2:
                        last.then_inc(mixed, 1)




HEADS2, HEAD2 = 16, 16


EXPERTS2, TOP2, CAPACITY = 16, 4, 128
WIDE2, SHARED2 = 176, 352
ROWS2 = WIDE2 // 2
INFO = 6


def route_stage(nc, w, late_weights, xn_tok, xnT, ident, earlier, banks, tables, xn_dram, y_dram, keep, y_shared):
    q, keys, v = keep
    slot_token, slot_target, slot_weight = tables
    tiles = -(-SHARED2 // P)
    width = [min(P, SHARED2 - i * P) for i in range(tiles)]
    halves = range(2)
    jobs = ([("k", 0, 0)] + [("q", g, half) for g in range(2) for half in halves] + [("v", 0, 0)]
            + [("s", i, half) for i in range(tiles) for half in halves])
    first_query = jobs.index(("q", 0, 0))
    before = 3
    dve_ends = [kind in "qs" for kind, _, _ in jobs]

    def ended(n, ends):
        return sum(e == ends for e in dve_ends[:n + 1])

    with ExitStack() as ctx:
        m = Core(nc, ctx)
        shape = [P, NT, EXPERTS2]
        logits = m.sbuf("logits2", shape)
        best = m.sbuf("best2", [P, NT])
        powers = m.sbuf("powers2", shape)
        total = m.sbuf("total2", [P, NT])
        score = m.sbuf("score2", shape)
        above = m.sbuf("above2", [P, NT, EXPERTS2, EXPERTS2])
        equal = m.sbuf("equal2", [P, NT, EXPERTS2, EXPERTS2])
        count = m.sbuf("count2", shape)
        chosen = m.sbuf("chosen2", shape)
        chosen_bf = m.sbuf("chosen_bf2", shape, BF16)
        weight = m.sbuf("weight2", shape)
        place = m.sbuf("place2", shape)
        kept = m.sbuf("kept2", shape)
        before_bf = m.sbuf("before_bf2", [P, P], BF16)
        ones_bf = m.sbuf("ones_bf2", [P, P], BF16)
        one_hot = m.sbuf("one_hot2", [P, NT, EXPERTS2, CAPACITY], BF16)
        info = m.sbuf("info2", [P, NT, EXPERTS2, INFO], BF16)
        rest = m.sbuf("rest2", shape)
        table = m.sbuf("table2", [P, EXPERTS2, INFO])
        empty = m.sbuf("empty2", [P, EXPERTS2])
        token = m.sbuf("token2", [P, EXPERTS2])
        krep = m.sbuf("krep", [P, N])
        silu = m.sbuf("shared_silu2", [P, 2, HALF])
        mid = m.sbuf("shared_mid2", [P, tiles, N])
        zeros = m.sbuf("zeros2", [P, D])
        consts_ready = nc.alloc_semaphore("route_consts2")
        logits_done = nc.alloc_semaphore("logits_done2")
        route_steps = nc.alloc_semaphore("route_steps2")
        shifted = nc.alloc_semaphore("shifted2")
        powers_ready = nc.alloc_semaphore("powers_ready2")
        chosen_ready = nc.alloc_semaphore("chosen_ready2")
        places_done = nc.alloc_semaphore("places_done2")
        slots_ready = nc.alloc_semaphore("slots_ready2")
        table_done = nc.alloc_semaphore("table_done2")
        job_done = nc.alloc_semaphore("job_done2")
        half_ended = nc.alloc_semaphore("job_half_ended2")
        act_ended = nc.alloc_semaphore("job_act_ended2")
        dve_ended = nc.alloc_semaphore("job_dve_ended2")
        krep_ready = nc.alloc_semaphore("krep_ready2")
        y_done = nc.alloc_semaphore("shared_y_done2")
        y_ready = nc.alloc_semaphore("shared_y_ready2")
        stored = nc.alloc_semaphore("route_stored2")
        cols = [slice(h * HALF, (h + 1) * HALF) for h in range(2)]

        with nc.Block(no_gpsimd_drain=True) as block:

            @block.sync
            def _(sp):
                def by_token(dram):
                    return dram.rearrange("(n p) d -> p n d", p=P)

                sp.dma_start(by_token(xn_dram), xn_tok[:, :, :]).then_inc(stored, DMA)
                sp.wait_ge(consts_ready, 2)
                sp.dma_start(y_dram[N:N + P, :], zeros[:, :]).then_inc(stored, DMA)
                sp.wait_ge(y_ready, NT // 2)
                sp.dma_start(by_token(y_dram[0:N, :]), y_shared[:, :, :]).then_inc(stored, DMA)
                sp.wait_ge(stored, 3 * DMA)

            @block.gpsimd
            def _(pool):
                nc.gpsimd.memset(ones_bf[:, :], 1.0).then_inc(consts_ready, 1)
                nc.gpsimd.memset(zeros[:, :], 0.0).then_inc(consts_ready, 1)
                nc.gpsimd.memset(info[:, :, :, INFO - 1:INFO], 1.0).then_inc(consts_ready, 1)

            @block.tensor
            def _(pe):
                def job(n):
                    kind, i, half = jobs[n]
                    pair = 2 + 2 * (n % 3)
                    if n >= 3:
                        ends = dve_ends[n - 3]
                        pe.wait_ge(dve_ended if ends else act_ended, ended(n - 3, ends))
                    if kind == "v":
                        for t in range(NT):
                            for k in range(KD):
                                last = nc.tensor.matmul(
                                    banks[:, pair, t * HEAD2:(t + 1) * HEAD2], xnT[:, k, t * P:(t + 1) * P],
                                    w["Wv"][:, k, :], start=(k == 0), stop=(k == KD - 1))
                        last.then_inc(job_done, 1)
                        return
                    if n == first_query:
                        pe.wait_ge(*late_weights)
                    part = slice(i * P, i * P + (width[i] if kind == "s" else P))
                    wide = {"k": ("Wk", "Wk"), "q": ("Wq", "Wq_swap"), "s": ("sw_gate", "sw_up")}[kind]
                    for j, name in enumerate(wide):
                        for k in range(KD):
                            last = nc.tensor.matmul(banks[0:part.stop - part.start, pair + j, :], w[name][:, k, part],
                                                    xnT[:, k, cols[j if kind == "k" else half]],
                                                    start=(k == 0), stop=(k == KD - 1))
                    last.then_inc(job_done, 1)

                for t in range(NT):
                    for k in range(KD):
                        last = nc.tensor.matmul(banks[:, 0, t * EXPERTS2:(t + 1) * EXPERTS2],
                                                xnT[:, k, t * P:(t + 1) * P], w["gate_w"][:, k, :],
                                                start=(k == 0), stop=(k == KD - 1))
                last.then_inc(logits_done, 1)
                for n in range(before):
                    job(n)
                pe.wait_ge(consts_ready, 1)
                pe.wait_ge(chosen_ready, 1)
                for t in range(NT):
                    for other in range(t + 1):
                        last = nc.tensor.matmul(banks[:, 1, t * EXPERTS2:(t + 1) * EXPERTS2],
                                                (before_bf if other == t else ones_bf)[:, :], chosen_bf[:, other, :],
                                                start=(other == 0), stop=(other == t))
                last.then_inc(places_done, 1)
                for n in range(before, len(jobs)):
                    job(n)
                pe.wait_ge(dve_ended, ended(len(jobs) - 1, True))
                for t in range(NT):
                    for i in range(tiles):
                        last = nc.tensor.matmul(banks[:, 4 + t // 2, (t % 2) * D:(t % 2 + 1) * D],
                                                mid[0:width[i], i, t * P:(t + 1) * P], w["sw_down"][0:width[i], i, :],
                                                start=(i == 0), stop=(i == tiles - 1))
                    if t % 2:
                        last.then_inc(y_done, 1)
                pe.wait_ge(consts_ready, 3)
                pe.wait_ge(slots_ready, 1)
                for e in range(EXPERTS2):
                    for t in range(NT):
                        last = nc.tensor.matmul(banks[:, 0, e * INFO:(e + 1) * INFO], one_hot[:, t, e, :],
                                                info[:, t, e, :], start=(t == 0), stop=(t == NT - 1))
                last.then_inc(table_done, 1)

            @block.scalar
            def _(act):
                def job(n):
                    kind, i, half = jobs[n]
                    pair = 2 + 2 * (n % 3)
                    act.wait_ge(job_done, n + 1)
                    if kind == "k":
                        for half in halves:
                            ins = nc.scalar.activation(krep[:, cols[half]], banks[:, pair + half, :], ACT.Identity)
                            ins.then_inc(act_ended if half else krep_ready, 1)
                    if kind == "q":
                        nc.scalar.activation(q[:, i, cols[half]], banks[:, pair, :], ACT.Identity,
                                             scale=w["cos"][:, i:i + 1]).then_inc(half_ended, 1)
                    if kind == "v":
                        nc.scalar.activation(v[:, :, :].rearrange("p t d -> p (t d)"), banks[:, pair, 0:NT * HEAD2],
                                             ACT.Identity).then_inc(act_ended, 1)
                    if kind == "s":
                        act.wait_ge(dve_ended, ended(n - 2, True))
                        nc.scalar.activation(silu[0:width[i], half, :], banks[0:width[i], pair, :], ACT.Silu
                                             ).then_inc(half_ended, 1)

                act.wait_ge(shifted, 1)
                nc.scalar.activation(powers[:, :, :], powers[:, :, :], ACT.Exp).then_inc(powers_ready, 1)
                for n in range(len(jobs)):
                    job(n)
                    if n == before - 1:
                        act.wait_ge(act_ended, 1)
                        act.wait_ge(krep_ready, 1)
                        for h in range(8):
                            nc.scalar.activation(keys[:, h, :], krep[:, :], ACT.Identity, scale=w["head_rows"][:, h:h + 1])
                for b in range(NT // 2):
                    act.wait_ge(y_done, b + 1)
                    nc.scalar.activation(y_shared[:, 2 * b:2 * b + 2, :].rearrange("p t d -> p (t d)"), banks[:, 4 + b, :],
                                         ACT.Identity).then_inc(y_ready, 1)

            @block.vector
            def _(dve):
                steps = Steps(dve, route_steps)

                def job(n):
                    kind, i, half = jobs[n]
                    if not dve_ends[n]:
                        return
                    bank = 3 + 2 * (n % 3)
                    dve.wait_ge(half_ended, ended(n, True))
                    if kind == "q":
                        nc.vector.scalar_tensor_tensor(q[:, i, cols[half]], banks[:, bank, :], w["sin"][:, i:i + 1],
                                                       q[:, i, cols[half]], ALU.mult, ALU.add).then_inc(dve_ended, 1)
                    else:
                        nc.vector.tensor_tensor(mid[0:width[i], i, cols[half]], silu[0:width[i], half, :],
                                                banks[0:width[i], bank, :], ALU.mult).then_inc(dve_ended, 1)

                def per_token(row):
                    return row.unsqueeze(2).broadcast_to(shape)

                steps.add(nc.vector.tensor_copy(before_bf[:, :], w["before"][:, :]))
                dve.wait_ge(logits_done, 1)
                steps.do(nc.vector.tensor_copy(logits[:, :, :].rearrange("p t e -> p (t e)"),
                                               banks[:, 0, 0:NT * EXPERTS2]))
                steps.do(nc.vector.tensor_reduce(best[:, :], logits[:, :, :], AX.X, ALU.max))
                nc.vector.tensor_tensor(powers[:, :, :], logits[:, :, :], per_token(best[:, :]), ALU.subtract
                                        ).then_inc(shifted, 1)
                dve.wait_ge(powers_ready, 1)
                steps.do(nc.vector.tensor_reduce(total[:, :], powers[:, :, :], AX.X, ALU.add))
                steps.do(nc.vector.reciprocal(best[:, :], total[:, :]))
                steps.do(nc.vector.tensor_tensor(score[:, :, :], powers[:, :, :], per_token(best[:, :]), ALU.mult))
                rank_mask(nc, steps, chosen[:, :, :], score[:, :, :],
                          (above[:, :, :, :], equal[:, :, :, :], count[:, :, :]), earlier, EXPERTS2, TOP2)
                nc.vector.tensor_copy(chosen_bf[:, :, :], chosen[:, :, :]).then_inc(chosen_ready, 1)
                for n in range(before):
                    job(n)
                steps.do(nc.vector.tensor_tensor(weight[:, :, :], chosen[:, :, :], score[:, :, :], ALU.mult))
                steps.do(nc.vector.tensor_reduce(total[:, :], weight[:, :, :], AX.X, ALU.add))
                steps.do(nc.vector.tensor_scalar(total[:, :], total[:, :], 1e-20, None, ALU.add))
                steps.do(nc.vector.reciprocal(best[:, :], total[:, :]))
                steps.do(nc.vector.tensor_tensor(weight[:, :, :], weight[:, :, :], per_token(best[:, :]), ALU.mult))
                steps.add(nc.vector.tensor_copy(
                    info[:, :, :, 0:2], w["token_place"][:, :, :].unsqueeze(2).broadcast_to([P, NT, EXPERTS2, 2])))
                rest_of = weight
                for part in range(3):
                    steps.do(nc.vector.tensor_copy(info[:, :, :, 2 + part], rest_of[:, :, :]))
                    if part < 2:
                        steps.do(nc.vector.tensor_tensor(rest[:, :, :], rest_of[:, :, :], info[:, :, :, 2 + part],
                                                         ALU.subtract))
                        rest_of = rest
                dve.wait_ge(places_done, 1)
                steps.do(nc.vector.tensor_copy(place[:, :, :].rearrange("p t e -> p (t e)"),
                                               banks[:, 1, 0:NT * EXPERTS2]))
                steps.do(nc.vector.scalar_tensor_tensor(kept[:, :, :], place[:, :, :], float(CAPACITY), chosen[:, :, :],
                                                        ALU.is_lt, ALU.mult))
                steps.do(nc.vector.scalar_tensor_tensor(place[:, :, :], place[:, :, :], 1.0, kept[:, :, :],
                                                        ALU.add, ALU.mult))
                steps.do(nc.vector.tensor_scalar(place[:, :, :], place[:, :, :], -1.0, None, ALU.add))
                for t in range(NT):
                    ins = nc.vector.tensor_tensor(
                        one_hot[:, t, :, :], w["slots"][:, :].unsqueeze(1).broadcast_to([P, EXPERTS2, CAPACITY]),
                        place[:, t, :].unsqueeze(2).broadcast_to([P, EXPERTS2, CAPACITY]), ALU.is_equal)
                    if t == NT - 1:
                        ins.then_inc(slots_ready, 1)
                    else:
                        steps.add(ins)
                    if before + t < len(jobs):
                        job(before + t)
                for n in range(before + NT, len(jobs)):
                    job(n)
                dve.wait_ge(table_done, 1)
                steps.do(nc.vector.tensor_copy(table[:, :, :].rearrange("p e i -> p (e i)"),
                                               banks[:, 0, 0:EXPERTS2 * INFO]))
                steps.do(nc.vector.tensor_tensor(token[:, :], table[:, :, 0], table[:, :, 1], ALU.add))
                steps.add(nc.vector.tensor_copy(slot_token[:, :], token[:, :]))
                steps.do(nc.vector.tensor_scalar(empty[:, :], table[:, :, INFO - 1], -1.0, 1.0, ALU.mult, ALU.add))
                steps.do(nc.vector.scalar_tensor_tensor(token[:, :], empty[:, :], w["spare_row"][:, 0:1], token[:, :],
                                                        ALU.mult, ALU.add))
                steps.add(nc.vector.tensor_copy(slot_target[:, :], token[:, :]))
                steps.do(nc.vector.tensor_tensor(slot_weight[:, :], table[:, :, 3], table[:, :, 4], ALU.add))
                steps.do(nc.vector.tensor_tensor(slot_weight[:, :], slot_weight[:, :], table[:, :, 2], ALU.add))


def attention_and_expert_stage(nc, w, keep, expert_w, tables, xn_dram, y_dram, x_tok, stats, ident, banks,
                               next_loads, next_w, q_weight):
    q, keys, v = keep
    slot_token, slot_target, slot_weight = tables
    w_gate, w_up, w_down = expert_w
    pairs = EXPERTS2 // 2
    group = 4
    seq_units = 3 * HEADS2 // group
    round_ = 2 * seq_units
    rounds = BATCH // 2
    turns = round_ // 3
    assert turns * rounds == EXPERTS2
    scale = HEAD2 ** -0.5
    with ExitStack() as ctx:
        m = Core(nc, ctx)
        q_now = m.sbuf("q_now", [P, 2, 2, SEQ])
        top = m.sbuf("score_top", [P, 4, group])
        shift = m.sbuf("score_shift", [P, 4, group])
        total = m.sbuf("prob_total", [P, 4, group])
        inverse = m.sbuf("prob_inverse", [P, 4, group])
        prob = m.sbuf("prob", [P, 4, BANK])
        probT = m.sbuf("probT", [P, 2, BANK // P, P])
        o_tok = m.sbuf("o_tok", [P, NT, D])
        oT = m.sbuf("oT2", [P, KD, N])
        gate_w = m.sbuf("slot_gate_w", [P, 2, KD, WIDE2])
        up_w = m.sbuf("slot_up_w", [P, 2, KD, WIDE2])
        down_w = m.sbuf("slot_down_w", [ROWS2, 2, 2, D])
        xg = m.sbuf("slot_x", [P, 2, D])
        xgT = m.sbuf("slot_xT", [P, 2, D])
        tanh = m.sbuf("slot_tanh", [ROWS2, 2, 2 * P])
        mid = m.sbuf("slot_mid", [ROWS2, 2, 2 * P])
        result = m.sbuf("slot_result", [P, 2, D])
        gated = m.sbuf("gated2", [P, NT, D])
        loaded = [nc.alloc_semaphore(f"slot_loaded{s}") for s in range(2)]
        gathered = [nc.alloc_semaphore(f"slot_gathered{s}") for s in range(2)]
        turned = nc.alloc_semaphore("slot_turned")
        xgT_ready = nc.alloc_semaphore("slot_xT_ready")
        widened = nc.alloc_semaphore("slot_widened")
        tanh_ready = nc.alloc_semaphore("slot_tanh_ready")
        gate_twice_ready = nc.alloc_semaphore("slot_gate_twice_ready")
        mid_ready = nc.alloc_semaphore("slot_mid_ready")
        lowered = nc.alloc_semaphore("slot_lowered")
        result_ready = nc.alloc_semaphore("slot_result_ready")
        scattered = nc.alloc_semaphore("slot_scattered")
        next_loaded = nc.alloc_semaphore("next_loaded2")
        q_weight_done = nc.alloc_semaphore("q_weight_done2")
        y_loaded = nc.alloc_semaphore("y_loaded2")
        gate_ready = nc.alloc_semaphore("gate_ready2")
        x_ready = nc.alloc_semaphore("x_ready2")
        q_ready = nc.alloc_semaphore("q_ready2")
        scored = nc.alloc_semaphore("scored2")
        masked_ready = nc.alloc_semaphore("masked_ready2")
        top_ready = nc.alloc_semaphore("top_ready2")
        shift_ready = nc.alloc_semaphore("shift_ready2")
        prob_ready = nc.alloc_semaphore("prob_ready2")
        prob_turned = nc.alloc_semaphore("prob_turned2")
        probT_ready = nc.alloc_semaphore("probT_ready2")
        summed = nc.alloc_semaphore("pv_summed2")
        inverse_ready = nc.alloc_semaphore("inverse_ready2")
        o_ready = nc.alloc_semaphore("o_ready2")
        o_turned = nc.alloc_semaphore("o_turned2")
        oT_ready = nc.alloc_semaphore("oT_ready2")
        mixed = nc.alloc_semaphore("mixed2")

        def unit(j):
            s, k, part = j // seq_units, j % seq_units // 3, j % 3
            if part == 0:
                return s, 0, group * k, group, P
            return s, 1, group * k + group // 2 * (part - 1), group // 2, SEQ

        def by_head(flat, j):
            return flat.rearrange("p (h k) -> p h k", h=unit(j)[3])


        with nc.Block(no_gpsimd_drain=True) as block:

            @block.sync
            def _(sp):
                def load(e, s):
                    for dst, src in ((gate_w, w_gate), (up_w, w_up)):
                        sp.dma_start(dst[:, s, :, :], src[bass.ds(e, 1), :, :].rearrange("e (k p) n -> p (e k) n", p=P)
                                     ).then_inc(loaded[s], DMA)
                    sp.dma_start(down_w[:, s, :, :], w_down[bass.ds(e, 1), :, :]
                                 .rearrange("e (i p) d -> p (e i) d", p=ROWS2)).then_inc(loaded[s], DMA)

                for s in range(2):
                    load(s, s)
                with sp.Fori(1, pairs) as i:
                    for s in range(2):
                        sp.wait_ge(lowered, 2 * i + s - 1)
                        load(2 * i + s, s)
                for dst, src in next_loads:
                    sp.dma_start(dst, src).then_inc(next_loaded, DMA)
                sp.wait_ge(scattered, DMA * EXPERTS2)
                sp.dma_start(gated[:, :, :], y_dram[0:N, :].rearrange("(n p) d -> p n d", p=P)).then_inc(y_loaded, DMA)
                sp.wait_ge(y_loaded, DMA)
                sp.wait_ge(next_loaded, DMA * len(next_loads))

            @block.gpsimd
            def _(pool):
                def copy(b):
                    nc.gpsimd.tensor_copy(q_now[:, b % 2, :, :], q[:, :, b * SEQ:(b + 1) * SEQ]).then_inc(q_ready, 1)

                def gather(e):
                    pool.indirect_dma_start(out=xg[:, e % 2, :], out_offset=None, in_=xn_dram[:, :],
                                            in_offset=bass.IndirectOffsetOnAxis(ap=slot_token[:, e:e + 1], axis=0)
                                            ).then_inc(gathered[e % 2], DMA)

                copy(0)
                copy(1)
                gather(0)
                gather(1)
                for e in range(EXPERTS2):
                    if e + 2 < EXPERTS2:
                        pool.wait_ge(turned, e + 1)
                        gather(e + 2)
                    pool.wait_ge(result_ready, e + 1)
                    if e:
                        pool.wait_ge(scattered, DMA * e)
                    pool.indirect_dma_start(out=y_dram[:, :],
                                            out_offset=bass.IndirectOffsetOnAxis(ap=slot_target[:, e:e + 1], axis=0),
                                            in_=result[:, e % 2, :], in_offset=None, compute_op=ALU.add
                                            ).then_inc(scattered, DMA)
                    if e in (turns // 2, turns - 1):
                        b = 2 if e < turns - 1 else 3
                        pool.wait_ge(scored, seq_units * (b - 1))
                        copy(b)
                pool.wait_ge(scattered, DMA * EXPERTS2)

            @block.tensor
            def _(pe):
                def score(i, j):
                    s, qt, head, heads, n_keys = unit(j)
                    if j % seq_units == 0:
                        pe.wait_ge(q_ready, 2 * i + s + 1)
                    if j >= 3:
                        pe.wait_ge(prob_ready, round_ * i + j - 2)
                    nc.tensor.matmul(
                        banks[:, j % 3, :], q_now[:, s, head // 8, qt * P:(qt + 1) * P],
                        keys[:, head % 8:head % 8 + heads, bass.ds((2 * i + s) * SEQ, n_keys)],
                        start=True, stop=True).then_inc(scored, 1)

                def turn(i, j):
                    s, qt, head, heads, n_keys = unit(j)
                    pe.wait_ge(prob_ready, round_ * i + j + 1)
                    if j >= 2:
                        pe.wait_ge(probT_ready, round_ * i + j - 1)
                    for c in range(BANK // P):
                        last = nc.tensor.transpose(banks[:, 3 + j % 2, c * P:(c + 1) * P],
                                                   prob[:, j % 4, c * P:(c + 1) * P], ident[:, :])
                    last.then_inc(prob_turned, 1)

                def weigh(i, j):
                    s, qt, head, heads, n_keys = unit(j)
                    pe.wait_ge(probT_ready, round_ * i + j + 1)
                    if j:
                        pe.wait_ge(o_ready, round_ * i + j)
                    for h in range(heads):
                        for kt in range(qt + 1):
                            last = nc.tensor.matmul(banks[:, 5, h * HEAD2:(h + 1) * HEAD2],
                                                    probT[:, j % 2, h * (qt + 1) + kt, :],
                                                    v[:, bass.ds(4 * i + 2 * s + kt, 1), :].rearrange("p a d -> p (a d)"),
                                                    start=(kt == 0), stop=(kt == qt))
                    last.then_inc(summed, 1)

                def turn_tokens(i, n):
                    e, s = turns * i + n, n % 2
                    pe.wait_ge(gathered[s], DMA * (turns // 2 * i + n // 2 + 1))
                    if n >= 2:
                        pe.wait_ge(result_ready, e - 1)
                    for k in range(KD):
                        last = nc.tensor.transpose(banks[:, 6, k * P:(k + 1) * P], xg[:, s, k * P:(k + 1) * P], ident[:, :])
                    last.then_inc(turned, 1)

                def widen(i, n, j):
                    e, s = turns * i + n, n % 2
                    if j == 0:
                        pe.wait_ge(loaded[s], 3 * DMA * (turns // 2 * i + n // 2 + 1))
                        pe.wait_ge(xgT_ready, e + 1)
                        if n:
                            pe.wait_ge(mid_ready, e)
                    wt = (gate_w, up_w)[j]
                    for part in range(2):
                        for k in range(KD):
                            last = nc.tensor.matmul(
                                banks[0:ROWS2, 7, (2 * j + part) * P:(2 * j + part + 1) * P],
                                wt[:, s, k, part * ROWS2:(part + 1) * ROWS2], xgT[:, s, k * P:(k + 1) * P],
                                start=(k == 0), stop=(k == KD - 1))
                    if j == 1:
                        last.then_inc(widened, 1)

                def lower(i, n):
                    e, s = turns * i + n, n % 2
                    pe.wait_ge(mid_ready, e + 1)
                    if n + 1 < turns:
                        pe.wait_ge(xgT_ready, e + 2)
                    for part in range(2):
                        last = nc.tensor.matmul(banks[:, 6, D:2 * D], mid[:, s, part * P:(part + 1) * P],
                                                down_w[:, s, part, :], start=(part == 0), stop=(part == 1))
                    last.then_inc(lowered, 1)

                with pe.Fori(0, rounds) as i:
                    for j in range(3):
                        score(i, j)
                    for j in range(round_):
                        turn(i, j)
                        if j % 3 == 0:
                            turn_tokens(i, j // 3)
                        if j + 3 < round_:
                            score(i, j + 3)
                        if j:
                            weigh(i, j - 1)
                        if j % 3 == 1:
                            if j > 1:
                                lower(i, j // 3 - 1)
                            widen(i, j // 3, 0)
                        if j % 3 == 2:
                            widen(i, j // 3, 1)
                    weigh(i, round_ - 1)
                    lower(i, turns - 1)
                    pe.wait_ge(o_ready, round_ * i + round_)
                    pe.wait_ge(result_ready, turns * (i + 1))
                for half in range(2):
                    for k in range(KD):
                        for t in range(4):
                            last = nc.tensor.transpose(banks[:, 2 * half + k, t * P:(t + 1) * P],
                                                       o_tok[:, 4 * half + t, k * P:(k + 1) * P], ident[:, :])
                        last.then_inc(o_turned, 1)
                for t in range(NT):
                    pe.wait_ge(oT_ready, 2 * (t // 4) + 2)
                    for k in range(KD):
                        last = nc.tensor.matmul(banks[:, 4 + t // 2, (t % 2) * D:(t % 2 + 1) * D],
                                                oT[:, k, t * P:(t + 1) * P], w["Wo"][:, k, :],
                                                start=(k == 0), stop=(k == KD - 1))
                    if t % 2:
                        last.then_inc(mixed, 1)
                pe.wait_ge(next_loaded, DMA * len(next_loads))
                for n in range(EARLY3):
                    query_weights(nc, next_w, banks[:, n, :], n).then_inc(q_weight_done, 1)

            @block.vector
            def _(dve):
                def tops(i, j):
                    s, qt, head, heads, n_keys = unit(j)
                    bank = by_head(banks[:, j % 3, :], j)
                    dve.wait_ge(scored, round_ * i + j + 1)
                    last_keys = bank[:, :, n_keys - P:n_keys]
                    nc.vector.tensor_tensor(last_keys, last_keys,
                                            w["causal"][:, SEQ - P:SEQ].unsqueeze(1).broadcast_to([P, heads, P]),
                                            ALU.add).then_inc(masked_ready, 1)
                    dve.wait_ge(masked_ready, round_ * i + j + 1)
                    nc.vector.tensor_reduce(top[:, j % 4, 0:heads], bank, AX.X, ALU.max).then_inc(top_ready, 1)
                    dve.wait_ge(top_ready, round_ * i + j + 1)
                    nc.vector.tensor_scalar(shift[:, j % 4, 0:heads], top[:, j % 4, 0:heads], -scale, None, ALU.mult
                                            ).then_inc(shift_ready, 1)

                def evacuate(i, j):
                    heads = unit(j)[3]
                    dve.wait_ge(prob_turned, round_ * i + j + 1)
                    nc.vector.tensor_copy(probT[:, j % 2, :, :].rearrange("p c k -> p (c k)"), banks[:, 3 + j % 2, :]
                                          ).then_inc(probT_ready, 1)
                    nc.vector.reciprocal(inverse[:, j % 4, 0:heads], total[:, j % 4, 0:heads]).then_inc(inverse_ready, 1)

                def normalize(i, j):
                    s, qt, head, heads, n_keys = unit(j)
                    dve.wait_ge(inverse_ready, round_ * i + j + 1)
                    dve.wait_ge(summed, round_ * i + j + 1)
                    nc.vector.tensor_tensor(
                        o_tok[:, bass.ds(4 * i + 2 * s + qt, 1), head * HEAD2:(head + heads) * HEAD2]
                        .rearrange("p a (h d) -> p (a h) d", h=heads),
                        banks[:, 5, 0:heads * HEAD2].rearrange("p (h d) -> p h d", h=heads),
                        inverse[:, j % 4, 0:heads].unsqueeze(2).broadcast_to([P, heads, HEAD2]), ALU.mult
                        ).then_inc(o_ready, 1)

                def middle(i, n):
                    e, s = turns * i + n, n % 2
                    dve.wait_ge(tanh_ready, e + 1)
                    nc.vector.scalar_tensor_tensor(tanh[:, s, :], tanh[:, s, :], 1.0, banks[0:ROWS2, 7, 0:2 * P],
                                                   ALU.add, ALU.mult).then_inc(gate_twice_ready, 1)
                    dve.wait_ge(gate_twice_ready, e + 1)
                    nc.vector.scalar_tensor_tensor(mid[:, s, :], tanh[:, s, :], 0.5, banks[0:ROWS2, 7, 2 * P:4 * P],
                                                   ALU.mult, ALU.mult).then_inc(mid_ready, 1)

                def weigh_result(i, n):
                    e, s = turns * i + n, n % 2
                    dve.wait_ge(lowered, e + 1)
                    if n >= 2:
                        dve.wait_ge(scattered, DMA * (e - 1))
                    nc.vector.tensor_scalar(result[:, s, :], banks[:, 6, D:2 * D], slot_weight[:, bass.ds(e, 1)],
                                            None, ALU.mult).then_inc(result_ready, 1)

                with dve.Fori(0, rounds) as i:
                    for j in range(3):
                        tops(i, j)
                    for j in range(round_):
                        evacuate(i, j)
                        if j % 3 == 2 and j > 2:
                            weigh_result(i, j // 3 - 1)
                        if j + 3 < round_:
                            tops(i, j + 3)
                        if j:
                            normalize(i, j - 1)
                        if j % 3 == 0 and j:
                            middle(i, j // 3 - 1)
                    normalize(i, round_ - 1)
                    middle(i, turns - 1)
                    weigh_result(i, turns - 1)
                    dve.wait_ge(scattered, DMA * (turns * (i + 1) - 1))
                for b in range(NT // 2):
                    dve.wait_ge(mixed, b + 1)
                    add_gated(nc, dve, b, x_tok, banks[:, 4 + b, :].rearrange("p (t d) -> p t d", t=2), gated,
                              gate_ready, x_ready, stats)

            @block.scalar
            def _(act):
                def exps(i, j):
                    heads = unit(j)[3]
                    act.wait_ge(shift_ready, round_ * i + j + 1)
                    if j >= 4:
                        act.wait_ge(prob_turned, round_ * i + j - 3)
                    for h in range(heads):
                        last = nc.scalar.activation(by_head(prob[:, j % 4, :], j)[:, h, :],
                                                    by_head(banks[:, j % 3, :], j)[:, h, :], ACT.Exp,
                                                    bias=shift[:, j % 4, h:h + 1], scale=scale,
                                                    accum_out=total[:, j % 4, h:h + 1])
                    last.then_inc(prob_ready, 1)

                def copy_tokens(i, n):
                    e, s = turns * i + n, n % 2
                    act.wait_ge(turned, e + 1)
                    nc.scalar.activation(xgT[:, s, :], banks[:, 6, 0:D], ACT.Identity).then_inc(xgT_ready, 1)

                def gate(i, n):
                    e, s = turns * i + n, n % 2
                    act.wait_ge(widened, e + 1)
                    nc.scalar.activation(tanh[:, s, :], banks[0:ROWS2, 7, 0:2 * P], ACT.Tanh, scale=0.5
                                         ).then_inc(tanh_ready, 1)

                with act.Fori(0, rounds) as i:
                    exps(i, 0)
                    exps(i, 1)
                    for j in range(round_):
                        if j % 3 == 0:
                            copy_tokens(i, j // 3)
                        if j + 2 < round_:
                            exps(i, j + 2)
                        if j % 3 == 2:
                            gate(i, j // 3)
                for half in range(2):
                    for k in range(KD):
                        act.wait_ge(o_turned, 2 * half + k + 1)
                        nc.scalar.activation(oT[:, k, half * HALF:(half + 1) * HALF], banks[:, 2 * half + k, :],
                                             ACT.Identity).then_inc(oT_ready, 1)
                act.wait_ge(y_loaded, DMA)
                for b in range(NT // 2):
                    pair = slice(2 * b, 2 * b + 2)
                    nc.scalar.activation(gated[:, pair, :], gated[:, pair, :], ACT.Silu).then_inc(gate_ready, 1)
                for n in range(EARLY3):
                    act.wait_ge(q_weight_done, n + 1)
                    nc.scalar.activation(query_weights_target(q_weight, n), banks[:, n, :], ACT.Identity)




HEADS3, LATENT, HEAD3 = 16, 64, 128
UNITS3 = HEADS3 // 2
Q_HEADS3 = BANK // LATENT
Q_BANKS3 = KD * HEADS3 // Q_HEADS3
EARLY3 = 3


def query_weights(nc, w, bank, n):
    k, first = n * Q_HEADS3 // HEADS3, n * Q_HEADS3 % HEADS3
    for h in range(Q_HEADS3):
        last = nc.tensor.matmul(bank[:, h * LATENT:(h + 1) * LATENT], w["WqT"][:, first + h, k * P:(k + 1) * P],
                                w["WupT"][:, first + h, :], start=True, stop=True)
    return last


def query_weights_target(q_weight, n):
    k, first = n * Q_HEADS3 // HEADS3, n * Q_HEADS3 % HEADS3
    return q_weight[:, k, first * LATENT:first * LATENT + BANK]


def work_on_weights(nc, w, banks, keep, weights, scratch):
    q_weight, o_weight, latT, lat_tok = keep
    done = nc.alloc_semaphore("latent_weights_done3")
    ready = nc.alloc_semaphore("latent_weights_ready3")

    def tensor(pe):
        for n in range(EARLY3, Q_BANKS3):
            query_weights(nc, w, banks[:, 4 + n, :], n).then_inc(done, 1)
        for u in range(UNITS3):
            if u % 2 == 0 and u // 2 >= EARLY3:
                pe.wait_ge(ready, u // 2 - EARLY3 + 1)
            for part in range(2):
                last = nc.tensor.matmul(
                    banks[part * LATENT:(part + 1) * LATENT, 4 + u // 2, (u % 2) * D:(u % 2 + 1) * D],
                    w["WupT"][:, 2 * u + part, :], w["Wo"][:, 2 * u + part, :], start=True, stop=True)
            if u % 2:
                last.then_inc(done, 1)

    def scalar(act):
        targets = [(n, query_weights_target(q_weight, n)) for n in range(EARLY3, Q_BANKS3)]
        targets += [(b, o_weight[:, 2 * b:2 * b + 2, :].rearrange("p u d -> p (u d)")) for b in range(UNITS3 // 2)]
        for n, (b, dst) in enumerate(targets):
            act.wait_ge(done, n + 1)
            nc.scalar.activation(dst, banks[:, 4 + b, :], ACT.Identity).then_inc(ready, 1)

    def vector(dve):
        for part in range(2):
            weights.unpack(dve, scratch, 0, 0, part)

    def sync(sp):
        for s in range(2):
            weights.load(sp, s, s)

    return {"tensor": tensor, "scalar": scalar, "vector": vector, "sync": sync}


def latent_prepare_stage(nc, w, xnT, banks, keep, weights, scratch):
    q_weight, o_weight, latT, lat_tok = keep
    done = nc.alloc_semaphore("latent_done3")
    cols = [slice(h * HALF, (h + 1) * HALF) for h in range(2)]

    with nc.Block(no_gpsimd_drain=True) as block:

        @block.tensor
        def _(pe):
            for half in range(2):
                for k in range(KD):
                    last = nc.tensor.matmul(banks[:, 4 + half, :], w["Wdown2"][:, k, :], xnT[:, k, cols[half]],
                                            start=(k == 0), stop=(k == KD - 1))
                last.then_inc(done, 1)
            for t in range(NT):
                for k in range(KD):
                    last = nc.tensor.matmul(banks[:, 6, t * LATENT:(t + 1) * LATENT], xnT[:, k, t * P:(t + 1) * P],
                                            w["Wdown2"][:, k, 0:LATENT], start=(k == 0), stop=(k == KD - 1))
            last.then_inc(done, 1)

        @block.vector
        def _(dve):
            for part in range(2, 4):
                weights.unpack(dve, scratch, 0, 0, part)

        @block.scalar
        def _(act):
            targets = [latT[:, cols[0]], latT[:, cols[1]], lat_tok[:, :, :].rearrange("p t c -> p (t c)")]
            for n, dst in enumerate(targets):
                act.wait_ge(done, n + 1)
                nc.scalar.activation(dst, banks[:, 4 + n, :], ACT.Identity)


def latent_attention_stage(nc, xnT, s_tok, ident, banks, keep):
    q_weight, o_weight, latT, lat_tok = keep
    scale = 1.0 / np.sqrt(HEAD3)
    round_ = 2 * HEADS3
    with ExitStack() as ctx:
        m = Core(nc, ctx)
        latT_now = m.sbuf("latT_now", [P, 2, 2, SEQ])
        lat_now = m.sbuf("lat_now", [P, 2, 2, LATENT])
        q_now = m.sbuf("q_now3", [P, 2, SEQ])
        top = m.sbuf("top3", [P, 4, 2])
        shift = m.sbuf("shift3", [P, 4, 2])
        total = m.sbuf("total3", [P, 4, 2])
        inverse = m.sbuf("inverse3", [P, 4, 2])
        prob = m.sbuf("prob3", [P, 4, 2, SEQ])
        probT = m.sbuf("probT3", [P, 2, 2, SEQ])
        o_tok = m.sbuf("o_tok3", [P, NT, HEADS3 * LATENT])
        oT = m.sbuf("oT3", [P, UNITS3, N])
        cleared = nc.alloc_semaphore("lat_now_cleared3")
        lat_ready = nc.alloc_semaphore("lat_now_ready3")
        q_done = nc.alloc_semaphore("q_done3")
        q_ready = nc.alloc_semaphore("q_ready3")
        scored = nc.alloc_semaphore("scored3")
        top_ready = nc.alloc_semaphore("top_ready3")
        shift_ready = nc.alloc_semaphore("shift_ready3")
        prob_ready = nc.alloc_semaphore("prob_ready3")
        prob_turned = nc.alloc_semaphore("prob_turned3")
        probT_ready = nc.alloc_semaphore("probT_ready3")
        summed = nc.alloc_semaphore("pv_summed3")
        inverse_ready = nc.alloc_semaphore("inverse_ready3")
        o_ready = nc.alloc_semaphore("o_ready3")
        o_turned = nc.alloc_semaphore("o_turned3")
        oT_ready = nc.alloc_semaphore("oT_ready3")
        mixed = nc.alloc_semaphore("mixed3")
        rounds = BATCH // 2

        with nc.Block(no_gpsimd_drain=True) as block:

            @block.gpsimd
            def _(pool):
                def copy(i, s):
                    b = 2 * i + s
                    for part in range(2):
                        rows = slice(part * LATENT, (part + 1) * LATENT)
                        nc.gpsimd.tensor_copy(latT_now[rows, s, part, :], latT[rows, bass.ds(b * SEQ, SEQ)]
                                              ).then_inc(lat_ready, 1)
                        pool.wait_ge(lat_ready, 6 * i + 3 * s + part + 1)
                    nc.gpsimd.tensor_copy(lat_now[:, s, :, :], lat_tok[:, bass.ds(2 * b, 2), :]).then_inc(lat_ready, 1)
                    pool.wait_ge(lat_ready, 6 * i + 3 * s + 3)

                nc.gpsimd.memset(latT_now[:, :, :, :], 0.0).then_inc(cleared, 1)
                pool.wait_ge(cleared, 1)
                copy(0, 0)
                copy(0, 1)
                with pool.Fori(1, rounds) as i:
                    for s in range(2):
                        pool.wait_ge(summed, round_ * i - HEADS3 + HEADS3 * s)
                        copy(i, s)

            @block.tensor
            def _(pe):
                def query(i, u):
                    s, pair = u // UNITS3, u % UNITS3
                    if u >= 1:
                        pe.wait_ge(q_ready, 2 * UNITS3 * i + u)
                    for k in range(KD):
                        last = nc.tensor.matmul(banks[:, 7, 0:SEQ], q_weight[:, k, pair * P:(pair + 1) * P],
                                                xnT[:, k, bass.ds((2 * i + s) * SEQ, SEQ)],
                                                start=(k == 0), stop=(k == KD - 1))
                    last.then_inc(q_done, 1)

                def score(i, j):
                    if j % HEADS3 == 0:
                        pe.wait_ge(lat_ready, 6 * i + 3 * (j // HEADS3) + 3)
                    if j % 2 == 0:
                        pe.wait_ge(q_ready, 2 * UNITS3 * i + j // 2 + 1)
                    if j >= 3:
                        pe.wait_ge(prob_ready, round_ * i + j - 2)
                    for qt in range(2):
                        last = nc.tensor.matmul(banks[:, j % 3, qt * SEQ:(qt + 1) * SEQ],
                                                q_now[:, (j // 2) % 2, qt * P:(qt + 1) * P],
                                                latT_now[:, j // HEADS3, j % 2, :], start=True, stop=True)
                    last.then_inc(scored, 1)

                def turn(i, j):
                    pe.wait_ge(prob_ready, round_ * i + j + 1)
                    for kt in range(2):
                        for qt in range(2):
                            last = nc.tensor.transpose(banks[:, 3 + j % 2, kt * SEQ + qt * P:kt * SEQ + (qt + 1) * P],
                                                       prob[:, j % 4, qt, kt * P:(kt + 1) * P], ident[:, :])
                    last.then_inc(prob_turned, 1)

                def weigh(i, j):
                    pe.wait_ge(probT_ready, round_ * i + j + 1)
                    if j >= 2:
                        pe.wait_ge(o_ready, round_ * i + j - 1)
                    for qt in range(2):
                        for kt in range(2):
                            last = nc.tensor.matmul(banks[:, 5 + j % 2, qt * LATENT:(qt + 1) * LATENT],
                                                    probT[:, j % 2, kt, qt * P:(qt + 1) * P],
                                                    lat_now[:, j // HEADS3, kt, :], start=(kt == 0), stop=(kt == 1))
                    last.then_inc(summed, 1)

                def mix(t):
                    pe.wait_ge(oT_ready, 2 * t + 2)
                    for u in range(UNITS3):
                        last = nc.tensor.matmul(banks[:, 4 + t // 2, (t % 2) * D:(t % 2 + 1) * D], oT[:, u, t * P:(t + 1) * P],
                                                o_weight[:, u, :], start=(u == 0), stop=(u == UNITS3 - 1))
                    if t % 2:
                        last.then_inc(mixed, 1)

                with pe.Fori(0, rounds) as i:
                    query(i, 0)
                    query(i, 1)
                    score(i, 0)
                    score(i, 1)
                    query(i, 2)
                    score(i, 2)
                    for j in range(round_):
                        if j % 2 and j // 2 + 3 < 2 * UNITS3:
                            query(i, j // 2 + 3)
                        turn(i, j)
                        if j + 3 < round_:
                            score(i, j + 3)
                        if j:
                            weigh(i, j - 1)
                    weigh(i, round_ - 1)
                    pe.wait_ge(o_ready, round_ * i + round_)
                for t in range(NT):
                    for u in range(UNITS3):
                        if t >= 2 and u % 4 == 0:
                            pe.wait_ge(oT_ready, 2 * (t - 2) + u // 4 + 1)
                        last = nc.tensor.transpose(banks[:, 2 * (t % 2) + u // 4, (u % 4) * P:(u % 4 + 1) * P],
                                                   o_tok[:, t, u * P:(u + 1) * P], ident[:, :])
                        if u % 4 == 3:
                            last.then_inc(o_turned, 1)
                    if t:
                        mix(t - 1)
                mix(NT - 1)

            @block.vector
            def _(dve):
                def tops(i, j):
                    dve.wait_ge(scored, round_ * i + j + 1)
                    nc.vector.tensor_reduce(top[:, j % 4, :], banks[:, j % 3, :].rearrange("p (q k) -> p q k", q=2),
                                            AX.X, ALU.max).then_inc(top_ready, 1)
                    dve.wait_ge(top_ready, round_ * i + j + 1)
                    nc.vector.tensor_scalar(shift[:, j % 4, :], top[:, j % 4, :], -scale, None, ALU.mult
                                            ).then_inc(shift_ready, 1)

                def evacuate(i, j):
                    dve.wait_ge(prob_turned, round_ * i + j + 1)
                    nc.vector.tensor_copy(probT[:, j % 2, :, :].rearrange("p a q -> p (a q)"), banks[:, 3 + j % 2, :]
                                          ).then_inc(probT_ready, 1)
                    nc.vector.reciprocal(inverse[:, j % 4, :], total[:, j % 4, :]).then_inc(inverse_ready, 1)

                def normalize(i, j):
                    s, h = j // HEADS3, j % HEADS3
                    dve.wait_ge(inverse_ready, round_ * i + j + 1)
                    dve.wait_ge(summed, round_ * i + j + 1)
                    nc.vector.tensor_tensor(
                        o_tok[:, bass.ds(4 * i + 2 * s, 2), h * LATENT:(h + 1) * LATENT],
                        banks[:, 5 + j % 2, 0:2 * LATENT].rearrange("p (q c) -> p q c", q=2),
                        inverse[:, j % 4, :].unsqueeze(2).broadcast_to([P, 2, LATENT]), ALU.mult).then_inc(o_ready, 1)

                with dve.Fori(0, rounds) as i:
                    for j in range(3):
                        tops(i, j)
                    for j in range(round_):
                        evacuate(i, j)
                        if j + 3 < round_:
                            tops(i, j + 3)
                        if j:
                            normalize(i, j - 1)
                    normalize(i, round_ - 1)
                for t in range(NT):
                    dve.wait_ge(o_turned, 2 * t + 1)
                    nc.vector.tensor_copy(oT[:, 0:4, t * P:(t + 1) * P],
                                          banks[:, 2 * (t % 2), :].rearrange("p (u c) -> p u c", u=4)).then_inc(oT_ready, 1)
                    dve.wait_ge(o_turned, 2 * t + 2)
                    nc.vector.tensor_copy(oT[:, 4:8, t * P:(t + 1) * P],
                                          banks[:, 2 * (t % 2) + 1, :].rearrange("p (u c) -> p u c", u=4)
                                          ).then_inc(oT_ready, 1)

            @block.scalar
            def _(act):
                def query(i, u):
                    act.wait_ge(q_done, 2 * UNITS3 * i + u + 1)
                    nc.scalar.activation(q_now[:, u % 2, :], banks[:, 7, 0:SEQ], ACT.Identity).then_inc(q_ready, 1)

                with act.Fori(0, rounds) as i:
                    for u in range(3):
                        query(i, u)
                    for j in range(round_):
                        act.wait_ge(shift_ready, round_ * i + j + 1)
                        if j >= 4:
                            act.wait_ge(prob_turned, round_ * i + j - 3)
                        for qt in range(2):
                            last = nc.scalar.activation(prob[:, j % 4, qt, :], banks[:, j % 3, qt * SEQ:(qt + 1) * SEQ],
                                                        ACT.Exp, bias=shift[:, j % 4, qt:qt + 1], scale=float(scale),
                                                        accum_out=total[:, j % 4, qt:qt + 1])
                        last.then_inc(prob_ready, 1)
                        if j % 2 == 0 and 3 <= j // 2 + 2 < 2 * UNITS3:
                            query(i, j // 2 + 2)
                for b in range(NT // 2):
                    act.wait_ge(mixed, b + 1)
                    nc.scalar.activation(s_tok[:, 2 * b:2 * b + 2, :].rearrange("p t d -> p (t d)"), banks[:, 4 + b, :],
                                         ACT.Identity)




MLP3 = 2048
PACKS3 = MLP3 // (2 * P)


class FourBitWeights:

    waits = 10

    def __init__(self, nc, m, packed, scales):
        self.nc, self.packed, self.scales = nc, packed, scales
        self.pack = m.sbuf("pack3", [P, 2, 3, D], I32)
        self.scale = m.sbuf("scale3", [P, 2, 3, D])
        self.weight = m.sbuf("weight3", [P, 2, 3, 2, D])
        self.loaded = [nc.alloc_semaphore(f"pack_loaded{s}") for s in range(2)]
        self.unpack_steps = nc.alloc_semaphore("unpack_steps3")
        self.weight_ready = nc.alloc_semaphore("weight_ready3")

    def scratch(self, m, name):
        shape = [P, 3, 2, D]
        return [m.sbuf(f"code3{name}", shape, I32)] + [
            m.sbuf(f"{part}3{name}", shape, BF16) for part in ("eight", "size", "twice", "fourfold", "sign")]

    def load(self, sp, n, s):
        for j in range(3):
            for dst, src in ((self.pack, self.packed[j]), (self.scale, self.scales[j])):
                sp.dma_start(dst[:, s, j, :], src[bass.ds(n, 1), :, :].rearrange("n p c -> p (n c)")
                             ).then_inc(self.loaded[s], DMA)

    def unpack(self, dve, scratch, i, s, part, lowered=None):
        vector = self.nc.vector
        code, eight, size, twice, fourfold, sign = scratch
        done = self.waits * (2 * i + s)

        def steps(at, *made):
            for ins in made:
                ins.then_inc(self.unpack_steps, 1)
            dve.wait_ge(self.unpack_steps, done + at)

        if part == 0:
            dve.wait_ge(self.loaded[s], 6 * DMA * i + 6 * DMA)
            pack = self.pack[:, s, :, :]
            steps(2, vector.tensor_scalar(code[:, :, 0, :], pack, 15, None, ALU.bitwise_and),
                  vector.tensor_scalar(code[:, :, 1, :], pack, 4, 15, ALU.logical_shift_right, ALU.bitwise_and))
            steps(3, vector.tensor_scalar(eight[:], code[:], 8.0, 8.0, ALU.is_ge, ALU.mult))
        if part == 1:
            steps(4, vector.tensor_tensor(size[:], code[:], eight[:], ALU.subtract))
            steps(6, vector.tensor_scalar(twice[:], size[:], 2.0, -4.0, ALU.mult, ALU.add),
                  vector.tensor_scalar(fourfold[:], size[:], 4.0, -16.0, ALU.mult, ALU.add))
        if part == 2:
            steps(7, vector.tensor_tensor(twice[:], twice[:], fourfold[:], ALU.max))
            steps(9, vector.tensor_tensor(size[:], size[:], twice[:], ALU.max),
                  vector.tensor_scalar(sign[:], eight[:], -0.125, 0.5, ALU.mult, ALU.add))
        if part == 3:
            steps(10, vector.tensor_tensor(size[:], size[:], sign[:], ALU.mult))
            if lowered is not None:
                dve.wait_ge(lowered, 4 * (2 * i + s) - 4)
            for j in range(3):
                ins = vector.tensor_tensor(self.weight[:, s, j, :, :], size[:, j, :, :],
                                           self.scale[:, s, j, :].unsqueeze(1).broadcast_to([P, 2, D]), ALU.mult)
            ins.then_inc(self.weight_ready, 1)


def four_bit_stage(nc, weights, x_tok, xnT, s_tok, banks, out):
    weight, weight_ready = weights.weight, weights.weight_ready
    with ExitStack() as ctx:
        m = Core(nc, ctx)
        scratch = weights.scratch(m, "")
        gelu = m.sbuf("gelu3", [P, 2, HALF])
        inter = m.sbuf("inter3", [P, 2, N])
        gated = m.sbuf("gated3", [P, NT, D])
        widened = nc.alloc_semaphore("widened3")
        gelu_ready = nc.alloc_semaphore("gelu_ready3")
        inter_ready = nc.alloc_semaphore("inter_ready3")
        lowered = nc.alloc_semaphore("lowered3")
        gate_ready = nc.alloc_semaphore("gate_ready3")
        x_ready = nc.alloc_semaphore("x_ready3")
        stored = nc.alloc_semaphore("out_stored")
        cols = [slice(h * HALF, (h + 1) * HALF) for h in range(2)]
        rounds = PACKS3 // 2
        parts_after = ((0, 1), (2,), (3,), ())

        with nc.Block(no_gpsimd_drain=True) as block:

            @block.sync
            def _(sp):
                with sp.Fori(1, rounds) as i:
                    for s in range(2):
                        sp.wait_ge(weight_ready, 2 * i + s - 1)
                        weights.load(sp, 2 * i + s, s)
                for b in range(NT // 2):
                    sp.wait_ge(x_ready, 2 * b + 2)
                    sp.dma_start(out[:, 2 * b:2 * b + 2, :], x_tok[:, 2 * b:2 * b + 2, :]).then_inc(stored, DMA)
                sp.wait_ge(stored, DMA * (NT // 2))

            @block.tensor
            def _(pe):
                def widen(i, job):
                    s, tile, half = job // 4, job // 2 % 2, job % 2
                    if job % 4 == 0:
                        pe.wait_ge(weight_ready, 2 * i + s + 1)
                    for j in range(2):
                        for k in range(KD):
                            last = nc.tensor.matmul(banks[:, 4 + 2 * half + j, :], weight[:, s, j, k, tile * P:(tile + 1) * P],
                                                    xnT[:, k, cols[half]], start=(k == 0), stop=(k == KD - 1))
                    last.then_inc(widened, 1)

                def lower(i, job, first=False):
                    s, tile, half = job // 4, job // 2 % 2, job % 2
                    pe.wait_ge(inter_ready, 8 * i + job + 1)
                    for t in range(4 * half, 4 * half + 4):
                        last = nc.tensor.matmul(banks[:, t // 2, (t % 2) * D:(t % 2 + 1) * D],
                                                inter[:, tile, t * P:(t + 1) * P], weight[:, s, 2, tile, :],
                                                start=first and t % 2 == 0, stop=False, skip_group_check=True)
                    last.then_inc(lowered, 1)

                def round_(i, first=False, final=False):
                    for job in range(8):
                        if job < 7:
                            widen(i, job + 1)
                        elif not final:
                            widen(i + 1, 0)
                        lower(i, job, first and job < 2)

                widen(0, 0)
                round_(0, first=True)
                with pe.Fori(1, rounds - 1) as i:
                    round_(i)
                round_(rounds - 1, final=True)

            @block.scalar
            def _(act):
                with act.Fori(0, rounds) as i:
                    for job in range(8):
                        act.wait_ge(widened, 8 * i + job + 1)
                        nc.scalar.activation(gelu[:, job % 2, :], banks[:, 4 + 2 * (job % 2), :], ACT.Gelu_apprx_tanh
                                             ).then_inc(gelu_ready, 1)
                silu_sum(nc, act, gated, banks, lowered, 8 * rounds, gate_ready)

            @block.vector
            def _(dve):
                def multiply(i, job):
                    tile, half = job // 2 % 2, job % 2
                    dve.wait_ge(gelu_ready, 8 * i + job + 1)
                    nc.vector.tensor_tensor(inter[:, tile, cols[half]], gelu[:, half, :], banks[:, 5 + 2 * half, :],
                                            ALU.mult).then_inc(inter_ready, 1)

                def round_(i, first=False, final=False):
                    for job in range(8):
                        multiply(i, job)
                        for part in parts_after[job % 4]:
                            if job < 4:
                                weights.unpack(dve, scratch, i, 1, part, None if first else lowered)
                            elif not final:
                                weights.unpack(dve, scratch, i + 1, 0, part, lowered)

                round_(0, first=True)
                with dve.Fori(1, rounds - 1) as i:
                    round_(i)
                round_(rounds - 1, final=True)
                for b in range(NT // 2):
                    add_gated(nc, dve, b, x_tok, s_tok[:, 2 * b:2 * b + 2, :], gated, gate_ready, x_ready)


def build(nc, A, out):
    with ExitStack() as ctx:
        m = Core(nc, ctx)
        banks = ctx.enter_context(nc.psum_tensor("banks", [P, 8, BANK], F32))
        x_tok = m.sbuf("x_tok", [P, NT, D])
        xn_tok = m.sbuf("xn_tok", [P, NT, D])
        s_tok = m.sbuf("s_tok", [P, NT, D])
        xnT = m.sbuf("xnT", [P, KD, N])
        ident = m.sbuf("ident", [P, P])
        earlier = m.sbuf("earlier", [P, 16, 16])

        x_stats = m.sbuf("x_stats", [P, NT, 6])

        x_loaded = [nc.alloc_semaphore(f"x_loaded{half}") for half in range(2)]
        consts_loaded = nc.alloc_semaphore("consts_loaded")
        x_in = A["L0_attn_x"].rearrange("b t d -> (b t) d").rearrange("(n p) d -> p n d", p=P)
        half_tiles = [slice(0, NT // 2), slice(NT // 2, NT)]
        with nc.Block(no_gpsimd_drain=True) as block:
            @block.sync
            def _(sp):
                sp.dma_start(x_tok[:, half_tiles[0], :], x_in[:, half_tiles[0], :]).then_inc(x_loaded[0], DMA)
                sp.dma_start(ident[:, :], A["ident"]).then_inc(consts_loaded, DMA)
                sp.dma_start(earlier[:, :, :].rearrange("p a b -> p (a b)"), A["earlier"].partition_broadcast(P)
                             ).then_inc(consts_loaded, DMA)
                sp.wait_ge(consts_loaded, 2 * DMA)

            @block.scalar
            def _(act):
                act.dma_start(x_tok[:, half_tiles[1], :], x_in[:, half_tiles[1], :]).then_inc(x_loaded[1], DMA)

            @block.vector
            def _(dve):
                for half in range(2):
                    dve.wait_ge(x_loaded[half], DMA)
                    for t in range(NT)[half_tiles[half]]:
                        nc.vector.bn_stats(x_stats[:, t, :], x_tok[:, t, :])

        def new_layer():
            nc.clear_and_free_semaphores(nc.allocated_since(outer))
            nc.all_engine_barrier()

        outer = nc.snapshot_sems()
        with ExitStack() as layer:
            w, loads, late = load_layer0(Core(nc, layer), A)
            late_loaded = nc.alloc_semaphore("late_loaded0")
            norm_stage(nc, 0, x_tok, x_stats, xn_tok, xnT, ident, banks, loads, (late, late_loaded))
            scratch = nc.dram_tensor("probs_dram0", [8, N], F32).ap()
            recurrent_layer_stage(nc, w, (late_loaded, DMA * len(late)), (A["L0_ffn_gate_up_w"], A["L0_ffn_down_w"]),
                                  scratch, x_tok, x_stats, xnT, s_tok, ident, earlier, banks)
        new_layer()
        with ExitStack() as layer:
            inner = Core(nc, layer)
            w, loads, late = load_layer1(inner, A)
            y = inner.sbuf("y1", [P, NT, D])
            late_loaded = nc.alloc_semaphore("late_loaded1")
            norm_stage(nc, 1, x_tok, x_stats, xn_tok, xnT, ident, banks, loads, (late, late_loaded), rms_tok=y)
            rows = nc.dram_tensor("bc_dram", [2 * STATES, N], F32).ap()
            with ExitStack() as mixer:
                inner = Core(nc, mixer)
                keep = (inner.sbuf("skip", [P, MI, N]), inner.sbuf("xs", [P, MI, N]), inner.sbuf("delta", [P, MI, N]),
                        inner.sbuf("delta_x", [P, MI, N]), inner.sbuf("A", [P, MI, STATES]),
                        inner.sbuf("diag_D", [P, MI, P]))
                scan_prepare_stage(nc, w, (late_loaded, DMA * len(late)), xnT, ident, banks, keep, rows, y)
                scan_stage(nc, w, A["L1_ffn_up_w"], A["L1_ffn_down_w"], x_tok, x_stats, xn_tok, xnT, s_tok, ident, banks,
                           keep, rows, y)
        new_layer()
        last_layer = ctx.enter_context(ExitStack())
        w3, loads3 = load_layer3(Core(nc, last_layer), A)
        q_weight3 = s_tok[:, :, :].rearrange("p (k a) d -> p k (a d)", k=KD)
        with ExitStack() as layer:
            w, loads, late = load_layer2(Core(nc, layer), A)
            late_loaded = nc.alloc_semaphore("late_loaded2")
            norm_stage(nc, 2, x_tok, x_stats, xn_tok, xnT, ident, banks, loads, (late, late_loaded))
            xn_dram = nc.dram_tensor("xn_dram2", [N, D], F32).ap()
            y_dram = nc.dram_tensor("y_dram2", [N + P, D], F32).ap()
            inner = Core(nc, layer)
            tables = (inner.sbuf("slot_token", [P, EXPERTS2], U32), inner.sbuf("slot_target", [P, EXPERTS2], U32),
                      inner.sbuf("slot_weight", [P, EXPERTS2]))
            keep = (inner.sbuf("q2", [P, 2, N]), inner.sbuf("keys2", [P, 8, N]), inner.sbuf("v2", [P, NT, HEAD2]))
            route_stage(nc, w, (late_loaded, DMA * len(late)), xn_tok, xnT, ident, earlier, banks, tables, xn_dram,
                        y_dram, keep, s_tok)
            attention_and_expert_stage(nc, w, keep, (A["L2_ffn_w_gate"], A["L2_ffn_w_up"], A["L2_ffn_w_down"]), tables,
                                       xn_dram, y_dram, x_tok, x_stats, ident, banks, loads3, w3, q_weight3)
        new_layer()
        inner = Core(nc, last_layer)
        keep = (q_weight3, inner.sbuf("o_weight3", [P, UNITS3, D]),
                inner.sbuf("latT3", [P, N]), inner.sbuf("lat_tok3", [P, NT, LATENT]))
        weights = FourBitWeights(nc, inner, [A[f"L3_ffn_{name}_W_packed"] for name in ("gate", "up", "down")],
                                 [A[f"L3_ffn_{name}_scales"] for name in ("gate", "up", "down")])
        with ExitStack() as first:
            scratch = weights.scratch(Core(nc, first), "_first")
            norm_stage(nc, 3, x_tok, x_stats, xn_tok, xnT, ident, banks, [], parity=True,
                       beside=work_on_weights(nc, w3, banks, keep, weights, scratch))
            latent_prepare_stage(nc, w3, xnT, banks, keep, weights, scratch)
        latent_attention_stage(nc, xnT, s_tok, ident, banks, keep)
        four_bit_stage(nc, weights, x_tok, xnT, s_tok, banks,
                       out.rearrange("b t d -> (b t) d").rearrange("(n p) d -> p n d", p=P))


def load_layer0(m, A):
    w, loads, late = {}, [], []

    def add(name, shape, src, to=loads):
        w[name] = m.sbuf("w0_" + name, shape)
        to.append((w[name][:], src))

    add("W_in", [P, KD, D], by_feature(A["L0_attn_W_in"]), late)
    add("W_ga", [P, KD, P], by_feature(A["L0_gates_a"]), late)
    add("W_gx", [P, KD, P], by_feature(A["L0_gates_x"]), late)
    add("W_out", [P, KD, D], by_feature(A["L0_attn_W_out"]), late)
    add("b_in", [P, KD], A["L0_attn_b_in"])
    add("b_ga", [P, 1], A["L0_attn_b_ga"])
    add("b_gx", [P, 1], A["L0_attn_b_gx"])
    add("a_real", [P, 1], A["L0_attn_a_real"])
    add("a_imag", [P, 1], A["L0_attn_a_imag"])
    add("b_out", [P, D], A["L0_attn_b_out"].partition_broadcast(P), late)
    add("router_w", [P, KD, 8], by_feature(A["L0_ffn_router_w"]))
    add("shared_gate_w", [P, KD, P], by_feature(A["L0_ffn_shared_gate_w"]), late)
    add("shared_up_w", [P, KD, P], by_feature(A["L0_ffn_shared_up_w"]), late)
    add("shared_down_w", [P, 1, D], by_feature(A["L0_ffn_shared_down_w"]), late)
    return w, loads, late


def load_layer1(m, A):
    w, loads, late = {}, [], []

    def add(name, shape, src, to=loads):
        w[name] = m.sbuf("w1_" + name, shape)
        to.append((w[name][:], src))

    add("A_log", [P, MI, STATES], by_feature(A["L1_attn_A_log"]))
    add("W_D", [P, MI], A["L1_attn_W_D"])
    add("norm_w", [P, KD], A["L1_attn_norm_w"])
    add("W_in", [P, KD, INNER], by_feature(A["L1_attn_W_in"]), late)
    add("W_skip", [P, KD, INNER], by_feature(A["L1_attn_W_skip"]), late)
    add("conv_w", [P, MI, 4], A["L1_attn_conv_w"].rearrange("(k p) a j -> p k (a j)", p=P))
    add("conv_b", [P, MI], A["L1_attn_conv_b"])
    add("W_d1", [P, MI, P], by_feature(A["L1_attn_W_d1"]), late)
    add("W_BC", [P, MI, 2 * STATES], by_feature(A["L1_attn_W_BC"]), late)
    add("W_d2", [P, 1, INNER], by_feature(A["L1_attn_W_d2"]), late)
    add("b_d2", [P, MI], A["L1_attn_b_d2"])
    add("W_out", [P, MI, D], by_feature(A["L1_attn_W_out"]), late)
    add("gate_w", [P, KD, 8], by_feature(A["L1_ffn_gate_w"]), late)
    add("expert_weight", [P, KD, D], by_feature(A["L1_ffn_expert_weight"]), late)
    add("ln_gamma", [P, D], A["L1_ffn_ln_gamma"].partition_broadcast(P), late)
    add("ln_beta", [P, D], A["L1_ffn_ln_beta"].partition_broadcast(P), late)
    return w, loads, late


def load_layer2(m, A):
    w, loads, late = {}, [], []

    def add(name, shape, src, to=loads, part=lambda t: t[:]):
        w[name] = m.sbuf("w2_" + name, shape)
        to.append((part(w[name]), src))

    for name in ("Wq", "Wq_swap", "Wo"):
        add(name, [P, KD, D], by_feature(A["L2_attn_" + name]), late)
    add("Wk", [P, KD, P], by_feature(A["L2_attn_Wk"]))
    add("Wv", [P, KD, HEAD2], by_feature(A["L2_attn_Wv"]))
    add("gate_w", [P, KD, EXPERTS2], by_feature(A["L2_ffn_gate_w"]))
    add("sw_gate", [P, KD, SHARED2], by_feature(A["L2_ffn_sw_gate"]), late)
    add("sw_up", [P, KD, SHARED2], by_feature(A["L2_ffn_sw_up"]), late)
    full = SHARED2 // P
    add("sw_down", [P, full + 1, D], by_feature(A["L2_ffn_sw_down"][0:full * P, :]), late, part=lambda t: t[:, 0:full, :])
    late.append((w["sw_down"][0:SHARED2 - full * P, full, :], A["L2_ffn_sw_down"][full * P:, :]))
    for name in ("cos", "sin", "head_rows", "causal", "before", "slots", "token_place", "spare_row"):
        add(name, list(A[name].shape), A[name])
    return w, loads, late


def load_layer3(m, A):
    w, loads = {}, []

    def add(name, shape, src):
        w[name] = m.sbuf("w3_" + name, shape)
        loads.append((w[name][:], src))

    add("WqT", [P, HEADS3, D], by_feature(A["L3_attn_W_q"]))
    add("WupT", [P, HEADS3, LATENT], by_feature(A["L3_attn_W_kv_up"]))
    add("Wdown2", [P, KD, 2 * LATENT], by_feature(A["L3_attn_W_kv_down"]))
    add("Wo", [P, HEADS3, D], by_feature(A["L3_attn_W_o"]))
    return w, loads


COLUMNS = ("L0_attn_b_in", "L0_attn_b_ga", "L0_attn_b_gx", "L0_attn_a_real", "L0_attn_a_imag",
           "L1_attn_W_D", "L1_attn_norm_w", "L1_attn_conv_b", "L1_attn_b_d2")
TRANSPOSED = ("L1_attn_W_skip", "L1_attn_W_in", "L1_attn_W_d1", "L1_attn_W_d2", "L1_attn_W_out")


def block_diagonal(blocks):
    h, i, j = blocks.shape
    full = np.zeros((h, i, h, j), blocks.dtype)
    for n in range(h):
        full[n, :, n, :] = blocks[n]
    return full.reshape(h * i, h * j)


def laid_out(inputs):
    A = {name: np.ascontiguousarray(value) for name, value in inputs.items()}
    A["L0_gates_a"] = block_diagonal(A.pop("L0_attn_W_ga"))
    A["L0_gates_x"] = block_diagonal(A.pop("L0_attn_W_gx"))
    A["ident"] = np.eye(P, dtype=np.float32)
    A["earlier"] = np.tril(np.ones((16, 16), np.float32), -1).reshape(-1)
    for name in COLUMNS:
        A[name] = A[name].reshape(-1, P).T
    A["L1_attn_W_BC"] = np.concatenate([A.pop("L1_attn_W_Bm"), A.pop("L1_attn_W_Cm")]).T
    for name in TRANSPOSED:
        A[name] = A[name].T
    A["L2_attn_Wq_swap"] = A["L2_attn_Wq"][np.arange(D) ^ 1].T
    A["L2_attn_Wk"] = np.tile(A["L2_attn_Wk"], (8, 1)).T
    A["L2_attn_Wq"] = A["L2_attn_Wq"].T
    A["L2_attn_Wv"], A["L2_attn_Wo"] = A["L2_attn_Wv"].T, A["L2_attn_Wo"].T
    half = HEAD2 // 2
    theta = 1.0 / np.float32(10000.0) ** (np.arange(0, half, 2, dtype=np.float32) / np.float32(half))
    freq = np.arange(HEADS2, dtype=np.float32)[:, None] * theta.astype(np.float32)[None, :]
    head, place = np.arange(D) // HEAD2, np.arange(D) % half
    A["cos"] = np.cos(freq)[head, place // 2].reshape(KD, P).T
    A["sin"] = (np.sin(freq)[head, place // 2] * np.where(place % 2, 1, -1).astype(np.float32)).reshape(KD, P).T
    A["head_rows"] = np.repeat(np.eye(8, dtype=np.float32), HEAD2, axis=0)
    later = np.triu(np.full((P, P), -1e30, np.float32), 1)
    A["causal"] = np.concatenate([np.zeros((P, P), np.float32), later], axis=1)
    A["L2_ffn_gate_w"] = A["L2_ffn_gate_w"].T
    A["before"] = np.triu(np.ones((P, P), np.float32), 1)
    A["slots"] = np.tile(np.arange(CAPACITY, dtype=np.float32), (P, 1))
    token = np.arange(N).reshape(NT, P).T
    A["token_place"] = np.stack([token % P, token - token % P], axis=-1).astype(np.float32)
    A["spare_row"] = np.arange(N, N + P, dtype=np.float32)[:, None]
    parity = np.concatenate([np.arange(0, D, 2), np.arange(1, D, 2)])
    A["L3_attn_W_q"] = A["L3_attn_W_q"][parity].T
    A["L3_attn_W_kv_up"] = A["L3_attn_W_kv_up"].T
    A["L3_attn_W_kv_down"] = np.tile(A["L3_attn_W_kv_down"][parity], (1, 2))
    hidden = np.arange(MLP3).reshape(PACKS3, P, 2).transpose(0, 2, 1).reshape(PACKS3, 2 * P)
    for name in ("gate", "up"):
        A[f"L3_ffn_{name}_W_packed"] = A[f"L3_ffn_{name}_W_packed"][hidden].transpose(0, 2, 1)
        A[f"L3_ffn_{name}_scales"] = np.repeat(A[f"L3_ffn_{name}_scales"][hidden].transpose(0, 2, 1), 16, axis=1)
    A["L3_ffn_down_W_packed"] = A["L3_ffn_down_W_packed"].T.reshape(PACKS3, P, D)
    A["L3_ffn_down_scales"] = np.repeat(A["L3_ffn_down_scales"].T, 16, axis=0).reshape(PACKS3, P, D)
    return {name: np.ascontiguousarray(value) for name, value in A.items()}


def kernel(**inputs):
    import concourse.bacc as bacc
    from concourse.bass_utils import run_bass_kernel_spmd

    nc = bacc.Bacc("TRN2", target_bir_lowering=False, num_devices=1)
    arrays = laid_out(inputs)
    aps = {name: nc.dram_tensor("in_" + name, a.shape, mybir.dt.from_np(a.dtype), kind="ExternalInput").ap()
           for name, a in arrays.items()}
    out = nc.dram_tensor("out_dram", (BATCH, SEQ, D), F32, kind="ExternalOutput").ap()
    build(nc, aps, out)
    result = run_bass_kernel_spmd(nc, [{"in_" + name: a for name, a in arrays.items()}], core_ids=[0])
    return result.results[0]["out_dram"]
```
